# Optimizing a Trainium2 kernel written in Bass

```python
import numpy as np
import jax
import jax.numpy as jnp

def _softmax(x, axis=-1):
    return jax.nn.softmax(x, axis=axis)

def _gelu(x):
    return jax.nn.gelu(x, approximate=True)

def _silu(x):
    return jax.nn.silu(x)

def _sigmoid(x):
    return jax.nn.sigmoid(x)

def _layernorm(x, axis=-1, eps=1e-05):
    m = jnp.mean(x, axis=axis, keepdims=True)
    v = jnp.var(x, axis=axis, keepdims=True)
    return (x - m) / jnp.sqrt(v + eps)

def _scatter_add(tgt, idx, src, axis=0):
    return tgt.at[idx].add(src)

def _segment_sum(src, seg, n):
    return jax.ops.segment_sum(src, seg, n)
kernel_name = 'mk_gnn_ffn_d4_gnn_r8_875a5f'

def setup_inputs(seed: int=0):
    np.random.seed(seed)
    _w = jnp.asarray

    def _rec_inputs():
        import jax
        import jax.numpy as jnp
        _gk = jax.random.key(seed)
        x = -0.0001126 + 1 * jax.random.normal(jax.random.fold_in(_gk, 1), (3750, 256), jnp.float32)
        src = jax.random.randint(jax.random.fold_in(_gk, 2), (60000,), 0, 3750, jnp.int32)
        dst = jax.random.randint(jax.random.fold_in(_gk, 3), (60000,), 0, 3750, jnp.int32)
        _o = jnp.argsort(dst, stable=True)
        src = src[_o]
        dst = dst[_o]
        edge_attr_256 = -5.16925e-05 + 1.00005 * jax.random.normal(jax.random.fold_in(_gk, 13), (60000, 256), jnp.float32)
        return (x, src, dst, edge_attr_256)
    x, src, dst, edge_attr_256 = _rec_inputs()

    def _L0_gnn_setup():
        import jax, jax.numpy as jnp
        import numpy as np
        N = 3750
        E = 60000
        G = 256
        H = 8
        D = G // H
        SCALE = G ** (-0.5)
        LN_EPS = 1e-05

        def _segment_softmax(logits, seg, num_segments):
            m = jax.ops.segment_max(logits, seg, num_segments=num_segments)
            e = jnp.exp(logits - m[seg])
            z = jax.ops.segment_sum(e, seg, num_segments=num_segments)
            return e / z[seg]
        key = jax.random.key(seed)
        k0, k1, k2, k3 = jax.random.split(key, 4)
        s = jax.random.normal(k0, (N, G), dtype=jnp.float32)
        src = jax.random.randint(k1, (E,), 0, N, dtype=jnp.int32)
        dst = jax.random.randint(k2, (E,), 0, N, dtype=jnp.int32)
        Wqkv = jax.random.normal(k3, (G, 3 * G), dtype=jnp.float32) * G ** (-0.5)
        gamma = jnp.ones((G,), dtype=jnp.float32)
        beta = jnp.zeros((G,), dtype=jnp.float32)
        return {'s': s, 'Wqkv': Wqkv, 'gamma': gamma, 'beta': beta, 'src': src, 'dst': dst}
    _L0_gnn_all = _L0_gnn_setup()
    _L0_gnn_in = {k: v for k, v in _L0_gnn_all.items() if k in ('Wqkv', 'gamma', 'beta')}
    del _L0_gnn_all

    def _L0_ffn_setup():
        import jax, jax.numpy as jnp
        import numpy as np
        B, A = (512, 8)
        IN, OUT = (256, 256)
        SH1, SH2 = (256, 128)
        EH1, EH2 = (128, 64)
        E, TOPK = (4, 2)

        def _shared_mlp(x, W1, b1, W2, b2, W3, b3):
            h = jax.nn.relu(x @ W1 + b1)
            h = jax.nn.relu(h @ W2 + b2)
            return h @ W3 + b3

        def _experts_mlp(x, eW1, eb1, eW2, eb2, eW3, eb3):
            h = jax.nn.relu(jnp.einsum('baf,efh->ebah', x, eW1) + eb1[:, None, None, :])
            h = jax.nn.relu(jnp.einsum('ebah,ehg->ebag', h, eW2) + eb2[:, None, None, :])
            o = jnp.einsum('ebag,ego->ebao', h, eW3) + eb3[:, None, None, :]
            return jnp.moveaxis(o, 0, -1)
        key = jax.random.key(seed)
        ks = jax.random.split(key, 16)
        s = 0.05
        return {'x': jax.random.normal(ks[0], (B, A, IN), jnp.float32), 'sW1': jax.random.normal(ks[1], (IN, SH1), jnp.float32) * s, 'sb1': jnp.zeros((SH1,), jnp.float32), 'sW2': jax.random.normal(ks[2], (SH1, SH2), jnp.float32) * s, 'sb2': jnp.zeros((SH2,), jnp.float32), 'sW3': jax.random.normal(ks[3], (SH2, OUT), jnp.float32) * s, 'sb3': jnp.zeros((OUT,), jnp.float32), 'eW1': jax.random.normal(ks[4], (E, IN, EH1), jnp.float32) * s, 'eb1': jnp.zeros((E, EH1), jnp.float32), 'eW2': jax.random.normal(ks[5], (E, EH1, EH2), jnp.float32) * s, 'eb2': jnp.zeros((E, EH2), jnp.float32), 'eW3': jax.random.normal(ks[6], (E, EH2, OUT), jnp.float32) * s, 'eb3': jnp.zeros((E, OUT), jnp.float32), 'gW': jax.random.normal(ks[7], (IN, E), jnp.float32) * s, 'gb': jnp.zeros((E,), jnp.float32)}
    _L0_ffn_all = _L0_ffn_setup()
    _L0_ffn_in = {k: v for k, v in _L0_ffn_all.items() if k in ('sW1', 'sb1', 'sW2', 'sb2', 'sW3', 'sb3', 'eW1', 'eb1', 'eW2', 'eb2', 'eW3', 'eb3', 'gW', 'gb')}
    del _L0_ffn_all

    def _L1_gnn_setup():
        import jax, jax.numpy as jnp
        import numpy as np
        N = 12500
        E = 200000
        IN_FEATS = 256
        OUT_FEATS = 256
        MAXK = 32

        def _maxk(x, k):
            _, idx = jax.lax.top_k(x, k)
            rows = jnp.arange(x.shape[0])[:, None]
            mask = jnp.zeros_like(x).at[rows, idx].set(1.0)
            return x * mask
        key = jax.random.key(seed)
        k1, k2, k3, k4, k5 = jax.random.split(key, 5)
        feat = jax.random.normal(k1, (N, IN_FEATS), dtype=jnp.float32)
        W_self = jax.random.normal(k2, (IN_FEATS, OUT_FEATS), dtype=jnp.float32) * (1.0 / np.sqrt(IN_FEATS))
        W_neigh = jax.random.normal(k3, (IN_FEATS, OUT_FEATS), dtype=jnp.float32) * (1.0 / np.sqrt(IN_FEATS))
        src = jax.random.randint(k4, (E,), 0, N, dtype=jnp.int64)
        dst = jax.random.randint(k5, (E,), 0, N, dtype=jnp.int64)
        return {'feat': feat, 'W_self': W_self, 'W_neigh': W_neigh, 'src': src, 'dst': dst}
    _L1_gnn_all = _L1_gnn_setup()
    _L1_gnn_in = {k: v for k, v in _L1_gnn_all.items() if k in ('W_self', 'W_neigh')}
    del _L1_gnn_all

    def _L1_ffn_setup():
        import jax, jax.numpy as jnp
        import numpy as np
        B, S, D, E, H, K = (4, 512, 256, 8, 512, 2)
        key = jax.random.key(seed)
        ks = jax.random.split(key, 6)
        x = jax.random.normal(ks[0], (B, S, D), jnp.float32)
        Wg = jax.random.normal(ks[1], (D, E), jnp.float32) * 0.02
        bg = jnp.zeros((E,), jnp.float32)
        W1 = jax.random.normal(ks[2], (E, D, H), jnp.float32) * 0.02
        b1 = jnp.zeros((E, H), jnp.float32)
        W2 = jax.random.normal(ks[3], (E, H, D), jnp.float32) * 0.02
        b2 = jnp.zeros((E, D), jnp.float32)
        return {'x': x, 'Wg': Wg, 'bg': bg, 'W1': W1, 'b1': b1, 'W2': W2, 'b2': b2}
    _L1_ffn_all = _L1_ffn_setup()
    _L1_ffn_in = {k: v for k, v in _L1_ffn_all.items() if k in ('Wg', 'bg', 'W1', 'b1', 'W2', 'b2')}
    del _L1_ffn_all

    def _L2_gnn_setup():
        import jax, jax.numpy as jnp
        import numpy as np
        N = 6250
        E = 100000
        HIDDEN = 256
        HEADS = 8
        HEAD_DIM = HIDDEN // HEADS

        def _linear_params(key, fan_in, fan_out):
            k1, k2 = jax.random.split(key)
            s = 1.0 / np.sqrt(fan_in)
            W = jax.random.uniform(k1, (fan_in, fan_out), jnp.float32, -s, s)
            b = jax.random.uniform(k2, (fan_out,), jnp.float32, -s, s)
            return (W, b)
        key = jax.random.key(seed)
        ks = jax.random.split(key, 7)
        h = jax.random.normal(ks[0], (N, HIDDEN), jnp.float32)
        row = jnp.sort(jax.random.randint(ks[1], (E,), 0, N))
        col = jax.random.randint(ks[2], (E,), 0, N)
        Wq, bq = _linear_params(ks[3], HIDDEN, HIDDEN)
        Wk, bk = _linear_params(ks[4], HIDDEN, HIDDEN)
        Wv, bv = _linear_params(ks[5], HIDDEN, HIDDEN)
        Wo, bo = _linear_params(ks[6], HIDDEN, HIDDEN)
        return dict(h=h, row=row, col=col, Wq=Wq, bq=bq, Wk=Wk, bk=bk, Wv=Wv, bv=bv, Wo=Wo, bo=bo)
    _L2_gnn_all = _L2_gnn_setup()
    _L2_gnn_in = {k: v for k, v in _L2_gnn_all.items() if k in ('Wq', 'bq', 'Wk', 'bk', 'Wv', 'bv', 'Wo', 'bo')}
    del _L2_gnn_all

    def _L2_ffn_setup():
        import jax, jax.numpy as jnp
        import numpy as np
        NUM_EXPERTS = 8
        TOP_K = 2
        B, S, D = (8, 1024, 256)

        def _moe(tokens, router_w, w1, b1, w2, b2):
            N = tokens.shape[0]
            E = router_w.shape[0]
            logits = tokens.astype(jnp.float32) @ router_w.astype(jnp.float32).T
            probs = jax.nn.softmax(logits, axis=-1)
            rw, re = jax.lax.top_k(probs, TOP_K)
            if TOP_K > 1:
                rw = rw / jnp.maximum(rw.sum(-1, keepdims=True), 1e-12)
            rw = rw.astype(tokens.dtype)
            combine = jnp.zeros((N, E), tokens.dtype).at[jnp.arange(N)[:, None], re].set(rw)
            out = tokens
            for e in range(E):
                h = jax.nn.gelu(tokens @ w1[e] + b1[e], approximate=False)
                y = h @ w2[e] + b2[e]
                out = out + combine[:, e:e + 1] * y
            return out
        key = jax.random.key(seed)
        ks = jax.random.split(key, 4)
        scale = 1.0 / np.sqrt(D).astype(np.float32)
        return {'input_embeddings': jax.random.normal(ks[0], (B, S, D), jnp.float32), 'router_w': jax.random.normal(ks[1], (NUM_EXPERTS, D), jnp.float32) * scale, 'w1': jax.random.normal(ks[2], (NUM_EXPERTS, D, D), jnp.float32) * scale, 'b1': jnp.zeros((NUM_EXPERTS, D), jnp.float32), 'w2': jax.random.normal(ks[3], (NUM_EXPERTS, D, D), jnp.float32) * scale, 'b2': jnp.zeros((NUM_EXPERTS, D), jnp.float32)}
    _L2_ffn_all = _L2_ffn_setup()
    _L2_ffn_in = {k: v for k, v in _L2_ffn_all.items() if k in ('router_w', 'w1', 'b1', 'w2', 'b2')}
    del _L2_ffn_all

    def _L3_gnn_setup():
        import jax, jax.numpy as jnp
        import numpy as np
        N_NODES = 12500
        N_EDGES = 50000
        C = 256
        NUM_GRAPHS = 512
        EPS = 1e-05
        key = jax.random.key(seed)
        ks = jax.random.split(key, 12)
        x = jax.random.normal(ks[0], (N_NODES, C), dtype=jnp.float32)
        edge_index = jax.random.randint(ks[1], (2, N_EDGES), 0, N_NODES, dtype=jnp.int32)
        edge_attr = jax.random.normal(ks[2], (N_EDGES, C), dtype=jnp.float32)
        batch = jnp.sort(jax.random.randint(ks[3], (N_NODES,), 0, NUM_GRAPHS, dtype=jnp.int32))
        s1 = 1.0 / np.sqrt(C)
        s2 = 1.0 / np.sqrt(2 * C)
        W1 = jax.random.normal(ks[4], (C, 2 * C), dtype=jnp.float32) * s1
        b1 = jnp.zeros((2 * C,), dtype=jnp.float32)
        bn_gamma = jnp.ones((2 * C,), dtype=jnp.float32)
        bn_beta = jnp.zeros((2 * C,), dtype=jnp.float32)
        W2 = jax.random.normal(ks[5], (2 * C, C), dtype=jnp.float32) * s2
        b2 = jnp.zeros((C,), dtype=jnp.float32)
        ln_w = jnp.ones((C,), dtype=jnp.float32)
        ln_b = jnp.zeros((C,), dtype=jnp.float32)
        gn_w = jnp.ones((C,), dtype=jnp.float32)
        gn_b = jnp.zeros((C,), dtype=jnp.float32)
        gn_ms = jnp.ones((C,), dtype=jnp.float32)
        return dict(x=x, edge_index=edge_index, edge_attr=edge_attr, batch=batch, W1=W1, b1=b1, bn_gamma=bn_gamma, bn_beta=bn_beta, W2=W2, b2=b2, ln_w=ln_w, ln_b=ln_b, gn_w=gn_w, gn_b=gn_b, gn_ms=gn_ms)
    _L3_gnn_all = _L3_gnn_setup()
    _L3_gnn_in = {k: v for k, v in _L3_gnn_all.items() if k in ('W1', 'b1', 'bn_gamma', 'bn_beta', 'W2', 'b2', 'ln_w', 'ln_b', 'gn_w', 'gn_b', 'gn_ms')}
    del _L3_gnn_all

    def _L3_ffn_setup():
        import math
        import jax, jax.numpy as jnp
        import numpy as np
        CAPACITY_FACTOR = 1.25
        TOP_K = 2
        LN_EPS = 1e-05

        def _layer_norm(x, gamma, beta):
            mu = jnp.mean(x, axis=-1, keepdims=True)
            var = jnp.var(x, axis=-1, keepdims=True)
            return (x - mu) * jax.lax.rsqrt(var + LN_EPS) * gamma + beta
        key = jax.random.key(seed)
        ks = jax.random.split(key, 4)
        B, S, D, F, E = (8, 512, 256, 512, 8)
        x = jax.random.normal(ks[0], (B, S, D), dtype=jnp.float32)
        Wr = jax.random.normal(ks[1], (D, E), dtype=jnp.float32) / np.sqrt(D)
        br = jnp.zeros((E,), jnp.float32)
        W1 = jax.random.normal(ks[2], (E, D, F), dtype=jnp.float32) / np.sqrt(D)
        b1 = jnp.zeros((E, F), jnp.float32)
        W2 = jax.random.normal(ks[3], (E, F, D), dtype=jnp.float32) / np.sqrt(F)
        b2 = jnp.zeros((E, D), jnp.float32)
        gamma = jnp.ones((D,), jnp.float32)
        beta = jnp.zeros((D,), jnp.float32)
        return {'x': x, 'Wr': Wr, 'br': br, 'W1': W1, 'b1': b1, 'W2': W2, 'b2': b2, 'gamma': gamma, 'beta': beta}
    _L3_ffn_all = _L3_ffn_setup()
    _L3_ffn_in = {k: v for k, v in _L3_ffn_all.items() if k in ('Wr', 'br', 'W1', 'b1', 'W2', 'b2', 'gamma', 'beta')}
    del _L3_ffn_all
    return {'x': x, 'src': src, 'dst': dst, 'edge_attr_256': edge_attr_256, 'L0_gnn_Wqkv': _L0_gnn_in['Wqkv'], 'L0_gnn_gamma': _L0_gnn_in['gamma'], 'L0_gnn_beta': _L0_gnn_in['beta'], 'L0_ffn_sW1': _L0_ffn_in['sW1'], 'L0_ffn_sb1': _L0_ffn_in['sb1'], 'L0_ffn_sW2': _L0_ffn_in['sW2'], 'L0_ffn_sb2': _L0_ffn_in['sb2'], 'L0_ffn_sW3': _L0_ffn_in['sW3'], 'L0_ffn_sb3': _L0_ffn_in['sb3'], 'L0_ffn_eW1': _L0_ffn_in['eW1'], 'L0_ffn_eb1': _L0_ffn_in['eb1'], 'L0_ffn_eW2': _L0_ffn_in['eW2'], 'L0_ffn_eb2': _L0_ffn_in['eb2'], 'L0_ffn_eW3': _L0_ffn_in['eW3'], 'L0_ffn_eb3': _L0_ffn_in['eb3'], 'L0_ffn_gW': _L0_ffn_in['gW'], 'L0_ffn_gb': _L0_ffn_in['gb'], 'L1_gnn_W_self': _L1_gnn_in['W_self'], 'L1_gnn_W_neigh': _L1_gnn_in['W_neigh'], 'L1_ffn_Wg': _L1_ffn_in['Wg'], 'L1_ffn_bg': _L1_ffn_in['bg'], 'L1_ffn_W1': _L1_ffn_in['W1'], 'L1_ffn_b1': _L1_ffn_in['b1'], 'L1_ffn_W2': _L1_ffn_in['W2'], 'L1_ffn_b2': _L1_ffn_in['b2'], 'L2_gnn_Wq': _L2_gnn_in['Wq'], 'L2_gnn_bq': _L2_gnn_in['bq'], 'L2_gnn_Wk': _L2_gnn_in['Wk'], 'L2_gnn_bk': _L2_gnn_in['bk'], 'L2_gnn_Wv': _L2_gnn_in['Wv'], 'L2_gnn_bv': _L2_gnn_in['bv'], 'L2_gnn_Wo': _L2_gnn_in['Wo'], 'L2_gnn_bo': _L2_gnn_in['bo'], 'L2_ffn_router_w': _L2_ffn_in['router_w'], 'L2_ffn_w1': _L2_ffn_in['w1'], 'L2_ffn_b1': _L2_ffn_in['b1'], 'L2_ffn_w2': _L2_ffn_in['w2'], 'L2_ffn_b2': _L2_ffn_in['b2'], 'L3_gnn_W1': _L3_gnn_in['W1'], 'L3_gnn_b1': _L3_gnn_in['b1'], 'L3_gnn_bn_gamma': _L3_gnn_in['bn_gamma'], 'L3_gnn_bn_beta': _L3_gnn_in['bn_beta'], 'L3_gnn_W2': _L3_gnn_in['W2'], 'L3_gnn_b2': _L3_gnn_in['b2'], 'L3_gnn_ln_w': _L3_gnn_in['ln_w'], 'L3_gnn_ln_b': _L3_gnn_in['ln_b'], 'L3_gnn_gn_w': _L3_gnn_in['gn_w'], 'L3_gnn_gn_b': _L3_gnn_in['gn_b'], 'L3_gnn_gn_ms': _L3_gnn_in['gn_ms'], 'L3_ffn_Wr': _L3_ffn_in['Wr'], 'L3_ffn_br': _L3_ffn_in['br'], 'L3_ffn_W1': _L3_ffn_in['W1'], 'L3_ffn_b1': _L3_ffn_in['b1'], 'L3_ffn_W2': _L3_ffn_in['W2'], 'L3_ffn_b2': _L3_ffn_in['b2'], 'L3_ffn_gamma': _L3_ffn_in['gamma'], 'L3_ffn_beta': _L3_ffn_in['beta']}

def reference(x, src, dst, edge_attr_256, L0_gnn_Wqkv, L0_gnn_gamma, L0_gnn_beta, L0_ffn_sW1, L0_ffn_sb1, L0_ffn_sW2, L0_ffn_sb2, L0_ffn_sW3, L0_ffn_sb3, L0_ffn_eW1, L0_ffn_eb1, L0_ffn_eW2, L0_ffn_eb2, L0_ffn_eW3, L0_ffn_eb3, L0_ffn_gW, L0_ffn_gb, L1_gnn_W_self, L1_gnn_W_neigh, L1_ffn_Wg, L1_ffn_bg, L1_ffn_W1, L1_ffn_b1, L1_ffn_W2, L1_ffn_b2, L2_gnn_Wq, L2_gnn_bq, L2_gnn_Wk, L2_gnn_bk, L2_gnn_Wv, L2_gnn_bv, L2_gnn_Wo, L2_gnn_bo, L2_ffn_router_w, L2_ffn_w1, L2_ffn_b1, L2_ffn_w2, L2_ffn_b2, L3_gnn_W1, L3_gnn_b1, L3_gnn_bn_gamma, L3_gnn_bn_beta, L3_gnn_W2, L3_gnn_b2, L3_gnn_ln_w, L3_gnn_ln_b, L3_gnn_gn_w, L3_gnn_gn_b, L3_gnn_gn_ms, L3_ffn_Wr, L3_ffn_br, L3_ffn_W1, L3_ffn_b1, L3_ffn_W2, L3_ffn_b2, L3_ffn_gamma, L3_ffn_beta):
    import jax
    import jax.numpy as jnp

    def _L0_gnn_ref(s, Wqkv, gamma, beta, src, dst):
        import jax, jax.numpy as jnp
        import numpy as np
        N = 3750
        E = 60000
        G = 256
        H = 8
        D = G // H
        SCALE = G ** (-0.5)
        LN_EPS = 1e-05

        def _segment_softmax(logits, seg, num_segments):
            m = jax.ops.segment_max(logits, seg, num_segments=num_segments)
            e = jnp.exp(logits - m[seg])
            z = jax.ops.segment_sum(e, seg, num_segments=num_segments)
            return e / z[seg]
        mu = jnp.mean(s, axis=-1, keepdims=True)
        var = jnp.mean((s - mu) ** 2, axis=-1, keepdims=True)
        x = (s - mu) * jax.lax.rsqrt(var + LN_EPS) * gamma + beta
        qkv = x @ Wqkv
        q, k, v = jnp.split(qkv, 3, axis=-1)
        q = q.reshape(N, H, D)
        k = k.reshape(N, H, D)
        v = v.reshape(N, H, D)
        att = q[src] * k[dst] * SCALE
        att = _segment_softmax(att, dst, N)
        msg = v[src] * att
        rst = jax.ops.segment_sum(msg, dst, num_segments=N)
        return rst.reshape(N, G)

    def _L0_ffn_ref(x, sW1, sb1, sW2, sb2, sW3, sb3, eW1, eb1, eW2, eb2, eW3, eb3, gW, gb):
        import jax, jax.numpy as jnp
        import numpy as np
        B, A = (512, 8)
        IN, OUT = (256, 256)
        SH1, SH2 = (256, 128)
        EH1, EH2 = (128, 64)
        E, TOPK = (4, 2)

        def _shared_mlp(x, W1, b1, W2, b2, W3, b3):
            h = jax.nn.relu(x @ W1 + b1)
            h = jax.nn.relu(h @ W2 + b2)
            return h @ W3 + b3

        def _experts_mlp(x, eW1, eb1, eW2, eb2, eW3, eb3):
            h = jax.nn.relu(jnp.einsum('baf,efh->ebah', x, eW1) + eb1[:, None, None, :])
            h = jax.nn.relu(jnp.einsum('ebah,ehg->ebag', h, eW2) + eb2[:, None, None, :])
            o = jnp.einsum('ebag,ego->ebao', h, eW3) + eb3[:, None, None, :]
            return jnp.moveaxis(o, 0, -1)
        all_out = _experts_mlp(x, eW1, eb1, eW2, eb2, eW3, eb3)
        shared = _shared_mlp(x, sW1, sb1, sW2, sb2, sW3, sb3)
        gates = jax.nn.softmax(x @ gW + gb, axis=-1)
        topv, topi = jax.lax.top_k(gates, TOPK)
        topw = jax.nn.softmax(topv, axis=-1)
        sel = jnp.take_along_axis(all_out, topi[:, :, None, :], axis=-1)
        gated = jnp.sum(sel * topw[:, :, None, :], axis=-1)
        return shared + gated

    def _L1_gnn_ref(feat, W_self, W_neigh, src, dst):
        import jax, jax.numpy as jnp
        import numpy as np
        N = 12500
        E = 200000
        IN_FEATS = 256
        OUT_FEATS = 256
        MAXK = 32

        def _maxk(x, k):
            _, idx = jax.lax.top_k(x, k)
            rows = jnp.arange(x.shape[0])[:, None]
            mask = jnp.zeros_like(x).at[rows, idx].set(1.0)
            return x * mask
        n = feat.shape[0]
        h_self = feat @ W_self
        h_neigh = feat @ W_neigh
        h_sparse = _maxk(h_neigh, MAXK)
        msg = h_sparse[src]
        summed = jax.ops.segment_sum(msg, dst, num_segments=n)
        deg = jax.ops.segment_sum(jnp.ones((src.shape[0],), dtype=feat.dtype), dst, num_segments=n)
        neigh = summed / jnp.maximum(deg, 1.0)[:, None]
        return h_self + neigh

    def _L1_ffn_ref(x, Wg, bg, W1, b1, W2, b2):
        import jax, jax.numpy as jnp
        import numpy as np
        B, S, D, E, H, K = (4, 512, 256, 8, 512, 2)
        Bv, Sv, Dv = x.shape
        gate_scores = x @ Wg + bg
        _, idx = jax.lax.top_k(gate_scores, K)
        mask = jax.nn.one_hot(idx, E, dtype=x.dtype).sum(axis=-2)
        xf = x.reshape(-1, Dv)
        mf = mask.reshape(-1, E)
        h = jax.nn.gelu(jnp.einsum('td,edh->teh', xf, W1) + b1[None], approximate=False)
        y = jnp.einsum('teh,ehd->ted', h, W2) + b2[None]
        out = jnp.einsum('ted,te->td', y, mf)
        return out.reshape(Bv, Sv, Dv)

    def _L2_gnn_ref(h, row, col, Wq, bq, Wk, bk, Wv, bv, Wo, bo):
        import jax, jax.numpy as jnp
        import numpy as np
        N = 6250
        E = 100000
        HIDDEN = 256
        HEADS = 8
        HEAD_DIM = HIDDEN // HEADS

        def _linear_params(key, fan_in, fan_out):
            k1, k2 = jax.random.split(key)
            s = 1.0 / np.sqrt(fan_in)
            W = jax.random.uniform(k1, (fan_in, fan_out), jnp.float32, -s, s)
            b = jax.random.uniform(k2, (fan_out,), jnp.float32, -s, s)
            return (W, b)
        n = h.shape[0]
        scaling = HEAD_DIM ** (-0.5)
        q = (h @ Wq + bq).reshape(n, HEADS, HEAD_DIM) * scaling
        k = (h @ Wk + bk).reshape(n, HEADS, HEAD_DIM)
        v = (h @ Wv + bv).reshape(n, HEADS, HEAD_DIM)
        s = jnp.einsum('ehd,ehd->eh', q[row], k[col])
        m = jax.ops.segment_max(s, row, num_segments=n)
        p = jnp.exp(s - m[row])
        denom = jax.ops.segment_sum(p, row, num_segments=n)
        attn = p / denom[row]
        out = jax.ops.segment_sum(attn[:, :, None] * v[col], row, num_segments=n)
        return out.reshape(n, HIDDEN) @ Wo + bo

    def _L2_ffn_ref(input_embeddings, router_w, w1, b1, w2, b2):
        import jax, jax.numpy as jnp
        import numpy as np
        NUM_EXPERTS = 8
        TOP_K = 2
        B, S, D = (8, 1024, 256)

        def _moe(tokens, router_w, w1, b1, w2, b2):
            N = tokens.shape[0]
            E = router_w.shape[0]
            logits = tokens.astype(jnp.float32) @ router_w.astype(jnp.float32).T
            probs = jax.nn.softmax(logits, axis=-1)
            rw, re = jax.lax.top_k(probs, TOP_K)
            if TOP_K > 1:
                rw = rw / jnp.maximum(rw.sum(-1, keepdims=True), 1e-12)
            rw = rw.astype(tokens.dtype)
            combine = jnp.zeros((N, E), tokens.dtype).at[jnp.arange(N)[:, None], re].set(rw)
            out = tokens
            for e in range(E):
                h = jax.nn.gelu(tokens @ w1[e] + b1[e], approximate=False)
                y = h @ w2[e] + b2[e]
                out = out + combine[:, e:e + 1] * y
            return out
        b, s, d = input_embeddings.shape
        tokens = input_embeddings.reshape(b * s, d)
        return _moe(tokens, router_w, w1, b1, w2, b2).reshape(b, s, d)

    def _L3_gnn_ref(x, edge_index, edge_attr, batch, W1, b1, bn_gamma, bn_beta, W2, b2, ln_w, ln_b, gn_w, gn_b, gn_ms):
        import jax, jax.numpy as jnp
        import numpy as np
        N_NODES = 12500
        N_EDGES = 50000
        C = 256
        NUM_GRAPHS = 512
        EPS = 1e-05
        src, dst = (edge_index[0], edge_index[1])
        msg = jax.nn.relu(x[src] + edge_attr)
        agg = jnp.zeros_like(x).at[dst].add(msg)
        h = x + agg
        h = h @ W1 + b1
        mu = jnp.mean(h, axis=0)
        var = jnp.mean((h - mu) ** 2, axis=0)
        h = (h - mu) / jnp.sqrt(var + EPS) * bn_gamma + bn_beta
        h = jax.nn.relu(h) @ W2 + b2
        cnt = jax.ops.segment_sum(jnp.ones((h.shape[0],), h.dtype), batch, NUM_GRAPHS)
        denom = jnp.maximum(cnt, 1.0) * C
        mean_g = jax.ops.segment_sum(h.sum(axis=1), batch, NUM_GRAPHS) / denom
        h = h - mean_g[batch][:, None]
        var_g = jax.ops.segment_sum((h * h).sum(axis=1), batch, NUM_GRAPHS) / denom
        h = h * jax.lax.rsqrt(var_g + EPS)[batch][:, None] * ln_w + ln_b
        cnt_c = jnp.maximum(cnt, 1.0)[:, None]
        mean = jax.ops.segment_sum(h, batch, NUM_GRAPHS) / cnt_c
        out = h - mean[batch] * gn_ms
        var2 = jax.ops.segment_sum(out * out, batch, NUM_GRAPHS) / cnt_c
        out = out * jax.lax.rsqrt(var2 + EPS)[batch] * gn_w + gn_b
        out = jax.nn.relu(out)
        return x + out

    def _L3_ffn_ref(x, Wr, br, W1, b1, W2, b2, gamma, beta):
        import math
        import jax, jax.numpy as jnp
        import numpy as np
        CAPACITY_FACTOR = 1.25
        TOP_K = 2
        LN_EPS = 1e-05

        def _layer_norm(x, gamma, beta):
            mu = jnp.mean(x, axis=-1, keepdims=True)
            var = jnp.var(x, axis=-1, keepdims=True)
            return (x - mu) * jax.lax.rsqrt(var + LN_EPS) * gamma + beta
        B, S, D = x.shape
        E = Wr.shape[1]
        N = B * S
        K = TOP_K
        logits = jnp.mean(x, axis=1) @ Wr + br
        routing_weights = jax.nn.softmax(logits, axis=-1)
        capacity = float(math.ceil(N * CAPACITY_FACTOR / E))
        expected_loads = routing_weights.sum(axis=0) * (N / B)
        scale = jnp.where(expected_loads > capacity, capacity / expected_loads, 1.0)
        routing_weights = jax.nn.softmax(routing_weights * scale, axis=-1)
        rw_tok = jnp.broadcast_to(routing_weights[:, None, :], (B, S, E)).reshape(N, E)
        top_w, top_i = jax.lax.top_k(rw_tok, K)
        top_w = jax.nn.softmax(top_w, axis=-1)
        xf = x.reshape(N, D)
        h = jax.nn.gelu(jnp.einsum('nd,edf->enf', xf, W1) + b1[:, None, :], approximate=False)
        y = jnp.einsum('enf,efd->end', h, W2) + b2[:, None, :]
        w_dense = jnp.zeros((N, E), x.dtype).at[jnp.arange(N)[:, None], top_i].add(top_w)
        out = jnp.einsum('ne,end->nd', w_dense, y).reshape(B, S, D)
        out = _layer_norm(out + x, gamma, beta)
        return out
    edge_index = jnp.stack([src, dst])
    batch0 = jnp.zeros((3750,), jnp.int32)
    x = x + _L0_gnn_ref(_layernorm(x, axis=-1), L0_gnn_Wqkv, L0_gnn_gamma, L0_gnn_beta, src, dst)
    x = x + _L0_ffn_ref(_layernorm(x, axis=-1)[None], L0_ffn_sW1, L0_ffn_sb1, L0_ffn_sW2, L0_ffn_sb2, L0_ffn_sW3, L0_ffn_sb3, L0_ffn_eW1, L0_ffn_eb1, L0_ffn_eW2, L0_ffn_eb2, L0_ffn_eW3, L0_ffn_eb3, L0_ffn_gW, L0_ffn_gb)[0]
    x = x + _L1_gnn_ref(_layernorm(x, axis=-1), L1_gnn_W_self, L1_gnn_W_neigh, src, dst)
    x = x + _L1_ffn_ref(_layernorm(x, axis=-1)[None], L1_ffn_Wg, L1_ffn_bg, L1_ffn_W1, L1_ffn_b1, L1_ffn_W2, L1_ffn_b2)[0]
    x = x + _L2_gnn_ref(_layernorm(x, axis=-1), src, dst, L2_gnn_Wq, L2_gnn_bq, L2_gnn_Wk, L2_gnn_bk, L2_gnn_Wv, L2_gnn_bv, L2_gnn_Wo, L2_gnn_bo)
    x = x + _L2_ffn_ref(_layernorm(x, axis=-1)[None], L2_ffn_router_w, L2_ffn_w1, L2_ffn_b1, L2_ffn_w2, L2_ffn_b2)[0]
    x = x + _L3_gnn_ref(_layernorm(x, axis=-1), edge_index, edge_attr_256, batch0, L3_gnn_W1, L3_gnn_b1, L3_gnn_bn_gamma, L3_gnn_bn_beta, L3_gnn_W2, L3_gnn_b2, L3_gnn_ln_w, L3_gnn_ln_b, L3_gnn_gn_w, L3_gnn_gn_b, L3_gnn_gn_ms)
    x = x + _L3_ffn_ref(_layernorm(x, axis=-1)[None], L3_ffn_Wr, L3_ffn_br, L3_ffn_W1, L3_ffn_b1, L3_ffn_W2, L3_ffn_b2, L3_ffn_gamma, L3_ffn_beta)[0]
    return x

_drawn_inputs = setup_inputs


def setup_inputs(seed=0):
    import zlib

    import numpy as np

    out = dict(_drawn_inputs(seed))
    spreads = {'L0_gnn_gamma': (1.0, 0.2),
     'L0_gnn_beta': (0.0, 0.1),
     'L0_ffn_sb1': (0.0, 0.1),
     'L0_ffn_sb2': (0.0, 0.1),
     'L0_ffn_sb3': (0.0, 0.1),
     'L0_ffn_eb1': (0.0, 0.381),
     'L0_ffn_eb2': (0.0, 0.1),
     'L0_ffn_eb3': (0.0, 0.1),
     'L0_ffn_gb': (0.0, 0.1),
     'L1_ffn_bg': (0.0, 0.1),
     'L1_ffn_b1': (0.0, 0.1),
     'L1_ffn_b2': (0.0, 0.1),
     'L2_ffn_b1': (0.0, 0.408),
     'L2_ffn_b2': (0.0, 0.269),
     'L3_gnn_b1': (0.0, 2.0),
     'L3_gnn_bn_gamma': (1.0, 0.2),
     'L3_gnn_bn_beta': (0.0, 0.476),
     'L3_gnn_b2': (0.0, 0.8),
     'L3_gnn_ln_w': (1.0, 0.6),
     'L3_gnn_ln_b': (0.0, 0.8),
     'L3_gnn_gn_w': (1.0, 0.2),
     'L3_gnn_gn_b': (0.0, 0.397),
     'L3_gnn_gn_ms': (1.0, 0.2),
     'L3_ffn_br': (0.0, 0.8),
     'L3_ffn_b1': (0.0, 0.795),
     'L3_ffn_b2': (0.0, 0.528),
     'L3_ffn_gamma': (1.0, 0.2),
     'L3_ffn_beta': (0.0, 0.379)}
    factors = {'L2_gnn_bq': 32.101, 'L2_gnn_bk': 200.0, 'L2_gnn_bv': 3.331}
    for name, (base, spread) in spreads.items():
        noise = np.random.default_rng([zlib.crc32(name.encode()), seed]).standard_normal(out[name].shape)
        drawn = base * np.exp(spread * noise) if base else spread * noise
        out[name] = jnp.asarray(drawn.astype(out[name].dtype))
    for name, factor in factors.items():
        out[name] = (out[name] * factor).astype(out[name].dtype)
    return out
```

```python
import concourse.bass as bass
from concourse import mybir
from contextlib import ExitStack

F32 = mybir.dt.float32
BF16 = mybir.dt.bfloat16
I32 = mybir.dt.int32
ALU = mybir.AluOpType
ACT = mybir.ActivationFunctionType
AX = mybir.AxisListType

P = 128
N = 3750
E = 60000
G = 256
H = 8
D = G // H
NT = -(-N // P)
NPAD = NT * P
LAST = N - (NT - 1) * P
LANES = 120
STEPS = E // LANES
B = 5
TURNS = STEPS // (2 * B)
NONE = -1.0e30
EPS = 1e-5
TB = 3
NB = NT // TB
BC = TB * P


class Chain:

    def __init__(self, eng, sem):
        self.eng, self.sem, self.base, self.n, self.turn, self.per = eng, sem, 0, 0, None, 0

    def __call__(self, ins):
        self.n += 1
        ins.then_inc(self.sem, 1)
        self.eng.wait_ge(self.sem, self.value())

    def value(self):
        if self.turn is None:
            return self.base + self.n
        return self.turn * self.per + (self.base + self.n)

    def enter(self, turn, per):
        self.base, self.n, self.turn, self.per = self.base + self.n, 0, turn, per

    def leave(self, turns):
        assert self.n == self.per, (self.n, self.per)
        self.base, self.n, self.turn = self.base + turns * self.per, 0, None


def tables_made(pool, r):
    pool.wait_ge(r.made, 1)


class Scope:

    def __init__(self, nc, tag):
        self.nc, self.tag, self.ctx, self.taken = nc, tag, ExitStack(), []

    def __enter__(self):
        return self

    def __exit__(self, *a):
        self.ctx.__exit__(*a)
        if self.taken and a[0] is None:
            self.nc.clear_and_free_semaphores(self.taken)
            self.nc.all_engine_barrier()

    def sb(self, name, shape, dt=F32):
        return self.ctx.enter_context(self.nc.sbuf_tensor(f"{self.tag}_{name}", shape, dt))

    def ps(self, name, shape, dt=F32):
        return self.ctx.enter_context(self.nc.psum_tensor(f"{self.tag}_{name}", shape, dt))

    def sem(self, name):
        self.taken.append(self.nc.alloc_semaphore(f"{self.tag}_{name}"))
        return self.taken[-1]

    def sems(self, name, n):
        return [self.sem(f"{name}{i}") for i in range(n)]

    def block(self):
        return self.ctx.enter_context(self.nc.Block())


class Resident:
    pass


class Order:
    pass


def bcast(ap, shape):
    return ap.broadcast_to(shape)


def load_constants(nc, r, x, src, dst):
    with Scope(nc, "load") as s:
        zeroed, loaded, made, eyed = s.sem("zeroed"), s.sem("loaded"), s.sem("made"), s.sem("eyed")
        block = s.block()

        @block.sync
        def _(sp):
            sp.dma_start(r.x[:, 0:NT - 1, :], x[0:(NT - 1) * P, :].rearrange("(t p) f -> p t f", p=P)).then_inc(loaded, 16)
            sp.wait_ge(zeroed, 1)
            sp.dma_start(r.x[0:LAST, NT - 1, :], x[(NT - 1) * P:N, :]).then_inc(loaded, 16)
            sp.dma_start(r.by_dst.far[:, 0:STEPS], src.rearrange("(p j) -> p j", p=LANES)).then_inc(loaded, 16)
            sp.dma_start(r.by_dst.key[:, 0:STEPS], dst.rearrange("(p j) -> p j", p=LANES)).then_inc(loaded, 16)
            sp.wait_ge(loaded, 64)

        @block.vector
        def _(dve):
            nc.vector.memset(r.x[:, NT - 1, :], 0.0).then_inc(zeroed, 1)
            nc.vector.memset(r.ones[:, :], 1.0)
            nc.vector.memset(r.wide_ones[:, :], 1.0)
            for o in (r.by_dst, r.by_src):
                nc.vector.memset(o.key[:, STEPS:], 0)
                last = nc.vector.memset(o.far[:, STEPS:], 0)
            last.then_inc(r.made, 1)

        @block.gpsimd
        def _(pool):
            nc.gpsimd.memset(r.eye[:, :], 0.0).then_inc(made, 1)
            nc.gpsimd.memset(r.below[:, :], 1.0).then_inc(made, 1)
            nc.gpsimd.memset(r.above[:, :], 1.0).then_inc(made, 1)
            pool.wait_ge(made, 3)
            nc.gpsimd.affine_select(out=r.eye[:, :], in_=r.eye[:, :], compare_op=ALU.not_equal, fill=1.0,
                                    base=0, pattern=[[-1, P]], channel_multiplier=1)
            nc.gpsimd.affine_select(out=r.below[:, :], in_=r.below[:, :], compare_op=ALU.is_gt, fill=0.0,
                                    base=0, pattern=[[-1, P]], channel_multiplier=1)
            nc.gpsimd.affine_select(out=r.above[:, :], in_=r.above[:, :], compare_op=ALU.is_gt, fill=0.0,
                                    base=0, pattern=[[1, P]], channel_multiplier=-1)
            nc.gpsimd.iota(r.column[:, :], pattern=[[1, P]], base=0, channel_multiplier=0,
                           allow_small_or_imprecise_dtypes=True)
            nc.gpsimd.iota(r.partition[:, :], pattern=[[0, 1]], base=0, channel_multiplier=1,
                           allow_small_or_imprecise_dtypes=True).then_inc(eyed, 1)


def count_keys(nc, r, o, tag, hist, key, keep):
    with Scope(nc, tag) as s:
        part = s.sb("part", [LANES, STEPS], I32)
        lo = s.sb("lo", [LANES, STEPS])
        hi = s.sb("hi", [LANES, STEPS])
        one_lo = s.sb("one_lo", [LANES, 2, B, P], BF16)
        one_hi = s.sb("one_hi", [LANES, 2, B, NT], BF16)
        count = s.sb("count", [P, NT])
        start = s.sb("start", [P, NT])
        total = s.sb("total", [P, NT + 1])
        end = s.sb("end", [P, NT])
        lane = s.sb("lane", [P, NT])
        lane_i = s.sb("lane_i", [P, NT], I32)
        t1 = s.sb("t1", [P, NT])
        t2 = s.sb("t2", [P, NT])
        ps = [s.ps(f"ps{k}", [P, B * NT]) for k in range(2)]
        ps_start = s.ps("ps_start", [P, 2 * NT])
        chain_sem, ready, counted = s.sem("chain"), s.sems("ready", 2), s.sems("counted", 2)
        kept = s.sems("kept", 2)
        summed, prefixed = s.sem("summed"), s.sem("prefixed")
        block = s.block()

        @block.vector
        def _(dve):
            link = Chain(dve, chain_sem)
            link(nc.vector.tensor_scalar(part[:, :], key[:, 0:STEPS], 7, None, ALU.arith_shift_right))
            link(nc.vector.tensor_copy(hi[:, :], part[:, :]))
            link(nc.vector.tensor_scalar(part[:, :], key[:, 0:STEPS], P - 1, None, ALU.bitwise_and))
            link(nc.vector.tensor_copy(lo[:, :], part[:, :]))
            with dve.Fori(0, TURNS) as i:
                for k in range(2):
                    j = (2 * i + k) * B
                    dve.wait_ge(counted[k], i)
                    nc.vector.tensor_tensor(
                        one_lo[:, k, :, :], r.column[0:LANES, :].unsqueeze(1).broadcast_to([LANES, B, P]),
                        lo[:, bass.ds(j, B)].unsqueeze(2).broadcast_to([LANES, B, P]), ALU.is_equal)
                    nc.vector.tensor_tensor(
                        one_hi[:, k, :, :], r.column[0:LANES, 0:NT].unsqueeze(1).broadcast_to([LANES, B, NT]),
                        hi[:, bass.ds(j, B)].unsqueeze(2).broadcast_to([LANES, B, NT]), ALU.is_equal).then_inc(ready[k], 1)
                    dve.wait_ge(counted[k], i + 1)
                    nc.vector.tensor_copy(hist[:, bass.ds(j + 1, B), :].rearrange("p a b -> p (a b)"), ps[k][:, :]).then_inc(kept[k], 1)
            for k in range(2):
                dve.wait_ge(kept[k], TURNS)
            link(nc.vector.tensor_reduce(count[:, :], hist[:, 1:, :].rearrange("p j h -> p h j"), AX.X, ALU.add))
            nc.vector.tensor_copy(o.count[:, :], count[:, :]).then_inc(summed, 1)
            dve.wait_ge(prefixed, 1)
            link(nc.vector.memset(total[:, 0:1], 0.0))
            link(nc.vector.tensor_tensor_scan(total[:, 1:NT + 1], r.ones[:, 0:NT], ps_start[:, NT:2 * NT], 0.0, ALU.mult, ALU.add))
            link(nc.vector.tensor_tensor(start[:, :], total[:, 0:NT], ps_start[:, 0:NT], ALU.add))
            link(nc.vector.tensor_tensor(end[:, :], start[:, :], count[:, :], ALU.add))
            link(nc.vector.tensor_scalar(end[:, :], end[:, :], -1.0, 0.0, ALU.add, ALU.max))
            link(nc.vector.tensor_scalar(lane_i[:, :], end[:, :], 1.0 / STEPS, None, ALU.mult))
            link(nc.vector.tensor_copy(lane[:, :], lane_i[:, :]))
            link(nc.vector.tensor_scalar(t1[:, :], lane[:, :], float(STEPS), None, ALU.mult))
            link(nc.vector.tensor_tensor(t2[:, :], t1[:, :], end[:, :], ALU.is_gt))
            link(nc.vector.tensor_tensor(lane[:, :], lane[:, :], t2[:, :], ALU.subtract))
            link(nc.vector.tensor_scalar(t1[:, :], lane[:, :], float(STEPS), float(STEPS), ALU.mult, ALU.add))
            link(nc.vector.tensor_tensor(t2[:, :], t1[:, :], end[:, :], ALU.is_le))
            link(nc.vector.tensor_tensor(lane[:, :], lane[:, :], t2[:, :], ALU.add))
            link(nc.vector.tensor_scalar(t1[:, :], lane[:, :], float(STEPS), None, ALU.mult))
            link(nc.vector.tensor_tensor(t1[:, :], start[:, :], t1[:, :], ALU.is_lt))
            link(nc.vector.tensor_scalar(t2[:, :], count[:, :], 0.0, None, ALU.is_gt))
            link(nc.vector.tensor_tensor(t1[:, :], t1[:, :], t2[:, :], ALU.mult))
            link(nc.vector.tensor_scalar(lane[:, :], lane[:, :], -1.0 - LANES, None, ALU.add))
            link(nc.vector.tensor_tensor(lane[:, :], lane[:, :], t1[:, :], ALU.mult))
            link(nc.vector.tensor_scalar(o.carry_row[:, :], lane[:, :], float(LANES), None, ALU.add))
            link(nc.vector.tensor_scalar(end[:, :], end[:, :], -float(E), None, ALU.add))
            link(nc.vector.tensor_tensor(end[:, :], end[:, :], t2[:, :], ALU.mult))
            link(nc.vector.tensor_scalar(o.end_row[:, :], end[:, :], float(E), None, ALU.add))
            if keep:
                link(nc.vector.tensor_copy(hist[:, 0, :], start[:, :]))
                for h in range(NT):
                    link(nc.vector.tensor_tensor_scan(hist[:, 1:, h], r.wide_ones[:, :], hist[:, 1:, h],
                                                      start[:, h:h + 1], ALU.mult, ALU.add))

        @block.tensor
        def _(pe):
            with pe.Fori(0, TURNS) as i:
                for k in range(2):
                    pe.wait_ge(ready[k], i + 1)
                    pe.wait_ge(kept[k], i)
                    for b in range(B):
                        last = nc.tensor.matmul(ps[k][:, b * NT:(b + 1) * NT], one_lo[:, k, b, :], one_hi[:, k, b, :],
                                                start=True, stop=True)
                    last.then_inc(counted[k], 1)
            pe.wait_ge(summed, 1)
            nc.tensor.matmul(ps_start[:, 0:NT], r.above[:, :], count[:, :], start=True, stop=True)
            nc.tensor.matmul(ps_start[:, NT:2 * NT], r.ones[:, :], count[:, :], start=True, stop=True).then_inc(prefixed, 1)


def sort_edges(nc, r, o, key, far, hist, keys_t, sorted_edges):
    with Scope(nc, "sort") as s:
        lof = s.sb("lof", [LANES, STEPS])
        keyf = s.sb("keyf", [LANES, STEPS])
        part = s.sb("part", [LANES, STEPS], I32)
        hi = s.sb("hi", [LANES, STEPS])
        rows = s.sb("rows", [P, 4, 2, LANES])
        keyrow = s.sb("keyrow", [P, 2, B, 2, LANES])
        one_lo = s.sb("one_lo", [P, 2, B, LANES])
        one_hi = s.sb("one_hi", [LANES, B, NT])
        picked = s.sb("picked", [LANES, B, NT])
        scratch = s.sb("scratch", [LANES, LANES])
        base = s.sb("base", [LANES, B])
        rank = s.sb("rank", [LANES, B])
        place = s.sb("place", [LANES, 2, B], I32)
        record = s.sb("record", [LANES, 2, B, 2], I32)
        flip = [s.ps(f"flip{k}", [P, 4, P]) for k in range(2)]
        ps = [s.ps(f"ps{k}", [LANES, B * NT]) for k in range(2)]
        chain_sem, split, flipped, copied, stored = s.sem("chain"), s.sem("split"), s.sem("flipped"), s.sem("copied"), s.sem("stored")
        came, hot, found, placed, sent = s.sems("came", 2), s.sems("hot", 2), s.sems("found", 2), s.sems("placed", 2), s.sems("sent", 2)
        block = s.block()
        CH = STEPS // 4

        @block.vector
        def _(dve):
            link = Chain(dve, chain_sem)
            link(nc.vector.tensor_scalar(part[:, :], key[:, 0:STEPS], 7, None, ALU.arith_shift_right))
            link(nc.vector.tensor_copy(hi[:, :], part[:, :]))
            link(nc.vector.tensor_scalar(part[:, :], key[:, 0:STEPS], P - 1, None, ALU.bitwise_and))
            link(nc.vector.tensor_copy(keyf[:, :], key[:, 0:STEPS]))
            nc.vector.tensor_copy(lof[:, :], part[:, :]).then_inc(split, 1)
            dve.wait_ge(flipped, 1)
            link(nc.vector.tensor_copy(rows[0:CH, :, 0, :], flip[0][0:CH, :, 0:LANES]))
            nc.vector.tensor_copy(rows[0:CH, :, 1, :], flip[1][0:CH, :, 0:LANES]).then_inc(copied, 1)
            with dve.Fori(0, TURNS) as i:
                link.enter(i, 2 * 10)
                for k in range(2):
                    j = (2 * i + k) * B
                    dve.wait_ge(came[k], i * 16 + 16)
                    nc.vector.tensor_scalar(one_lo[:, k, :, :], keyrow[:, k, :, 1, :], r.partition[:, 0:1], None, ALU.is_equal).then_inc(hot[k], 1)
                    link(nc.vector.tensor_tensor(
                        one_hi[:, :, :], r.column[0:LANES, 0:NT].unsqueeze(1).broadcast_to([LANES, B, NT]),
                        hi[:, bass.ds(j, B)].unsqueeze(2).broadcast_to([LANES, B, NT]), ALU.is_equal))
                    for b in range(B):
                        link(nc.vector.scalar_tensor_tensor(
                            scratch[:, :], keyrow[0:LANES, k, b, 0, :], keyf[:, bass.ds(j + b, 1)], r.below[0:LANES, 0:LANES],
                            ALU.is_equal, ALU.mult, accum_out=rank[:, b:b + 1]))
                    dve.wait_ge(found[k], i + 1)
                    link(nc.vector.tensor_tensor(picked[:, :, :].rearrange("p a b -> p (a b)"), ps[k][:, :],
                                                 one_hi[:, :, :].rearrange("p a b -> p (a b)"), ALU.mult))
                    link(nc.vector.tensor_reduce(base[:, :], picked[:, :, :], AX.X, ALU.add))
                    dve.wait_ge(sent[k], i * (16 * B))
                    nc.vector.tensor_tensor(place[:, k, :], base[:, :], rank[:, :], ALU.add)
                    link(nc.vector.tensor_copy(record[:, k, :, 0], key[:, bass.ds(j, B)]))
                    nc.vector.tensor_copy(record[:, k, :, 1], far[:, bass.ds(j, B)]).then_inc(placed[k], 1)
                    link(nc.vector.memset(scratch[0:1, 0:1], 0.0))
                link.leave(TURNS)

        @block.tensor
        def _(pe):
            pe.wait_ge(split, 1)
            for c in range(4):
                nc.tensor.transpose(flip[0][0:CH, c, 0:LANES], keyf[:, c * CH:(c + 1) * CH], r.eye[0:LANES, 0:LANES])
                last = nc.tensor.transpose(flip[1][0:CH, c, 0:LANES], lof[:, c * CH:(c + 1) * CH], r.eye[0:LANES, 0:LANES])
            last.then_inc(flipped, 1)
            with pe.Fori(0, TURNS) as i:
                for k in range(2):
                    pe.wait_ge(hot[k], i + 1)
                    pe.wait_ge(placed[k], i)
                    for b in range(B):
                        last = nc.tensor.matmul(ps[k][:, b * NT:(b + 1) * NT], one_lo[:, k, b, :],
                                                hist[:, bass.ds((2 * i + k) * B + b, 1), :].rearrange("p a b -> p (a b)"), start=True, stop=True)
                    last.then_inc(found[k], 1)

        @block.sync
        def _(sp):
            sp.wait_ge(copied, 1)
            sp.dma_start(keys_t.rearrange("(c j) k l -> j c k l", c=4), rows[0:CH, :, :, :]).then_inc(stored, 16)
            sp.wait_ge(stored, 16)
            with sp.Fori(0, TURNS) as i:
                for k in range(2):
                    sp.wait_ge(placed[k], i)
                    sp.dma_start(keyrow[:, k, :, :, :].rearrange("p a b c -> p (a b c)"),
                                 keys_t[bass.ds((2 * i + k) * B, B), :, :].rearrange("a b c -> (a b c)").unsqueeze(0).broadcast_to([P, B * 2 * LANES])).then_inc(came[k], 16)

        @block.gpsimd
        def _(pool):
            last_edge, turn = pool.to_reg(E - 1), pool.alloc_register(f"{s.tag}_next_turn")
            with pool.Fori(0, TURNS) as i:
                pool.reg_add(turn, i, 1)
                for k in range(2):
                    tables_made(pool, r)
                    pool.wait_ge(placed[k], turn)
                    for b in range(B):
                        pool.indirect_dma_start(sorted_edges, bass.IndirectOffsetOnAxis(ap=place[:, k, b:b + 1], axis=0),
                                                record[:, k, b, :], None, bounds_check=last_edge, oob_is_err=False).then_inc(sent[k], 16)
            for k in range(2):
                pool.wait_ge(sent[k], 16 * B * TURNS)

    with Scope(nc, "sorted") as s:
        both = s.sb("both", [LANES, STEPS, 2], I32)
        loaded, done = s.sem("loaded"), s.sem("done")
        block = s.block()

        @block.sync
        def _(sp):
            sp.dma_start(both[:, :, :], sorted_edges.rearrange("(p j) k -> p j k", p=LANES)).then_inc(loaded, 16)

        @block.vector
        def _(dve):
            dve.wait_ge(loaded, 16)
            nc.vector.tensor_copy(o.key[:, 0:STEPS], both[:, :, 0]).then_inc(done, 1)
            nc.vector.tensor_copy(o.far[:, 0:STEPS], both[:, :, 1]).then_inc(done, 1)


def lane_tables(nc, r, o, tag, keys):
    with Scope(nc, tag) as s:
        keyf = s.sb("keyf", [LANES, STEPS])
        ends = s.sb("ends", [1, 3, LANES], I32)
        endf = s.sb("endf", [1, 3, LANES])
        whole = s.sb("whole", [1, 3, LANES])
        ps_gate = s.ps("ps_gate", [P, LANES])
        chain_sem, gated, spread, key_ends = s.sem("chain"), s.sem("gated"), s.sem("spread"), s.sem("key_ends")
        block = s.block()
        firsts = keys.rearrange("(q j) -> j q", j=STEPS)

        @block.sync
        def _(sp):
            sp.dma_start(ends[:, 0, :], firsts[0:1, :], allow_slow_non_contiguous=True).then_inc(key_ends, 16)
            sp.dma_start(ends[:, 1, :], firsts[STEPS - 1:STEPS, :], allow_slow_non_contiguous=True).then_inc(key_ends, 16)
            sp.dma_start(ends[:, 2, 1:LANES], firsts[STEPS - 1:STEPS, 0:LANES - 1], allow_slow_non_contiguous=True).then_inc(key_ends, 16)
            sp.dma_start(ends[:, 2, 0:1], firsts[0:1, 0:1], allow_slow_non_contiguous=True).then_inc(key_ends, 16)

        @block.vector
        def _(dve):
            link = Chain(dve, chain_sem)
            link(nc.vector.tensor_copy(keyf[:, :], o.key[:, 0:STEPS]))
            link(nc.vector.memset(o.cont[:, 0:1], 0.0))
            link(nc.vector.tensor_tensor(o.cont[:, 1:STEPS], keyf[:, 1:STEPS], keyf[:, 0:STEPS - 1], ALU.is_equal))
            link(nc.vector.tensor_scalar(o.pen[:, :], o.cont[:, :], -NONE, NONE, ALU.mult, ALU.add))
            dve.wait_ge(key_ends, 64)
            link(nc.vector.tensor_copy(endf[:, :, :], ends[:, :, :]))
            link(nc.vector.tensor_tensor(whole[:, 0, :], endf[:, 0, :], endf[:, 1, :], ALU.is_equal))
            link(nc.vector.tensor_tensor(whole[:, 1, :], endf[:, 0, :], endf[:, 2, :], ALU.is_equal))
            link(nc.vector.memset(whole[:, 1, 0:1], 0.0))
            nc.vector.tensor_tensor(whole[:, 2, :], whole[:, 0, :], whole[:, 1, :], ALU.mult).then_inc(gated, 1)
            dve.wait_ge(spread, 1)
            link(nc.vector.tensor_copy(o.gate[:, :], ps_gate[:, :]))
            link(nc.vector.tensor_scalar(o.gate_pen[:, :], o.gate[:, :], -NONE, NONE, ALU.mult, ALU.add))

        @block.tensor
        def _(pe):
            pe.wait_ge(gated, 1)
            nc.tensor.matmul(ps_gate[:, :], r.ones[0:1, :], whole[:, 2, :], start=True, stop=True).then_inc(spread, 1)


def normalize(nc, r, tag, x):
    with Scope(nc, tag) as s:
        stats = s.sb("stats", [P, NT, 6])
        moments = s.sb("moments", [P, NT, 2])
        std = s.sb("std", [P, NT])
        rstd = s.sb("rstd", [P, NT])
        chain_sem, added, rooted = s.sem("chain"), s.sem("added"), s.sem("rooted")
        block = s.block()

        @block.vector
        def _(dve):
            link = Chain(dve, chain_sem)
            for t in range(NT):
                last = nc.vector.bn_stats(stats[:, t, :], x[:, t, :])
            link(last)
            for t in range(NT):
                last = nc.vector.bn_aggr(moments[:, t, :], stats[:, t, :])
            link(last)
            link(nc.vector.tensor_copy(r.var[:, :], moments[:, :, 1]))
            nc.vector.tensor_scalar(std[:, :], r.var[:, :], EPS, None, ALU.add).then_inc(added, 1)
            dve.wait_ge(rooted, 1)
            link(nc.vector.reciprocal(rstd[:, :], std[:, :]))
            with dve.Fori(0, NT // 2) as i:
                for k in range(2):
                    t = 2 * i + k
                    nc.vector.tensor_scalar(r.xh[:, bass.ds(t, 1), :].rearrange("p a b -> p (a b)"),
                                            x[:, bass.ds(t, 1), :].rearrange("p a b -> p (a b)"),
                                            moments[:, bass.ds(t, 1), 0:1].rearrange("p a b -> p (a b)"), rstd[:, bass.ds(t, 1)],
                                            ALU.subtract, ALU.mult)

        @block.scalar
        def _(act):
            act.wait_ge(added, 1)
            nc.scalar.activation(std[:, :], std[:, :], ACT.Sqrt).then_inc(rooted, 1)


def tile_of(t3, t):
    return t3[:, bass.ds(t, 1), :].rearrange("p a b -> p (a b)")


def flip_tile(nc, pe, out, xh_tile, eye):
    nc.tensor.transpose(out[:, 0, :], xh_tile[:, 0:P], eye)
    return nc.tensor.transpose(out[:, 1, :], xh_tile[:, P:2 * P], eye)


def stage_tiles(nc, dve, stage, tiles, i, flipped, staged):
    for k in range(2):
        dve.wait_ge(flipped[k], i)
        nc.vector.tensor_scalar(stage[:, k, :], tile_of(tiles, 2 * i + k), 1.0, None, ALU.mult).then_inc(staged[k], 1)


def project_l0(nc, r, w_qkv, gamma, beta, qv, kd):
    with Scope(nc, "l0p") as s:
        w = s.sb("w", [P, 2, 3 * G])
        gb = s.sb("gb", [P, 2, 2])
        x2 = s.sb("x2", [P, 2, G])
        r2 = s.sb("r2", [P, NT])
        xT = s.sb("xT", [P, 2, 2, P])
        o = s.sb("o", [P, 2, 3 * G])
        flip = [s.ps(f"flip{k}", [P, 2, P]) for k in range(2)]
        ps_qv = [s.ps(f"ps_qv{k}", [P, 2 * G]) for k in range(2)]
        ps_k = [s.ps(f"ps_k{k}", [P, G]) for k in range(2)]
        loaded, chain_sem, added, rooted = s.sem("loaded"), s.sem("chain"), s.sem("added"), s.sem("rooted")
        scaled, flipped, copied = s.sems("scaled", 2), s.sems("flipped", 2), s.sems("copied", 2)
        projected, taken, stored = s.sems("projected", 2), s.sems("taken", 2), s.sems("stored", 2)
        block = s.block()
        T2 = NT // 2

        @block.sync
        def _(sp):
            sp.dma_start(w[:, :, :], w_qkv.rearrange("(c p) n -> p c n", p=P)).then_inc(loaded, 16)
            sp.dma_start(gb[:, 0, :], gamma.rearrange("(c p) -> p c", p=P), allow_slow_non_contiguous=True).then_inc(loaded, 16)
            sp.dma_start(gb[:, 1, :], beta.rearrange("(c p) -> p c", p=P), allow_slow_non_contiguous=True).then_inc(loaded, 16)
            with sp.Fori(0, T2) as i:
                for k in range(2):
                    row = (2 * i + k) * P
                    sp.wait_ge(taken[k], i + 1)
                    sp.dma_start(qv[bass.ds(row, P), :], o[:, k, 0:2 * G]).then_inc(stored[k], 16)
                    sp.dma_start(kd[bass.ds(row, P), :], o[:, k, 2 * G:3 * G]).then_inc(stored[k], 16)
            for k in range(2):
                sp.wait_ge(stored[k], 32 * T2)

        @block.vector
        def _(dve):
            link = Chain(dve, chain_sem)
            link(nc.vector.tensor_scalar(r2[:, :], r.var[:, :], EPS, None, ALU.add))
            link(nc.vector.reciprocal(r2[:, :], r2[:, :]))
            link(nc.vector.tensor_tensor(r2[:, :], r.var[:, :], r2[:, :], ALU.mult))
            nc.vector.tensor_scalar(r2[:, :], r2[:, :], EPS, None, ALU.add).then_inc(added, 1)
            dve.wait_ge(rooted, 1)
            link(nc.vector.reciprocal(r2[:, :], r2[:, :]))
            with dve.Fori(0, T2) as i:
                for k in range(2):
                    dve.wait_ge(flipped[k], i)
                    nc.vector.tensor_scalar(x2[:, k, :], tile_of(r.xh, 2 * i + k), r2[:, bass.ds(2 * i + k, 1)], None, ALU.mult).then_inc(scaled[k], 1)
                for k in range(2):
                    dve.wait_ge(projected[k], i + 1)
                    dve.wait_ge(stored[k], i * 32)
                    nc.vector.tensor_copy(o[:, k, 0:2 * G], ps_qv[k][:, :])
                    nc.vector.tensor_scalar(o[:, k, 2 * G:3 * G], ps_k[k][:, :], float(G) ** -0.5, None, ALU.mult).then_inc(taken[k], 1)

        @block.scalar
        def _(act):
            act.wait_ge(added, 1)
            nc.scalar.activation(r2[:, :], r2[:, :], ACT.Sqrt).then_inc(rooted, 1)
            act.wait_ge(loaded, 48)
            with act.Fori(0, T2) as i:
                for k in range(2):
                    act.wait_ge(flipped[k], i + 1)
                    act.wait_ge(projected[k], i)
                    nc.scalar.activation(xT[:, k, 0, :], flip[k][:, 0, :], ACT.Identity, bias=gb[:, 1, 0:1], scale=gb[:, 0, 0:1])
                    nc.scalar.activation(xT[:, k, 1, :], flip[k][:, 1, :], ACT.Identity, bias=gb[:, 1, 1:2], scale=gb[:, 0, 1:2]).then_inc(copied[k], 1)

        @block.tensor
        def _(pe):
            pe.wait_ge(loaded, 48)
            with pe.Fori(0, T2) as i:
                for k in range(2):
                    pe.wait_ge(scaled[k], i + 1)
                    pe.wait_ge(copied[k], i)
                    flip_tile(nc, pe, flip[k], x2[:, k, :], r.eye[:, :]).then_inc(flipped[k], 1)
                for k in range(2):
                    pe.wait_ge(copied[k], i + 1)
                    pe.wait_ge(taken[k], i)
                    for c in range(2):
                        nc.tensor.matmul(ps_qv[k][:, 0:G], xT[:, k, c, :], w[:, c, 0:G], start=(c == 0), stop=(c == 1))
                    for c in range(2):
                        nc.tensor.matmul(ps_qv[k][:, G:2 * G], xT[:, k, c, :], w[:, c, 2 * G:3 * G], start=(c == 0), stop=(c == 1))
                    for c in range(2):
                        last = nc.tensor.matmul(ps_k[k][:, :], xT[:, k, c, :], w[:, c, G:2 * G], start=(c == 0), stop=(c == 1))
                    last.then_inc(projected[k], 1)


def edges_l0(nc, r, o, qv, kd, states, tail):
    with Scope(nc, "l0e") as s:
        index = s.sb("index", [LANES, 2, 2, B], I32)
        got = s.sb("got", [LANES, 2, B, 2 * G])
        keyed = s.sb("keyed", [LANES, 2, B, G])
        logit = s.sb("logit", [LANES, B, G])
        grown = s.sb("grown", [LANES, B, G])
        both = s.sb("both", [LANES, B, 2, G])
        st = s.sb("st", [LANES, 2, B, 3 * G])
        scratch = s.sb("scratch", [LANES, 2 * G])
        chain_sem, begun = s.sem("chain"), s.sem("begun")
        indexed, came, used = s.sems("indexed", 2), s.sems("came", 2), s.sems("used", 2)
        raised, exped, stepped, stored = s.sems("raised", 2), s.sems("exped", 2), s.sems("stepped", 2), s.sems("stored", 2)
        block = s.block()
        out = states[0:E, :].rearrange("(p j) w -> p j w", p=LANES)

        @block.gpsimd
        def _(pool):
            last_row, turn = pool.to_reg(N - 1), pool.alloc_register(f"{s.tag}_next_turn")
            with pool.Fori(0, TURNS) as i:
                pool.reg_add(turn, i, 1)
                for k in range(2):
                    tables_made(pool, r)
                    pool.wait_ge(indexed[k], turn)
                    pool.wait_ge(used[k], i)
                    for b in range(B):
                        pool.indirect_dma_start(got[:, k, b, :], None, qv, bass.IndirectOffsetOnAxis(ap=index[:, k, 0, b:b + 1], axis=0),
                                                bounds_check=last_row, oob_is_err=False).then_inc(came[k], 16)
                        pool.indirect_dma_start(keyed[:, k, b, :], None, kd, bass.IndirectOffsetOnAxis(ap=index[:, k, 1, b:b + 1], axis=0),
                                                bounds_check=last_row, oob_is_err=False).then_inc(came[k], 16)

        @block.vector
        def _(dve):
            link = Chain(dve, chain_sem)
            link(nc.vector.memset(st[:, 1, B - 1, 0:G], NONE))
            link(nc.vector.memset(st[:, 1, B - 1, G:3 * G], 0.0))
            for k in range(2):
                nc.vector.tensor_copy(index[:, k, 0, :], o.far[:, k * B:(k + 1) * B])
                nc.vector.tensor_copy(index[:, k, 1, :], o.key[:, k * B:(k + 1) * B]).then_inc(indexed[k], 1)
            with dve.Fori(0, TURNS) as i:
                link.enter(i, 2 * (1 + B + 2 * B - 1))
                for k in range(2):
                    j = (2 * i + k) * B
                    dve.wait_ge(came[k], (i + 1) * (32 * B))
                    ahead = j + 2 * B
                    nc.vector.tensor_copy(index[:, k, 0, :], o.far[:, bass.ds(ahead, B)])
                    nc.vector.tensor_copy(index[:, k, 1, :], o.key[:, bass.ds(ahead, B)]).then_inc(indexed[k], 1)
                    link(nc.vector.tensor_tensor(logit[:, :, :], got[:, k, :, 0:G], keyed[:, k, :, :], ALU.mult))
                    dve.wait_ge(stored[k], i * 16)
                    for b in range(B):
                        before = st[:, k, b - 1, 0:G] if b else st[:, 1 - k, B - 1, 0:G]
                        link(nc.vector.scalar_tensor_tensor(st[:, k, b, 0:G], before, o.pen[:, bass.ds(j + b, 1)], logit[:, b, :], ALU.add, ALU.max))
                    for b in range(B):
                        before = st[:, k, b - 1, 0:G] if b else st[:, 1 - k, B - 1, 0:G]
                        nc.vector.scalar_tensor_tensor(grown[:, b, :], before, o.pen[:, bass.ds(j + b, 1)], st[:, k, b, 0:G], ALU.add, ALU.subtract)
                    nc.vector.tensor_tensor(logit[:, :, :], logit[:, :, :], st[:, k, :, 0:G], ALU.subtract).then_inc(raised[k], 1)
                    dve.wait_ge(exped[k], i + 1)
                    nc.vector.tensor_tensor(both[:, :, 1, :], both[:, :, 0, :], got[:, k, :, G:2 * G], ALU.mult).then_inc(used[k], 1)
                    dve.wait_ge(used[k], i + 1)
                    for b in range(B):
                        before = st[:, k, b - 1, G:3 * G] if b else st[:, 1 - k, B - 1, G:3 * G]
                        link(nc.vector.tensor_tensor(scratch[:, :].rearrange("p (a f) -> p a f", a=2), before.rearrange("p (a f) -> p a f", a=2),
                                                     grown[:, b, :].unsqueeze(1).broadcast_to([LANES, 2, G]), ALU.mult))
                        ins = nc.vector.tensor_tensor(st[:, k, b, G:3 * G], scratch[:, :], both[:, b, :, :].rearrange("p a f -> p (a f)"), ALU.add)
                        if b < B - 1:
                            link(ins)
                    ins.then_inc(stepped[k], 1)
                    dve.wait_ge(stepped[k], i + 1)
                link.leave(TURNS)
            nc.vector.tensor_copy(tail[:, :], st[:, 1, B - 1, :])

        @block.scalar
        def _(act):
            with act.Fori(0, TURNS) as i:
                for k in range(2):
                    act.wait_ge(raised[k], i + 1)
                    nc.scalar.activation(grown[:, :, :], grown[:, :, :], ACT.Exp)
                    nc.scalar.activation(both[:, :, 0, :], logit[:, :, :], ACT.Exp).then_inc(exped[k], 1)

        @block.sync
        def _(sp):
            with sp.Fori(0, TURNS) as i:
                for k in range(2):
                    sp.wait_ge(stepped[k], i + 1)
                    sp.dma_start(out[:, bass.ds((2 * i + k) * B, B), :], st[:, k, :, :]).then_inc(stored[k], 16)
            for k in range(2):
                sp.wait_ge(stored[k], 16 * TURNS)


def carry_softmax(nc, r, o, tag, tail, carries, states, heads):
    with Scope(nc, tag) as s:
        t = s.sb("t", [P, 2, 3, LANES])
        m = s.sb("m", [P, 2, LANES + 1])
        a = s.sb("a", [P, 2, LANES])
        c = s.sb("c", [P, 2, 3, LANES])
        rows = s.sb("rows", [LANES, 3, 2, P])
        empty = s.sb("empty", [1, 3 * G])
        empty_heads = s.sb("empty_heads", [1, 2 * H + G])
        flip = [s.ps(f"flip{h}", [P, 3, P]) for h in range(2)]
        back = [s.ps(f"back{h}", [LANES, 3, P]) for h in range(2)]
        chain_sem, flipped, raised, exped, scanned, returned, done, stored = (
            s.sem(n) for n in ("chain", "flipped", "raised", "exped", "scanned", "returned", "done", "stored"))
        block = s.block()

        @block.tensor
        def _(pe):
            for h in range(2):
                for n in range(3):
                    last = nc.tensor.transpose(flip[h][:, n, 0:LANES], tail[:, n * G + h * P:n * G + (h + 1) * P], r.eye[0:LANES, 0:LANES])
            last.then_inc(flipped, 1)
            pe.wait_ge(scanned, 1)
            for h in range(2):
                for n in range(3):
                    last = nc.tensor.transpose(back[h][:, n, :], c[:, h, n, :], r.eye[:, :])
            last.then_inc(returned, 1)

        @block.vector
        def _(dve):
            link = Chain(dve, chain_sem)
            link(nc.vector.memset(empty[:, 0:G], NONE))
            link(nc.vector.memset(empty[:, G:3 * G], 0.0))
            link(nc.vector.memset(empty_heads[:, 0:H], NONE))
            link(nc.vector.memset(empty_heads[:, H:], 0.0))
            dve.wait_ge(flipped, 1)
            for h in range(2):
                link(nc.vector.tensor_copy(t[:, h, :, :], flip[h][:, :, 0:LANES]))
                link(nc.vector.memset(m[:, h, 0:1], 0.0))
                link(nc.vector.tensor_tensor_scan(m[:, h, 1:], o.gate_pen[:, :], t[:, h, 0, :], NONE, ALU.add, ALU.max))
                link(nc.vector.tensor_copy(c[:, h, 0, :], m[:, h, 1:]))
                link(nc.vector.tensor_tensor(a[:, h, :], m[:, h, 0:LANES], o.gate_pen[:, :], ALU.add))
                link(nc.vector.tensor_tensor(a[:, h, :], a[:, h, :], m[:, h, 1:], ALU.subtract))
                link(nc.vector.tensor_tensor(t[:, h, 0, :], t[:, h, 0, :], m[:, h, 1:], ALU.subtract))
            link(nc.vector.memset(m[:, 0, 0:1], 0.0))
            nc.vector.memset(m[:, 0, 0:1], 0.0).then_inc(raised, 1)
            dve.wait_ge(exped, 1)
            for h in range(2):
                for n in (1, 2):
                    link(nc.vector.tensor_tensor(t[:, h, n, :], t[:, h, n, :], t[:, h, 0, :], ALU.mult))
                    link(nc.vector.tensor_tensor_scan(c[:, h, n, :], a[:, h, :], t[:, h, n, :], 0.0, ALU.mult, ALU.add))
            nc.vector.memset(m[:, 0, 0:1], 0.0).then_inc(scanned, 1)
            dve.wait_ge(returned, 1)
            for h in range(2):
                link(nc.vector.tensor_copy(rows[:, :, h, :], back[h][:, :, :]))
            nc.vector.memset(m[:, 0, 0:1], 0.0).then_inc(done, 1)

        @block.scalar
        def _(act):
            act.wait_ge(raised, 1)
            nc.scalar.activation(a[:, :, :], a[:, :, :], ACT.Exp)
            nc.scalar.activation(t[:, :, 0, :], t[:, :, 0, :], ACT.Exp).then_inc(exped, 1)

        @block.sync
        def _(sp):
            sp.wait_ge(done, 1)
            sp.dma_start(carries[0:LANES, :], rows[:, :, :, :].rearrange("q n h f -> q (n h f)")).then_inc(stored, 16)
            sp.dma_start(carries[LANES:LANES + 1, :], empty[:, :]).then_inc(stored, 16)
            sp.dma_start(states[E:E + 1, :], empty[:, 3 * G - states.shape[1]:] if heads == G else empty_heads[:, :]).then_inc(stored, 16)
            sp.wait_ge(stored, 48)


def finish_softmax(nc, r, o, tag, states, carries, heads, out):
    with Scope(nc, tag) as s:
        W = states.shape[1]
        index = s.sb("index", [P, 2, 2], I32)
        mine = s.sb("mine", [P, 2, W])
        carry = s.sb("carry", [P, 2, 3 * G])
        top = s.sb("top", [P, 2, G])
        fac = s.sb("fac", [P, 2, 2, G])
        z = s.sb("z", [P, G])
        u = s.sb("u", [P, G])
        t1 = s.sb("t1", [P, G])
        chain_sem = s.sem("chain")
        indexed, came, topped, exped, used = (s.sems(n, 2) for n in ("indexed", "came", "topped", "exped", "used"))
        block = s.block()
        T2 = NT // 2

        def three(ap):
            return ap.rearrange("p (h d) -> p h d", d=D)

        def own(k, n):
            if n == 2:
                return three(mine[:, k, W - G:W])
            if heads == G:
                return three(mine[:, k, n * G:(n + 1) * G])
            return mine[:, k, n * H:(n + 1) * H].unsqueeze(2).broadcast_to([P, H, D])

        def carried(k, n):
            return three(carry[:, k, n * G:(n + 1) * G])

        @block.gpsimd
        def _(pool):
            last_state, last_carry, turn = pool.to_reg(E), pool.to_reg(LANES), pool.alloc_register(f"{s.tag}_next_turn")
            with pool.Fori(0, T2) as i:
                pool.reg_add(turn, i, 1)
                for k in range(2):
                    tables_made(pool, r)
                    pool.wait_ge(indexed[k], turn)
                    pool.wait_ge(used[k], i)
                    pool.indirect_dma_start(mine[:, k, :], None, states, bass.IndirectOffsetOnAxis(ap=index[:, k, 0:1], axis=0),
                                            bounds_check=last_state, oob_is_err=False).then_inc(came[k], 16)
                    pool.indirect_dma_start(carry[:, k, :], None, carries, bass.IndirectOffsetOnAxis(ap=index[:, k, 1:2], axis=0),
                                            bounds_check=last_carry, oob_is_err=False).then_inc(came[k], 16)

        @block.vector
        def _(dve):
            link = Chain(dve, chain_sem)
            with dve.Fori(0, T2) as i:
                link.enter(i, 2 * 12)
                for k in range(2):
                    t = 2 * i + k
                    dve.wait_ge(came[k], i * 32)
                    nc.vector.tensor_copy(index[:, k, 0:1], o.end_row[:, bass.ds(t, 1)])
                    nc.vector.tensor_copy(index[:, k, 1:2], o.carry_row[:, bass.ds(t, 1)]).then_inc(indexed[k], 1)
                for k in range(2):
                    dve.wait_ge(came[k], (i + 1) * 32)
                    link(nc.vector.tensor_tensor(three(top[:, k, :]), own(k, 0), carried(k, 0), ALU.max))
                    nc.vector.tensor_tensor(three(fac[:, k, 0, :]), own(k, 0), three(top[:, k, :]), ALU.subtract)
                    nc.vector.tensor_tensor(three(fac[:, k, 1, :]), carried(k, 0), three(top[:, k, :]), ALU.subtract).then_inc(topped[k], 1)
                for k in range(2):
                    t = 2 * i + k
                    dve.wait_ge(exped[k], i + 1)
                    for n, acc in ((1, z), (2, u)):
                        link(nc.vector.tensor_tensor(three(acc[:, :]), own(k, n), three(fac[:, k, 0, :]), ALU.mult))
                        link(nc.vector.tensor_tensor(three(t1[:, :]), carried(k, n), three(fac[:, k, 1, :]), ALU.mult))
                        link(nc.vector.tensor_tensor(acc[:, :], acc[:, :], t1[:, :], ALU.add))
                    link(nc.vector.tensor_scalar(t1[:, :], z[:, :], 0.0, None, ALU.is_equal))
                    link(nc.vector.tensor_tensor(z[:, :], z[:, :], t1[:, :], ALU.add))
                    link(nc.vector.reciprocal(z[:, :], z[:, :]))
                    link(nc.vector.tensor_tensor(u[:, :], u[:, :], z[:, :], ALU.mult))
                    if out is r.x:
                        link(nc.vector.tensor_tensor(tile_of(r.x, t), tile_of(r.x, t), u[:, :], ALU.add))
                    else:
                        link(nc.vector.tensor_copy(tile_of(out, t), u[:, :]))
                    nc.vector.memset(t1[0:1, 0:1], 0.0).then_inc(used[k], 1)
                link.leave(T2)

        @block.scalar
        def _(act):
            with act.Fori(0, T2) as i:
                for k in range(2):
                    act.wait_ge(topped[k], i + 1)
                    nc.scalar.activation(fac[:, k, :, :], fac[:, k, :, :], ACT.Exp).then_inc(exped[k], 1)


def edges_sum(nc, r, o, tag, table, states, tail, edge_rows=None):
    with Scope(nc, tag) as s:
        index = s.sb("index", [LANES, 2, B], I32)
        got = s.sb("got", [LANES, 2, B, G])
        own = rows = None
        if edge_rows is not None:
            own = s.sb("own", [LANES, 2, B, G])
            rows = edge_rows.rearrange("(p j) w -> p j w", p=LANES)
        st = s.sb("st", [LANES, 2, B, G])
        chain_sem = s.sem("chain")
        names = ("indexed", "came", "owned", "used", "added", "cut", "stepped", "stored")
        indexed, came, owned, used, added, cut, stepped, stored = (s.sems(n, 2) for n in names)
        block = s.block()
        out = states[0:E, :].rearrange("(p j) w -> p j w", p=LANES)

        def sum_batch(i, k, link, dve):
            j = (2 * i + k) * B
            dve.wait_ge(stored[k], i * 16)
            for b in range(B):
                before = st[:, k, b - 1, :] if b else st[:, 1 - k, B - 1, :]
                ins = nc.vector.scalar_tensor_tensor(st[:, k, b, :], before, o.cont[:, bass.ds(j + b, 1)], got[:, k, b, :], ALU.mult, ALU.add)
                if b < B - 1:
                    link(ins)
            ins.then_inc(stepped[k], 1)
            dve.wait_ge(stepped[k], i + 1)

        @block.gpsimd
        def _(pool):
            last_row, turn = pool.to_reg(N - 1), pool.alloc_register(f"{s.tag}_next_turn")
            with pool.Fori(0, TURNS) as i:
                pool.reg_add(turn, i, 1)
                for k in range(2):
                    tables_made(pool, r)
                    pool.wait_ge(indexed[k], turn)
                    pool.wait_ge(stepped[k], i)
                    for b in range(B):
                        pool.indirect_dma_start(got[:, k, b, :], None, table, bass.IndirectOffsetOnAxis(ap=index[:, k, b:b + 1], axis=0),
                                                bounds_check=last_row, oob_is_err=False).then_inc(came[k], 16)

        @block.vector
        def _(dve):
            link = Chain(dve, chain_sem)
            link(nc.vector.memset(st[:, 1, B - 1, :], 0.0))
            for k in range(2):
                nc.vector.tensor_copy(index[:, k, :], o.far[:, k * B:(k + 1) * B]).then_inc(indexed[k], 1)
            with dve.Fori(0, TURNS) as i:
                link.enter(i, 2 * (B - 1))
                for k in range(2):
                    j = (2 * i + k) * B
                    dve.wait_ge(came[k], (i + 1) * (16 * B))
                    nc.vector.tensor_copy(index[:, k, :], o.far[:, bass.ds(j + 2 * B, B)]).then_inc(indexed[k], 1)
                    if own is not None:
                        dve.wait_ge(owned[k], (i + 1) * 16)
                        nc.vector.tensor_tensor(got[:, k, :, :], got[:, k, :, :], own[:, k, :, :], ALU.add).then_inc(added[k], 1)
                if own is None:
                    for k in range(2):
                        sum_batch(i, k, link, dve)
                else:
                    for k in range(2):
                        dve.wait_ge(cut[k], i + 1)
                        sum_batch(i, k, link, dve)
                link.leave(TURNS)
            nc.vector.tensor_copy(tail[:, 0:G], st[:, 1, B - 1, :])

        @block.scalar
        def _(act):
            if own is not None:
                with act.Fori(0, TURNS - 1) as i:
                    for k in range(2):
                        act.wait_ge(added[k], i + 1)
                        nc.scalar.activation(got[:, k, :, :], got[:, k, :, :], ACT.Relu).then_inc(cut[k], 1)
                        act.dma_start(own[:, k, :, :], rows[:, bass.ds((2 * i + 2 + k) * B, B), :]).then_inc(owned[k], 16)
                for k in range(2):
                    act.wait_ge(added[k], TURNS)
                    nc.scalar.activation(got[:, k, :, :], got[:, k, :, :], ACT.Relu).then_inc(cut[k], 1)

        @block.sync
        def _(sp):
            if own is not None:
                for k in range(2):
                    sp.dma_start(own[:, k, :, :], rows[:, k * B:(k + 1) * B, :]).then_inc(owned[k], 16)
            with sp.Fori(0, TURNS) as i:
                for k in range(2):
                    sp.wait_ge(stepped[k], i + 1)
                    sp.dma_start(out[:, bass.ds((2 * i + k) * B, B), :], st[:, k, :, :]).then_inc(stored[k], 16)
            for k in range(2):
                sp.wait_ge(stored[k], 16 * TURNS)


def carry_sum(nc, r, o, tag, tail, carries, states):
    with Scope(nc, tag) as s:
        t = s.sb("t", [P, 2, LANES])
        c = s.sb("c", [P, 2, LANES])
        rows = s.sb("rows", [LANES, 2, P])
        empty = s.sb("empty", [1, G])
        flip = s.ps("flip", [P, 2, P])
        back = s.ps("back", [LANES, 2, P])
        chain_sem, flipped, scanned, returned, done, stored = (
            s.sem(n) for n in ("chain", "flipped", "scanned", "returned", "done", "stored"))
        block = s.block()

        @block.tensor
        def _(pe):
            for h in range(2):
                last = nc.tensor.transpose(flip[:, h, 0:LANES], tail[:, h * P:(h + 1) * P], r.eye[0:LANES, 0:LANES])
            last.then_inc(flipped, 1)
            pe.wait_ge(scanned, 1)
            for h in range(2):
                last = nc.tensor.transpose(back[:, h, :], c[:, h, :], r.eye[:, :])
            last.then_inc(returned, 1)

        @block.vector
        def _(dve):
            link = Chain(dve, chain_sem)
            link(nc.vector.memset(empty[:, :], 0.0))
            dve.wait_ge(flipped, 1)
            link(nc.vector.tensor_copy(t[:, :, :], flip[:, :, 0:LANES]))
            nc.vector.tensor_tensor_scan(c[:, 0, :], o.gate[:, :], t[:, 0, :], 0.0, ALU.mult, ALU.add)
            nc.vector.tensor_tensor_scan(c[:, 1, :], o.gate[:, :], t[:, 1, :], 0.0, ALU.mult, ALU.add).then_inc(scanned, 1)
            dve.wait_ge(returned, 1)
            nc.vector.tensor_copy(rows[:, :, :], back[:, :, :]).then_inc(done, 1)

        @block.sync
        def _(sp):
            sp.wait_ge(done, 1)
            sp.dma_start(carries[0:LANES, :], rows[:, :, :].rearrange("q h f -> q (h f)")).then_inc(stored, 16)
            sp.dma_start(carries[LANES:LANES + 1, :], empty[:, :]).then_inc(stored, 16)
            sp.dma_start(states[E:E + 1, :], empty[:, :]).then_inc(stored, 16)
            sp.wait_ge(stored, 48)


def finish_sum(nc, r, o, tag, states, carries, mean, out):
    with Scope(nc, tag) as s:
        index = s.sb("index", [P, 2, 2], I32)
        mine = s.sb("mine", [P, 2, G])
        carry = s.sb("carry", [P, 2, G])
        share = s.sb("share", [P, NT])
        chain_sem = s.sem("chain")
        indexed, came, used = (s.sems(n, 2) for n in ("indexed", "came", "used"))
        block = s.block()
        T2 = NT // 2

        @block.gpsimd
        def _(pool):
            last_state, last_carry, turn = pool.to_reg(E), pool.to_reg(LANES), pool.alloc_register(f"{s.tag}_next_turn")
            with pool.Fori(0, T2) as i:
                pool.reg_add(turn, i, 1)
                for k in range(2):
                    tables_made(pool, r)
                    pool.wait_ge(indexed[k], turn)
                    pool.wait_ge(used[k], i)
                    pool.indirect_dma_start(mine[:, k, :], None, states, bass.IndirectOffsetOnAxis(ap=index[:, k, 0:1], axis=0),
                                            bounds_check=last_state, oob_is_err=False).then_inc(came[k], 16)
                    pool.indirect_dma_start(carry[:, k, :], None, carries, bass.IndirectOffsetOnAxis(ap=index[:, k, 1:2], axis=0),
                                            bounds_check=last_carry, oob_is_err=False).then_inc(came[k], 16)

        @block.vector
        def _(dve):
            link = Chain(dve, chain_sem)
            link(nc.vector.tensor_scalar(share[:, :], o.count[:, :], 1.0, None, ALU.max))
            link(nc.vector.reciprocal(share[:, :], share[:, :]))
            with dve.Fori(0, T2) as i:
                link.enter(i, 2 * 1)
                for k in range(2):
                    t = 2 * i + k
                    dve.wait_ge(came[k], i * 32)
                    nc.vector.tensor_copy(index[:, k, 0:1], o.end_row[:, bass.ds(t, 1)])
                    nc.vector.tensor_copy(index[:, k, 1:2], o.carry_row[:, bass.ds(t, 1)]).then_inc(indexed[k], 1)
                for k in range(2):
                    t = 2 * i + k
                    dve.wait_ge(came[k], (i + 1) * 32)
                    link(nc.vector.tensor_tensor(mine[:, k, :], mine[:, k, :], carry[:, k, :], ALU.add))
                    by = share[:, bass.ds(t, 1)] if mean else 1.0
                    nc.vector.scalar_tensor_tensor(tile_of(out, t), mine[:, k, :], by, tile_of(out, t), ALU.mult, ALU.add).then_inc(used[k], 1)
                link.leave(T2)


def project_l1(nc, r, w_self, w_neigh, table):
    MAXK = 32
    with Scope(nc, "l1p") as s:
        w = s.sb("w", [P, 2, 2 * G])
        xT = s.sb("xT", [P, 2, 2, P])
        h = s.sb("h", [P, 2, G])
        left = s.sb("left", [P, 2, G])
        top = s.sb("top", [P, 2, 8])
        beat = s.sb("beat", [1, 1])
        o = s.sb("o", [P, 2, G])
        stage = s.sb("stage", [P, 2, G])
        staged = s.sems("staged", 2)
        flip = [s.ps(f"flip{k}", [P, 2, P]) for k in range(2)]
        ps = [s.ps(f"ps{k}", [P, 2 * G]) for k in range(2)]
        loaded, chain_sem = s.sem("loaded"), s.sem("chain")
        flipped, copied, projected, taken, chosen, stored = (
            s.sems(n, 2) for n in ("flipped", "copied", "projected", "taken", "chosen", "stored"))
        block = s.block()
        T2 = NT // 2

        @block.sync
        def _(sp):
            sp.dma_start(w[:, :, 0:G], w_self.rearrange("(c p) n -> p c n", p=P)).then_inc(loaded, 16)
            sp.dma_start(w[:, :, G:2 * G], w_neigh.rearrange("(c p) n -> p c n", p=P)).then_inc(loaded, 16)
            with sp.Fori(0, T2) as i:
                for k in range(2):
                    sp.wait_ge(chosen[k], i + 1)
                    sp.dma_start(table[bass.ds((2 * i + k) * P, P), :], o[:, k, :]).then_inc(stored[k], 16)
            for k in range(2):
                sp.wait_ge(stored[k], 16 * T2)

        @block.vector
        def _(dve):
            link = Chain(dve, chain_sem)
            with dve.Fori(0, T2) as i:
                link.enter(i, 2 * (MAXK // 8))
                stage_tiles(nc, dve, stage, r.xh, i, flipped, staged)
                for k in range(2):
                    t = 2 * i + k
                    dve.wait_ge(projected[k], i + 1)
                    nc.vector.tensor_tensor(tile_of(r.x, t), tile_of(r.x, t), ps[k][:, 0:G], ALU.add)
                    nc.vector.tensor_copy(h[:, k, :], ps[k][:, G:2 * G]).then_inc(taken[k], 1)
                for k in range(2):
                    dve.wait_ge(taken[k], i + 1)
                for n in range(MAXK // 8):
                    nc.vector.memset(beat[:, :], 0.0)
                    for k in range(2):
                        last = nc.vector.max(top[:, k, :], (left if n else h)[:, k, :])
                    link(last)
                    nc.vector.memset(beat[:, :], 0.0)
                    for k in range(2):
                        last = nc.vector.match_replace(left[:, k, :], top[:, k, :], (left if n else h)[:, k, :], NONE)
                    link(last)
                for k in range(2):
                    dve.wait_ge(stored[k], i * 16)
                    nc.vector.scalar_tensor_tensor(o[:, k, :], left[:, k, :], NONE / 2, h[:, k, :], ALU.is_le, ALU.mult).then_inc(chosen[k], 1)
                link.leave(T2)

        @block.scalar
        def _(act):
            with act.Fori(0, T2) as i:
                for k in range(2):
                    act.wait_ge(flipped[k], i + 1)
                    act.wait_ge(projected[k], i)
                    nc.scalar.activation(xT[:, k, :, :], flip[k][:, :, :], ACT.Copy).then_inc(copied[k], 1)

        @block.tensor
        def _(pe):
            pe.wait_ge(loaded, 32)
            with pe.Fori(0, T2) as i:
                for k in range(2):
                    pe.wait_ge(staged[k], i + 1)
                    pe.wait_ge(copied[k], i)
                    flip_tile(nc, pe, flip[k], stage[:, k, :], r.eye[:, :]).then_inc(flipped[k], 1)
                for k in range(2):
                    pe.wait_ge(copied[k], i + 1)
                    pe.wait_ge(taken[k], i)
                    for c in range(2):
                        last = nc.tensor.matmul(ps[k][:, :], xT[:, k, c, :], w[:, c, :], start=(c == 0), stop=(c == 1))
                    last.then_inc(projected[k], 1)


def project_l2(nc, r, ws, biases, qd, kv):
    with Scope(nc, "l2p") as s:
        w = s.sb("w", [P, 2, 3 * G])
        row = s.sb("row", [1, 3 * G])
        xT = s.sb("xT", [P, 2, 2, P])
        o = s.sb("o", [P, 2, 3 * G])
        stage = s.sb("stage", [P, 2, G])
        staged = s.sems("staged", 2)
        flip = [s.ps(f"flip{k}", [P, 2, P]) for k in range(2)]
        ps_kv = [s.ps(f"ps_kv{k}", [P, 2 * G]) for k in range(2)]
        ps_q = [s.ps(f"ps_q{k}", [P, G]) for k in range(2)]
        loaded = s.sem("loaded")
        flipped, copied, projected, taken, stored = (
            s.sems(n, 2) for n in ("flipped", "copied", "projected", "taken", "stored"))
        block = s.block()
        T2 = NT // 2

        @block.sync
        def _(sp):
            for n in range(3):
                sp.dma_start(w[:, :, n * G:(n + 1) * G], ws[n].rearrange("(c p) n -> p c n", p=P)).then_inc(loaded, 16)
                sp.dma_start(row[:, n * G:(n + 1) * G], biases[n].unsqueeze(0)).then_inc(loaded, 16)
            with sp.Fori(0, T2) as i:
                for k in range(2):
                    sp.wait_ge(taken[k], i + 1)
                    sp.dma_start(kv[bass.ds((2 * i + k) * P, P), :], o[:, k, 0:2 * G]).then_inc(stored[k], 16)
                    sp.dma_start(qd[bass.ds((2 * i + k) * P, P), :], o[:, k, 2 * G:3 * G]).then_inc(stored[k], 16)
            for k in range(2):
                sp.wait_ge(stored[k], 32 * T2)

        @block.vector
        def _(dve):
            with dve.Fori(0, T2) as i:
                stage_tiles(nc, dve, stage, r.xh, i, flipped, staged)
                for k in range(2):
                    dve.wait_ge(projected[k], i + 1)
                    dve.wait_ge(stored[k], i * 32)
                    nc.vector.tensor_copy(o[:, k, 0:2 * G], ps_kv[k][:, :])
                    nc.vector.tensor_scalar(o[:, k, 2 * G:3 * G], ps_q[k][:, :], float(D) ** -0.5, None, ALU.mult).then_inc(taken[k], 1)

        @block.scalar
        def _(act):
            with act.Fori(0, T2) as i:
                for k in range(2):
                    act.wait_ge(flipped[k], i + 1)
                    act.wait_ge(projected[k], i)
                    nc.scalar.activation(xT[:, k, :, :], flip[k][:, :, :], ACT.Copy).then_inc(copied[k], 1)

        @block.tensor
        def _(pe):
            pe.wait_ge(loaded, 96)
            with pe.Fori(0, T2) as i:
                for k in range(2):
                    pe.wait_ge(staged[k], i + 1)
                    pe.wait_ge(copied[k], i)
                    flip_tile(nc, pe, flip[k], stage[:, k, :], r.eye[:, :]).then_inc(flipped[k], 1)
                for k in range(2):
                    pe.wait_ge(copied[k], i + 1)
                    pe.wait_ge(taken[k], i)
                    nc.tensor.matmul(ps_kv[k][:, :], r.ones[0:1, :], row[:, 0:2 * G], start=True, stop=False)
                    for c in range(2):
                        nc.tensor.matmul(ps_kv[k][:, :], xT[:, k, c, :], w[:, c, 0:2 * G], start=False, stop=(c == 1))
                    nc.tensor.matmul(ps_q[k][:, :], r.ones[0:1, :], row[:, 2 * G:3 * G], start=True, stop=False)
                    for c in range(2):
                        last = nc.tensor.matmul(ps_q[k][:, :], xT[:, k, c, :], w[:, c, 2 * G:3 * G], start=False, stop=(c == 1))
                    last.then_inc(projected[k], 1)


def edges_l2(nc, r, o, qd, kv, states, tail):
    with Scope(nc, "l2e") as s:
        index = s.sb("index", [LANES, 2, 2, B], I32)
        got = s.sb("got", [LANES, 2, B, 2 * G])
        keyed = s.sb("keyed", [LANES, 2, B, G])
        logit = s.sb("logit", [LANES, B, H])
        grown = s.sb("grown", [LANES, B, H])
        weight = s.sb("weight", [LANES, B, H])
        st = s.sb("st", [LANES, 2, B, 2 * H + G])
        prod = s.sb("prod", [LANES, B, G])
        scratch = s.sb("scratch", [LANES, G])
        tiny = s.sb("tiny", [LANES, B, H])
        chain_sem = s.sem("chain")
        indexed, came, used = s.sems("indexed", 2), s.sems("came", 2), s.sems("used", 2)
        raised, exped, stepped, stored = s.sems("raised", 2), s.sems("exped", 2), s.sems("stepped", 2), s.sems("stored", 2)
        block = s.block()
        out = states[0:E, :].rearrange("(p j) w -> p j w", p=LANES)
        M, Z, U = slice(0, H), slice(H, 2 * H), slice(2 * H, 2 * H + G)

        def heads(ap):
            return ap.rearrange("p (h d) -> p h d", d=D)

        @block.gpsimd
        def _(pool):
            last_row, turn = pool.to_reg(N - 1), pool.alloc_register(f"{s.tag}_next_turn")
            with pool.Fori(0, TURNS) as i:
                pool.reg_add(turn, i, 1)
                for k in range(2):
                    tables_made(pool, r)
                    pool.wait_ge(indexed[k], turn)
                    pool.wait_ge(used[k], i)
                    for b in range(B):
                        pool.indirect_dma_start(got[:, k, b, :], None, kv, bass.IndirectOffsetOnAxis(ap=index[:, k, 0, b:b + 1], axis=0),
                                                bounds_check=last_row, oob_is_err=False).then_inc(came[k], 16)
                        pool.indirect_dma_start(keyed[:, k, b, :], None, qd, bass.IndirectOffsetOnAxis(ap=index[:, k, 1, b:b + 1], axis=0),
                                                bounds_check=last_row, oob_is_err=False).then_inc(came[k], 16)

        @block.vector
        def _(dve):
            link = Chain(dve, chain_sem)
            link(nc.vector.memset(st[:, 1, B - 1, M], NONE))
            link(nc.vector.memset(st[:, 1, B - 1, H:], 0.0))
            for k in range(2):
                nc.vector.tensor_copy(index[:, k, 0, :], o.far[:, k * B:(k + 1) * B])
                nc.vector.tensor_copy(index[:, k, 1, :], o.key[:, k * B:(k + 1) * B]).then_inc(indexed[k], 1)
            with dve.Fori(0, TURNS) as i:
                link.enter(i, 2 * (2 + B + 2 * B - 1))
                for k in range(2):
                    j = (2 * i + k) * B
                    dve.wait_ge(came[k], (i + 1) * (32 * B))
                    ahead = j + 2 * B
                    nc.vector.tensor_copy(index[:, k, 0, :], o.far[:, bass.ds(ahead, B)])
                    nc.vector.tensor_copy(index[:, k, 1, :], o.key[:, bass.ds(ahead, B)]).then_inc(indexed[k], 1)
                    link(nc.vector.tensor_tensor(prod[:, :, :], got[:, k, :, 0:G], keyed[:, k, :, :], ALU.mult))
                    link(nc.vector.tensor_reduce(logit[:, :, :], prod[:, :, :].rearrange("p b (h d) -> p b h d", d=D), AX.X, ALU.add))
                    dve.wait_ge(stored[k], i * 16)
                    for b in range(B):
                        before = st[:, k, b - 1, M] if b else st[:, 1 - k, B - 1, M]
                        link(nc.vector.scalar_tensor_tensor(st[:, k, b, M], before, o.pen[:, bass.ds(j + b, 1)], logit[:, b, :], ALU.add, ALU.max))
                    for b in range(B):
                        before = st[:, k, b - 1, M] if b else st[:, 1 - k, B - 1, M]
                        nc.vector.scalar_tensor_tensor(grown[:, b, :], before, o.pen[:, bass.ds(j + b, 1)], st[:, k, b, M], ALU.add, ALU.subtract)
                    nc.vector.tensor_tensor(weight[:, :, :], logit[:, :, :], st[:, k, :, M], ALU.subtract).then_inc(raised[k], 1)
                    dve.wait_ge(exped[k], i + 1)
                    nc.vector.tensor_tensor(prod[:, :, :].rearrange("p b (h d) -> p b h d", d=D),
                                            got[:, k, :, G:2 * G].rearrange("p b (h d) -> p b h d", d=D),
                                            weight[:, :, :].unsqueeze(3).broadcast_to([LANES, B, H, D]), ALU.mult).then_inc(used[k], 1)
                    dve.wait_ge(used[k], i + 1)
                    for b in range(B):
                        last = st[:, k, b - 1, :] if b else st[:, 1 - k, B - 1, :]
                        nc.vector.tensor_tensor(tiny[:, b, :], last[:, Z], grown[:, b, :], ALU.mult)
                        link(nc.vector.tensor_tensor(heads(scratch[:, :]), heads(last[:, U]), grown[:, b, :].unsqueeze(2).broadcast_to([LANES, H, D]), ALU.mult))
                        nc.vector.tensor_tensor(st[:, k, b, Z], tiny[:, b, :], weight[:, b, :], ALU.add)
                        ins = nc.vector.tensor_tensor(st[:, k, b, U], scratch[:, :], prod[:, b, :], ALU.add)
                        if b < B - 1:
                            link(ins)
                    ins.then_inc(stepped[k], 1)
                    dve.wait_ge(stepped[k], i + 1)
                link.leave(TURNS)
            nc.vector.tensor_copy(heads(tail[:, 0:G]), st[:, 1, B - 1, M].unsqueeze(2).broadcast_to([LANES, H, D]))
            nc.vector.tensor_copy(heads(tail[:, G:2 * G]), st[:, 1, B - 1, Z].unsqueeze(2).broadcast_to([LANES, H, D]))
            nc.vector.tensor_copy(tail[:, 2 * G:3 * G], st[:, 1, B - 1, U])

        @block.scalar
        def _(act):
            with act.Fori(0, TURNS) as i:
                for k in range(2):
                    act.wait_ge(raised[k], i + 1)
                    nc.scalar.activation(grown[:, :, :], grown[:, :, :], ACT.Exp)
                    nc.scalar.activation(weight[:, :, :], weight[:, :, :], ACT.Exp).then_inc(exped[k], 1)

        @block.sync
        def _(sp):
            with sp.Fori(0, TURNS) as i:
                for k in range(2):
                    sp.wait_ge(stepped[k], i + 1)
                    sp.dma_start(out[:, bass.ds((2 * i + k) * B, B), :], st[:, k, :, :]).then_inc(stored[k], 16)
            for k in range(2):
                sp.wait_ge(stored[k], 16 * TURNS)


def project_out(nc, r, agg, w_out, bias):
    with Scope(nc, "l2o") as s:
        w = s.sb("w", [P, 2, G])
        row = s.sb("row", [1, G])
        xT = s.sb("xT", [P, 2, 2, P])
        stage = s.sb("stage", [P, 2, G])
        staged = s.sems("staged", 2)
        flip = [s.ps(f"flip{k}", [P, 2, P]) for k in range(2)]
        ps = [s.ps(f"ps{k}", [P, G]) for k in range(2)]
        loaded = s.sem("loaded")
        flipped, copied, projected, taken = (s.sems(n, 2) for n in ("flipped", "copied", "projected", "taken"))
        block = s.block()
        T2 = NT // 2

        @block.sync
        def _(sp):
            sp.dma_start(w[:, :, :], w_out.rearrange("(c p) n -> p c n", p=P)).then_inc(loaded, 16)
            sp.dma_start(row[:, :], bias.unsqueeze(0)).then_inc(loaded, 16)

        @block.vector
        def _(dve):
            with dve.Fori(0, T2) as i:
                stage_tiles(nc, dve, stage, agg, i, flipped, staged)
                for k in range(2):
                    dve.wait_ge(projected[k], i + 1)
                    nc.vector.tensor_tensor(tile_of(r.x, 2 * i + k), tile_of(r.x, 2 * i + k), ps[k][:, :], ALU.add).then_inc(taken[k], 1)

        @block.scalar
        def _(act):
            with act.Fori(0, T2) as i:
                for k in range(2):
                    act.wait_ge(flipped[k], i + 1)
                    act.wait_ge(projected[k], i)
                    nc.scalar.activation(xT[:, k, :, :], flip[k][:, :, :], ACT.Copy).then_inc(copied[k], 1)

        @block.tensor
        def _(pe):
            pe.wait_ge(loaded, 32)
            with pe.Fori(0, T2) as i:
                for k in range(2):
                    pe.wait_ge(staged[k], i + 1)
                    pe.wait_ge(copied[k], i)
                    flip_tile(nc, pe, flip[k], stage[:, k, :], r.eye[:, :]).then_inc(flipped[k], 1)
                for k in range(2):
                    pe.wait_ge(copied[k], i + 1)
                    pe.wait_ge(taken[k], i)
                    nc.tensor.matmul(ps[k][:, :], r.ones[0:1, :], row[:, :], start=True, stop=False)
                    for c in range(2):
                        last = nc.tensor.matmul(ps[k][:, :], xT[:, k, c, :], w[:, c, :], start=False, stop=(c == 1))
                    last.then_inc(projected[k], 1)

def route(nc, r, tag, w_gate, bias, experts, kind):
    with Scope(nc, tag) as s:
        w = s.sb("w", [P, 2, experts])
        row = s.sb("row", [1, experts])
        xs = s.sb("xs", [P, 2, 2, P])
        score = s.sb("score", [P, NT, 8])
        worst = s.sb("worst", [P, NT])
        top = s.sb("top", [P, NT, 8])
        which = s.sb("which", [P, NT, 8], mybir.dt.uint32)
        whichf = s.sb("whichf", [P, NT, 2])
        wt = s.sb("wt", [P, NT, 2])
        t1 = s.sb("t1", [P, NT])
        second = s.sb("second", [P, NT, 8])
        stage = s.sb("stage", [P, 2, G])
        staged = s.sems("staged", 2)
        flip = [s.ps(f"flip{k}", [P, 2, P]) for k in range(2)]
        ps = s.ps("ps", [P, NT, experts])
        loaded, chain_sem, shifted, exped, differed, weighed = (s.sem(n) for n in ("loaded", "chain", "shifted", "exped", "differed", "weighed"))
        flipped, copied, kept, scored = (s.sems(n, 2) for n in ("flipped", "copied", "kept", "scored"))
        block = s.block()
        T2 = NT // 2

        def col(ap, n=None):
            return ap.unsqueeze(2).broadcast_to([P, NT, n or 8])

        @block.sync
        def _(sp):
            if w_gate is not None:
                for c in range(2):
                    sp.dma_start(w[:, c, :], w_gate[c * P:(c + 1) * P, :], allow_slow_non_contiguous=True).then_inc(loaded, 16)
            if bias is not None:
                sp.dma_start(row[:, :], bias.unsqueeze(0)).then_inc(loaded, 16)

        @block.tensor
        def _(pe):
            if w_gate is not None:
                pe.wait_ge(loaded, 32 if bias is None else 48)
            with pe.Fori(0, T2) as i:
                for k in range(2):
                    pe.wait_ge(staged[k], i + 1)
                    pe.wait_ge(copied[k], i)
                    flip_tile(nc, pe, flip[k], stage[:, k, :], r.eye[:, :]).then_inc(flipped[k], 1)
                for k in range(2 if w_gate is not None else 0):
                    score_of = ps[:, bass.ds(2 * i + k, 1), :].rearrange("p a e -> p (a e)")
                    pe.wait_ge(copied[k], i + 1)
                    if bias is not None:
                        nc.tensor.matmul(score_of, r.ones[0:1, :], row[:, :], start=True, stop=False)
                    for c in range(2):
                        last = nc.tensor.matmul(score_of, xs[:, k, c, :], w[:, c, :], start=(bias is None and c == 0), stop=(c == 1))
                    last.then_inc(scored[k], 1)

        @block.scalar
        def _(act):
            with act.Fori(0, T2) as i:
                for k in range(2):
                    act.wait_ge(flipped[k], i + 1)
                    if w_gate is not None:
                        act.wait_ge(scored[k], i)
                    act.wait_ge(kept[k], i)
                    nc.scalar.activation(xs[:, k, :, :], flip[k][:, :, :], ACT.Copy).then_inc(copied[k], 1)
            if kind in ("softmax of two", "share"):
                act.wait_ge(shifted, 1)
                nc.scalar.activation(score[:, :, :], score[:, :, :], ACT.Exp).then_inc(exped, 1)
            if kind == "softmax of two":
                act.wait_ge(differed, 1)
                nc.scalar.activation(t1[:, :], t1[:, :], ACT.Exp).then_inc(weighed, 1)

        @block.vector
        def _(dve):
            link = Chain(dve, chain_sem)
            link(nc.vector.memset(score[:, :, :], NONE))
            with dve.Fori(0, T2) as i:
                stage_tiles(nc, dve, stage, r.xh, i, flipped, staged)
                for k in range(2):
                    dve.wait_ge(copied[k], i + 1)
                    nc.vector.tensor_copy(r.xT[:, :, bass.ds((2 * i + k) * P, P)], xs[:, k, :, :]).then_inc(kept[k], 1)
            if w_gate is None:
                return
            for k in range(2):
                dve.wait_ge(scored[k], T2)
            link(nc.vector.tensor_copy(score[:, :, 0:experts], ps[:, :, :]))
            if kind != "ones":
                link(nc.vector.tensor_reduce(worst[:, :], score[:, :, :], AX.X, ALU.max))
                nc.vector.tensor_tensor(score[:, :, :], score[:, :, :], col(worst[:, :]), ALU.subtract).then_inc(shifted, 1)
                dve.wait_ge(exped, 1)
                link(nc.vector.tensor_reduce(worst[:, :], score[:, :, :], AX.X, ALU.add))
                link(nc.vector.reciprocal(worst[:, :], worst[:, :]))
                link(nc.vector.tensor_tensor(score[:, :, :], score[:, :, :], col(worst[:, :]), ALU.mult))
            for t in range(NT):
                last = nc.vector.max(top[:, t, :], score[:, t, :])
            link(last)
            for t in range(NT):
                last = nc.vector.max_index(which[:, t, :], top[:, t, :], score[:, t, :])
            link(last)
            link(nc.vector.tensor_copy(whichf[:, :, :], which[:, :, 0:2]))
            if kind == "ones":
                link(nc.vector.memset(wt[:, :, :], 1.0))
            elif kind == "softmax of two":
                nc.vector.tensor_tensor(t1[:, :], top[:, :, 1], top[:, :, 0], ALU.subtract).then_inc(differed, 1)
                dve.wait_ge(weighed, 1)
                link(nc.vector.tensor_scalar(wt[:, :, 0], t1[:, :], 1.0, None, ALU.add))
                link(nc.vector.reciprocal(wt[:, :, 0], wt[:, :, 0]))
                link(nc.vector.tensor_tensor(wt[:, :, 1], wt[:, :, 0], t1[:, :], ALU.mult))
            else:
                link(nc.vector.tensor_tensor(t1[:, :], top[:, :, 0], top[:, :, 1], ALU.add))
                link(nc.vector.tensor_scalar(t1[:, :], t1[:, :], 1e-12, None, ALU.max))
                link(nc.vector.reciprocal(t1[:, :], t1[:, :]))
                link(nc.vector.tensor_tensor(wt[:, :, :], top[:, :, 0:2], col(t1[:, :], 2), ALU.mult))
            eight = r.column[:, 0:8].unsqueeze(1).broadcast_to([P, NT, 8])
            link(nc.vector.tensor_tensor(r.gate[:, :, :], eight, col(whichf[:, :, 0]), ALU.is_equal))
            link(nc.vector.tensor_tensor(second[:, :, :], eight, col(whichf[:, :, 1]), ALU.is_equal))
            link(nc.vector.tensor_tensor(r.gate[:, :, :], r.gate[:, :, :], col(wt[:, :, 0]), ALU.mult))
            link(nc.vector.tensor_tensor(second[:, :, :], second[:, :, :], col(wt[:, :, 1]), ALU.mult))
            link(nc.vector.tensor_tensor(r.gate[:, :, :], r.gate[:, :, :], second[:, :, :], ALU.add))


def experts_gelu(nc, r, tag, w1, b1, w2, b2, experts, hidden, gates, out, load):
    HC = hidden // P
    with Scope(nc, tag) as s:
        W1 = s.sb("W1", [P, experts, 2, hidden])
        W2 = s.sb("W2", [P, experts, HC, G])
        B1 = s.sb("B1", [P, experts, HC])
        B2 = s.sb("B2", [P if experts == 2 else 1, experts, G])
        hT = s.sb("hT", [P, 2, HC, BC])
        ps_h = [s.ps(f"ps_h{k}", [P, BC]) for k in range(2)]
        ps_y = [s.ps(f"ps_y{k}", [P, 4, G]) for k in range(2)]
        loaded = s.sem("loaded")
        hidden_made, acted, summed, added = (s.sems(n, 2) for n in ("hidden_made", "acted", "summed", "added"))
        block = s.block()
        PER_H, PER_Y = experts * HC // 2, experts // 2

        n_loads, rows = load(nc, s, W1, W2, B1, B2, w1, b1, w2, b2, loaded, block, hidden)

        @block.tensor
        def _(pe):
            pe.wait_ge(loaded, n_loads)

            def up(i, e):
                for c in range(HC):
                    q = e * HC + c
                    pe.wait_ge(acted[q % 2], i * PER_H + q // 2)
                    for n in range(2):
                        last = nc.tensor.matmul(ps_h[q % 2][:, :], W1[:, e, n, c * P:(c + 1) * P], r.xT[:, n, bass.ds(i * BC, BC)],
                                                start=(n == 0), stop=(n == 1))
                    last.then_inc(hidden_made[q % 2], 1)

            def down(i, e):
                for k in range(2):
                    pe.wait_ge(acted[k], i * PER_H + (e + 1) * HC // 2)
                pe.wait_ge(added[e % 2], i * PER_Y + e // 2)
                for t in range(TB):
                    nc.tensor.matmul(ps_y[e % 2][:, t, :], r.ones[0:1, :], B2[0:1, e, :], start=True, stop=False)
                    for c in range(HC):
                        last = nc.tensor.matmul(ps_y[e % 2][:, t, :], hT[:, e % 2, c, t * P:(t + 1) * P], W2[:, e, c, :],
                                                start=False, stop=(c == HC - 1))
                last.then_inc(summed[e % 2], 1)

            with pe.Fori(0, NB) as i:
                up(i, 0)
                for e in range(experts):
                    if e + 1 < experts:
                        up(i, e + 1)
                    down(i, e)

        @block.scalar
        def _(act):
            act.wait_ge(loaded, n_loads)
            with act.Fori(0, NB) as i:
                for e in range(experts):
                    act.wait_ge(summed[e % 2], i * PER_Y + e // 2)
                    for c in range(HC):
                        q = e * HC + c
                        act.wait_ge(hidden_made[q % 2], i * PER_H + (q // 2 + 1))
                        nc.scalar.activation(hT[:, e % 2, c, :], ps_h[q % 2][:, :], ACT.Gelu, bias=B1[:, e, c:c + 1]).then_inc(acted[q % 2], 1)

        @block.vector
        def _(dve):
            if rows is not None:
                rows(dve)
            with dve.Fori(0, NB) as i:
                for e in range(experts):
                    dve.wait_ge(summed[e % 2], i * PER_Y + (e // 2 + 1))
                    if e:
                        dve.wait_ge(added[(e - 1) % 2], i * PER_Y + ((e - 1) // 2 + 1))
                    for t in range(TB):
                        last = nc.vector.scalar_tensor_tensor(tile_of(out, i * TB + t), ps_y[e % 2][:, t, :], gates(i * TB + t, e),
                                                              tile_of(out, i * TB + t), ALU.mult, ALU.add)
                    last.then_inc(added[e % 2], 1)


def load_all(nc, s, W1, W2, B1, B2, w1, b1, w2, b2, loaded, block, hidden):
    @block.sync
    def _(sp):
        E_ = w1.shape[0]
        for e in range(E_):
            sp.dma_start(W1[:, e, :, :], w1[e].rearrange("(c p) n -> p c n", p=P)).then_inc(loaded, 16)
            sp.dma_start(W2[:, e, :, :], w2[e].rearrange("(c p) n -> p c n", p=P)).then_inc(loaded, 16)
        sp.dma_start(B1[:, :, :], b1.rearrange("e (c p) -> p e c", p=P), allow_slow_non_contiguous=True).then_inc(loaded, 16)
        sp.dma_start(B2[:, :, :], b2.unsqueeze(0)).then_inc(loaded, 16)
    return 16 * (2 * w1.shape[0] + 2), None


def layer_l0_ffn(nc, r, t):
    EX, H1, H2 = 4, 128, 64
    with Scope(nc, "l0f") as s:
        W1 = s.sb("W1", [P, 6, 2, P])
        W2 = s.sb("W2", [P, 2, P])
        V2 = s.sb("V2", [P, EX, H2])
        W3 = s.sb("W3", [P, G])
        V3 = s.sb("V3", [H2, EX, G])
        B1 = s.sb("B1", [P, 6])
        B2 = s.sb("B2", [P, 5])
        B3 = s.sb("B3", [1, 5, G])
        h1 = s.sb("h1", [P, 6, BC])
        h2 = s.sb("h2", [P, 5, BC])
        ps_h = [s.ps(f"ps_h{k}", [P, BC]) for k in range(3)]
        ps_y = [s.ps(f"ps_y{k}", [P, 4, G]) for k in range(2)]
        loaded = s.sem("loaded")
        made, acted, summed, added = s.sems("made", 3), s.sems("acted", 3), s.sems("summed", 2), s.sems("added", 2)
        block = s.block()
        Q = 12
        PER = 4

        @block.sync
        def _(sp):
            g = lambda n: t["L0_ffn_" + n]
            for c in range(2):
                sp.dma_start(W1[:, c, :, :], g("sW1")[:, c * P:(c + 1) * P].rearrange("(k p) n -> p k n", p=P)).then_inc(loaded, 16)
            for e in range(EX):
                sp.dma_start(W1[:, 2 + e, :, :], g("eW1")[e].rearrange("(k p) n -> p k n", p=P)).then_inc(loaded, 16)
            sp.dma_start(W2[:, :, :], g("sW2").rearrange("(k p) n -> p k n", p=P)).then_inc(loaded, 16)
            sp.dma_start(V2[:, :, :], g("eW2").rearrange("e p n -> p e n")).then_inc(loaded, 16)
            sp.dma_start(W3[:, :], g("sW3")).then_inc(loaded, 16)
            sp.dma_start(V3[:, :, :], g("eW3").rearrange("e p n -> p e n")).then_inc(loaded, 16)
            with nc.allow_non_contiguous_dma("biases"):
                sp.dma_start(B1[:, 0:2], g("sb1").rearrange("(c p) -> p c", p=P), allow_slow_non_contiguous=True).then_inc(loaded, 16)
                sp.dma_start(B1[:, 2:6], g("eb1").rearrange("e p -> p e"), allow_slow_non_contiguous=True).then_inc(loaded, 16)
                sp.dma_start(B2[:, 0:1], g("sb2").rearrange("(c p) -> p c", p=P), allow_slow_non_contiguous=True).then_inc(loaded, 16)
                sp.dma_start(B2[0:H2, 1:5], g("eb2").rearrange("e p -> p e"), allow_slow_non_contiguous=True).then_inc(loaded, 16)
            sp.dma_start(B3[:, 0, :], g("sb3").unsqueeze(0)).then_inc(loaded, 16)
            sp.dma_start(B3[:, 1:5, :], g("eb3").unsqueeze(0)).then_inc(loaded, 16)

        def rows(q):
            return P if q <= 6 else H2

        USES = [len(range(b, 11, 3)) for b in range(3)]

        @block.tensor
        def _(pe):
            pe.wait_ge(loaded, 16 * 16)
            with pe.Fori(0, NB) as i:
                for q in range(11):
                    b, n = q % 3, q // 3
                    pe.wait_ge(acted[b], i * USES[b] + n)
                    if q < 6:
                        for c in range(2):
                            last = nc.tensor.matmul(ps_h[b][:, :], W1[:, q, c, :], r.xT[:, c, bass.ds(i * BC, BC)], start=(c == 0), stop=(c == 1))
                    elif q == 6:
                        for z in range(3):
                            pe.wait_ge(acted[z], i * USES[z] + 2)
                        for c in range(2):
                            last = nc.tensor.matmul(ps_h[b][:, :], W2[:, c, :], h1[:, c, :], start=(c == 0), stop=(c == 1))
                    else:
                        last = nc.tensor.matmul(ps_h[b][0:H2, :], V2[:, q - 7, :], h1[:, q - 5, :], start=True, stop=True)
                    last.then_inc(made[b], 1)
                for z in range(3):
                    pe.wait_ge(acted[z], (i + 1) * USES[z])
                for e in range(5):
                    n, per = e // 2, (3, 2)[e % 2]
                    pe.wait_ge(added[e % 2], i * per + n)
                    for tt in range(TB):
                        nc.tensor.matmul(ps_y[e % 2][:, tt, :], r.ones[0:1, :], B3[:, e, :], start=True, stop=False)
                        if e == 0:
                            last = nc.tensor.matmul(ps_y[e % 2][:, tt, :], h2[:, 0, tt * P:(tt + 1) * P], W3[:, :], start=False, stop=True)
                        else:
                            last = nc.tensor.matmul(ps_y[e % 2][:, tt, :], h2[0:H2, e, tt * P:(tt + 1) * P], V3[:, e - 1, :], start=False, stop=True)
                    last.then_inc(summed[e % 2], 1)

        @block.scalar
        def _(act):
            act.wait_ge(loaded, 16 * 16)
            with act.Fori(0, NB) as i:
                for q in range(11):
                    b, n = q % 3, q // 3
                    if q == 6:
                        act.wait_ge(summed[0], i * 3)
                        act.wait_ge(summed[1], i * 2)
                    act.wait_ge(made[b], i * USES[b] + (n + 1))
                    if q < 6:
                        ins = nc.scalar.activation(h1[:, q, :], ps_h[b][:, :], ACT.Relu, bias=B1[:, q:q + 1])
                    else:
                        m = rows(q)
                        ins = nc.scalar.activation(h2[0:m, q - 6, :], ps_h[b][0:m, :], ACT.Relu, bias=B2[0:m, q - 6:q - 5])
                    ins.then_inc(acted[b], 1)

        @block.vector
        def _(dve):
            with dve.Fori(0, NB) as i:
                for e in range(5):
                    n, per = e // 2, (3, 2)[e % 2]
                    dve.wait_ge(summed[e % 2], i * per + (n + 1))
                    if e:
                        dve.wait_ge(added[(e - 1) % 2], i * (3, 2)[(e - 1) % 2] + ((e - 1) // 2 + 1))
                    for tt in range(TB):
                        xt = tile_of(r.x, i * TB + tt)
                        by = r.gate[:, bass.ds(i * TB + tt, 1), e - 1].rearrange("p a -> p a") if e else 1.0
                        last = nc.vector.scalar_tensor_tensor(xt, ps_y[e % 2][:, tt, :], by, xt, ALU.mult, ALU.add)
                    last.then_inc(added[e % 2], 1)


def up_l3(nc, r, w1, b1, hf):
    with Scope(nc, "l3a") as s:
        W = s.sb("W", [P, 2, 2 * G])
        B1 = s.sb("B1", [P, 4])
        ps = [s.ps(f"ps{k}", [P, BC]) for k in range(4)]
        loaded = s.sem("loaded")
        made, taken = s.sems("made", 4), s.sems("taken", 4)
        block = s.block()

        @block.sync
        def _(sp):
            sp.dma_start(W[:, :, :], w1.rearrange("(c p) n -> p c n", p=P)).then_inc(loaded, 16)
            sp.dma_start(B1[:, :], b1.rearrange("(c p) -> p c", p=P), allow_slow_non_contiguous=True).then_inc(loaded, 16)

        @block.tensor
        def _(pe):
            pe.wait_ge(loaded, 32)
            with pe.Fori(0, NB) as i:
                for c in range(4):
                    pe.wait_ge(taken[c], i)
                    for k in range(2):
                        last = nc.tensor.matmul(ps[c][:, :], W[:, k, c * P:(c + 1) * P], r.xT[:, k, bass.ds(i * BC, BC)], start=(k == 0), stop=(k == 1))
                    last.then_inc(made[c], 1)

        @block.vector
        def _(dve):
            dve.wait_ge(loaded, 32)
            with dve.Fori(0, NB) as i:
                for c in range(4):
                    dve.wait_ge(made[c], i + 1)
                    nc.vector.tensor_scalar(hf[:, c, bass.ds(i * BC, BC)], ps[c][:, :], B1[:, c:c + 1], None, ALU.add).then_inc(taken[c], 1)


def column_moments(nc, link, stats, moments, rows, chunks):
    cuts = [(a, min(a + 512, N)) for a in range(0, N, 512)]
    for c in range(chunks):
        for n, (a, b) in enumerate(cuts):
            last = nc.vector.bn_stats(stats[:, c, n, :], rows[:, c, a:b])
    link(last)
    for c in range(chunks):
        last = nc.vector.bn_aggr(moments[:, c, :], stats[:, c, :, :].rearrange("p n s -> p (n s)"))
    link(last)


def batch_norm_l3(nc, r, gamma, beta, hf):
    with Scope(nc, "l3b") as s:
        stats = s.sb("stats", [P, 4, 8, 6])
        moments = s.sb("moments", [P, 4, 2])
        gb = s.sb("gb", [P, 2, 4])
        std = s.sb("std", [P, 4])
        scale = s.sb("scale", [P, 4])
        shift = s.sb("shift", [P, 4])
        loaded, chain_sem, added, rooted, ready = (s.sem(n) for n in ("loaded", "chain", "added", "rooted", "ready"))
        block = s.block()

        @block.sync
        def _(sp):
            sp.dma_start(gb[:, 0, :], gamma.rearrange("(c p) -> p c", p=P), allow_slow_non_contiguous=True).then_inc(loaded, 16)
            sp.dma_start(gb[:, 1, :], beta.rearrange("(c p) -> p c", p=P), allow_slow_non_contiguous=True).then_inc(loaded, 16)

        @block.vector
        def _(dve):
            link = Chain(dve, chain_sem)
            column_moments(nc, link, stats, moments, hf, 4)
            nc.vector.tensor_scalar(std[:, :], moments[:, :, 1], EPS, None, ALU.add).then_inc(added, 1)
            dve.wait_ge(rooted, 1)
            dve.wait_ge(loaded, 32)
            link(nc.vector.reciprocal(std[:, :], std[:, :]))
            link(nc.vector.tensor_tensor(scale[:, :], std[:, :], gb[:, 0, :], ALU.mult))
            link(nc.vector.tensor_tensor(shift[:, :], moments[:, :, 0], scale[:, :], ALU.mult))
            nc.vector.tensor_tensor(shift[:, :], gb[:, 1, :], shift[:, :], ALU.subtract).then_inc(ready, 1)

        @block.scalar
        def _(act):
            act.wait_ge(added, 1)
            nc.scalar.activation(std[:, :], std[:, :], ACT.Sqrt).then_inc(rooted, 1)
            act.wait_ge(ready, 1)
            for c in range(4):
                nc.scalar.activation(hf[:, c, :], hf[:, c, :], ACT.Relu, bias=shift[:, c:c + 1], scale=scale[:, c:c + 1])


def down_l3(nc, r, w2, b2, hf):
    with Scope(nc, "l3d") as s:
        W = s.sb("W", [P, 4, G])
        B2 = s.sb("B2", [P, 2])
        ps = [s.ps(f"ps{k}", [P, BC]) for k in range(2)]
        loaded = s.sem("loaded")
        made, taken = s.sems("made", 2), s.sems("taken", 2)
        block = s.block()

        @block.sync
        def _(sp):
            sp.dma_start(W[:, :, :], w2.rearrange("(c p) n -> p c n", p=P)).then_inc(loaded, 16)
            sp.dma_start(B2[:, :], b2.rearrange("(c p) -> p c", p=P), allow_slow_non_contiguous=True).then_inc(loaded, 16)

        @block.tensor
        def _(pe):
            pe.wait_ge(loaded, 32)
            with pe.Fori(0, NB) as i:
                for c in range(2):
                    pe.wait_ge(taken[c], i)
                    for k in range(4):
                        last = nc.tensor.matmul(ps[c][:, :], W[:, k, c * P:(c + 1) * P], hf[:, k, bass.ds(i * BC, BC)], start=(k == 0), stop=(k == 3))
                    last.then_inc(made[c], 1)

        @block.vector
        def _(dve):
            dve.wait_ge(loaded, 32)
            with dve.Fori(0, NB) as i:
                for c in range(2):
                    dve.wait_ge(made[c], i + 1)
                    nc.vector.tensor_scalar(r.xT[:, c, bass.ds(i * BC, BC)], ps[c][:, :], B2[:, c:c + 1], None, ALU.add).then_inc(taken[c], 1)


def graph_norm_l3(nc, r, t):
    with Scope(nc, "l3n") as s:
        stats = s.sb("stats", [P, 2, 8, 6])
        moments = s.sb("moments", [P, 2, 2])
        par = s.sb("par", [P, 5, 2])
        mu, var, d, q, s1, m1, v2, rest, s2, scale, shift = (
            s.sb(n, [P, 2]) for n in ("mu", "var_c", "d", "q", "s1", "m1", "v2", "rest", "s2", "scale", "shift"))
        mean_g = s.sb("mean_g", [P, 1])
        rg = s.sb("rg", [P, 1])
        stage = s.sb("stage", [P, 2, 2, P])
        ps_sum = s.ps("ps_sum", [P, 4])
        back = [s.ps(f"back{k}", [P, 2, P]) for k in range(2)]
        names = ("loaded", "chain", "averaged", "summed", "squared", "summed2", "g_added", "g_rooted", "c_added", "c_rooted", "ready", "cut")
        loaded, chain_sem, averaged, summed, squared, summed2, g_added, g_rooted, c_added, c_rooted, ready, cut = (s.sem(n) for n in names)
        staged, flipped, taken = (s.sems(n, 2) for n in ("staged", "flipped", "taken"))
        block = s.block()
        LW, LB, GW, GB, MS = range(5)
        T2 = NT // 2

        @block.sync
        def _(sp):
            for n, name in enumerate(("ln_w", "ln_b", "gn_w", "gn_b", "gn_ms")):
                sp.dma_start(par[:, n, :], t["L3_gnn_" + name].rearrange("(c p) -> p c", p=P), allow_slow_non_contiguous=True).then_inc(loaded, 16)

        @block.vector
        def _(dve):
            link = Chain(dve, chain_sem)
            column_moments(nc, link, stats, moments, r.xT, 2)
            link(nc.vector.tensor_copy(mu[:, :], moments[:, :, 0]))
            nc.vector.tensor_copy(var[:, :], moments[:, :, 1]).then_inc(averaged, 1)
            dve.wait_ge(summed, 1)
            link(nc.vector.tensor_reduce(mean_g[:, :], ps_sum[:, 0:2], AX.X, ALU.add))
            link(nc.vector.tensor_scalar(mean_g[:, :], mean_g[:, :], 1.0 / G, None, ALU.mult))
            link(nc.vector.tensor_scalar(d[:, :], mu[:, :], mean_g[:, 0:1], None, ALU.subtract))
            link(nc.vector.tensor_tensor(q[:, :], d[:, :], d[:, :], ALU.mult))
            nc.vector.tensor_tensor(q[:, :], q[:, :], var[:, :], ALU.add).then_inc(squared, 1)
            dve.wait_ge(summed2, 1)
            link(nc.vector.tensor_reduce(rg[:, :], ps_sum[:, 2:4], AX.X, ALU.add))
            nc.vector.tensor_scalar(rg[:, :], rg[:, :], 1.0 / G, EPS, ALU.mult, ALU.add).then_inc(g_added, 1)
            dve.wait_ge(g_rooted, 1)
            dve.wait_ge(loaded, 80)
            link(nc.vector.reciprocal(rg[:, :], rg[:, :]))
            link(nc.vector.tensor_scalar(s1[:, :], par[:, LW, :], rg[:, 0:1], None, ALU.mult))
            link(nc.vector.tensor_tensor(m1[:, :], d[:, :], s1[:, :], ALU.mult))
            link(nc.vector.tensor_tensor(m1[:, :], m1[:, :], par[:, LB, :], ALU.add))
            link(nc.vector.tensor_tensor(v2[:, :], m1[:, :], par[:, MS, :], ALU.mult))
            link(nc.vector.tensor_tensor(rest[:, :], m1[:, :], v2[:, :], ALU.subtract))
            link(nc.vector.tensor_tensor(q[:, :], rest[:, :], rest[:, :], ALU.mult))
            link(nc.vector.tensor_tensor(v2[:, :], s1[:, :], s1[:, :], ALU.mult))
            link(nc.vector.tensor_tensor(v2[:, :], v2[:, :], var[:, :], ALU.mult))
            link(nc.vector.tensor_tensor(v2[:, :], v2[:, :], q[:, :], ALU.add))
            nc.vector.tensor_scalar(v2[:, :], v2[:, :], EPS, None, ALU.add).then_inc(c_added, 1)
            dve.wait_ge(c_rooted, 1)
            link(nc.vector.reciprocal(s2[:, :], v2[:, :]))
            link(nc.vector.tensor_tensor(s2[:, :], s2[:, :], par[:, GW, :], ALU.mult))
            link(nc.vector.tensor_tensor(scale[:, :], s1[:, :], s2[:, :], ALU.mult))
            link(nc.vector.tensor_tensor(shift[:, :], rest[:, :], s2[:, :], ALU.mult))
            link(nc.vector.tensor_tensor(shift[:, :], shift[:, :], par[:, GB, :], ALU.add))
            link(nc.vector.tensor_tensor(q[:, :], scale[:, :], mu[:, :], ALU.mult))
            nc.vector.tensor_tensor(shift[:, :], shift[:, :], q[:, :], ALU.subtract).then_inc(ready, 1)
            dve.wait_ge(cut, 2)
            with dve.Fori(0, T2) as i:
                for k in range(2):
                    dve.wait_ge(flipped[k], i)
                    nc.vector.tensor_scalar(stage[:, k, :, :], r.xT[:, :, bass.ds((2 * i + k) * P, P)], 1.0, None, ALU.mult).then_inc(staged[k], 1)
                for k in range(2):
                    xt = tile_of(r.x, 2 * i + k)
                    dve.wait_ge(flipped[k], i + 1)
                    nc.vector.tensor_tensor(xt, xt, back[k][:, :, :].rearrange("p c n -> p (c n)"), ALU.add).then_inc(taken[k], 1)

        @block.scalar
        def _(act):
            act.wait_ge(g_added, 1)
            nc.scalar.activation(rg[:, :], rg[:, :], ACT.Sqrt).then_inc(g_rooted, 1)
            act.wait_ge(c_added, 1)
            nc.scalar.activation(v2[:, :], v2[:, :], ACT.Sqrt).then_inc(c_rooted, 1)
            act.wait_ge(ready, 1)
            for c in range(2):
                nc.scalar.activation(r.xT[:, c, :], r.xT[:, c, :], ACT.Relu, bias=shift[:, c:c + 1], scale=scale[:, c:c + 1]).then_inc(cut, 1)

        @block.tensor
        def _(pe):
            pe.wait_ge(averaged, 1)
            nc.tensor.matmul(ps_sum[:, 0:2], r.ones[:, :], mu[:, :], start=True, stop=True).then_inc(summed, 1)
            pe.wait_ge(squared, 1)
            nc.tensor.matmul(ps_sum[:, 2:4], r.ones[:, :], q[:, :], start=True, stop=True).then_inc(summed2, 1)
            with pe.Fori(0, T2) as i:
                for k in range(2):
                    pe.wait_ge(staged[k], i + 1)
                    pe.wait_ge(taken[k], i)
                    for c in range(2):
                        last = nc.tensor.transpose(back[k][:, c, :], stage[:, k, c, :], r.eye[:, :])
                    last.then_inc(flipped[k], 1)


def route_l3(nc, r, w_router, bias, which, weight):
    EX = 8
    CAPACITY = float(-(-(N * 5) // (4 * EX)))
    with Scope(nc, "l3r") as s:
        w = s.sb("w", [P, 2, EX])
        row = s.sb("row", [1, EX])
        mean = s.sb("mean", [P, 2])
        p = s.sb("p", [1, EX])
        load = s.sb("load", [1, EX])
        one = s.sb("one", [1, 1])
        top = s.sb("top", [1, 8])
        idx = s.sb("idx", [1, 8], mybir.dt.uint32)
        pair = s.sb("pair", [1, 4])
        ps = s.ps("ps", [1, EX])
        ps4 = s.ps("ps4", [P, 4])
        names = ("loaded", "chain", "averaged", "scored", "e1", "e1_done", "e2", "e2_done", "e3", "e3_done", "paired", "spread")
        loaded, chain_sem, averaged, scored, e1, e1_done, e2, e2_done, e3, e3_done, paired, spread = (s.sem(n) for n in names)
        block = s.block()

        @block.sync
        def _(sp):
            sp.dma_start(w[:, :, :], w_router.rearrange("(c p) n -> p c n", p=P)).then_inc(loaded, 16)
            sp.dma_start(row[:, :], bias.unsqueeze(0)).then_inc(loaded, 16)

        @block.tensor
        def _(pe):
            pe.wait_ge(loaded, 32)
            pe.wait_ge(averaged, 1)
            nc.tensor.matmul(ps[:, :], r.ones[0:1, 0:1], row[:, :], start=True, stop=False)
            for c in range(2):
                last = nc.tensor.matmul(ps[:, :], mean[:, c:c + 1], w[:, c, :], start=False, stop=(c == 1))
            last.then_inc(scored, 1)
            pe.wait_ge(paired, 1)
            nc.tensor.matmul(ps4[:, :], r.ones[0:1, :], pair[:, :], start=True, stop=True).then_inc(spread, 1)

        @block.scalar
        def _(act):
            for begun, done, what in ((e1, e1_done, p[:, :]), (e2, e2_done, p[:, :]), (e3, e3_done, pair[:, 1:2])):
                act.wait_ge(begun, 1)
                nc.scalar.activation(what, what, ACT.Exp).then_inc(done, 1)

        @block.vector
        def _(dve):
            link = Chain(dve, chain_sem)

            def softmax(begun, done):
                link(nc.vector.tensor_reduce(one[:, :], p[:, :], AX.X, ALU.max))
                nc.vector.tensor_scalar(p[:, :], p[:, :], one[:, 0:1], None, ALU.subtract).then_inc(begun, 1)
                dve.wait_ge(done, 1)
                link(nc.vector.tensor_reduce(one[:, :], p[:, :], AX.X, ALU.add))
                link(nc.vector.reciprocal(one[:, :], one[:, :]))
                link(nc.vector.tensor_scalar(p[:, :], p[:, :], one[:, 0:1], None, ALU.mult))

            link(nc.vector.tensor_reduce(mean[:, :], r.xT[:, :, 0:N], AX.X, ALU.add))
            nc.vector.tensor_scalar(mean[:, :], mean[:, :], 1.0 / N, None, ALU.mult).then_inc(averaged, 1)
            dve.wait_ge(scored, 1)
            link(nc.vector.tensor_copy(p[:, :], ps[:, :]))
            softmax(e1, e1_done)
            link(nc.vector.tensor_scalar(load[:, :], p[:, :], float(N), 1e-30, ALU.mult, ALU.max))
            link(nc.vector.reciprocal(load[:, :], load[:, :]))
            link(nc.vector.tensor_scalar(load[:, :], load[:, :], CAPACITY, 1.0, ALU.mult, ALU.min))
            link(nc.vector.tensor_tensor(p[:, :], p[:, :], load[:, :], ALU.mult))
            softmax(e2, e2_done)
            link(nc.vector.max(top[:, :], p[:, :]))
            link(nc.vector.max_index(idx[:, :], top[:, :], p[:, :]))
            link(nc.vector.tensor_copy(pair[:, 2:4], idx[:, 0:2]))
            nc.vector.tensor_tensor(pair[:, 1:2], top[:, 1:2], top[:, 0:1], ALU.subtract).then_inc(e3, 1)
            dve.wait_ge(e3_done, 1)
            link(nc.vector.tensor_scalar(one[:, :], pair[:, 1:2], 1.0, None, ALU.add))
            link(nc.vector.reciprocal(pair[:, 0:1], one[:, :]))
            nc.vector.tensor_tensor(pair[:, 1:2], pair[:, 1:2], pair[:, 0:1], ALU.mult).then_inc(paired, 1)
            dve.wait_ge(spread, 1)
            link(nc.vector.tensor_copy(weight[:, :], ps4[:, 0:2]))
            link(nc.vector.tensor_copy(which[:, :], ps4[:, 2:4]))


def load_two(nc, r, which):
    def load(nc, s, W1, W2, B1, B2, w1, b1, w2, b2, loaded, block, hidden):
        HC = hidden // P
        base = s.sb("base", [P, 2, 1 + 2 + HC])
        row = s.sb("row_of", [P, 2, 1 + 2 + HC], I32)
        rowed, chain_sem = s.sem("rowed"), s.sem("chain")
        EX = w1.shape[0]
        w1_rows, w2_rows = w1.rearrange("e d f -> (e d) f"), w2.rearrange("e f d -> (e f) d")
        b1_rows = b1.rearrange("e (f o) -> (e f) o", o=1)

        @block.gpsimd
        def _(pool):
            pool.wait_ge(rowed, 1)
            for n in range(2):
                def at(m):
                    return bass.IndirectOffsetOnAxis(ap=row[:, n, m:m + 1], axis=0)
                pool.indirect_dma_start(B2[:, n, :], None, b2, at(0), bounds_check=EX - 1, oob_is_err=False).then_inc(loaded, 16)
                for c in range(2):
                    pool.indirect_dma_start(W1[:, n, c, :], None, w1_rows, at(1 + c), bounds_check=EX * G - 1, oob_is_err=False).then_inc(loaded, 16)
                for c in range(HC):
                    pool.indirect_dma_start(W2[:, n, c, :], None, w2_rows, at(3 + c), bounds_check=EX * hidden - 1, oob_is_err=False).then_inc(loaded, 16)
                    pool.indirect_dma_start(B1[:, n, c:c + 1], None, b1_rows, at(3 + c), bounds_check=EX * hidden - 1, oob_is_err=False).then_inc(loaded, 16)

        def rows(dve):
            link = Chain(dve, chain_sem)
            for n in range(2):
                link(nc.vector.tensor_copy(base[:, n, 0:1], which[:, n:n + 1]))
                for m, (size, c) in enumerate([(G, c) for c in range(2)] + [(hidden, c) for c in range(HC)]):
                    link(nc.vector.tensor_scalar(base[:, n, 1 + m:2 + m], which[:, n:n + 1], float(size), float(c * P), ALU.mult, ALU.add))
                    link(nc.vector.tensor_tensor(base[:, n, 1 + m:2 + m], base[:, n, 1 + m:2 + m], r.partition[:, :], ALU.add))
            nc.vector.tensor_copy(row[:, :, :], base[:, :, :]).then_inc(rowed, 1)
        return 16 * 2 * (3 + 2 * HC), rows
    return load


def finish_l3(nc, r, gamma, beta):
    with Scope(nc, "l3z") as s:
        gb = s.sb("gb", [P, 2, G])
        loaded, chain_sem = s.sem("loaded"), s.sem("chain")
        block = s.block()

        @block.sync
        def _(sp):
            sp.dma_start(gb[:, 0, :], gamma.unsqueeze(0).broadcast_to([P, G])).then_inc(loaded, 16)
            sp.dma_start(gb[:, 1, :], beta.unsqueeze(0).broadcast_to([P, G])).then_inc(loaded, 16)

        @block.vector
        def _(dve):
            link = Chain(dve, chain_sem)

            def all_tiles(n):
                return gb[:, n, :].unsqueeze(1).broadcast_to([P, NT, G])

            dve.wait_ge(loaded, 32)
            link(nc.vector.tensor_tensor(r.xh[:, :, :], r.xh[:, :, :], all_tiles(0), ALU.mult))
            link(nc.vector.tensor_tensor(r.x[:, :, :], r.x[:, :, :], all_tiles(1), ALU.add))
            link(nc.vector.tensor_tensor(r.x[:, :, :], r.x[:, :, :], r.xh[:, :, :], ALU.add))


def save_features(nc, r, table):
    with Scope(nc, "sv") as s:
        stored = s.sem("stored")
        block = s.block()

        @block.sync
        def _(sp):
            sp.dma_start(table.rearrange("(t p) f -> p t f", p=P), r.xh[:, :, :]).then_inc(stored, 16)
            sp.wait_ge(stored, 16)


def build(nc, t, out, upto=99):
    f = t
    qv = nc.dram_tensor("qv", [NPAD, 2 * G], F32, kind="Internal").ap()
    kd = nc.dram_tensor("kd", [NPAD, G], F32, kind="Internal").ap()
    wide_states = nc.dram_tensor("wide_states", [E + 1, 3 * G], F32, kind="Internal").ap()
    carries = nc.dram_tensor("carries", [LANES + 1, 3 * G], F32, kind="Internal").ap()
    head_states = nc.dram_tensor("head_states", [E + 1, 2 * H + G], F32, kind="Internal").ap()
    row_table = nc.dram_tensor("row_table", [NPAD, G], F32, kind="Internal").ap()
    sum_states = nc.dram_tensor("sum_states", [E + 1, G], F32, kind="Internal").ap()
    sum_carries = nc.dram_tensor("sum_carries", [LANES + 1, G], F32, kind="Internal").ap()
    keys_t = nc.dram_tensor("keys_t", [STEPS, 2, LANES], F32, kind="Internal").ap()
    sorted_edges = nc.dram_tensor("sorted_edges", [E, 2], I32, kind="Internal").ap()
    with Scope(nc, "r") as s:
        r = Resident()
        r.x = s.sb("x", [P, NT, G])
        r.gate = s.sb("gate", [P, NT, 8])
        r.xT = s.sb("xT", [P, 2, NPAD])
        r.xh = s.sb("xh", [P, NT, G])
        r.var = s.sb("var", [P, NT])
        r.eye = s.sb("eye", [P, P])
        r.below = s.sb("below", [P, P])
        r.above = s.sb("above", [P, P])
        r.ones = s.sb("ones", [P, P])
        r.wide_ones = s.sb("wide_ones", [P, STEPS])
        r.column = s.sb("column", [P, P])
        r.partition = s.sb("partition", [P, 1])
        r.made = s.sem("made")
        r.by_dst, r.by_src = Order(), Order()
        for tag, o in (("dst", r.by_dst), ("src", r.by_src)):
            o.key = s.sb(f"key_{tag}", [LANES, STEPS + 2 * B], I32)
            o.far = s.sb(f"far_{tag}", [LANES, STEPS + 2 * B], I32)
            o.cont = s.sb(f"cont_{tag}", [LANES, STEPS])
            o.pen = s.sb(f"pen_{tag}", [LANES, STEPS])
            o.count = s.sb(f"count_{tag}", [P, NT])
            o.end_row = s.sb(f"end_row_{tag}", [P, NT], I32)
            o.carry_row = s.sb(f"carry_row_{tag}", [P, NT], I32)
            o.gate = s.sb(f"gate_{tag}", [P, LANES])
            o.gate_pen = s.sb(f"gate_pen_{tag}", [P, LANES])
        load_constants(nc, r, t["x"], t["src"], t["dst"])
        with Scope(nc, "h") as hs:
            hist = hs.sb("hist", [P, STEPS + 1, NT])
            count_keys(nc, r, r.by_dst, "cd", hist, r.by_dst.key, False)
            if upto >= 5:
                count_keys(nc, r, r.by_src, "cs", hist, r.by_dst.far, True)
                sort_edges(nc, r, r.by_src, r.by_dst.far, r.by_dst.key, hist, keys_t, sorted_edges)
        lane_tables(nc, r, r.by_dst, "ld", t["dst"])
        if upto >= 5:
            lane_tables(nc, r, r.by_src, "ls", sorted_edges[:, 0])
        if upto >= 1:
            normalize(nc, r, "n0", r.x)
            project_l0(nc, r, t["L0_gnn_Wqkv"], t["L0_gnn_gamma"], t["L0_gnn_beta"], qv, kd)
            with Scope(nc, "e0") as es:
                tail = es.sb("tail", [LANES, 3 * G])
                edges_l0(nc, r, r.by_dst, qv, kd, wide_states, tail)
                carry_softmax(nc, r, r.by_dst, "c0", tail, carries, wide_states, G)
            finish_softmax(nc, r, r.by_dst, "f0", wide_states, carries, G, r.x)
        agg = r.xT[:, :, :].rearrange("p c n -> p (c n)").rearrange("p (t f) -> p t f", f=G)
        def gate(n, e):
            return r.gate[:, bass.ds(n, 1), e]

        if upto >= 2:
            normalize(nc, r, "n1", r.x)
            route(nc, r, "g0", t["L0_ffn_gW"], t["L0_ffn_gb"], 4, "softmax of two")
            layer_l0_ffn(nc, r, t)
        if upto >= 3:
            normalize(nc, r, "n2", r.x)
            project_l1(nc, r, t["L1_gnn_W_self"], t["L1_gnn_W_neigh"], row_table)
            with Scope(nc, "e1") as es:
                tail = es.sb("tail", [LANES, 3 * G])
                edges_sum(nc, r, r.by_dst, "l1e", row_table, sum_states, tail)
                carry_sum(nc, r, r.by_dst, "c1", tail, sum_carries, sum_states)
            finish_sum(nc, r, r.by_dst, "f1", sum_states, sum_carries, True, r.x)
        if upto >= 4:
            normalize(nc, r, "n3", r.x)
            route(nc, r, "g1", t["L1_ffn_Wg"], t["L1_ffn_bg"], 8, "ones")
            experts_gelu(nc, r, "l1f", t["L1_ffn_W1"], t["L1_ffn_b1"], t["L1_ffn_W2"], t["L1_ffn_b2"], 8, 512, gate, r.x, load_all)
        if upto >= 5:
            normalize(nc, r, "n4", r.x)
            project_l2(nc, r, [t["L2_gnn_Wk"], t["L2_gnn_Wv"], t["L2_gnn_Wq"]], [t["L2_gnn_bk"], t["L2_gnn_bv"], t["L2_gnn_bq"]], kd, qv)
            with Scope(nc, "e2") as es:
                tail = es.sb("tail", [LANES, 3 * G])
                edges_l2(nc, r, r.by_src, kd, qv, head_states, tail)
                carry_softmax(nc, r, r.by_src, "c2", tail, carries, head_states, H)
            finish_softmax(nc, r, r.by_src, "f2", head_states, carries, H, agg)
            project_out(nc, r, agg, t["L2_gnn_Wo"], t["L2_gnn_bo"])
        if upto >= 6:
            normalize(nc, r, "n5", r.x)
            route(nc, r, "g2", t["L2_ffn_router_w"].rearrange("e d -> d e"), None, 8, "share")
            experts_gelu(nc, r, "l2f", t["L2_ffn_w1"], t["L2_ffn_b1"], t["L2_ffn_w2"], t["L2_ffn_b2"], 8, 256, gate, r.x, load_all)
            add_features(nc, r, "l2r", r.xh)
        if upto >= 7:
            normalize(nc, r, "n6", r.x)
            save_features(nc, r, row_table)
            add_features(nc, r, "l3r0", r.xh)
            with Scope(nc, "e3") as es:
                tail = es.sb("tail", [LANES, 3 * G])
                edges_sum(nc, r, r.by_dst, "l3e", row_table, sum_states, tail, t["edge_attr_256"])
                carry_sum(nc, r, r.by_dst, "c3", tail, sum_carries, sum_states)
            finish_sum(nc, r, r.by_dst, "f3", sum_states, sum_carries, False, r.xh)
            route(nc, r, "g3", None, None, 8, None)
            with Scope(nc, "hf") as es:
                hf = es.sb("hf", [P, 4, NPAD])
                up_l3(nc, r, t["L3_gnn_W1"], t["L3_gnn_b1"], hf)
                batch_norm_l3(nc, r, t["L3_gnn_bn_gamma"], t["L3_gnn_bn_beta"], hf)
                down_l3(nc, r, t["L3_gnn_W2"], t["L3_gnn_b2"], hf)
            graph_norm_l3(nc, r, t)
        if upto >= 8:
            normalize(nc, r, "n7", r.x)
            route(nc, r, "g4", None, None, 8, None)
            with Scope(nc, "w3") as es:
                which = es.sb("which", [P, 2])
                weight = es.sb("weight", [P, 2])
                route_l3(nc, r, t["L3_ffn_Wr"], t["L3_ffn_br"], which, weight)
                experts_gelu(nc, r, "l3f", t["L3_ffn_W1"], t["L3_ffn_b1"], t["L3_ffn_W2"], t["L3_ffn_b2"], 2, 512,
                             lambda n, e: weight[:, e:e + 1], r.xh, load_two(nc, r, which))
            normalize(nc, r, "n8", r.xh)
            finish_l3(nc, r, t["L3_ffn_gamma"], t["L3_ffn_beta"])
        store(nc, r, out)


def add_features(nc, r, tag, more):
    with Scope(nc, tag) as s:
        block = s.block()

        @block.vector
        def _(dve):
            nc.vector.tensor_tensor(r.x[:, 0:NT // 2, :], r.x[:, 0:NT // 2, :], more[:, 0:NT // 2, :], ALU.add)

        @block.gpsimd
        def _(pool):
            nc.gpsimd.tensor_tensor(r.x[:, NT // 2:, :], r.x[:, NT // 2:, :], more[:, NT // 2:, :], ALU.add)


def store(nc, r, out):
    with Scope(nc, "st") as s:
        stored = s.sem("stored")
        block = s.block()

        @block.sync
        def _(sp):
            sp.dma_start(out[0:(NT - 1) * P, :].rearrange("(t p) f -> p t f", p=P), r.x[:, 0:NT - 1, :]).then_inc(stored, 16)
            sp.dma_start(out[(NT - 1) * P:N, :], r.x[0:LAST, NT - 1, :]).then_inc(stored, 16)
            sp.wait_ge(stored, 32)


def kernel(**inputs):
    import numpy as np
    import concourse.bacc as bacc
    from concourse.bass_utils import run_bass_kernel_spmd

    nc = bacc.Bacc("TRN2", target_bir_lowering=False, num_devices=1)
    arrays, t = {}, {}
    for name, a in inputs.items():
        a = np.ascontiguousarray(a)
        arrays[f"in_{name}"] = a
        t[name] = nc.dram_tensor(f"in_{name}", a.shape, mybir.dt.from_np(a.dtype), kind="ExternalInput").ap()
    out = nc.dram_tensor("out_x", (N, G), F32, kind="ExternalOutput").ap()
    build(nc, t, out)
    got = run_bass_kernel_spmd(nc, [arrays], core_ids=[0])
    return got.results[0]["out_x"]
```

```python
import concourse.bass as bass
from concourse import mybir
from contextlib import ExitStack, contextmanager

F32 = mybir.dt.float32
BF16 = mybir.dt.bfloat16
I32 = mybir.dt.int32
ALU = mybir.AluOpType
ACT = mybir.ActivationFunctionType
AX = mybir.AxisListType

P = 128
N = 3750
E = 60000
G = 256
H = 8
D = G // H
NT = -(-N // P)
NPAD = NT * P
LAST = N - (NT - 1) * P
LANES = 120
STEPS = E // LANES
B = 5
U = 4
TURNS = STEPS // (U * B)
TURNS2 = STEPS // (2 * B)
NONE = -1.0e30
EPS = 1e-5
TB = 3
NB = NT // TB
BC = TB * P


class Chain:

    def __init__(self, eng, sem):
        self.eng, self.sem, self.base, self.n, self.turn, self.per = eng, sem, 0, 0, None, 0

    def __call__(self, ins):
        self.n += 1
        ins.then_inc(self.sem, 1)
        self.eng.wait_ge(self.sem, self.value())

    def mark(self, ins):
        self.n += 1
        ins.then_inc(self.sem, 1)

    def all_but(self, few):
        self.eng.wait_ge(self.sem, self.value() - few)

    def value(self):
        if self.turn is None:
            return self.base + self.n
        return self.turn * self.per + (self.base + self.n)

    def enter(self, turn, per):
        self.base, self.n, self.turn, self.per = self.base + self.n, 0, turn, per

    def leave(self, turns):
        assert self.n == self.per, (self.n, self.per)
        self.base, self.n, self.turn = self.base + turns * self.per, 0, None


def tables_made(pool, r):
    pool.wait_ge(r.made, 1)


class Scope:

    def __init__(self, nc, tag):
        self.nc, self.tag, self.ctx, self.taken = nc, tag, ExitStack(), []

    def __enter__(self):
        return self

    def __exit__(self, *a):
        self.ctx.__exit__(*a)
        if self.taken and a[0] is None:
            self.nc.clear_and_free_semaphores(self.taken)
            self.nc.all_engine_barrier()

    def sb(self, name, shape, dt=F32):
        return self.ctx.enter_context(self.nc.sbuf_tensor(f"{self.tag}_{name}", shape, dt))

    def ps(self, name, shape, dt=F32):
        return self.ctx.enter_context(self.nc.psum_tensor(f"{self.tag}_{name}", shape, dt))

    def sem(self, name):
        self.taken.append(self.nc.alloc_semaphore(f"{self.tag}_{name}"))
        return self.taken[-1]

    def sems(self, name, n):
        return [self.sem(f"{name}{i}") for i in range(n)]

    def block(self):
        return self.ctx.enter_context(self.nc.Block())


class Resident:
    pass


class Order:
    pass


def bcast(ap, shape):
    return ap.broadcast_to(shape)


def load_constants(nc, r, x, src, dst):
    with Scope(nc, "load") as s:
        zeroed, loaded, made, eyed = s.sem("zeroed"), s.sem("loaded"), s.sem("made"), s.sem("eyed")
        block = s.block()

        @block.sync
        def _(sp):
            sp.dma_start(r.x[:, 0:NT - 1, :], x[0:(NT - 1) * P, :].rearrange("(t p) f -> p t f", p=P)).then_inc(loaded, 16)
            sp.wait_ge(zeroed, 1)
            sp.dma_start(r.x[0:LAST, NT - 1, :], x[(NT - 1) * P:N, :]).then_inc(loaded, 16)
            sp.dma_start(r.by_dst.far[:, 0:STEPS], src.rearrange("(p j) -> p j", p=LANES)).then_inc(loaded, 16)
            sp.dma_start(r.by_dst.key[:, 0:STEPS], dst.rearrange("(p j) -> p j", p=LANES)).then_inc(loaded, 16)
            sp.wait_ge(loaded, 64)

        @block.vector
        def _(dve):
            nc.vector.memset(r.x[:, NT - 1, :], 0.0).then_inc(zeroed, 1)
            nc.vector.memset(r.ones[:, :], 1.0)
            nc.vector.memset(r.wide_ones[:, :], 1.0)
            for o in (r.by_dst, r.by_src):
                nc.vector.memset(o.key[:, STEPS:], 0)
                last = nc.vector.memset(o.far[:, STEPS:], 0)
            last.then_inc(r.made, 1)

        @block.gpsimd
        def _(pool):
            nc.gpsimd.memset(r.eye[:, :], 0.0).then_inc(made, 1)
            nc.gpsimd.memset(r.below[:, :], 1.0).then_inc(made, 1)
            nc.gpsimd.memset(r.above[:, :], 1.0).then_inc(made, 1)
            pool.wait_ge(made, 3)
            nc.gpsimd.affine_select(out=r.eye[:, :], in_=r.eye[:, :], compare_op=ALU.not_equal, fill=1.0,
                                    base=0, pattern=[[-1, P]], channel_multiplier=1)
            nc.gpsimd.affine_select(out=r.below[:, :], in_=r.below[:, :], compare_op=ALU.is_gt, fill=0.0,
                                    base=0, pattern=[[-1, P]], channel_multiplier=1)
            nc.gpsimd.affine_select(out=r.above[:, :], in_=r.above[:, :], compare_op=ALU.is_gt, fill=0.0,
                                    base=0, pattern=[[1, P]], channel_multiplier=-1)
            nc.gpsimd.iota(r.column[:, :], pattern=[[1, P]], base=0, channel_multiplier=0,
                           allow_small_or_imprecise_dtypes=True)
            nc.gpsimd.iota(r.partition[:, :], pattern=[[0, 1]], base=0, channel_multiplier=1,
                           allow_small_or_imprecise_dtypes=True).then_inc(eyed, 1)


def count_keys(nc, r, o, tag, hist, key, keep):
    with Scope(nc, tag) as s:
        part = s.sb("part", [LANES, STEPS], I32)
        lo = s.sb("lo", [LANES, STEPS])
        hi = s.sb("hi", [LANES, STEPS])
        one_lo = s.sb("one_lo", [LANES, 2, B, P], BF16)
        one_hi = s.sb("one_hi", [LANES, 2, B, NT], BF16)
        count = s.sb("count", [P, NT])
        start = s.sb("start", [P, NT])
        total = s.sb("total", [P, NT + 1])
        end = s.sb("end", [P, NT])
        lane = s.sb("lane", [P, NT])
        lane_i = s.sb("lane_i", [P, NT], I32)
        t1 = s.sb("t1", [P, NT])
        t2 = s.sb("t2", [P, NT])
        ps = [s.ps(f"ps{k}", [P, B * NT]) for k in range(2)]
        ps_start = s.ps("ps_start", [P, 2 * NT])
        chain_sem, ready, counted = s.sem("chain"), s.sems("ready", 2), s.sems("counted", 2)
        kept = s.sems("kept", 2)
        summed, prefixed = s.sem("summed"), s.sem("prefixed")
        block = s.block()

        @block.vector
        def _(dve):
            link = Chain(dve, chain_sem)
            link(nc.vector.tensor_scalar(part[:, :], key[:, 0:STEPS], 7, None, ALU.arith_shift_right))
            link(nc.vector.tensor_copy(hi[:, :], part[:, :]))
            link(nc.vector.tensor_scalar(part[:, :], key[:, 0:STEPS], P - 1, None, ALU.bitwise_and))
            link(nc.vector.tensor_copy(lo[:, :], part[:, :]))
            with dve.Fori(0, TURNS2) as i:
                for k in range(2):
                    j = (2 * i + k) * B
                    dve.wait_ge(counted[k], i)
                    nc.vector.tensor_tensor(
                        one_lo[:, k, :, :], r.column[0:LANES, :].unsqueeze(1).broadcast_to([LANES, B, P]),
                        lo[:, bass.ds(j, B)].unsqueeze(2).broadcast_to([LANES, B, P]), ALU.is_equal)
                    nc.vector.tensor_tensor(
                        one_hi[:, k, :, :], r.column[0:LANES, 0:NT].unsqueeze(1).broadcast_to([LANES, B, NT]),
                        hi[:, bass.ds(j, B)].unsqueeze(2).broadcast_to([LANES, B, NT]), ALU.is_equal).then_inc(ready[k], 1)
                    dve.wait_ge(counted[k], i + 1)
                    nc.vector.tensor_copy(hist[:, bass.ds(j + 1, B), :].rearrange("p a b -> p (a b)"), ps[k][:, :]).then_inc(kept[k], 1)
            for k in range(2):
                dve.wait_ge(kept[k], TURNS2)
            link(nc.vector.tensor_reduce(count[:, :], hist[:, 1:, :].rearrange("p j h -> p h j"), AX.X, ALU.add))
            nc.vector.tensor_copy(o.count[:, :], count[:, :]).then_inc(summed, 1)
            dve.wait_ge(prefixed, 1)
            link(nc.vector.memset(total[:, 0:1], 0.0))
            link(nc.vector.tensor_tensor_scan(total[:, 1:NT + 1], r.ones[:, 0:NT], ps_start[:, NT:2 * NT], 0.0, ALU.mult, ALU.add))
            link(nc.vector.tensor_tensor(start[:, :], total[:, 0:NT], ps_start[:, 0:NT], ALU.add))
            link(nc.vector.tensor_tensor(end[:, :], start[:, :], count[:, :], ALU.add))
            link(nc.vector.tensor_scalar(end[:, :], end[:, :], -1.0, 0.0, ALU.add, ALU.max))
            link(nc.vector.tensor_scalar(lane_i[:, :], end[:, :], 1.0 / STEPS, None, ALU.mult))
            link(nc.vector.tensor_copy(lane[:, :], lane_i[:, :]))
            link(nc.vector.tensor_scalar(t1[:, :], lane[:, :], float(STEPS), None, ALU.mult))
            link(nc.vector.tensor_tensor(t2[:, :], t1[:, :], end[:, :], ALU.is_gt))
            link(nc.vector.tensor_tensor(lane[:, :], lane[:, :], t2[:, :], ALU.subtract))
            link(nc.vector.tensor_scalar(t1[:, :], lane[:, :], float(STEPS), float(STEPS), ALU.mult, ALU.add))
            link(nc.vector.tensor_tensor(t2[:, :], t1[:, :], end[:, :], ALU.is_le))
            link(nc.vector.tensor_tensor(lane[:, :], lane[:, :], t2[:, :], ALU.add))
            link(nc.vector.tensor_scalar(t1[:, :], lane[:, :], float(STEPS), None, ALU.mult))
            link(nc.vector.tensor_tensor(t1[:, :], start[:, :], t1[:, :], ALU.is_lt))
            link(nc.vector.tensor_scalar(t2[:, :], count[:, :], 0.0, None, ALU.is_gt))
            link(nc.vector.tensor_tensor(t1[:, :], t1[:, :], t2[:, :], ALU.mult))
            link(nc.vector.tensor_scalar(lane[:, :], lane[:, :], -1.0 - LANES, None, ALU.add))
            link(nc.vector.tensor_tensor(lane[:, :], lane[:, :], t1[:, :], ALU.mult))
            link(nc.vector.tensor_scalar(o.carry_row[:, :], lane[:, :], float(LANES), None, ALU.add))
            link(nc.vector.tensor_scalar(end[:, :], end[:, :], -float(E), None, ALU.add))
            link(nc.vector.tensor_tensor(end[:, :], end[:, :], t2[:, :], ALU.mult))
            link(nc.vector.tensor_scalar(o.end_row[:, :], end[:, :], float(E), None, ALU.add))
            if keep:
                link(nc.vector.tensor_copy(hist[:, 0, :], start[:, :]))
                for h in range(NT):
                    link(nc.vector.tensor_tensor_scan(hist[:, 1:, h], r.wide_ones[:, :], hist[:, 1:, h],
                                                      start[:, h:h + 1], ALU.mult, ALU.add))

        @block.tensor
        def _(pe):
            with pe.Fori(0, TURNS2) as i:
                for k in range(2):
                    pe.wait_ge(ready[k], i + 1)
                    pe.wait_ge(kept[k], i)
                    for b in range(B):
                        last = nc.tensor.matmul(ps[k][:, b * NT:(b + 1) * NT], one_lo[:, k, b, :], one_hi[:, k, b, :],
                                                start=True, stop=True)
                    last.then_inc(counted[k], 1)
            pe.wait_ge(summed, 1)
            nc.tensor.matmul(ps_start[:, 0:NT], r.above[:, :], count[:, :], start=True, stop=True)
            nc.tensor.matmul(ps_start[:, NT:2 * NT], r.ones[:, :], count[:, :], start=True, stop=True).then_inc(prefixed, 1)


def sort_edges(nc, r, o, key, far, hist, keys_t, sorted_edges):
    with Scope(nc, "sort") as s:
        lof = s.sb("lof", [LANES, STEPS])
        keyf = s.sb("keyf", [LANES, STEPS])
        part = s.sb("part", [LANES, STEPS], I32)
        hi = s.sb("hi", [LANES, STEPS])
        rows = s.sb("rows", [P, 4, 2, LANES])
        keyrow = s.sb("keyrow", [P, 2, B, 2, LANES])
        one_lo = s.sb("one_lo", [P, 2, B, LANES])
        one_hi = s.sb("one_hi", [LANES, B, NT])
        picked = s.sb("picked", [LANES, B, NT])
        scratch = s.sb("scratch", [LANES, LANES])
        base = s.sb("base", [LANES, B])
        rank = s.sb("rank", [LANES, B])
        place = s.sb("place", [LANES, 2, B], I32)
        record = s.sb("record", [LANES, 2, B, 2], I32)
        flip = [s.ps(f"flip{k}", [P, 4, P]) for k in range(2)]
        ps = [s.ps(f"ps{k}", [LANES, B * NT]) for k in range(2)]
        chain_sem, split, flipped, copied, stored = s.sem("chain"), s.sem("split"), s.sem("flipped"), s.sem("copied"), s.sem("stored")
        came, hot, found, placed, sent = s.sems("came", 2), s.sems("hot", 2), s.sems("found", 2), s.sems("placed", 2), s.sems("sent", 2)
        block = s.block()
        CH = STEPS // 4

        @block.vector
        def _(dve):
            link = Chain(dve, chain_sem)
            link(nc.vector.tensor_scalar(part[:, :], key[:, 0:STEPS], 7, None, ALU.arith_shift_right))
            link(nc.vector.tensor_copy(hi[:, :], part[:, :]))
            link(nc.vector.tensor_scalar(part[:, :], key[:, 0:STEPS], P - 1, None, ALU.bitwise_and))
            link(nc.vector.tensor_copy(keyf[:, :], key[:, 0:STEPS]))
            nc.vector.tensor_copy(lof[:, :], part[:, :]).then_inc(split, 1)
            dve.wait_ge(flipped, 1)
            link(nc.vector.tensor_copy(rows[0:CH, :, 0, :], flip[0][0:CH, :, 0:LANES]))
            nc.vector.tensor_copy(rows[0:CH, :, 1, :], flip[1][0:CH, :, 0:LANES]).then_inc(copied, 1)
            with dve.Fori(0, TURNS2) as i:
                link.enter(i, 2 * 10)
                for k in range(2):
                    j = (2 * i + k) * B
                    dve.wait_ge(came[k], i * 16 + 16)
                    nc.vector.tensor_scalar(one_lo[:, k, :, :], keyrow[:, k, :, 1, :], r.partition[:, 0:1], None, ALU.is_equal).then_inc(hot[k], 1)
                    link(nc.vector.tensor_tensor(
                        one_hi[:, :, :], r.column[0:LANES, 0:NT].unsqueeze(1).broadcast_to([LANES, B, NT]),
                        hi[:, bass.ds(j, B)].unsqueeze(2).broadcast_to([LANES, B, NT]), ALU.is_equal))
                    for b in range(B):
                        link(nc.vector.scalar_tensor_tensor(
                            scratch[:, :], keyrow[0:LANES, k, b, 0, :], keyf[:, bass.ds(j + b, 1)], r.below[0:LANES, 0:LANES],
                            ALU.is_equal, ALU.mult, accum_out=rank[:, b:b + 1]))
                    dve.wait_ge(found[k], i + 1)
                    link(nc.vector.tensor_tensor(picked[:, :, :].rearrange("p a b -> p (a b)"), ps[k][:, :],
                                                 one_hi[:, :, :].rearrange("p a b -> p (a b)"), ALU.mult))
                    link(nc.vector.tensor_reduce(base[:, :], picked[:, :, :], AX.X, ALU.add))
                    dve.wait_ge(sent[k], i * (16 * B))
                    nc.vector.tensor_tensor(place[:, k, :], base[:, :], rank[:, :], ALU.add)
                    link(nc.vector.tensor_copy(record[:, k, :, 0], key[:, bass.ds(j, B)]))
                    nc.vector.tensor_copy(record[:, k, :, 1], far[:, bass.ds(j, B)]).then_inc(placed[k], 1)
                    link(nc.vector.memset(scratch[0:1, 0:1], 0.0))
                link.leave(TURNS2)

        @block.tensor
        def _(pe):
            pe.wait_ge(split, 1)
            for c in range(4):
                nc.tensor.transpose(flip[0][0:CH, c, 0:LANES], keyf[:, c * CH:(c + 1) * CH], r.eye[0:LANES, 0:LANES])
                last = nc.tensor.transpose(flip[1][0:CH, c, 0:LANES], lof[:, c * CH:(c + 1) * CH], r.eye[0:LANES, 0:LANES])
            last.then_inc(flipped, 1)
            with pe.Fori(0, TURNS2) as i:
                for k in range(2):
                    pe.wait_ge(hot[k], i + 1)
                    pe.wait_ge(placed[k], i)
                    for b in range(B):
                        last = nc.tensor.matmul(ps[k][:, b * NT:(b + 1) * NT], one_lo[:, k, b, :],
                                                hist[:, bass.ds((2 * i + k) * B + b, 1), :].rearrange("p a b -> p (a b)"), start=True, stop=True)
                    last.then_inc(found[k], 1)

        @block.sync
        def _(sp):
            sp.wait_ge(copied, 1)
            sp.dma_start(keys_t.rearrange("(c j) k l -> j c k l", c=4), rows[0:CH, :, :, :]).then_inc(stored, 16)
            sp.wait_ge(stored, 16)
            with sp.Fori(0, TURNS2) as i:
                for k in range(2):
                    sp.wait_ge(placed[k], i)
                    sp.dma_start(keyrow[:, k, :, :, :].rearrange("p a b c -> p (a b c)"),
                                 keys_t[bass.ds((2 * i + k) * B, B), :, :].rearrange("a b c -> (a b c)").unsqueeze(0).broadcast_to([P, B * 2 * LANES])).then_inc(came[k], 16)

        @block.gpsimd
        def _(pool):
            last_edge, turn = pool.to_reg(E - 1), pool.alloc_register(f"{s.tag}_next_turn")
            with pool.Fori(0, TURNS2) as i:
                pool.reg_add(turn, i, 1)
                for k in range(2):
                    tables_made(pool, r)
                    pool.wait_ge(placed[k], turn)
                    for b in range(B):
                        pool.indirect_dma_start(sorted_edges, bass.IndirectOffsetOnAxis(ap=place[:, k, b:b + 1], axis=0),
                                                record[:, k, b, :], None, bounds_check=last_edge, oob_is_err=False).then_inc(sent[k], 16)
            for k in range(2):
                pool.wait_ge(sent[k], 16 * B * TURNS2)

    with Scope(nc, "sorted") as s:
        both = s.sb("both", [LANES, STEPS, 2], I32)
        loaded, done = s.sem("loaded"), s.sem("done")
        block = s.block()

        @block.sync
        def _(sp):
            sp.dma_start(both[:, :, :], sorted_edges.rearrange("(p j) k -> p j k", p=LANES)).then_inc(loaded, 16)

        @block.vector
        def _(dve):
            dve.wait_ge(loaded, 16)
            nc.vector.tensor_copy(o.key[:, 0:STEPS], both[:, :, 0]).then_inc(done, 1)
            nc.vector.tensor_copy(o.far[:, 0:STEPS], both[:, :, 1]).then_inc(done, 1)


def lane_tables(nc, r, o, tag, keys):
    with Scope(nc, tag) as s:
        keyf = s.sb("keyf", [LANES, STEPS])
        ends = s.sb("ends", [1, 3, LANES], I32)
        endf = s.sb("endf", [1, 3, LANES])
        whole = s.sb("whole", [1, 3, LANES])
        ps_gate = s.ps("ps_gate", [P, LANES])
        chain_sem, gated, spread, key_ends = s.sem("chain"), s.sem("gated"), s.sem("spread"), s.sem("key_ends")
        block = s.block()
        firsts = keys.rearrange("(q j) -> j q", j=STEPS)

        @block.sync
        def _(sp):
            sp.dma_start(ends[:, 0, :], firsts[0:1, :], allow_slow_non_contiguous=True).then_inc(key_ends, 16)
            sp.dma_start(ends[:, 1, :], firsts[STEPS - 1:STEPS, :], allow_slow_non_contiguous=True).then_inc(key_ends, 16)
            sp.dma_start(ends[:, 2, 1:LANES], firsts[STEPS - 1:STEPS, 0:LANES - 1], allow_slow_non_contiguous=True).then_inc(key_ends, 16)
            sp.dma_start(ends[:, 2, 0:1], firsts[0:1, 0:1], allow_slow_non_contiguous=True).then_inc(key_ends, 16)

        @block.vector
        def _(dve):
            link = Chain(dve, chain_sem)
            link(nc.vector.tensor_copy(keyf[:, :], o.key[:, 0:STEPS]))
            link(nc.vector.memset(o.cont[:, 0:1], 0.0))
            link(nc.vector.tensor_tensor(o.cont[:, 1:STEPS], keyf[:, 1:STEPS], keyf[:, 0:STEPS - 1], ALU.is_equal))
            link(nc.vector.tensor_scalar(o.pen[:, :], o.cont[:, :], -NONE, NONE, ALU.mult, ALU.add))
            dve.wait_ge(key_ends, 64)
            link(nc.vector.tensor_copy(endf[:, :, :], ends[:, :, :]))
            link(nc.vector.tensor_tensor(whole[:, 0, :], endf[:, 0, :], endf[:, 1, :], ALU.is_equal))
            link(nc.vector.tensor_tensor(whole[:, 1, :], endf[:, 0, :], endf[:, 2, :], ALU.is_equal))
            link(nc.vector.memset(whole[:, 1, 0:1], 0.0))
            nc.vector.tensor_tensor(whole[:, 2, :], whole[:, 0, :], whole[:, 1, :], ALU.mult).then_inc(gated, 1)
            dve.wait_ge(spread, 1)
            link(nc.vector.tensor_copy(o.gate[:, :], ps_gate[:, :]))
            link(nc.vector.tensor_scalar(o.gate_pen[:, :], o.gate[:, :], -NONE, NONE, ALU.mult, ALU.add))

        @block.tensor
        def _(pe):
            pe.wait_ge(gated, 1)
            nc.tensor.matmul(ps_gate[:, :], r.ones[0:1, :], whole[:, 2, :], start=True, stop=True).then_inc(spread, 1)


def normalize(nc, r, tag, x):
    with Scope(nc, tag) as s:
        stats = s.sb("stats", [P, NT, 6])
        moments = s.sb("moments", [P, NT, 2])
        std = s.sb("std", [P, NT])
        rstd = s.sb("rstd", [P, NT])
        chain_sem, added, rooted = s.sem("chain"), s.sem("added"), s.sem("rooted")
        block = s.block()

        @block.vector
        def _(dve):
            link = Chain(dve, chain_sem)
            for t in range(NT):
                last = nc.vector.bn_stats(stats[:, t, :], x[:, t, :])
            link(last)
            for t in range(NT):
                last = nc.vector.bn_aggr(moments[:, t, :], stats[:, t, :])
            link(last)
            link(nc.vector.tensor_copy(r.var[:, :], moments[:, :, 1]))
            nc.vector.tensor_scalar(std[:, :], r.var[:, :], EPS, None, ALU.add).then_inc(added, 1)
            dve.wait_ge(rooted, 1)
            link(nc.vector.reciprocal(rstd[:, :], std[:, :]))
            with dve.Fori(0, NT // 2) as i:
                for k in range(2):
                    t = 2 * i + k
                    nc.vector.tensor_scalar(r.xh[:, bass.ds(t, 1), :].rearrange("p a b -> p (a b)"),
                                            x[:, bass.ds(t, 1), :].rearrange("p a b -> p (a b)"),
                                            moments[:, bass.ds(t, 1), 0:1].rearrange("p a b -> p (a b)"), rstd[:, bass.ds(t, 1)],
                                            ALU.subtract, ALU.mult)

        @block.scalar
        def _(act):
            act.wait_ge(added, 1)
            nc.scalar.activation(std[:, :], std[:, :], ACT.Sqrt).then_inc(rooted, 1)


def tile_of(t3, t):
    return t3[:, bass.ds(t, 1), :].rearrange("p a b -> p (a b)")


def flip_tile(nc, pe, out, xh_tile, eye):
    nc.tensor.transpose(out[:, 0, :], xh_tile[:, 0:P], eye)
    return nc.tensor.transpose(out[:, 1, :], xh_tile[:, P:2 * P], eye)


def stage_tiles(nc, dve, stage, tiles, i, flipped, staged):
    for k in range(2):
        dve.wait_ge(flipped[k], i)
        nc.vector.tensor_scalar(stage[:, k, :], tile_of(tiles, 2 * i + k), 1.0, None, ALU.mult).then_inc(staged[k], 1)


def project_l0(nc, r, w_qkv, gamma, beta, qv, kd):
    with Scope(nc, "l0p") as s:
        w = s.sb("w", [P, 2, 3 * G])
        gb = s.sb("gb", [P, 2, 2])
        x2 = s.sb("x2", [P, 2, G])
        r2 = s.sb("r2", [P, NT])
        xT = s.sb("xT", [P, 2, 2, P])
        o = s.sb("o", [P, 2, 3 * G])
        flip = [s.ps(f"flip{k}", [P, 2, P]) for k in range(2)]
        ps_qv = [s.ps(f"ps_qv{k}", [P, 2 * G]) for k in range(2)]
        ps_k = [s.ps(f"ps_k{k}", [P, G]) for k in range(2)]
        loaded, chain_sem, added, rooted = s.sem("loaded"), s.sem("chain"), s.sem("added"), s.sem("rooted")
        scaled, flipped, copied = s.sems("scaled", 2), s.sems("flipped", 2), s.sems("copied", 2)
        projected, taken, stored = s.sems("projected", 2), s.sems("taken", 2), s.sems("stored", 2)
        block = s.block()
        T2 = NT // 2

        @block.sync
        def _(sp):
            sp.dma_start(w[:, :, :], w_qkv.rearrange("(c p) n -> p c n", p=P)).then_inc(loaded, 16)
            sp.dma_start(gb[:, 0, :], gamma.rearrange("(c p) -> p c", p=P), allow_slow_non_contiguous=True).then_inc(loaded, 16)
            sp.dma_start(gb[:, 1, :], beta.rearrange("(c p) -> p c", p=P), allow_slow_non_contiguous=True).then_inc(loaded, 16)
            with sp.Fori(0, T2) as i:
                for k in range(2):
                    row = (2 * i + k) * P
                    sp.wait_ge(taken[k], i + 1)
                    sp.dma_start(qv[bass.ds(row, P), :], o[:, k, 0:2 * G]).then_inc(stored[k], 16)
                    sp.dma_start(kd[bass.ds(row, P), :], o[:, k, 2 * G:3 * G]).then_inc(stored[k], 16)
            for k in range(2):
                sp.wait_ge(stored[k], 32 * T2)

        @block.vector
        def _(dve):
            link = Chain(dve, chain_sem)
            link(nc.vector.tensor_scalar(r2[:, :], r.var[:, :], EPS, None, ALU.add))
            link(nc.vector.reciprocal(r2[:, :], r2[:, :]))
            link(nc.vector.tensor_tensor(r2[:, :], r.var[:, :], r2[:, :], ALU.mult))
            nc.vector.tensor_scalar(r2[:, :], r2[:, :], EPS, None, ALU.add).then_inc(added, 1)
            dve.wait_ge(rooted, 1)
            link(nc.vector.reciprocal(r2[:, :], r2[:, :]))
            with dve.Fori(0, T2) as i:
                for k in range(2):
                    dve.wait_ge(flipped[k], i)
                    nc.vector.tensor_scalar(x2[:, k, :], tile_of(r.xh, 2 * i + k), r2[:, bass.ds(2 * i + k, 1)], None, ALU.mult).then_inc(scaled[k], 1)
                for k in range(2):
                    dve.wait_ge(projected[k], i + 1)
                    dve.wait_ge(stored[k], i * 32)
                    nc.vector.tensor_copy(o[:, k, 0:2 * G], ps_qv[k][:, :])
                    nc.vector.tensor_scalar(o[:, k, 2 * G:3 * G], ps_k[k][:, :], float(G) ** -0.5, None, ALU.mult).then_inc(taken[k], 1)

        @block.scalar
        def _(act):
            act.wait_ge(added, 1)
            nc.scalar.activation(r2[:, :], r2[:, :], ACT.Sqrt).then_inc(rooted, 1)
            act.wait_ge(loaded, 48)
            with act.Fori(0, T2) as i:
                for k in range(2):
                    act.wait_ge(flipped[k], i + 1)
                    act.wait_ge(projected[k], i)
                    nc.scalar.activation(xT[:, k, 0, :], flip[k][:, 0, :], ACT.Identity, bias=gb[:, 1, 0:1], scale=gb[:, 0, 0:1])
                    nc.scalar.activation(xT[:, k, 1, :], flip[k][:, 1, :], ACT.Identity, bias=gb[:, 1, 1:2], scale=gb[:, 0, 1:2]).then_inc(copied[k], 1)

        @block.tensor
        def _(pe):
            pe.wait_ge(loaded, 48)
            with pe.Fori(0, T2) as i:
                for k in range(2):
                    pe.wait_ge(scaled[k], i + 1)
                    pe.wait_ge(copied[k], i)
                    flip_tile(nc, pe, flip[k], x2[:, k, :], r.eye[:, :]).then_inc(flipped[k], 1)
                for k in range(2):
                    pe.wait_ge(copied[k], i + 1)
                    pe.wait_ge(taken[k], i)
                    for c in range(2):
                        nc.tensor.matmul(ps_qv[k][:, 0:G], xT[:, k, c, :], w[:, c, 0:G], start=(c == 0), stop=(c == 1))
                    for c in range(2):
                        nc.tensor.matmul(ps_qv[k][:, G:2 * G], xT[:, k, c, :], w[:, c, 2 * G:3 * G], start=(c == 0), stop=(c == 1))
                    for c in range(2):
                        last = nc.tensor.matmul(ps_k[k][:, :], xT[:, k, c, :], w[:, c, G:2 * G], start=(c == 0), stop=(c == 1))
                    last.then_inc(projected[k], 1)


def lane_gathers(nc, r, pool, tag, gathers, indexed, used, came):
    last_row, turn = pool.to_reg(N - 1), pool.alloc_register(f"{tag}_next_turn")
    with pool.Fori(0, TURNS) as i:
        pool.reg_add(turn, i, 1)
        for k in range(U):
            tables_made(pool, r)
            pool.wait_ge(indexed[k], turn)
            pool.wait_ge(used[k], i)
            for to, table, at in gathers(k):
                pool.indirect_dma_start(to, None, table, bass.IndirectOffsetOnAxis(ap=at, axis=0),
                                        bounds_check=last_row, oob_is_err=False).then_inc(came[k], 16)


def skewed(eng, link, per, first, both, last):
    first()
    with eng.Fori(0, TURNS - 1) as i:
        link.enter(i, per)
        for k in range(U):
            both(i, k)
        link.leave(TURNS - 1)
    for k in range(U - 1):
        both(TURNS - 1, k)
    last(TURNS - 1)


def after(i, k):
    return (i, k + 1) if k < U - 1 else (i + 1, 0)


def wait_for_state_buffer(dve, stored, i, k):
    if k >= 2:
        dve.wait_ge(stored[k - 2], (i + 1) * 16)
    else:
        dve.wait_ge(stored[k - 2 + U], i * 16)


def store_states(sp, out, st, stepped, stored):
    with sp.Fori(0, TURNS) as i:
        for k in range(U):
            sp.wait_ge(stepped[k], i + 1)
            sp.dma_start(out[:, bass.ds((i * U + k) * B, B), :], st[:, k % 2, :, :]).then_inc(stored[k], 16)
    for k in range(U):
        sp.wait_ge(stored[k], 16 * TURNS)


def edges_softmax(nc, r, o, tag, far_table, key_table, heads, states, tail):
    W = heads
    with Scope(nc, tag) as s:
        index = s.sb("index", [LANES, U, 2, B], I32)
        got = s.sb("got", [LANES, U, B, 2 * G])
        keyed = s.sb("keyed", [LANES, U, B, G])
        prod = s.sb("prod", [LANES, B, G]) if heads == H else None
        logit = s.sb("logit", [LANES, 2, B, W])
        grown = s.sb("grown", [LANES, W])
        term = s.sb("term", [LANES, B, W + G])
        scaled = s.sb("scaled", [LANES, W + G])
        st = s.sb("st", [LANES, 2, B, 2 * W + G])
        chain_sem = s.sem("chain")
        indexed, came = s.sems("indexed", U), s.sems("came", U)
        raised, exped, stepped, stored = (s.sems(n, U) for n in ("raised", "exped", "stepped", "stored"))
        block = s.block()
        out = states[0:E, :].rearrange("(p j) w -> p j w", p=LANES)

        @block.gpsimd
        def _(pool):
            lane_gathers(nc, r, pool, s.tag,
                         lambda k: [(got[:, k, b, :], far_table, index[:, k, 0, b:b + 1]) for b in range(B)]
                         + [(keyed[:, k, b, :], key_table, index[:, k, 1, b:b + 1]) for b in range(B)],
                         indexed, stepped, came)

        @block.vector
        def _(dve):
            link = Chain(dve, chain_sem)

            def m_of(k, b):
                return st[:, k % 2, b, 0:W] if b >= 0 else st[:, (k + 1) % 2, B - 1, 0:W]

            def zu_of(k, b):
                return st[:, k % 2, b, W:] if b >= 0 else st[:, (k + 1) % 2, B - 1, W:]

            def of_heads(ap):
                return ap.rearrange("p b (h d) -> p b h d", d=D)

            def begin(i, k):
                j = (i * U + k) * B
                dve.wait_ge(came[k], (i + 1) * (32 * B))
                nc.vector.tensor_copy(index[:, k, 0, :], o.far[:, bass.ds(j + U * B, B)])
                nc.vector.tensor_copy(index[:, k, 1, :], o.key[:, bass.ds(j + U * B, B)]).then_inc(indexed[k], 1)
                if heads == G:
                    link.mark(nc.vector.tensor_tensor(logit[:, k % 2, :, :], got[:, k, :, 0:G], keyed[:, k, :, :], ALU.mult))
                else:
                    link(nc.vector.tensor_tensor(prod[:, :, :], got[:, k, :, 0:G], keyed[:, k, :, :], ALU.mult))
                    link.mark(nc.vector.tensor_reduce(logit[:, k % 2, :, :], of_heads(prod[:, :, :]), AX.X, ALU.add))

            BEGIN = 1 if heads == G else 2

            def forward(i, k, b):
                pen = o.pen[:, bass.ds((i * U + k) * B + b, 1)]
                link.mark(nc.vector.scalar_tensor_tensor(m_of(k, b), m_of(k, b - 1), pen, logit[:, k % 2, b, :], ALU.add, ALU.max))

            def backward(i, k):
                j = (i * U + k) * B
                link.all_but(0)
                for b in reversed(range(B - 1)):
                    link(nc.vector.scalar_tensor_tensor(m_of(k, b), m_of(k, b + 1), o.pen[:, bass.ds(j + b + 1, 1)], m_of(k, b), ALU.add, ALU.max))
                nc.vector.scalar_tensor_tensor(grown[:, :], m_of(k, -1), o.pen[:, bass.ds(j, 1)], m_of(k, 0), ALU.add, ALU.subtract)
                nc.vector.tensor_tensor(logit[:, k % 2, :, :], logit[:, k % 2, :, :], st[:, k % 2, :, 0:W], ALU.subtract).then_inc(raised[k], 1)

            def weigh(i, k):
                dve.wait_ge(exped[k], i + 1)
                if heads == G:
                    link.mark(nc.vector.tensor_tensor(term[:, :, W:], term[:, :, 0:W], got[:, k, :, G:2 * G], ALU.mult))
                    link.mark(nc.vector.tensor_tensor(scaled[:, :].rearrange("p (a f) -> p a f", a=2), zu_of(k, -1).rearrange("p (a f) -> p a f", a=2),
                                                      grown[:, :].unsqueeze(1).broadcast_to([LANES, 2, G]), ALU.mult))
                else:
                    nc.vector.tensor_tensor(scaled[:, 0:W], zu_of(k, -1)[:, 0:W], grown[:, :], ALU.mult)
                    link.mark(nc.vector.tensor_tensor(of_heads(term[:, :, W:]), of_heads(got[:, k, :, G:2 * G]),
                                                      term[:, :, 0:W].unsqueeze(3).broadcast_to([LANES, B, H, D]), ALU.mult))
                    link.mark(nc.vector.tensor_tensor(scaled[:, W:].rearrange("p (h d) -> p h d", d=D), zu_of(k, -1)[:, W:].rearrange("p (h d) -> p h d", d=D),
                                                      grown[:, :].unsqueeze(2).broadcast_to([LANES, H, D]), ALU.mult))

            def step(i, k, b):
                if b == 0:
                    return link.mark(nc.vector.tensor_tensor(zu_of(k, 0), scaled[:, :], term[:, 0, :], ALU.add))
                cont = o.cont[:, bass.ds((i * U + k) * B + b, 1)]
                ins = nc.vector.scalar_tensor_tensor(zu_of(k, b), zu_of(k, b - 1), cont, term[:, b, :], ALU.mult, ALU.add)
                if b < B - 1:
                    link.mark(ins)
                else:
                    ins.then_inc(stepped[k], 1)

            def first():
                link.mark(nc.vector.memset(m_of(0, -1), NONE))
                link.mark(nc.vector.memset(zu_of(0, -1), 0.0))
                for k in range(U):
                    nc.vector.tensor_copy(index[:, k, 0, :], o.far[:, k * B:(k + 1) * B])
                    nc.vector.tensor_copy(index[:, k, 1, :], o.key[:, k * B:(k + 1) * B]).then_inc(indexed[k], 1)
                begin(0, 0)
                for b in range(B):
                    link.all_but(0)
                    forward(0, 0, b)
                backward(0, 0)

            def both(i, k):
                new = after(i, k)
                begin(*new)
                weigh(i, k)
                wait_for_state_buffer(dve, stored, *new)
                for b in range(B):
                    link.all_but(1 if b else 0)
                    forward(*new, b)
                    link.all_but(1)
                    step(i, k, b)
                dve.wait_ge(stepped[k], i + 1)
                backward(*new)

            def last(i):
                weigh(i, U - 1)
                for b in range(B):
                    link.all_but(0)
                    step(i, U - 1, b)
                dve.wait_ge(stepped[U - 1], i + 1)

            skewed(dve, link, U * (BEGIN + 2 + B + (B - 1) + (B - 1)), first, both, last)
            if heads == G:
                nc.vector.tensor_copy(tail[:, :], st[:, 1, B - 1, :])
            else:
                for n in range(2):
                    nc.vector.tensor_copy(tail[:, n * G:(n + 1) * G].rearrange("p (h d) -> p h d", d=D),
                                          st[:, 1, B - 1, n * H:(n + 1) * H].unsqueeze(2).broadcast_to([LANES, H, D]))
                nc.vector.tensor_copy(tail[:, 2 * G:3 * G], st[:, 1, B - 1, 2 * H:])

        @block.scalar
        def _(act):
            with act.Fori(0, TURNS) as i:
                for k in range(U):
                    act.wait_ge(raised[k], i + 1)
                    nc.scalar.activation(grown[:, :], grown[:, :], ACT.Exp)
                    nc.scalar.activation(term[:, :, 0:W], logit[:, k % 2, :, :], ACT.Exp).then_inc(exped[k], 1)

        @block.sync
        def _(sp):
            store_states(sp, out, st, stepped, stored)


def carry_softmax(nc, r, o, tag, tail, carries, states, heads):
    with Scope(nc, tag) as s:
        t = s.sb("t", [P, 2, 3, LANES])
        m = s.sb("m", [P, 2, LANES + 1])
        a = s.sb("a", [P, 2, LANES])
        c = s.sb("c", [P, 2, 3, LANES])
        rows = s.sb("rows", [LANES, 3, 2, P])
        empty = s.sb("empty", [1, 3 * G])
        empty_heads = s.sb("empty_heads", [1, 2 * H + G])
        flip = [s.ps(f"flip{h}", [P, 3, P]) for h in range(2)]
        back = [s.ps(f"back{h}", [LANES, 3, P]) for h in range(2)]
        chain_sem, flipped, raised, exped, scanned, returned, done, stored = (
            s.sem(n) for n in ("chain", "flipped", "raised", "exped", "scanned", "returned", "done", "stored"))
        block = s.block()

        @block.tensor
        def _(pe):
            for h in range(2):
                for n in range(3):
                    last = nc.tensor.transpose(flip[h][:, n, 0:LANES], tail[:, n * G + h * P:n * G + (h + 1) * P], r.eye[0:LANES, 0:LANES])
            last.then_inc(flipped, 1)
            pe.wait_ge(scanned, 1)
            for h in range(2):
                for n in range(3):
                    last = nc.tensor.transpose(back[h][:, n, :], c[:, h, n, :], r.eye[:, :])
            last.then_inc(returned, 1)

        @block.vector
        def _(dve):
            link = Chain(dve, chain_sem)
            link(nc.vector.memset(empty[:, 0:G], NONE))
            link(nc.vector.memset(empty[:, G:3 * G], 0.0))
            link(nc.vector.memset(empty_heads[:, 0:H], NONE))
            link(nc.vector.memset(empty_heads[:, H:], 0.0))
            dve.wait_ge(flipped, 1)
            for h in range(2):
                link(nc.vector.tensor_copy(t[:, h, :, :], flip[h][:, :, 0:LANES]))
                link(nc.vector.memset(m[:, h, 0:1], 0.0))
                link(nc.vector.tensor_tensor_scan(m[:, h, 1:], o.gate_pen[:, :], t[:, h, 0, :], NONE, ALU.add, ALU.max))
                link(nc.vector.tensor_copy(c[:, h, 0, :], m[:, h, 1:]))
                link(nc.vector.tensor_tensor(a[:, h, :], m[:, h, 0:LANES], o.gate_pen[:, :], ALU.add))
                link(nc.vector.tensor_tensor(a[:, h, :], a[:, h, :], m[:, h, 1:], ALU.subtract))
                link(nc.vector.tensor_tensor(t[:, h, 0, :], t[:, h, 0, :], m[:, h, 1:], ALU.subtract))
            link(nc.vector.memset(m[:, 0, 0:1], 0.0))
            nc.vector.memset(m[:, 0, 0:1], 0.0).then_inc(raised, 1)
            dve.wait_ge(exped, 1)
            for h in range(2):
                for n in (1, 2):
                    link(nc.vector.tensor_tensor(t[:, h, n, :], t[:, h, n, :], t[:, h, 0, :], ALU.mult))
                    link(nc.vector.tensor_tensor_scan(c[:, h, n, :], a[:, h, :], t[:, h, n, :], 0.0, ALU.mult, ALU.add))
            nc.vector.memset(m[:, 0, 0:1], 0.0).then_inc(scanned, 1)
            dve.wait_ge(returned, 1)
            for h in range(2):
                link(nc.vector.tensor_copy(rows[:, :, h, :], back[h][:, :, :]))
            nc.vector.memset(m[:, 0, 0:1], 0.0).then_inc(done, 1)

        @block.scalar
        def _(act):
            act.wait_ge(raised, 1)
            nc.scalar.activation(a[:, :, :], a[:, :, :], ACT.Exp)
            nc.scalar.activation(t[:, :, 0, :], t[:, :, 0, :], ACT.Exp).then_inc(exped, 1)

        @block.sync
        def _(sp):
            sp.wait_ge(done, 1)
            sp.dma_start(carries[0:LANES, :], rows[:, :, :, :].rearrange("q n h f -> q (n h f)")).then_inc(stored, 16)
            sp.dma_start(carries[LANES:LANES + 1, :], empty[:, :]).then_inc(stored, 16)
            sp.dma_start(states[E:E + 1, :], empty[:, 3 * G - states.shape[1]:] if heads == G else empty_heads[:, :]).then_inc(stored, 16)
            sp.wait_ge(stored, 48)


def finish_softmax(nc, r, o, tag, states, carries, heads, out):
    with Scope(nc, tag) as s:
        W = states.shape[1]
        index = s.sb("index", [P, 2, 2], I32)
        mine = s.sb("mine", [P, 2, W])
        carry = s.sb("carry", [P, 2, 3 * G])
        top = s.sb("top", [P, 2, G])
        fac = s.sb("fac", [P, 2, 2, G])
        z = s.sb("z", [P, G])
        u = s.sb("u", [P, G])
        t1 = s.sb("t1", [P, G])
        chain_sem = s.sem("chain")
        indexed, came, topped, exped, used = (s.sems(n, 2) for n in ("indexed", "came", "topped", "exped", "used"))
        block = s.block()
        T2 = NT // 2

        def three(ap):
            return ap.rearrange("p (h d) -> p h d", d=D)

        def own(k, n):
            if n == 2:
                return three(mine[:, k, W - G:W])
            if heads == G:
                return three(mine[:, k, n * G:(n + 1) * G])
            return mine[:, k, n * H:(n + 1) * H].unsqueeze(2).broadcast_to([P, H, D])

        def carried(k, n):
            return three(carry[:, k, n * G:(n + 1) * G])

        @block.gpsimd
        def _(pool):
            last_state, last_carry, turn = pool.to_reg(E), pool.to_reg(LANES), pool.alloc_register(f"{s.tag}_next_turn")
            with pool.Fori(0, T2) as i:
                pool.reg_add(turn, i, 1)
                for k in range(2):
                    tables_made(pool, r)
                    pool.wait_ge(indexed[k], turn)
                    pool.wait_ge(used[k], i)
                    pool.indirect_dma_start(mine[:, k, :], None, states, bass.IndirectOffsetOnAxis(ap=index[:, k, 0:1], axis=0),
                                            bounds_check=last_state, oob_is_err=False).then_inc(came[k], 16)
                    pool.indirect_dma_start(carry[:, k, :], None, carries, bass.IndirectOffsetOnAxis(ap=index[:, k, 1:2], axis=0),
                                            bounds_check=last_carry, oob_is_err=False).then_inc(came[k], 16)

        @block.vector
        def _(dve):
            link = Chain(dve, chain_sem)
            with dve.Fori(0, T2) as i:
                link.enter(i, 2 * 12)
                for k in range(2):
                    t = 2 * i + k
                    dve.wait_ge(came[k], i * 32)
                    nc.vector.tensor_copy(index[:, k, 0:1], o.end_row[:, bass.ds(t, 1)])
                    nc.vector.tensor_copy(index[:, k, 1:2], o.carry_row[:, bass.ds(t, 1)]).then_inc(indexed[k], 1)
                for k in range(2):
                    dve.wait_ge(came[k], (i + 1) * 32)
                    link(nc.vector.tensor_tensor(three(top[:, k, :]), own(k, 0), carried(k, 0), ALU.max))
                    nc.vector.tensor_tensor(three(fac[:, k, 0, :]), own(k, 0), three(top[:, k, :]), ALU.subtract)
                    nc.vector.tensor_tensor(three(fac[:, k, 1, :]), carried(k, 0), three(top[:, k, :]), ALU.subtract).then_inc(topped[k], 1)
                for k in range(2):
                    t = 2 * i + k
                    dve.wait_ge(exped[k], i + 1)
                    for n, acc in ((1, z), (2, u)):
                        link(nc.vector.tensor_tensor(three(acc[:, :]), own(k, n), three(fac[:, k, 0, :]), ALU.mult))
                        link(nc.vector.tensor_tensor(three(t1[:, :]), carried(k, n), three(fac[:, k, 1, :]), ALU.mult))
                        link(nc.vector.tensor_tensor(acc[:, :], acc[:, :], t1[:, :], ALU.add))
                    link(nc.vector.tensor_scalar(t1[:, :], z[:, :], 0.0, None, ALU.is_equal))
                    link(nc.vector.tensor_tensor(z[:, :], z[:, :], t1[:, :], ALU.add))
                    link(nc.vector.reciprocal(z[:, :], z[:, :]))
                    link(nc.vector.tensor_tensor(u[:, :], u[:, :], z[:, :], ALU.mult))
                    if out is r.x:
                        link(nc.vector.tensor_tensor(tile_of(r.x, t), tile_of(r.x, t), u[:, :], ALU.add))
                    else:
                        link(nc.vector.tensor_copy(tile_of(out, t), u[:, :]))
                    nc.vector.memset(t1[0:1, 0:1], 0.0).then_inc(used[k], 1)
                link.leave(T2)

        @block.scalar
        def _(act):
            with act.Fori(0, T2) as i:
                for k in range(2):
                    act.wait_ge(topped[k], i + 1)
                    nc.scalar.activation(fac[:, k, :, :], fac[:, k, :, :], ACT.Exp).then_inc(exped[k], 1)


def edges_sum(nc, r, o, tag, table, states, tail, edge_rows=None):
    with Scope(nc, tag) as s:
        index = s.sb("index", [LANES, U, B], I32)
        got = s.sb("got", [LANES, U, B, G])
        own = rows = None
        if edge_rows is not None:
            own = s.sb("own", [LANES, U, B, G])
            rows = edge_rows.rearrange("(p j) w -> p j w", p=LANES)
        st = s.sb("st", [LANES, 2, B, G])
        chain_sem = s.sem("chain")
        names = ("indexed", "came", "owned", "added", "cut", "stepped", "stored")
        indexed, came, owned, added, cut, stepped, stored = (s.sems(n, U) for n in names)
        block = s.block()
        out = states[0:E, :].rearrange("(p j) w -> p j w", p=LANES)

        @block.gpsimd
        def _(pool):
            lane_gathers(nc, r, pool, s.tag, lambda k: [(got[:, k, b, :], table, index[:, k, b:b + 1]) for b in range(B)],
                         indexed, stepped, came)

        @block.vector
        def _(dve):
            link = Chain(dve, chain_sem)

            def begin(i, k):
                j = (i * U + k) * B
                dve.wait_ge(came[k], (i + 1) * (16 * B))
                nc.vector.tensor_copy(index[:, k, :], o.far[:, bass.ds(j + U * B, B)]).then_inc(indexed[k], 1)
                if own is not None:
                    dve.wait_ge(owned[k], (i + 1) * 16)
                    nc.vector.tensor_tensor(got[:, k, :, :], got[:, k, :, :], own[:, k, :, :], ALU.add).then_inc(added[k], 1)

            def steps(i, k):
                j = (i * U + k) * B
                if own is not None:
                    dve.wait_ge(cut[k], i + 1)
                wait_for_state_buffer(dve, stored, i, k)
                for b in range(B):
                    before = st[:, k % 2, b - 1, :] if b else st[:, 1 - k % 2, B - 1, :]
                    ins = nc.vector.scalar_tensor_tensor(st[:, k % 2, b, :], before, o.cont[:, bass.ds(j + b, 1)], got[:, k, b, :], ALU.mult, ALU.add)
                    if b < B - 1:
                        link(ins)
                ins.then_inc(stepped[k], 1)
                dve.wait_ge(stepped[k], i + 1)

            def first():
                link(nc.vector.memset(st[:, 1, B - 1, :], 0.0))
                for k in range(U):
                    nc.vector.tensor_copy(index[:, k, :], o.far[:, k * B:(k + 1) * B]).then_inc(indexed[k], 1)
                begin(0, 0)

            def both(i, k):
                begin(*after(i, k))
                steps(i, k)

            skewed(dve, link, U * (B - 1), first, both, lambda i: steps(i, U - 1))
            nc.vector.tensor_copy(tail[:, 0:G], st[:, 1, B - 1, :])

        @block.scalar
        def _(act):
            if own is not None:
                def cut_batch(i, k):
                    act.wait_ge(added[k], i + 1)
                    nc.scalar.activation(got[:, k, :, :], got[:, k, :, :], ACT.Relu).then_inc(cut[k], 1)

                with act.Fori(0, TURNS - 1) as i:
                    for k in range(U):
                        cut_batch(i, k)
                        act.dma_start(own[:, k, :, :], rows[:, bass.ds(((i + 1) * U + k) * B, B), :]).then_inc(owned[k], 16)
                for k in range(U):
                    cut_batch(TURNS - 1, k)

        @block.sync
        def _(sp):
            if own is not None:
                for k in range(U):
                    sp.dma_start(own[:, k, :, :], rows[:, k * B:(k + 1) * B, :]).then_inc(owned[k], 16)
            store_states(sp, out, st, stepped, stored)


def carry_sum(nc, r, o, tag, tail, carries, states):
    with Scope(nc, tag) as s:
        t = s.sb("t", [P, 2, LANES])
        c = s.sb("c", [P, 2, LANES])
        rows = s.sb("rows", [LANES, 2, P])
        empty = s.sb("empty", [1, G])
        flip = s.ps("flip", [P, 2, P])
        back = s.ps("back", [LANES, 2, P])
        chain_sem, flipped, scanned, returned, done, stored = (
            s.sem(n) for n in ("chain", "flipped", "scanned", "returned", "done", "stored"))
        block = s.block()

        @block.tensor
        def _(pe):
            for h in range(2):
                last = nc.tensor.transpose(flip[:, h, 0:LANES], tail[:, h * P:(h + 1) * P], r.eye[0:LANES, 0:LANES])
            last.then_inc(flipped, 1)
            pe.wait_ge(scanned, 1)
            for h in range(2):
                last = nc.tensor.transpose(back[:, h, :], c[:, h, :], r.eye[:, :])
            last.then_inc(returned, 1)

        @block.vector
        def _(dve):
            link = Chain(dve, chain_sem)
            link(nc.vector.memset(empty[:, :], 0.0))
            dve.wait_ge(flipped, 1)
            link(nc.vector.tensor_copy(t[:, :, :], flip[:, :, 0:LANES]))
            nc.vector.tensor_tensor_scan(c[:, 0, :], o.gate[:, :], t[:, 0, :], 0.0, ALU.mult, ALU.add)
            nc.vector.tensor_tensor_scan(c[:, 1, :], o.gate[:, :], t[:, 1, :], 0.0, ALU.mult, ALU.add).then_inc(scanned, 1)
            dve.wait_ge(returned, 1)
            nc.vector.tensor_copy(rows[:, :, :], back[:, :, :]).then_inc(done, 1)

        @block.sync
        def _(sp):
            sp.wait_ge(done, 1)
            sp.dma_start(carries[0:LANES, :], rows[:, :, :].rearrange("q h f -> q (h f)")).then_inc(stored, 16)
            sp.dma_start(carries[LANES:LANES + 1, :], empty[:, :]).then_inc(stored, 16)
            sp.dma_start(states[E:E + 1, :], empty[:, :]).then_inc(stored, 16)
            sp.wait_ge(stored, 48)


def finish_sum(nc, r, o, tag, states, carries, mean, out):
    with Scope(nc, tag) as s:
        index = s.sb("index", [P, 2, 2], I32)
        mine = s.sb("mine", [P, 2, G])
        carry = s.sb("carry", [P, 2, G])
        share = s.sb("share", [P, NT])
        chain_sem = s.sem("chain")
        indexed, came, used = (s.sems(n, 2) for n in ("indexed", "came", "used"))
        block = s.block()
        T2 = NT // 2

        @block.gpsimd
        def _(pool):
            last_state, last_carry, turn = pool.to_reg(E), pool.to_reg(LANES), pool.alloc_register(f"{s.tag}_next_turn")
            with pool.Fori(0, T2) as i:
                pool.reg_add(turn, i, 1)
                for k in range(2):
                    tables_made(pool, r)
                    pool.wait_ge(indexed[k], turn)
                    pool.wait_ge(used[k], i)
                    pool.indirect_dma_start(mine[:, k, :], None, states, bass.IndirectOffsetOnAxis(ap=index[:, k, 0:1], axis=0),
                                            bounds_check=last_state, oob_is_err=False).then_inc(came[k], 16)
                    pool.indirect_dma_start(carry[:, k, :], None, carries, bass.IndirectOffsetOnAxis(ap=index[:, k, 1:2], axis=0),
                                            bounds_check=last_carry, oob_is_err=False).then_inc(came[k], 16)

        @block.vector
        def _(dve):
            link = Chain(dve, chain_sem)
            link(nc.vector.tensor_scalar(share[:, :], o.count[:, :], 1.0, None, ALU.max))
            link(nc.vector.reciprocal(share[:, :], share[:, :]))
            with dve.Fori(0, T2) as i:
                link.enter(i, 2 * 1)
                for k in range(2):
                    t = 2 * i + k
                    dve.wait_ge(came[k], i * 32)
                    nc.vector.tensor_copy(index[:, k, 0:1], o.end_row[:, bass.ds(t, 1)])
                    nc.vector.tensor_copy(index[:, k, 1:2], o.carry_row[:, bass.ds(t, 1)]).then_inc(indexed[k], 1)
                for k in range(2):
                    t = 2 * i + k
                    dve.wait_ge(came[k], (i + 1) * 32)
                    link(nc.vector.tensor_tensor(mine[:, k, :], mine[:, k, :], carry[:, k, :], ALU.add))
                    by = share[:, bass.ds(t, 1)] if mean else 1.0
                    nc.vector.scalar_tensor_tensor(tile_of(out, t), mine[:, k, :], by, tile_of(out, t), ALU.mult, ALU.add).then_inc(used[k], 1)
                link.leave(T2)


def project_l1(nc, r, w_self, w_neigh, table):
    MAXK = 32
    with Scope(nc, "l1p") as s:
        w = s.sb("w", [P, 2, 2 * G])
        xT = s.sb("xT", [P, 2, 2, P])
        h = s.sb("h", [P, 2, G])
        left = s.sb("left", [P, 2, G])
        top = s.sb("top", [P, 2, 8])
        beat = s.sb("beat", [1, 1])
        o = s.sb("o", [P, 2, G])
        stage = s.sb("stage", [P, 2, G])
        staged = s.sems("staged", 2)
        flip = [s.ps(f"flip{k}", [P, 2, P]) for k in range(2)]
        ps = [s.ps(f"ps{k}", [P, 2 * G]) for k in range(2)]
        loaded, chain_sem = s.sem("loaded"), s.sem("chain")
        flipped, copied, projected, taken, chosen, stored = (
            s.sems(n, 2) for n in ("flipped", "copied", "projected", "taken", "chosen", "stored"))
        block = s.block()
        T2 = NT // 2

        @block.sync
        def _(sp):
            sp.dma_start(w[:, :, 0:G], w_self.rearrange("(c p) n -> p c n", p=P)).then_inc(loaded, 16)
            sp.dma_start(w[:, :, G:2 * G], w_neigh.rearrange("(c p) n -> p c n", p=P)).then_inc(loaded, 16)
            with sp.Fori(0, T2) as i:
                for k in range(2):
                    sp.wait_ge(chosen[k], i + 1)
                    sp.dma_start(table[bass.ds((2 * i + k) * P, P), :], o[:, k, :]).then_inc(stored[k], 16)
            for k in range(2):
                sp.wait_ge(stored[k], 16 * T2)

        @block.vector
        def _(dve):
            link = Chain(dve, chain_sem)
            with dve.Fori(0, T2) as i:
                link.enter(i, 2 * (MAXK // 8))
                stage_tiles(nc, dve, stage, r.xh, i, flipped, staged)
                for k in range(2):
                    t = 2 * i + k
                    dve.wait_ge(projected[k], i + 1)
                    nc.vector.tensor_tensor(tile_of(r.x, t), tile_of(r.x, t), ps[k][:, 0:G], ALU.add)
                    nc.vector.tensor_copy(h[:, k, :], ps[k][:, G:2 * G]).then_inc(taken[k], 1)
                for k in range(2):
                    dve.wait_ge(taken[k], i + 1)
                for n in range(MAXK // 8):
                    nc.vector.memset(beat[:, :], 0.0)
                    for k in range(2):
                        last = nc.vector.max(top[:, k, :], (left if n else h)[:, k, :])
                    link(last)
                    nc.vector.memset(beat[:, :], 0.0)
                    for k in range(2):
                        last = nc.vector.match_replace(left[:, k, :], top[:, k, :], (left if n else h)[:, k, :], NONE)
                    link(last)
                for k in range(2):
                    dve.wait_ge(stored[k], i * 16)
                    nc.vector.scalar_tensor_tensor(o[:, k, :], left[:, k, :], NONE / 2, h[:, k, :], ALU.is_le, ALU.mult).then_inc(chosen[k], 1)
                link.leave(T2)

        @block.scalar
        def _(act):
            with act.Fori(0, T2) as i:
                for k in range(2):
                    act.wait_ge(flipped[k], i + 1)
                    act.wait_ge(projected[k], i)
                    nc.scalar.activation(xT[:, k, :, :], flip[k][:, :, :], ACT.Copy).then_inc(copied[k], 1)

        @block.tensor
        def _(pe):
            pe.wait_ge(loaded, 32)
            with pe.Fori(0, T2) as i:
                for k in range(2):
                    pe.wait_ge(staged[k], i + 1)
                    pe.wait_ge(copied[k], i)
                    flip_tile(nc, pe, flip[k], stage[:, k, :], r.eye[:, :]).then_inc(flipped[k], 1)
                for k in range(2):
                    pe.wait_ge(copied[k], i + 1)
                    pe.wait_ge(taken[k], i)
                    for c in range(2):
                        last = nc.tensor.matmul(ps[k][:, :], xT[:, k, c, :], w[:, c, :], start=(c == 0), stop=(c == 1))
                    last.then_inc(projected[k], 1)


def project_l2(nc, r, ws, biases, qd, kv):
    with Scope(nc, "l2p") as s:
        w = s.sb("w", [P, 2, 3 * G])
        row = s.sb("row", [1, 3 * G])
        xT = s.sb("xT", [P, 2, 2, P])
        o = s.sb("o", [P, 2, 3 * G])
        stage = s.sb("stage", [P, 2, G])
        staged = s.sems("staged", 2)
        flip = [s.ps(f"flip{k}", [P, 2, P]) for k in range(2)]
        ps_kv = [s.ps(f"ps_kv{k}", [P, 2 * G]) for k in range(2)]
        ps_q = [s.ps(f"ps_q{k}", [P, G]) for k in range(2)]
        loaded = s.sem("loaded")
        flipped, copied, projected, taken, stored = (
            s.sems(n, 2) for n in ("flipped", "copied", "projected", "taken", "stored"))
        block = s.block()
        T2 = NT // 2

        @block.sync
        def _(sp):
            for n in range(3):
                sp.dma_start(w[:, :, n * G:(n + 1) * G], ws[n].rearrange("(c p) n -> p c n", p=P)).then_inc(loaded, 16)
                sp.dma_start(row[:, n * G:(n + 1) * G], biases[n].unsqueeze(0)).then_inc(loaded, 16)
            with sp.Fori(0, T2) as i:
                for k in range(2):
                    sp.wait_ge(taken[k], i + 1)
                    sp.dma_start(kv[bass.ds((2 * i + k) * P, P), :], o[:, k, 0:2 * G]).then_inc(stored[k], 16)
                    sp.dma_start(qd[bass.ds((2 * i + k) * P, P), :], o[:, k, 2 * G:3 * G]).then_inc(stored[k], 16)
            for k in range(2):
                sp.wait_ge(stored[k], 32 * T2)

        @block.vector
        def _(dve):
            with dve.Fori(0, T2) as i:
                stage_tiles(nc, dve, stage, r.xh, i, flipped, staged)
                for k in range(2):
                    dve.wait_ge(projected[k], i + 1)
                    dve.wait_ge(stored[k], i * 32)
                    nc.vector.tensor_copy(o[:, k, 0:2 * G], ps_kv[k][:, :])
                    nc.vector.tensor_scalar(o[:, k, 2 * G:3 * G], ps_q[k][:, :], float(D) ** -0.5, None, ALU.mult).then_inc(taken[k], 1)

        @block.scalar
        def _(act):
            with act.Fori(0, T2) as i:
                for k in range(2):
                    act.wait_ge(flipped[k], i + 1)
                    act.wait_ge(projected[k], i)
                    nc.scalar.activation(xT[:, k, :, :], flip[k][:, :, :], ACT.Copy).then_inc(copied[k], 1)

        @block.tensor
        def _(pe):
            pe.wait_ge(loaded, 96)
            with pe.Fori(0, T2) as i:
                for k in range(2):
                    pe.wait_ge(staged[k], i + 1)
                    pe.wait_ge(copied[k], i)
                    flip_tile(nc, pe, flip[k], stage[:, k, :], r.eye[:, :]).then_inc(flipped[k], 1)
                for k in range(2):
                    pe.wait_ge(copied[k], i + 1)
                    pe.wait_ge(taken[k], i)
                    nc.tensor.matmul(ps_kv[k][:, :], r.ones[0:1, :], row[:, 0:2 * G], start=True, stop=False)
                    for c in range(2):
                        nc.tensor.matmul(ps_kv[k][:, :], xT[:, k, c, :], w[:, c, 0:2 * G], start=False, stop=(c == 1))
                    nc.tensor.matmul(ps_q[k][:, :], r.ones[0:1, :], row[:, 2 * G:3 * G], start=True, stop=False)
                    for c in range(2):
                        last = nc.tensor.matmul(ps_q[k][:, :], xT[:, k, c, :], w[:, c, 2 * G:3 * G], start=False, stop=(c == 1))
                    last.then_inc(projected[k], 1)


def project_out(nc, r, agg, w_out, bias):
    with Scope(nc, "l2o") as s:
        w = s.sb("w", [P, 2, G])
        row = s.sb("row", [1, G])
        xT = s.sb("xT", [P, 2, 2, P])
        stage = s.sb("stage", [P, 2, G])
        staged = s.sems("staged", 2)
        flip = [s.ps(f"flip{k}", [P, 2, P]) for k in range(2)]
        ps = [s.ps(f"ps{k}", [P, G]) for k in range(2)]
        loaded = s.sem("loaded")
        flipped, copied, projected, taken = (s.sems(n, 2) for n in ("flipped", "copied", "projected", "taken"))
        block = s.block()
        T2 = NT // 2

        @block.sync
        def _(sp):
            sp.dma_start(w[:, :, :], w_out.rearrange("(c p) n -> p c n", p=P)).then_inc(loaded, 16)
            sp.dma_start(row[:, :], bias.unsqueeze(0)).then_inc(loaded, 16)

        @block.vector
        def _(dve):
            with dve.Fori(0, T2) as i:
                stage_tiles(nc, dve, stage, agg, i, flipped, staged)
                for k in range(2):
                    dve.wait_ge(projected[k], i + 1)
                    nc.vector.tensor_tensor(tile_of(r.x, 2 * i + k), tile_of(r.x, 2 * i + k), ps[k][:, :], ALU.add).then_inc(taken[k], 1)

        @block.scalar
        def _(act):
            with act.Fori(0, T2) as i:
                for k in range(2):
                    act.wait_ge(flipped[k], i + 1)
                    act.wait_ge(projected[k], i)
                    nc.scalar.activation(xT[:, k, :, :], flip[k][:, :, :], ACT.Copy).then_inc(copied[k], 1)

        @block.tensor
        def _(pe):
            pe.wait_ge(loaded, 32)
            with pe.Fori(0, T2) as i:
                for k in range(2):
                    pe.wait_ge(staged[k], i + 1)
                    pe.wait_ge(copied[k], i)
                    flip_tile(nc, pe, flip[k], stage[:, k, :], r.eye[:, :]).then_inc(flipped[k], 1)
                for k in range(2):
                    pe.wait_ge(copied[k], i + 1)
                    pe.wait_ge(taken[k], i)
                    nc.tensor.matmul(ps[k][:, :], r.ones[0:1, :], row[:, :], start=True, stop=False)
                    for c in range(2):
                        last = nc.tensor.matmul(ps[k][:, :], xT[:, k, c, :], w[:, c, :], start=False, stop=(c == 1))
                    last.then_inc(projected[k], 1)

def route(nc, r, tag, w_gate, bias, experts, kind):
    with Scope(nc, tag) as s:
        w = s.sb("w", [P, 2, experts])
        row = s.sb("row", [1, experts])
        xs = s.sb("xs", [P, 2, 2, P])
        score = s.sb("score", [P, NT, 8])
        worst = s.sb("worst", [P, NT])
        top = s.sb("top", [P, NT, 8])
        which = s.sb("which", [P, NT, 8], mybir.dt.uint32)
        whichf = s.sb("whichf", [P, NT, 2])
        wt = s.sb("wt", [P, NT, 2])
        t1 = s.sb("t1", [P, NT])
        second = s.sb("second", [P, NT, 8])
        stage = s.sb("stage", [P, 2, G])
        staged = s.sems("staged", 2)
        flip = [s.ps(f"flip{k}", [P, 2, P]) for k in range(2)]
        ps = s.ps("ps", [P, NT, experts])
        loaded, chain_sem, shifted, exped, differed, weighed = (s.sem(n) for n in ("loaded", "chain", "shifted", "exped", "differed", "weighed"))
        flipped, copied, kept, scored = (s.sems(n, 2) for n in ("flipped", "copied", "kept", "scored"))
        block = s.block()
        T2 = NT // 2

        def col(ap, n=None):
            return ap.unsqueeze(2).broadcast_to([P, NT, n or 8])

        @block.sync
        def _(sp):
            if w_gate is not None:
                for c in range(2):
                    sp.dma_start(w[:, c, :], w_gate[c * P:(c + 1) * P, :], allow_slow_non_contiguous=True).then_inc(loaded, 16)
            if bias is not None:
                sp.dma_start(row[:, :], bias.unsqueeze(0)).then_inc(loaded, 16)

        @block.tensor
        def _(pe):
            if w_gate is not None:
                pe.wait_ge(loaded, 32 if bias is None else 48)
            with pe.Fori(0, T2) as i:
                for k in range(2):
                    pe.wait_ge(staged[k], i + 1)
                    pe.wait_ge(copied[k], i)
                    flip_tile(nc, pe, flip[k], stage[:, k, :], r.eye[:, :]).then_inc(flipped[k], 1)
                for k in range(2 if w_gate is not None else 0):
                    score_of = ps[:, bass.ds(2 * i + k, 1), :].rearrange("p a e -> p (a e)")
                    pe.wait_ge(copied[k], i + 1)
                    if bias is not None:
                        nc.tensor.matmul(score_of, r.ones[0:1, :], row[:, :], start=True, stop=False)
                    for c in range(2):
                        last = nc.tensor.matmul(score_of, xs[:, k, c, :], w[:, c, :], start=(bias is None and c == 0), stop=(c == 1))
                    last.then_inc(scored[k], 1)

        @block.scalar
        def _(act):
            with act.Fori(0, T2) as i:
                for k in range(2):
                    act.wait_ge(flipped[k], i + 1)
                    if w_gate is not None:
                        act.wait_ge(scored[k], i)
                    act.wait_ge(kept[k], i)
                    nc.scalar.activation(xs[:, k, :, :], flip[k][:, :, :], ACT.Copy).then_inc(copied[k], 1)
            if kind in ("softmax of two", "share"):
                act.wait_ge(shifted, 1)
                nc.scalar.activation(score[:, :, :], score[:, :, :], ACT.Exp).then_inc(exped, 1)
            if kind == "softmax of two":
                act.wait_ge(differed, 1)
                nc.scalar.activation(t1[:, :], t1[:, :], ACT.Exp).then_inc(weighed, 1)

        @block.vector
        def _(dve):
            link = Chain(dve, chain_sem)
            link(nc.vector.memset(score[:, :, :], NONE))
            with dve.Fori(0, T2) as i:
                stage_tiles(nc, dve, stage, r.xh, i, flipped, staged)
                for k in range(2):
                    dve.wait_ge(copied[k], i + 1)
                    nc.vector.tensor_copy(r.xT[:, :, bass.ds((2 * i + k) * P, P)], xs[:, k, :, :]).then_inc(kept[k], 1)
            if w_gate is None:
                return
            for k in range(2):
                dve.wait_ge(scored[k], T2)
            link(nc.vector.tensor_copy(score[:, :, 0:experts], ps[:, :, :]))
            if kind != "ones":
                link(nc.vector.tensor_reduce(worst[:, :], score[:, :, :], AX.X, ALU.max))
                nc.vector.tensor_tensor(score[:, :, :], score[:, :, :], col(worst[:, :]), ALU.subtract).then_inc(shifted, 1)
                dve.wait_ge(exped, 1)
                link(nc.vector.tensor_reduce(worst[:, :], score[:, :, :], AX.X, ALU.add))
                link(nc.vector.reciprocal(worst[:, :], worst[:, :]))
                link(nc.vector.tensor_tensor(score[:, :, :], score[:, :, :], col(worst[:, :]), ALU.mult))
            for t in range(NT):
                last = nc.vector.max(top[:, t, :], score[:, t, :])
            link(last)
            for t in range(NT):
                last = nc.vector.max_index(which[:, t, :], top[:, t, :], score[:, t, :])
            link(last)
            link(nc.vector.tensor_copy(whichf[:, :, :], which[:, :, 0:2]))
            if kind == "ones":
                link(nc.vector.memset(wt[:, :, :], 1.0))
            elif kind == "softmax of two":
                nc.vector.tensor_tensor(t1[:, :], top[:, :, 1], top[:, :, 0], ALU.subtract).then_inc(differed, 1)
                dve.wait_ge(weighed, 1)
                link(nc.vector.tensor_scalar(wt[:, :, 0], t1[:, :], 1.0, None, ALU.add))
                link(nc.vector.reciprocal(wt[:, :, 0], wt[:, :, 0]))
                link(nc.vector.tensor_tensor(wt[:, :, 1], wt[:, :, 0], t1[:, :], ALU.mult))
            else:
                link(nc.vector.tensor_tensor(t1[:, :], top[:, :, 0], top[:, :, 1], ALU.add))
                link(nc.vector.tensor_scalar(t1[:, :], t1[:, :], 1e-12, None, ALU.max))
                link(nc.vector.reciprocal(t1[:, :], t1[:, :]))
                link(nc.vector.tensor_tensor(wt[:, :, :], top[:, :, 0:2], col(t1[:, :], 2), ALU.mult))
            eight = r.column[:, 0:8].unsqueeze(1).broadcast_to([P, NT, 8])
            link(nc.vector.tensor_tensor(r.gate[:, :, :], eight, col(whichf[:, :, 0]), ALU.is_equal))
            link(nc.vector.tensor_tensor(second[:, :, :], eight, col(whichf[:, :, 1]), ALU.is_equal))
            link(nc.vector.tensor_tensor(r.gate[:, :, :], r.gate[:, :, :], col(wt[:, :, 0]), ALU.mult))
            link(nc.vector.tensor_tensor(second[:, :, :], second[:, :, :], col(wt[:, :, 1]), ALU.mult))
            link(nc.vector.tensor_tensor(r.gate[:, :, :], r.gate[:, :, :], second[:, :, :], ALU.add))


def experts_gelu(nc, r, tag, w1, b1, w2, b2, experts, hidden, gates, out, load):
    HC = hidden // P
    with Scope(nc, tag) as s:
        W1 = s.sb("W1", [P, experts, 2, hidden])
        W2 = s.sb("W2", [P, experts, HC, G])
        B1 = s.sb("B1", [P, experts, HC])
        B2 = s.sb("B2", [P if experts == 2 else 1, experts, G])
        hT = s.sb("hT", [P, 2, HC, BC])
        ps_h = [s.ps(f"ps_h{k}", [P, BC]) for k in range(2)]
        ps_y = [s.ps(f"ps_y{k}", [P, 4, G]) for k in range(2)]
        loaded = s.sem("loaded")
        hidden_made, acted, summed, added = (s.sems(n, 2) for n in ("hidden_made", "acted", "summed", "added"))
        block = s.block()
        PER_H, PER_Y = experts * HC // 2, experts // 2

        n_loads, rows = load(nc, s, W1, W2, B1, B2, w1, b1, w2, b2, loaded, block, hidden)

        @block.tensor
        def _(pe):
            pe.wait_ge(loaded, n_loads)

            def up(i, e):
                for c in range(HC):
                    q = e * HC + c
                    pe.wait_ge(acted[q % 2], i * PER_H + q // 2)
                    for n in range(2):
                        last = nc.tensor.matmul(ps_h[q % 2][:, :], W1[:, e, n, c * P:(c + 1) * P], r.xT[:, n, bass.ds(i * BC, BC)],
                                                start=(n == 0), stop=(n == 1))
                    last.then_inc(hidden_made[q % 2], 1)

            def down(i, e):
                for k in range(2):
                    pe.wait_ge(acted[k], i * PER_H + (e + 1) * HC // 2)
                pe.wait_ge(added[e % 2], i * PER_Y + e // 2)
                for t in range(TB):
                    nc.tensor.matmul(ps_y[e % 2][:, t, :], r.ones[0:1, :], B2[0:1, e, :], start=True, stop=False)
                    for c in range(HC):
                        last = nc.tensor.matmul(ps_y[e % 2][:, t, :], hT[:, e % 2, c, t * P:(t + 1) * P], W2[:, e, c, :],
                                                start=False, stop=(c == HC - 1))
                last.then_inc(summed[e % 2], 1)

            with pe.Fori(0, NB) as i:
                up(i, 0)
                for e in range(experts):
                    if e + 1 < experts:
                        up(i, e + 1)
                    down(i, e)

        @block.scalar
        def _(act):
            act.wait_ge(loaded, n_loads)
            with act.Fori(0, NB) as i:
                for e in range(experts):
                    act.wait_ge(summed[e % 2], i * PER_Y + e // 2)
                    for c in range(HC):
                        q = e * HC + c
                        act.wait_ge(hidden_made[q % 2], i * PER_H + (q // 2 + 1))
                        nc.scalar.activation(hT[:, e % 2, c, :], ps_h[q % 2][:, :], ACT.Gelu, bias=B1[:, e, c:c + 1]).then_inc(acted[q % 2], 1)

        @block.vector
        def _(dve):
            if rows is not None:
                rows(dve)
            with dve.Fori(0, NB) as i:
                for e in range(experts):
                    dve.wait_ge(summed[e % 2], i * PER_Y + (e // 2 + 1))
                    if e:
                        dve.wait_ge(added[(e - 1) % 2], i * PER_Y + ((e - 1) // 2 + 1))
                    for t in range(TB):
                        last = nc.vector.scalar_tensor_tensor(tile_of(out, i * TB + t), ps_y[e % 2][:, t, :], gates(i * TB + t, e),
                                                              tile_of(out, i * TB + t), ALU.mult, ALU.add)
                    last.then_inc(added[e % 2], 1)


def load_all(nc, s, W1, W2, B1, B2, w1, b1, w2, b2, loaded, block, hidden):
    @block.sync
    def _(sp):
        E_ = w1.shape[0]
        for e in range(E_):
            sp.dma_start(W1[:, e, :, :], w1[e].rearrange("(c p) n -> p c n", p=P)).then_inc(loaded, 16)
            sp.dma_start(W2[:, e, :, :], w2[e].rearrange("(c p) n -> p c n", p=P)).then_inc(loaded, 16)
        sp.dma_start(B1[:, :, :], b1.rearrange("e (c p) -> p e c", p=P), allow_slow_non_contiguous=True).then_inc(loaded, 16)
        sp.dma_start(B2[:, :, :], b2.unsqueeze(0)).then_inc(loaded, 16)
    return 16 * (2 * w1.shape[0] + 2), None


def layer_l0_ffn(nc, r, t):
    EX, H1, H2 = 4, 128, 64
    with Scope(nc, "l0f") as s:
        W1 = s.sb("W1", [P, 6, 2, P])
        W2 = s.sb("W2", [P, 2, P])
        V2 = s.sb("V2", [P, EX, H2])
        W3 = s.sb("W3", [P, G])
        V3 = s.sb("V3", [H2, EX, G])
        B1 = s.sb("B1", [P, 6])
        B2 = s.sb("B2", [P, 5])
        B3 = s.sb("B3", [1, 5, G])
        h1 = s.sb("h1", [P, 6, BC])
        h2 = s.sb("h2", [P, 5, BC])
        ps_h = [s.ps(f"ps_h{k}", [P, BC]) for k in range(3)]
        ps_y = [s.ps(f"ps_y{k}", [P, 4, G]) for k in range(2)]
        loaded = s.sem("loaded")
        made, acted, summed, added = s.sems("made", 3), s.sems("acted", 3), s.sems("summed", 2), s.sems("added", 2)
        block = s.block()
        Q = 12
        PER = 4

        @block.sync
        def _(sp):
            g = lambda n: t["L0_ffn_" + n]
            for c in range(2):
                sp.dma_start(W1[:, c, :, :], g("sW1")[:, c * P:(c + 1) * P].rearrange("(k p) n -> p k n", p=P)).then_inc(loaded, 16)
            for e in range(EX):
                sp.dma_start(W1[:, 2 + e, :, :], g("eW1")[e].rearrange("(k p) n -> p k n", p=P)).then_inc(loaded, 16)
            sp.dma_start(W2[:, :, :], g("sW2").rearrange("(k p) n -> p k n", p=P)).then_inc(loaded, 16)
            sp.dma_start(V2[:, :, :], g("eW2").rearrange("e p n -> p e n")).then_inc(loaded, 16)
            sp.dma_start(W3[:, :], g("sW3")).then_inc(loaded, 16)
            sp.dma_start(V3[:, :, :], g("eW3").rearrange("e p n -> p e n")).then_inc(loaded, 16)
            with nc.allow_non_contiguous_dma("biases"):
                sp.dma_start(B1[:, 0:2], g("sb1").rearrange("(c p) -> p c", p=P), allow_slow_non_contiguous=True).then_inc(loaded, 16)
                sp.dma_start(B1[:, 2:6], g("eb1").rearrange("e p -> p e"), allow_slow_non_contiguous=True).then_inc(loaded, 16)
                sp.dma_start(B2[:, 0:1], g("sb2").rearrange("(c p) -> p c", p=P), allow_slow_non_contiguous=True).then_inc(loaded, 16)
                sp.dma_start(B2[0:H2, 1:5], g("eb2").rearrange("e p -> p e"), allow_slow_non_contiguous=True).then_inc(loaded, 16)
            sp.dma_start(B3[:, 0, :], g("sb3").unsqueeze(0)).then_inc(loaded, 16)
            sp.dma_start(B3[:, 1:5, :], g("eb3").unsqueeze(0)).then_inc(loaded, 16)

        def rows(q):
            return P if q <= 6 else H2

        USES = [len(range(b, 11, 3)) for b in range(3)]

        @block.tensor
        def _(pe):
            pe.wait_ge(loaded, 16 * 16)
            with pe.Fori(0, NB) as i:
                for q in range(11):
                    b, n = q % 3, q // 3
                    pe.wait_ge(acted[b], i * USES[b] + n)
                    if q < 6:
                        for c in range(2):
                            last = nc.tensor.matmul(ps_h[b][:, :], W1[:, q, c, :], r.xT[:, c, bass.ds(i * BC, BC)], start=(c == 0), stop=(c == 1))
                    elif q == 6:
                        for z in range(3):
                            pe.wait_ge(acted[z], i * USES[z] + 2)
                        for c in range(2):
                            last = nc.tensor.matmul(ps_h[b][:, :], W2[:, c, :], h1[:, c, :], start=(c == 0), stop=(c == 1))
                    else:
                        last = nc.tensor.matmul(ps_h[b][0:H2, :], V2[:, q - 7, :], h1[:, q - 5, :], start=True, stop=True)
                    last.then_inc(made[b], 1)
                for z in range(3):
                    pe.wait_ge(acted[z], (i + 1) * USES[z])
                for e in range(5):
                    n, per = e // 2, (3, 2)[e % 2]
                    pe.wait_ge(added[e % 2], i * per + n)
                    for tt in range(TB):
                        nc.tensor.matmul(ps_y[e % 2][:, tt, :], r.ones[0:1, :], B3[:, e, :], start=True, stop=False)
                        if e == 0:
                            last = nc.tensor.matmul(ps_y[e % 2][:, tt, :], h2[:, 0, tt * P:(tt + 1) * P], W3[:, :], start=False, stop=True)
                        else:
                            last = nc.tensor.matmul(ps_y[e % 2][:, tt, :], h2[0:H2, e, tt * P:(tt + 1) * P], V3[:, e - 1, :], start=False, stop=True)
                    last.then_inc(summed[e % 2], 1)

        @block.scalar
        def _(act):
            act.wait_ge(loaded, 16 * 16)
            with act.Fori(0, NB) as i:
                for q in range(11):
                    b, n = q % 3, q // 3
                    if q == 6:
                        act.wait_ge(summed[0], i * 3)
                        act.wait_ge(summed[1], i * 2)
                    act.wait_ge(made[b], i * USES[b] + (n + 1))
                    if q < 6:
                        ins = nc.scalar.activation(h1[:, q, :], ps_h[b][:, :], ACT.Relu, bias=B1[:, q:q + 1])
                    else:
                        m = rows(q)
                        ins = nc.scalar.activation(h2[0:m, q - 6, :], ps_h[b][0:m, :], ACT.Relu, bias=B2[0:m, q - 6:q - 5])
                    ins.then_inc(acted[b], 1)

        @block.vector
        def _(dve):
            with dve.Fori(0, NB) as i:
                for e in range(5):
                    n, per = e // 2, (3, 2)[e % 2]
                    dve.wait_ge(summed[e % 2], i * per + (n + 1))
                    if e:
                        dve.wait_ge(added[(e - 1) % 2], i * (3, 2)[(e - 1) % 2] + ((e - 1) // 2 + 1))
                    for tt in range(TB):
                        xt = tile_of(r.x, i * TB + tt)
                        by = r.gate[:, bass.ds(i * TB + tt, 1), e - 1].rearrange("p a -> p a") if e else 1.0
                        last = nc.vector.scalar_tensor_tensor(xt, ps_y[e % 2][:, tt, :], by, xt, ALU.mult, ALU.add)
                    last.then_inc(added[e % 2], 1)


def up_l3(nc, r, w1, b1, hf):
    with Scope(nc, "l3a") as s:
        W = s.sb("W", [P, 2, 2 * G])
        B1 = s.sb("B1", [P, 4])
        ps = [s.ps(f"ps{k}", [P, BC]) for k in range(4)]
        loaded = s.sem("loaded")
        made, taken = s.sems("made", 4), s.sems("taken", 4)
        block = s.block()

        @block.sync
        def _(sp):
            sp.dma_start(W[:, :, :], w1.rearrange("(c p) n -> p c n", p=P)).then_inc(loaded, 16)
            sp.dma_start(B1[:, :], b1.rearrange("(c p) -> p c", p=P), allow_slow_non_contiguous=True).then_inc(loaded, 16)

        @block.tensor
        def _(pe):
            pe.wait_ge(loaded, 32)
            with pe.Fori(0, NB) as i:
                for c in range(4):
                    pe.wait_ge(taken[c], i)
                    for k in range(2):
                        last = nc.tensor.matmul(ps[c][:, :], W[:, k, c * P:(c + 1) * P], r.xT[:, k, bass.ds(i * BC, BC)], start=(k == 0), stop=(k == 1))
                    last.then_inc(made[c], 1)

        @block.vector
        def _(dve):
            dve.wait_ge(loaded, 32)
            with dve.Fori(0, NB) as i:
                for c in range(4):
                    dve.wait_ge(made[c], i + 1)
                    nc.vector.tensor_scalar(hf[:, c, bass.ds(i * BC, BC)], ps[c][:, :], B1[:, c:c + 1], None, ALU.add).then_inc(taken[c], 1)


def column_moments(nc, link, stats, moments, rows, chunks):
    cuts = [(a, min(a + 512, N)) for a in range(0, N, 512)]
    for c in range(chunks):
        for n, (a, b) in enumerate(cuts):
            last = nc.vector.bn_stats(stats[:, c, n, :], rows[:, c, a:b])
    link(last)
    for c in range(chunks):
        last = nc.vector.bn_aggr(moments[:, c, :], stats[:, c, :, :].rearrange("p n s -> p (n s)"))
    link(last)


def batch_norm_l3(nc, r, gamma, beta, hf):
    with Scope(nc, "l3b") as s:
        stats = s.sb("stats", [P, 4, 8, 6])
        moments = s.sb("moments", [P, 4, 2])
        gb = s.sb("gb", [P, 2, 4])
        std = s.sb("std", [P, 4])
        scale = s.sb("scale", [P, 4])
        shift = s.sb("shift", [P, 4])
        loaded, chain_sem, added, rooted, ready = (s.sem(n) for n in ("loaded", "chain", "added", "rooted", "ready"))
        block = s.block()

        @block.sync
        def _(sp):
            sp.dma_start(gb[:, 0, :], gamma.rearrange("(c p) -> p c", p=P), allow_slow_non_contiguous=True).then_inc(loaded, 16)
            sp.dma_start(gb[:, 1, :], beta.rearrange("(c p) -> p c", p=P), allow_slow_non_contiguous=True).then_inc(loaded, 16)

        @block.vector
        def _(dve):
            link = Chain(dve, chain_sem)
            column_moments(nc, link, stats, moments, hf, 4)
            nc.vector.tensor_scalar(std[:, :], moments[:, :, 1], EPS, None, ALU.add).then_inc(added, 1)
            dve.wait_ge(rooted, 1)
            dve.wait_ge(loaded, 32)
            link(nc.vector.reciprocal(std[:, :], std[:, :]))
            link(nc.vector.tensor_tensor(scale[:, :], std[:, :], gb[:, 0, :], ALU.mult))
            link(nc.vector.tensor_tensor(shift[:, :], moments[:, :, 0], scale[:, :], ALU.mult))
            nc.vector.tensor_tensor(shift[:, :], gb[:, 1, :], shift[:, :], ALU.subtract).then_inc(ready, 1)

        @block.scalar
        def _(act):
            act.wait_ge(added, 1)
            nc.scalar.activation(std[:, :], std[:, :], ACT.Sqrt).then_inc(rooted, 1)
            act.wait_ge(ready, 1)
            for c in range(4):
                nc.scalar.activation(hf[:, c, :], hf[:, c, :], ACT.Relu, bias=shift[:, c:c + 1], scale=scale[:, c:c + 1])


def down_l3(nc, r, w2, b2, hf):
    with Scope(nc, "l3d") as s:
        W = s.sb("W", [P, 4, G])
        B2 = s.sb("B2", [P, 2])
        ps = [s.ps(f"ps{k}", [P, BC]) for k in range(2)]
        loaded = s.sem("loaded")
        made, taken = s.sems("made", 2), s.sems("taken", 2)
        block = s.block()

        @block.sync
        def _(sp):
            sp.dma_start(W[:, :, :], w2.rearrange("(c p) n -> p c n", p=P)).then_inc(loaded, 16)
            sp.dma_start(B2[:, :], b2.rearrange("(c p) -> p c", p=P), allow_slow_non_contiguous=True).then_inc(loaded, 16)

        @block.tensor
        def _(pe):
            pe.wait_ge(loaded, 32)
            with pe.Fori(0, NB) as i:
                for c in range(2):
                    pe.wait_ge(taken[c], i)
                    for k in range(4):
                        last = nc.tensor.matmul(ps[c][:, :], W[:, k, c * P:(c + 1) * P], hf[:, k, bass.ds(i * BC, BC)], start=(k == 0), stop=(k == 3))
                    last.then_inc(made[c], 1)

        @block.vector
        def _(dve):
            dve.wait_ge(loaded, 32)
            with dve.Fori(0, NB) as i:
                for c in range(2):
                    dve.wait_ge(made[c], i + 1)
                    nc.vector.tensor_scalar(r.xT[:, c, bass.ds(i * BC, BC)], ps[c][:, :], B2[:, c:c + 1], None, ALU.add).then_inc(taken[c], 1)


def graph_norm_l3(nc, r, t):
    with Scope(nc, "l3n") as s:
        stats = s.sb("stats", [P, 2, 8, 6])
        moments = s.sb("moments", [P, 2, 2])
        par = s.sb("par", [P, 5, 2])
        mu, var, d, q, s1, m1, v2, rest, s2, scale, shift = (
            s.sb(n, [P, 2]) for n in ("mu", "var_c", "d", "q", "s1", "m1", "v2", "rest", "s2", "scale", "shift"))
        mean_g = s.sb("mean_g", [P, 1])
        rg = s.sb("rg", [P, 1])
        stage = s.sb("stage", [P, 2, 2, P])
        ps_sum = s.ps("ps_sum", [P, 4])
        back = [s.ps(f"back{k}", [P, 2, P]) for k in range(2)]
        names = ("loaded", "chain", "averaged", "summed", "squared", "summed2", "g_added", "g_rooted", "c_added", "c_rooted", "ready", "cut")
        loaded, chain_sem, averaged, summed, squared, summed2, g_added, g_rooted, c_added, c_rooted, ready, cut = (s.sem(n) for n in names)
        staged, flipped, taken = (s.sems(n, 2) for n in ("staged", "flipped", "taken"))
        block = s.block()
        LW, LB, GW, GB, MS = range(5)
        T2 = NT // 2

        @block.sync
        def _(sp):
            for n, name in enumerate(("ln_w", "ln_b", "gn_w", "gn_b", "gn_ms")):
                sp.dma_start(par[:, n, :], t["L3_gnn_" + name].rearrange("(c p) -> p c", p=P), allow_slow_non_contiguous=True).then_inc(loaded, 16)

        @block.vector
        def _(dve):
            link = Chain(dve, chain_sem)
            column_moments(nc, link, stats, moments, r.xT, 2)
            link(nc.vector.tensor_copy(mu[:, :], moments[:, :, 0]))
            nc.vector.tensor_copy(var[:, :], moments[:, :, 1]).then_inc(averaged, 1)
            dve.wait_ge(summed, 1)
            link(nc.vector.tensor_reduce(mean_g[:, :], ps_sum[:, 0:2], AX.X, ALU.add))
            link(nc.vector.tensor_scalar(mean_g[:, :], mean_g[:, :], 1.0 / G, None, ALU.mult))
            link(nc.vector.tensor_scalar(d[:, :], mu[:, :], mean_g[:, 0:1], None, ALU.subtract))
            link(nc.vector.tensor_tensor(q[:, :], d[:, :], d[:, :], ALU.mult))
            nc.vector.tensor_tensor(q[:, :], q[:, :], var[:, :], ALU.add).then_inc(squared, 1)
            dve.wait_ge(summed2, 1)
            link(nc.vector.tensor_reduce(rg[:, :], ps_sum[:, 2:4], AX.X, ALU.add))
            nc.vector.tensor_scalar(rg[:, :], rg[:, :], 1.0 / G, EPS, ALU.mult, ALU.add).then_inc(g_added, 1)
            dve.wait_ge(g_rooted, 1)
            dve.wait_ge(loaded, 80)
            link(nc.vector.reciprocal(rg[:, :], rg[:, :]))
            link(nc.vector.tensor_scalar(s1[:, :], par[:, LW, :], rg[:, 0:1], None, ALU.mult))
            link(nc.vector.tensor_tensor(m1[:, :], d[:, :], s1[:, :], ALU.mult))
            link(nc.vector.tensor_tensor(m1[:, :], m1[:, :], par[:, LB, :], ALU.add))
            link(nc.vector.tensor_tensor(v2[:, :], m1[:, :], par[:, MS, :], ALU.mult))
            link(nc.vector.tensor_tensor(rest[:, :], m1[:, :], v2[:, :], ALU.subtract))
            link(nc.vector.tensor_tensor(q[:, :], rest[:, :], rest[:, :], ALU.mult))
            link(nc.vector.tensor_tensor(v2[:, :], s1[:, :], s1[:, :], ALU.mult))
            link(nc.vector.tensor_tensor(v2[:, :], v2[:, :], var[:, :], ALU.mult))
            link(nc.vector.tensor_tensor(v2[:, :], v2[:, :], q[:, :], ALU.add))
            nc.vector.tensor_scalar(v2[:, :], v2[:, :], EPS, None, ALU.add).then_inc(c_added, 1)
            dve.wait_ge(c_rooted, 1)
            link(nc.vector.reciprocal(s2[:, :], v2[:, :]))
            link(nc.vector.tensor_tensor(s2[:, :], s2[:, :], par[:, GW, :], ALU.mult))
            link(nc.vector.tensor_tensor(scale[:, :], s1[:, :], s2[:, :], ALU.mult))
            link(nc.vector.tensor_tensor(shift[:, :], rest[:, :], s2[:, :], ALU.mult))
            link(nc.vector.tensor_tensor(shift[:, :], shift[:, :], par[:, GB, :], ALU.add))
            link(nc.vector.tensor_tensor(q[:, :], scale[:, :], mu[:, :], ALU.mult))
            nc.vector.tensor_tensor(shift[:, :], shift[:, :], q[:, :], ALU.subtract).then_inc(ready, 1)
            dve.wait_ge(cut, 2)
            with dve.Fori(0, T2) as i:
                for k in range(2):
                    dve.wait_ge(flipped[k], i)
                    nc.vector.tensor_scalar(stage[:, k, :, :], r.xT[:, :, bass.ds((2 * i + k) * P, P)], 1.0, None, ALU.mult).then_inc(staged[k], 1)
                for k in range(2):
                    xt = tile_of(r.x, 2 * i + k)
                    dve.wait_ge(flipped[k], i + 1)
                    nc.vector.tensor_tensor(xt, xt, back[k][:, :, :].rearrange("p c n -> p (c n)"), ALU.add).then_inc(taken[k], 1)

        @block.scalar
        def _(act):
            act.wait_ge(g_added, 1)
            nc.scalar.activation(rg[:, :], rg[:, :], ACT.Sqrt).then_inc(g_rooted, 1)
            act.wait_ge(c_added, 1)
            nc.scalar.activation(v2[:, :], v2[:, :], ACT.Sqrt).then_inc(c_rooted, 1)
            act.wait_ge(ready, 1)
            for c in range(2):
                nc.scalar.activation(r.xT[:, c, :], r.xT[:, c, :], ACT.Relu, bias=shift[:, c:c + 1], scale=scale[:, c:c + 1]).then_inc(cut, 1)

        @block.tensor
        def _(pe):
            pe.wait_ge(averaged, 1)
            nc.tensor.matmul(ps_sum[:, 0:2], r.ones[:, :], mu[:, :], start=True, stop=True).then_inc(summed, 1)
            pe.wait_ge(squared, 1)
            nc.tensor.matmul(ps_sum[:, 2:4], r.ones[:, :], q[:, :], start=True, stop=True).then_inc(summed2, 1)
            with pe.Fori(0, T2) as i:
                for k in range(2):
                    pe.wait_ge(staged[k], i + 1)
                    pe.wait_ge(taken[k], i)
                    for c in range(2):
                        last = nc.tensor.transpose(back[k][:, c, :], stage[:, k, c, :], r.eye[:, :])
                    last.then_inc(flipped[k], 1)


def route_l3(nc, r, w_router, bias, which, weight):
    EX = 8
    CAPACITY = float(-(-(N * 5) // (4 * EX)))
    with Scope(nc, "l3r") as s:
        w = s.sb("w", [P, 2, EX])
        row = s.sb("row", [1, EX])
        mean = s.sb("mean", [P, 2])
        p = s.sb("p", [1, EX])
        load = s.sb("load", [1, EX])
        one = s.sb("one", [1, 1])
        top = s.sb("top", [1, 8])
        idx = s.sb("idx", [1, 8], mybir.dt.uint32)
        pair = s.sb("pair", [1, 4])
        ps = s.ps("ps", [1, EX])
        ps4 = s.ps("ps4", [P, 4])
        names = ("loaded", "chain", "averaged", "scored", "e1", "e1_done", "e2", "e2_done", "e3", "e3_done", "paired", "spread")
        loaded, chain_sem, averaged, scored, e1, e1_done, e2, e2_done, e3, e3_done, paired, spread = (s.sem(n) for n in names)
        block = s.block()

        @block.sync
        def _(sp):
            sp.dma_start(w[:, :, :], w_router.rearrange("(c p) n -> p c n", p=P)).then_inc(loaded, 16)
            sp.dma_start(row[:, :], bias.unsqueeze(0)).then_inc(loaded, 16)

        @block.tensor
        def _(pe):
            pe.wait_ge(loaded, 32)
            pe.wait_ge(averaged, 1)
            nc.tensor.matmul(ps[:, :], r.ones[0:1, 0:1], row[:, :], start=True, stop=False)
            for c in range(2):
                last = nc.tensor.matmul(ps[:, :], mean[:, c:c + 1], w[:, c, :], start=False, stop=(c == 1))
            last.then_inc(scored, 1)
            pe.wait_ge(paired, 1)
            nc.tensor.matmul(ps4[:, :], r.ones[0:1, :], pair[:, :], start=True, stop=True).then_inc(spread, 1)

        @block.scalar
        def _(act):
            for begun, done, what in ((e1, e1_done, p[:, :]), (e2, e2_done, p[:, :]), (e3, e3_done, pair[:, 1:2])):
                act.wait_ge(begun, 1)
                nc.scalar.activation(what, what, ACT.Exp).then_inc(done, 1)

        @block.vector
        def _(dve):
            link = Chain(dve, chain_sem)

            def softmax(begun, done):
                link(nc.vector.tensor_reduce(one[:, :], p[:, :], AX.X, ALU.max))
                nc.vector.tensor_scalar(p[:, :], p[:, :], one[:, 0:1], None, ALU.subtract).then_inc(begun, 1)
                dve.wait_ge(done, 1)
                link(nc.vector.tensor_reduce(one[:, :], p[:, :], AX.X, ALU.add))
                link(nc.vector.reciprocal(one[:, :], one[:, :]))
                link(nc.vector.tensor_scalar(p[:, :], p[:, :], one[:, 0:1], None, ALU.mult))

            link(nc.vector.tensor_reduce(mean[:, :], r.xT[:, :, 0:N], AX.X, ALU.add))
            nc.vector.tensor_scalar(mean[:, :], mean[:, :], 1.0 / N, None, ALU.mult).then_inc(averaged, 1)
            dve.wait_ge(scored, 1)
            link(nc.vector.tensor_copy(p[:, :], ps[:, :]))
            softmax(e1, e1_done)
            link(nc.vector.tensor_scalar(load[:, :], p[:, :], float(N), 1e-30, ALU.mult, ALU.max))
            link(nc.vector.reciprocal(load[:, :], load[:, :]))
            link(nc.vector.tensor_scalar(load[:, :], load[:, :], CAPACITY, 1.0, ALU.mult, ALU.min))
            link(nc.vector.tensor_tensor(p[:, :], p[:, :], load[:, :], ALU.mult))
            softmax(e2, e2_done)
            link(nc.vector.max(top[:, :], p[:, :]))
            link(nc.vector.max_index(idx[:, :], top[:, :], p[:, :]))
            link(nc.vector.tensor_copy(pair[:, 2:4], idx[:, 0:2]))
            nc.vector.tensor_tensor(pair[:, 1:2], top[:, 1:2], top[:, 0:1], ALU.subtract).then_inc(e3, 1)
            dve.wait_ge(e3_done, 1)
            link(nc.vector.tensor_scalar(one[:, :], pair[:, 1:2], 1.0, None, ALU.add))
            link(nc.vector.reciprocal(pair[:, 0:1], one[:, :]))
            nc.vector.tensor_tensor(pair[:, 1:2], pair[:, 1:2], pair[:, 0:1], ALU.mult).then_inc(paired, 1)
            dve.wait_ge(spread, 1)
            link(nc.vector.tensor_copy(weight[:, :], ps4[:, 0:2]))
            link(nc.vector.tensor_copy(which[:, :], ps4[:, 2:4]))


def load_two(nc, r, which):
    def load(nc, s, W1, W2, B1, B2, w1, b1, w2, b2, loaded, block, hidden):
        HC = hidden // P
        base = s.sb("base", [P, 2, 1 + 2 + HC])
        row = s.sb("row_of", [P, 2, 1 + 2 + HC], I32)
        rowed, chain_sem = s.sem("rowed"), s.sem("chain")
        EX = w1.shape[0]
        w1_rows, w2_rows = w1.rearrange("e d f -> (e d) f"), w2.rearrange("e f d -> (e f) d")
        b1_rows = b1.rearrange("e (f o) -> (e f) o", o=1)

        @block.gpsimd
        def _(pool):
            pool.wait_ge(rowed, 1)
            for n in range(2):
                def at(m):
                    return bass.IndirectOffsetOnAxis(ap=row[:, n, m:m + 1], axis=0)
                pool.indirect_dma_start(B2[:, n, :], None, b2, at(0), bounds_check=EX - 1, oob_is_err=False).then_inc(loaded, 16)
                for c in range(2):
                    pool.indirect_dma_start(W1[:, n, c, :], None, w1_rows, at(1 + c), bounds_check=EX * G - 1, oob_is_err=False).then_inc(loaded, 16)
                for c in range(HC):
                    pool.indirect_dma_start(W2[:, n, c, :], None, w2_rows, at(3 + c), bounds_check=EX * hidden - 1, oob_is_err=False).then_inc(loaded, 16)
                    pool.indirect_dma_start(B1[:, n, c:c + 1], None, b1_rows, at(3 + c), bounds_check=EX * hidden - 1, oob_is_err=False).then_inc(loaded, 16)

        def rows(dve):
            link = Chain(dve, chain_sem)
            for n in range(2):
                link(nc.vector.tensor_copy(base[:, n, 0:1], which[:, n:n + 1]))
                for m, (size, c) in enumerate([(G, c) for c in range(2)] + [(hidden, c) for c in range(HC)]):
                    link(nc.vector.tensor_scalar(base[:, n, 1 + m:2 + m], which[:, n:n + 1], float(size), float(c * P), ALU.mult, ALU.add))
                    link(nc.vector.tensor_tensor(base[:, n, 1 + m:2 + m], base[:, n, 1 + m:2 + m], r.partition[:, :], ALU.add))
            nc.vector.tensor_copy(row[:, :, :], base[:, :, :]).then_inc(rowed, 1)
        return 16 * 2 * (3 + 2 * HC), rows
    return load


def finish_l3(nc, r, gamma, beta):
    with Scope(nc, "l3z") as s:
        gb = s.sb("gb", [P, 2, G])
        loaded, chain_sem = s.sem("loaded"), s.sem("chain")
        block = s.block()

        @block.sync
        def _(sp):
            sp.dma_start(gb[:, 0, :], gamma.unsqueeze(0).broadcast_to([P, G])).then_inc(loaded, 16)
            sp.dma_start(gb[:, 1, :], beta.unsqueeze(0).broadcast_to([P, G])).then_inc(loaded, 16)

        @block.vector
        def _(dve):
            link = Chain(dve, chain_sem)

            def all_tiles(n):
                return gb[:, n, :].unsqueeze(1).broadcast_to([P, NT, G])

            dve.wait_ge(loaded, 32)
            link(nc.vector.tensor_tensor(r.xh[:, :, :], r.xh[:, :, :], all_tiles(0), ALU.mult))
            link(nc.vector.tensor_tensor(r.x[:, :, :], r.x[:, :, :], all_tiles(1), ALU.add))
            link(nc.vector.tensor_tensor(r.x[:, :, :], r.x[:, :, :], r.xh[:, :, :], ALU.add))


def save_features(nc, r, table):
    with Scope(nc, "sv") as s:
        stored = s.sem("stored")
        block = s.block()

        @block.sync
        def _(sp):
            sp.dma_start(table.rearrange("(t p) f -> p t f", p=P), r.xh[:, :, :]).then_inc(stored, 16)
            sp.wait_ge(stored, 16)


@contextmanager
def features(nc, r, tag):
    with Scope(nc, tag) as s:
        r.xT = s.sb("xT", [P, 2, NPAD])
        yield


def build(nc, t, out, upto=99):
    f = t
    qv = nc.dram_tensor("qv", [NPAD, 2 * G], F32, kind="Internal").ap()
    kd = nc.dram_tensor("kd", [NPAD, G], F32, kind="Internal").ap()
    wide_states = nc.dram_tensor("wide_states", [E + 1, 3 * G], F32, kind="Internal").ap()
    carries = nc.dram_tensor("carries", [LANES + 1, 3 * G], F32, kind="Internal").ap()
    head_states = nc.dram_tensor("head_states", [E + 1, 2 * H + G], F32, kind="Internal").ap()
    row_table = nc.dram_tensor("row_table", [NPAD, G], F32, kind="Internal").ap()
    sum_states = nc.dram_tensor("sum_states", [E + 1, G], F32, kind="Internal").ap()
    sum_carries = nc.dram_tensor("sum_carries", [LANES + 1, G], F32, kind="Internal").ap()
    keys_t = nc.dram_tensor("keys_t", [STEPS, 2, LANES], F32, kind="Internal").ap()
    sorted_edges = nc.dram_tensor("sorted_edges", [E, 2], I32, kind="Internal").ap()
    with Scope(nc, "r") as s:
        r = Resident()
        r.x = s.sb("x", [P, NT, G])
        r.gate = s.sb("gate", [P, NT, 8])
        r.xh = s.sb("xh", [P, NT, G])
        r.var = s.sb("var", [P, NT])
        r.eye = s.sb("eye", [P, P])
        r.below = s.sb("below", [P, P])
        r.above = s.sb("above", [P, P])
        r.ones = s.sb("ones", [P, P])
        r.wide_ones = s.sb("wide_ones", [P, STEPS])
        r.column = s.sb("column", [P, P])
        r.partition = s.sb("partition", [P, 1])
        r.made = s.sem("made")
        r.by_dst, r.by_src = Order(), Order()
        for tag, o in (("dst", r.by_dst), ("src", r.by_src)):
            o.key = s.sb(f"key_{tag}", [LANES, STEPS + U * B], I32)
            o.far = s.sb(f"far_{tag}", [LANES, STEPS + U * B], I32)
            o.cont = s.sb(f"cont_{tag}", [LANES, STEPS])
            o.pen = s.sb(f"pen_{tag}", [LANES, STEPS])
            o.count = s.sb(f"count_{tag}", [P, NT])
            o.end_row = s.sb(f"end_row_{tag}", [P, NT], I32)
            o.carry_row = s.sb(f"carry_row_{tag}", [P, NT], I32)
            o.gate = s.sb(f"gate_{tag}", [P, LANES])
            o.gate_pen = s.sb(f"gate_pen_{tag}", [P, LANES])
        load_constants(nc, r, t["x"], t["src"], t["dst"])
        with Scope(nc, "h") as hs:
            hist = hs.sb("hist", [P, STEPS + 1, NT])
            count_keys(nc, r, r.by_dst, "cd", hist, r.by_dst.key, False)
            if upto >= 5:
                count_keys(nc, r, r.by_src, "cs", hist, r.by_dst.far, True)
                sort_edges(nc, r, r.by_src, r.by_dst.far, r.by_dst.key, hist, keys_t, sorted_edges)
        lane_tables(nc, r, r.by_dst, "ld", t["dst"])
        if upto >= 5:
            lane_tables(nc, r, r.by_src, "ls", sorted_edges[:, 0])
        if upto >= 1:
            normalize(nc, r, "n0", r.x)
            project_l0(nc, r, t["L0_gnn_Wqkv"], t["L0_gnn_gamma"], t["L0_gnn_beta"], qv, kd)
            with Scope(nc, "e0") as es:
                tail = es.sb("tail", [LANES, 3 * G])
                edges_softmax(nc, r, r.by_dst, "l0e", qv, kd, G, wide_states, tail)
                carry_softmax(nc, r, r.by_dst, "c0", tail, carries, wide_states, G)
            finish_softmax(nc, r, r.by_dst, "f0", wide_states, carries, G, r.x)
        def gate(n, e):
            return r.gate[:, bass.ds(n, 1), e]

        if upto >= 2:
            normalize(nc, r, "n1", r.x)
            with features(nc, r, "x0"):
                route(nc, r, "g0", t["L0_ffn_gW"], t["L0_ffn_gb"], 4, "softmax of two")
                layer_l0_ffn(nc, r, t)
        if upto >= 3:
            normalize(nc, r, "n2", r.x)
            project_l1(nc, r, t["L1_gnn_W_self"], t["L1_gnn_W_neigh"], row_table)
            with Scope(nc, "e1") as es:
                tail = es.sb("tail", [LANES, 3 * G])
                edges_sum(nc, r, r.by_dst, "l1e", row_table, sum_states, tail)
                carry_sum(nc, r, r.by_dst, "c1", tail, sum_carries, sum_states)
            finish_sum(nc, r, r.by_dst, "f1", sum_states, sum_carries, True, r.x)
        if upto >= 4:
            normalize(nc, r, "n3", r.x)
            with features(nc, r, "x1"):
                route(nc, r, "g1", t["L1_ffn_Wg"], t["L1_ffn_bg"], 8, "ones")
                experts_gelu(nc, r, "l1f", t["L1_ffn_W1"], t["L1_ffn_b1"], t["L1_ffn_W2"], t["L1_ffn_b2"], 8, 512, gate, r.x, load_all)
        if upto >= 5:
            normalize(nc, r, "n4", r.x)
            project_l2(nc, r, [t["L2_gnn_Wk"], t["L2_gnn_Wv"], t["L2_gnn_Wq"]], [t["L2_gnn_bk"], t["L2_gnn_bv"], t["L2_gnn_bq"]], kd, qv)
            with Scope(nc, "e2") as es:
                tail = es.sb("tail", [LANES, 3 * G])
                edges_softmax(nc, r, r.by_src, "l2e", qv, kd, H, head_states, tail)
                carry_softmax(nc, r, r.by_src, "c2", tail, carries, head_states, H)
            with Scope(nc, "a2") as xs:
                agg = xs.sb("agg", [P, NT, G])
                finish_softmax(nc, r, r.by_src, "f2", head_states, carries, H, agg)
                project_out(nc, r, agg, t["L2_gnn_Wo"], t["L2_gnn_bo"])
        if upto >= 6:
            normalize(nc, r, "n5", r.x)
            with features(nc, r, "x2"):
                route(nc, r, "g2", t["L2_ffn_router_w"].rearrange("e d -> d e"), None, 8, "share")
                experts_gelu(nc, r, "l2f", t["L2_ffn_w1"], t["L2_ffn_b1"], t["L2_ffn_w2"], t["L2_ffn_b2"], 8, 256, gate, r.x, load_all)
            add_features(nc, r, "l2r", r.xh)
        if upto >= 7:
            normalize(nc, r, "n6", r.x)
            save_features(nc, r, row_table)
            add_features(nc, r, "l3r0", r.xh)
            with Scope(nc, "e3") as es:
                tail = es.sb("tail", [LANES, 3 * G])
                edges_sum(nc, r, r.by_dst, "l3e", row_table, sum_states, tail, t["edge_attr_256"])
                carry_sum(nc, r, r.by_dst, "c3", tail, sum_carries, sum_states)
            finish_sum(nc, r, r.by_dst, "f3", sum_states, sum_carries, False, r.xh)
            with features(nc, r, "x3"):
                route(nc, r, "g3", None, None, 8, None)
                with Scope(nc, "hf") as es:
                    hf = es.sb("hf", [P, 4, NPAD])
                    up_l3(nc, r, t["L3_gnn_W1"], t["L3_gnn_b1"], hf)
                    batch_norm_l3(nc, r, t["L3_gnn_bn_gamma"], t["L3_gnn_bn_beta"], hf)
                    down_l3(nc, r, t["L3_gnn_W2"], t["L3_gnn_b2"], hf)
                graph_norm_l3(nc, r, t)
        if upto >= 8:
            normalize(nc, r, "n7", r.x)
            with features(nc, r, "x4"):
                route(nc, r, "g4", None, None, 8, None)
                with Scope(nc, "w3") as es:
                    which = es.sb("which", [P, 2])
                    weight = es.sb("weight", [P, 2])
                    route_l3(nc, r, t["L3_ffn_Wr"], t["L3_ffn_br"], which, weight)
                    experts_gelu(nc, r, "l3f", t["L3_ffn_W1"], t["L3_ffn_b1"], t["L3_ffn_W2"], t["L3_ffn_b2"], 2, 512,
                                 lambda n, e: weight[:, e:e + 1], r.xh, load_two(nc, r, which))
            normalize(nc, r, "n8", r.xh)
            finish_l3(nc, r, t["L3_ffn_gamma"], t["L3_ffn_beta"])
        store(nc, r, out)


def add_features(nc, r, tag, more):
    with Scope(nc, tag) as s:
        block = s.block()

        @block.vector
        def _(dve):
            nc.vector.tensor_tensor(r.x[:, 0:NT // 2, :], r.x[:, 0:NT // 2, :], more[:, 0:NT // 2, :], ALU.add)

        @block.gpsimd
        def _(pool):
            nc.gpsimd.tensor_tensor(r.x[:, NT // 2:, :], r.x[:, NT // 2:, :], more[:, NT // 2:, :], ALU.add)


def store(nc, r, out):
    with Scope(nc, "st") as s:
        stored = s.sem("stored")
        block = s.block()

        @block.sync
        def _(sp):
            sp.dma_start(out[0:(NT - 1) * P, :].rearrange("(t p) f -> p t f", p=P), r.x[:, 0:NT - 1, :]).then_inc(stored, 16)
            sp.dma_start(out[(NT - 1) * P:N, :], r.x[0:LAST, NT - 1, :]).then_inc(stored, 16)
            sp.wait_ge(stored, 32)


def kernel(**inputs):
    import numpy as np
    import concourse.bacc as bacc
    from concourse.bass_utils import run_bass_kernel_spmd

    nc = bacc.Bacc("TRN2", target_bir_lowering=False, num_devices=1)
    arrays, t = {}, {}
    for name, a in inputs.items():
        a = np.ascontiguousarray(a)
        arrays[f"in_{name}"] = a
        t[name] = nc.dram_tensor(f"in_{name}", a.shape, mybir.dt.from_np(a.dtype), kind="ExternalInput").ap()
    out = nc.dram_tensor("out_x", (N, G), F32, kind="ExternalOutput").ap()
    build(nc, t, out)
    got = run_bass_kernel_spmd(nc, [arrays], core_ids=[0])
    return got.results[0]["out_x"]
```

```python
import concourse.bass as bass
from concourse import mybir
from contextlib import ExitStack, contextmanager

F32 = mybir.dt.float32
BF16 = mybir.dt.bfloat16
I32 = mybir.dt.int32
ALU = mybir.AluOpType
ACT = mybir.ActivationFunctionType
AX = mybir.AxisListType

P = 128
N = 3750
E = 60000
G = 256
H = 8
D = G // H
NT = -(-N // P)
NPAD = NT * P
LAST = N - (NT - 1) * P
LANES = 120
STEPS = E // LANES
B = 5
U = 4
TURNS = STEPS // (U * B)
TURNS2 = STEPS // (2 * B)
NONE = -1.0e30
EPS = 1e-5
TB = 3
NB = NT // TB
BC = TB * P
GROUP = 256
GB = 3
GROUPS = -(-((2 * NPAD + 8 * (GROUP - 1)) // GROUP) // GB) * GB
SLOT_TILES = 6
BESIDE = {"l0p": (0, 3), "g0": (3 * NT, 1), "l0f": (4 * NT, 10), "l1p": (4 * NT + 20 * NB, 4), "g1": (8 * NT + 20 * NB, 2)}
assert 10 * NT + 20 * NB == STEPS


class Chain:

    def __init__(self, eng, sem):
        self.eng, self.sem, self.base, self.n, self.turn, self.per = eng, sem, 0, 0, None, 0

    def __call__(self, ins):
        self.n += 1
        ins.then_inc(self.sem, 1)
        self.eng.wait_ge(self.sem, self.value())

    def mark(self, ins):
        self.n += 1
        ins.then_inc(self.sem, 1)

    def all_but(self, few):
        self.eng.wait_ge(self.sem, self.value() - few)

    def value(self):
        if self.turn is None:
            return self.base + self.n
        return self.turn * self.per + (self.base + self.n)

    def enter(self, turn, per):
        self.base, self.n, self.turn, self.per = self.base + self.n, 0, turn, per

    def leave(self, turns):
        assert self.n == self.per, (self.n, self.per)
        self.base, self.n, self.turn = self.base + turns * self.per, 0, None


def tables_made(pool, r):
    pool.wait_ge(r.made, 1)


class Scope:

    def __init__(self, nc, tag):
        self.nc, self.tag, self.ctx, self.taken = nc, tag, ExitStack(), []

    def __enter__(self):
        return self

    def __exit__(self, *a):
        self.ctx.__exit__(*a)
        if self.taken and a[0] is None:
            self.nc.clear_and_free_semaphores(self.taken)
            self.nc.all_engine_barrier()

    def sb(self, name, shape, dt=F32):
        return self.ctx.enter_context(self.nc.sbuf_tensor(f"{self.tag}_{name}", shape, dt))

    def ps(self, name, shape, dt=F32):
        return self.ctx.enter_context(self.nc.psum_tensor(f"{self.tag}_{name}", shape, dt))

    def sem(self, name):
        self.taken.append(self.nc.alloc_semaphore(f"{self.tag}_{name}"))
        return self.taken[-1]

    def sems(self, name, n):
        return [self.sem(f"{name}{i}") for i in range(n)]

    def block(self):
        return self.ctx.enter_context(self.nc.Block())


class Resident:
    pass


class Order:
    pass


def load_constants(nc, r, x, src, dst):
    with Scope(nc, "load") as s:
        zeroed, loaded, made, eyed = s.sem("zeroed"), s.sem("loaded"), s.sem("made"), s.sem("eyed")
        block = s.block()

        @block.sync
        def _(sp):
            sp.dma_start(r.x[:, 0:NT - 1, :], x[0:(NT - 1) * P, :].rearrange("(t p) f -> p t f", p=P)).then_inc(loaded, 16)
            sp.wait_ge(zeroed, 1)
            sp.dma_start(r.x[0:LAST, NT - 1, :], x[(NT - 1) * P:N, :]).then_inc(loaded, 16)
            sp.dma_start(r.by_dst.far[:, 0:STEPS], src.rearrange("(p j) -> p j", p=LANES)).then_inc(loaded, 16)
            sp.dma_start(r.by_dst.key[:, 0:STEPS], dst.rearrange("(p j) -> p j", p=LANES)).then_inc(loaded, 16)
            sp.wait_ge(loaded, 64)

        @block.vector
        def _(dve):
            nc.vector.memset(r.x[:, NT - 1, :], 0.0).then_inc(zeroed, 1)
            nc.vector.memset(r.ones[:, :], 1.0)
            nc.vector.memset(r.wide_ones[:, :], 1.0)
            for o in (r.by_dst, r.by_src):
                nc.vector.memset(o.key[:, STEPS:], 0)
                nc.vector.memset(o.end_row[:, NT:], 0)
                last = nc.vector.memset(o.far[:, STEPS:], 0)
            last.then_inc(r.made, 1)

        @block.gpsimd
        def _(pool):
            nc.gpsimd.memset(r.eye[:, :], 0.0).then_inc(made, 1)
            nc.gpsimd.memset(r.below[:, :], 1.0).then_inc(made, 1)
            nc.gpsimd.memset(r.above[:, :], 1.0).then_inc(made, 1)
            pool.wait_ge(made, 3)
            nc.gpsimd.affine_select(out=r.eye[:, :], in_=r.eye[:, :], compare_op=ALU.not_equal, fill=1.0,
                                    base=0, pattern=[[-1, P]], channel_multiplier=1)
            nc.gpsimd.affine_select(out=r.below[:, :], in_=r.below[:, :], compare_op=ALU.is_gt, fill=0.0,
                                    base=0, pattern=[[-1, P]], channel_multiplier=1)
            nc.gpsimd.affine_select(out=r.above[:, :], in_=r.above[:, :], compare_op=ALU.is_gt, fill=0.0,
                                    base=0, pattern=[[1, P]], channel_multiplier=-1)
            nc.gpsimd.iota(r.column[:, :], pattern=[[1, P]], base=0, channel_multiplier=0,
                           allow_small_or_imprecise_dtypes=True)
            nc.gpsimd.iota(r.partition[:, :], pattern=[[0, 1]], base=0, channel_multiplier=1,
                           allow_small_or_imprecise_dtypes=True).then_inc(eyed, 1)


def one_hot(nc, columns, n, out, numbers):
    return nc.vector.tensor_tensor(out, columns[:, 0:n, :], numbers.unsqueeze(1).broadcast_to([LANES, n, B]), ALU.is_equal)


class NodeRows:

    def __init__(self, nc, s, r, o):
        self.nc, self.r, self.o = nc, r, o
        self.count = s.sb("count", [P, NT])
        self.start = s.sb("start", [P, NT])
        self.total = s.sb("total", [P, NT + 1])
        self.end = s.sb("end", [P, NT])
        self.some = s.sb("some", [P, NT])
        self.ps = s.ps("ps_start", [P, 2 * NT])
        self.summed, self.prefixed = s.sem("summed"), s.sem("prefixed")

    def vector(self, dve, link):
        nc, r, o, count, start, total, end, some = self.nc, self.r, self.o, self.count, self.start, self.total, self.end, self.some
        nc.vector.tensor_copy(o.count[:, :], count[:, :]).then_inc(self.summed, 1)
        dve.wait_ge(self.prefixed, 1)
        link(nc.vector.memset(total[:, 0:1], 0.0))
        link(nc.vector.tensor_tensor_scan(total[:, 1:NT + 1], r.ones[:, 0:NT], self.ps[:, NT:2 * NT], 0.0, ALU.mult, ALU.add))
        link(nc.vector.tensor_tensor(start[:, :], total[:, 0:NT], self.ps[:, 0:NT], ALU.add))
        link(nc.vector.tensor_tensor(end[:, :], start[:, :], count[:, :], ALU.add))
        link(nc.vector.tensor_scalar(end[:, :], end[:, :], -1.0, 0.0, ALU.add, ALU.max))
        link(nc.vector.tensor_scalar(some[:, :], count[:, :], 0.0, None, ALU.is_gt))
        link(nc.vector.tensor_scalar(end[:, :], end[:, :], -float(E), None, ALU.add))
        link(nc.vector.tensor_tensor(end[:, :], end[:, :], some[:, :], ALU.mult))
        link(nc.vector.tensor_scalar(o.end_row[:, 0:NT], end[:, :], float(E), None, ALU.add))

    def tensor(self, pe):
        pe.wait_ge(self.summed, 1)
        self.nc.tensor.matmul(self.ps[:, 0:NT], self.r.above[:, :], self.count[:, :], start=True, stop=True)
        self.nc.tensor.matmul(self.ps[:, NT:2 * NT], self.r.ones[:, :], self.count[:, :], start=True, stop=True).then_inc(self.prefixed, 1)


def count_keys(nc, r, o, tag, hist, key, cleared):
    with Scope(nc, tag) as s:
        part = s.sb("part", [LANES, STEPS], I32)
        columns = s.sb("columns", [LANES, P, B], BF16)
        lo = s.sb("lo", [LANES, STEPS], BF16)
        hi = s.sb("hi", [LANES, STEPS], BF16)
        one_lo = s.sb("one_lo", [LANES, 2, P, B], BF16)
        one_hi = s.sb("one_hi", [LANES, 2, NT, B], BF16)
        nodes = NodeRows(nc, s, r, o)
        none = s.sb("none", [LANES, P], BF16)
        ps_count = s.ps("ps_count", [P, NT])
        none_made, all_counted = s.sem("none_made"), s.sem("all_counted")
        ps = [s.ps(f"ps{k}", [P, B * NT]) for k in range(2)]
        chain_sem, ready, counted = s.sem("chain"), s.sems("ready", 2), s.sems("counted", 2)
        kept = s.sems("kept", 2)
        zero = s.sb("zero", [P, G])
        zeroed, cleared_all = s.sem("zeroed"), s.sem("cleared_all")
        block = s.block()

        @block.sync
        def _(sp):
            rows = cleared.shape[0] // P
            sp.wait_ge(zeroed, 1)
            sp.dma_start(cleared.rearrange("(p n) f -> p n f", p=P), zero[:, :].unsqueeze(1).broadcast_to([P, rows, G])).then_inc(cleared_all, 16)
            sp.wait_ge(cleared_all, 16)

        @block.vector
        def _(dve):
            link = Chain(dve, chain_sem)
            nc.vector.memset(none[:, :], 0.0).then_inc(none_made, 1)
            nc.vector.memset(zero[:, :], 0.0).then_inc(zeroed, 1)
            link(nc.vector.tensor_scalar(part[:, :], key[:, 0:STEPS], 7, None, ALU.arith_shift_right))
            link(nc.vector.tensor_copy(hi[:, :], part[:, :]))
            link(nc.vector.tensor_scalar(part[:, :], key[:, 0:STEPS], P - 1, None, ALU.bitwise_and))
            link(nc.vector.tensor_copy(lo[:, :], part[:, :]))
            link(nc.vector.tensor_copy(columns[:, :, :], r.column[0:LANES, :].unsqueeze(2).broadcast_to([LANES, P, B])))

            def make_rows(i, k):
                j = (i * 2 + k) * B
                dve.wait_ge(counted[k], i)
                one_hot(nc, columns, P, one_lo[:, k, :, :], lo[:, bass.ds(j, B)])
                one_hot(nc, columns, NT, one_hi[:, k, :, :], hi[:, bass.ds(j, B)]).then_inc(ready[k], 1)

            def keep_counts(i, k):
                dve.wait_ge(counted[k], i + 1)
                nc.vector.tensor_copy(hist[:, bass.ds((i * 2 + k) * B + 1, B), :].rearrange("p a b -> p (a b)"), ps[k][:, :]).then_inc(kept[k], 1)

            make_rows(0, 0)
            with dve.Fori(0, TURNS2 - 1) as i:
                make_rows(i, 1)
                keep_counts(i, 0)
                make_rows(i + 1, 0)
                keep_counts(i, 1)
            make_rows(TURNS2 - 1, 1)
            keep_counts(TURNS2 - 1, 0)
            keep_counts(TURNS2 - 1, 1)
            for k in range(2):
                dve.wait_ge(kept[k], TURNS2)
            dve.wait_ge(all_counted, 1)
            link(nc.vector.tensor_copy(nodes.count[:, :], ps_count[:, :]))
            nodes.vector(dve, link)
            link(nc.vector.tensor_copy(hist[:, 0, :], nodes.start[:, :]))
            for h in range(NT):
                link.mark(nc.vector.tensor_tensor_scan(hist[:, 1:, h], r.wide_ones[:, :], hist[:, 1:, h],
                                                       nodes.start[:, h:h + 1], ALU.mult, ALU.add))

        @block.tensor
        def _(pe):
            pe.wait_ge(none_made, 1)
            nc.tensor.matmul(ps_count[:, :], none[:, :], none[:, 0:NT], start=True, stop=False)
            with pe.Fori(0, TURNS2) as i:
                for k in range(2):
                    pe.wait_ge(ready[k], i + 1)
                    pe.wait_ge(kept[k], i)
                    for b in range(B):
                        last = nc.tensor.matmul(ps[k][:, b * NT:(b + 1) * NT], one_lo[:, k, :, b], one_hi[:, k, :, b],
                                                start=True, stop=True)
                    for b in range(B):
                        last = nc.tensor.matmul(ps_count[:, :], one_lo[:, k, :, b], one_hi[:, k, :, b], start=False, stop=False)
                    last.then_inc(counted[k], 1)
            nc.tensor.matmul(ps_count[:, :], none[:, :], none[:, 0:NT], start=False, stop=True).then_inc(all_counted, 1)
            nodes.tensor(pe)


def place_edges(nc, r, places, other, hist, keys_t):
    key, far = other.far, other.key
    with Scope(nc, "sort") as s:
        lof = s.sb("lof", [LANES, STEPS])
        keyf = s.sb("keyf", [LANES, STEPS])
        part = s.sb("part", [LANES, STEPS], I32)
        hi = s.sb("hi", [LANES, STEPS])
        columns = s.sb("columns", [LANES, P, B], BF16)
        other_lo = s.sb("other_lo", [LANES, STEPS], BF16)
        other_hi = s.sb("other_hi", [LANES, STEPS], BF16)
        row_lo = s.sb("row_lo", [LANES, 2, P, B], BF16)
        row_hi = s.sb("row_hi", [LANES, 2, NT, B], BF16)
        none = s.sb("none", [LANES, P], BF16)
        nodes = NodeRows(nc, s, r, other)
        ps_count = s.ps("ps_count", [P, NT])
        counted = s.sem("counted")
        rows = s.sb("rows", [P, 4, 2, LANES])
        keyrow = s.sb("keyrow", [P, U, B, 2, LANES])
        one_lo = s.sb("one_lo", [P, 2, B, LANES])
        one_hi = s.sb("one_hi", [LANES, 2, B, NT])
        picked = s.sb("picked", [LANES, B, NT])
        scratch = s.sb("scratch", [LANES, 2, B, LANES])
        base = s.sb("base", [LANES, B])
        rank = s.sb("rank", [LANES, 2, B])
        flip = [s.ps(f"flip{k}", [P, 4, P]) for k in range(2)]
        ps = [s.ps(f"ps{k}", [LANES, B * NT]) for k in range(2)]
        chain_sem, split, flipped, copied, stored = s.sem("chain"), s.sem("split"), s.sem("flipped"), s.sem("copied"), s.sem("stored")
        came, hot, ranked, found, placed = (s.sems(n, U) for n in ("came", "hot", "ranked", "found", "placed"))
        block = s.block()
        CH = STEPS // 4

        @block.vector
        def _(dve):
            link = Chain(dve, chain_sem)
            link(nc.vector.memset(none[:, :], 0.0))
            link(nc.vector.tensor_scalar(part[:, :], far[:, 0:STEPS], 7, None, ALU.arith_shift_right))
            link(nc.vector.tensor_copy(other_hi[:, :], part[:, :]))
            link(nc.vector.tensor_scalar(part[:, :], far[:, 0:STEPS], P - 1, None, ALU.bitwise_and))
            link(nc.vector.tensor_copy(other_lo[:, :], part[:, :]))
            link(nc.vector.tensor_copy(columns[:, :, :], r.column[0:LANES, :].unsqueeze(2).broadcast_to([LANES, P, B])))
            link(nc.vector.tensor_scalar(part[:, :], key[:, 0:STEPS], 7, None, ALU.arith_shift_right))
            link(nc.vector.tensor_copy(hi[:, :], part[:, :]))
            link(nc.vector.tensor_scalar(part[:, :], key[:, 0:STEPS], P - 1, None, ALU.bitwise_and))
            link(nc.vector.tensor_copy(keyf[:, :], key[:, 0:STEPS]))
            nc.vector.tensor_copy(lof[:, :], part[:, :]).then_inc(split, 1)
            dve.wait_ge(flipped, 1)
            link(nc.vector.tensor_copy(rows[0:CH, :, 0, :], flip[0][0:CH, :, 0:LANES]))
            nc.vector.tensor_copy(rows[0:CH, :, 1, :], flip[1][0:CH, :, 0:LANES]).then_inc(copied, 1)

            def rank_batch(i, k):
                j = (i * U + k) * B
                dve.wait_ge(came[k], (i + 1) * 16)
                nc.vector.tensor_scalar(one_lo[:, k % 2, :, :], keyrow[:, k, :, 1, :], r.partition[:, 0:1], None, ALU.is_equal)
                one_hot(nc, columns, P, row_lo[:, k % 2, :, :], other_lo[:, bass.ds(j, B)])
                one_hot(nc, columns, NT, row_hi[:, k % 2, :, :], other_hi[:, bass.ds(j, B)]).then_inc(hot[k], 1)
                link.mark(nc.vector.tensor_tensor(
                    one_hi[:, k % 2, :, :], r.column[0:LANES, 0:NT].unsqueeze(1).broadcast_to([LANES, B, NT]),
                    hi[:, bass.ds(j, B)].unsqueeze(2).broadcast_to([LANES, B, NT]), ALU.is_equal))
                for b in range(B):
                    last = nc.vector.scalar_tensor_tensor(
                        scratch[:, k % 2, b, :], keyrow[0:LANES, k, b, 0, :], keyf[:, bass.ds(j + b, 1)], r.below[0:LANES, 0:LANES],
                        ALU.is_equal, ALU.mult, accum_out=rank[:, k % 2, b:b + 1])
                last.then_inc(ranked[k], 1)

            def place_batch(i, k):
                j = (i * U + k) * B
                dve.wait_ge(ranked[k], i + 1)
                dve.wait_ge(found[k], i + 1)
                link(nc.vector.tensor_tensor(picked[:, :, :].rearrange("p a b -> p (a b)"), ps[k % 2][:, :],
                                             one_hi[:, k % 2, :, :].rearrange("p a b -> p (a b)"), ALU.mult))
                link(nc.vector.tensor_reduce(base[:, :], picked[:, :, :], AX.X, ALU.add))
                nc.vector.tensor_tensor(places[:, bass.ds(j, B)], base[:, :], rank[:, k % 2, :], ALU.add).then_inc(placed[k], 1)
                dve.wait_ge(placed[k], i + 1)

            def both(i, k):
                rank_batch(*after(i, k))
                place_batch(i, k)

            skewed(dve, link, U * 3, lambda: rank_batch(0, 0), both, lambda i: place_batch(i, U - 1))
            dve.wait_ge(counted, 1)
            link(nc.vector.tensor_copy(nodes.count[:, :], ps_count[:, :]))
            nodes.vector(dve, link)

        @block.tensor
        def _(pe):
            pe.wait_ge(split, 1)
            for c in range(4):
                nc.tensor.transpose(flip[0][0:CH, c, 0:LANES], keyf[:, c * CH:(c + 1) * CH], r.eye[0:LANES, 0:LANES])
                last = nc.tensor.transpose(flip[1][0:CH, c, 0:LANES], lof[:, c * CH:(c + 1) * CH], r.eye[0:LANES, 0:LANES])
            last.then_inc(flipped, 1)
            nc.tensor.matmul(ps_count[:, :], none[:, :], none[:, 0:NT], start=True, stop=False)
            with pe.Fori(0, TURNS) as i:
                for k in range(U):
                    pe.wait_ge(hot[k], i + 1)
                    if k >= 2:
                        pe.wait_ge(placed[k - 2], i + 1)
                    else:
                        pe.wait_ge(placed[k - 2 + U], i)
                    for b in range(B):
                        last = nc.tensor.matmul(ps[k % 2][:, b * NT:(b + 1) * NT], one_lo[:, k % 2, b, :],
                                                hist[:, bass.ds((i * U + k) * B + b, 1), :].rearrange("p a b -> p (a b)"), start=True, stop=True)
                    for b in range(B):
                        last = nc.tensor.matmul(ps_count[:, :], row_lo[:, k % 2, :, b], row_hi[:, k % 2, :, b], start=False, stop=False)
                    last.then_inc(found[k], 1)
            nc.tensor.matmul(ps_count[:, :], none[:, :], none[:, 0:NT], start=False, stop=True).then_inc(counted, 1)
            nodes.tensor(pe)

        @block.sync
        def _(sp):
            sp.wait_ge(copied, 1)
            sp.dma_start(keys_t.rearrange("(c j) k l -> j c k l", c=4), rows[0:CH, :, :, :]).then_inc(stored, 16)
            sp.wait_ge(stored, 16)
            with sp.Fori(0, TURNS) as i:
                for k in range(U):
                    sp.wait_ge(ranked[k], i)
                    sp.dma_start(keyrow[:, k, :, :, :].rearrange("p a b c -> p (a b c)"),
                                 keys_t[bass.ds((i * U + k) * B, B), :, :].rearrange("a b c -> (a b c)").unsqueeze(0).broadcast_to([P, B * 2 * LANES])).then_inc(came[k], 16)


class Sender:

    def __init__(self, nc, s, r, start, steps, turns, sorted_edges):
        self.nc, self.r, self.start, self.steps, self.turns, self.sorted_edges = nc, r, start, steps, turns, sorted_edges
        self.place = s.sb("place", [LANES, 2, steps], I32)
        self.record = s.sb("record", [LANES, 2, steps, 2], I32)
        self.staged, self.sent, self.next_turn = s.sems("staged_edges", 2), s.sems("sent_edges", 2), f"{s.tag}_next_turn"

    def vector(self, dve, i, k):
        nc, r, at = self.nc, self.r, bass.ds(self.start + (i * 2 + k) * self.steps, self.steps)
        dve.wait_ge(self.sent[k], i * (16 * self.steps))
        nc.vector.tensor_copy(self.place[:, k, :], r.by_src.key[:, at])
        nc.vector.tensor_copy(self.record[:, k, :, 0], r.by_dst.far[:, at])
        nc.vector.tensor_copy(self.record[:, k, :, 1], r.by_dst.key[:, at]).then_inc(self.staged[k], 1)

    def gpsimd(self, pool):
        last_edge, turn = pool.to_reg(E - 1), pool.alloc_register(self.next_turn)
        with pool.Fori(0, self.turns) as i:
            pool.reg_add(turn, i, 1)
            for k in range(2):
                tables_made(pool, self.r)
                pool.wait_ge(self.staged[k], turn)
                for b in range(self.steps):
                    pool.indirect_dma_start(self.sorted_edges, bass.IndirectOffsetOnAxis(ap=self.place[:, k, b:b + 1], axis=0),
                                            self.record[:, k, b, :], None, bounds_check=last_edge, oob_is_err=False).then_inc(self.sent[k], 16)
        for k in range(2):
            pool.wait_ge(self.sent[k], 16 * self.steps * self.turns)


def take_sorted(nc, o, sorted_edges):
    with Scope(nc, "sorted") as s:
        both = s.sb("both", [LANES, STEPS, 2], I32)
        loaded, done = s.sem("loaded"), s.sem("done")
        block = s.block()

        @block.sync
        def _(sp):
            sp.dma_start(both[:, :, :], sorted_edges.rearrange("(p j) k -> p j k", p=LANES)).then_inc(loaded, 16)

        @block.vector
        def _(dve):
            dve.wait_ge(loaded, 16)
            nc.vector.tensor_copy(o.key[:, 0:STEPS], both[:, :, 0]).then_inc(done, 1)
            nc.vector.tensor_copy(o.far[:, 0:STEPS], both[:, :, 1]).then_inc(done, 1)


def lane_tables(nc, r, o, tag, keys):
    with Scope(nc, tag) as s:
        keyf = s.sb("keyf", [LANES, STEPS])
        ends = s.sb("ends", [1, 3, LANES], I32)
        endf = s.sb("endf", [1, 3, LANES])
        whole = s.sb("whole", [1, 3, LANES])
        first_run = s.sb("first_run", [LANES, STEPS])
        head = s.sb("head", [LANES, 2])
        ps_gate = s.ps("ps_gate", [P, 2, LANES])
        chain_sem, gated, spread, key_ends = s.sem("chain"), s.sem("gated"), s.sem("spread"), s.sem("key_ends")
        block = s.block()
        firsts = keys.rearrange("(q j) -> j q", j=STEPS)

        @block.sync
        def _(sp):
            sp.dma_start(ends[:, 0, :], firsts[0:1, :], allow_slow_non_contiguous=True).then_inc(key_ends, 16)
            sp.dma_start(ends[:, 1, :], firsts[STEPS - 1:STEPS, :], allow_slow_non_contiguous=True).then_inc(key_ends, 16)
            sp.dma_start(ends[:, 2, 1:LANES], firsts[STEPS - 1:STEPS, 0:LANES - 1], allow_slow_non_contiguous=True).then_inc(key_ends, 16)
            sp.dma_start(ends[:, 2, 0:1], firsts[0:1, 0:1], allow_slow_non_contiguous=True).then_inc(key_ends, 16)

        @block.vector
        def _(dve):
            link = Chain(dve, chain_sem)
            link(nc.vector.tensor_copy(keyf[:, :], o.key[:, 0:STEPS]))
            link(nc.vector.memset(o.cont[:, 0:1], 0.0))
            link(nc.vector.tensor_tensor(o.cont[:, 1:STEPS], keyf[:, 1:STEPS], keyf[:, 0:STEPS - 1], ALU.is_equal))
            link(nc.vector.tensor_scalar(o.pen[:, :], o.cont[:, :], -NONE, NONE, ALU.mult, ALU.add))
            link(nc.vector.tensor_scalar(first_run[:, :], keyf[:, :], keyf[:, 0:1], None, ALU.is_equal))
            link(nc.vector.tensor_reduce(head[:, 0:1], first_run[:, :], AX.X, ALU.add))
            link(nc.vector.tensor_scalar(head[:, 1:2], r.partition[0:LANES, :], float(STEPS), -1.0, ALU.mult, ALU.add))
            link(nc.vector.tensor_tensor(o.head_row[:, :], head[:, 0:1], head[:, 1:2], ALU.add))
            dve.wait_ge(key_ends, 64)
            link(nc.vector.tensor_copy(endf[:, :, :], ends[:, :, :]))
            link(nc.vector.tensor_tensor(whole[:, 0, :], endf[:, 0, :], endf[:, 1, :], ALU.is_equal))
            link(nc.vector.tensor_tensor(whole[:, 1, :], endf[:, 0, :], endf[:, 2, :], ALU.is_equal))
            link(nc.vector.memset(whole[:, 1, 0:1], 0.0))
            nc.vector.tensor_tensor(whole[:, 2, :], whole[:, 0, :], whole[:, 1, :], ALU.mult).then_inc(gated, 1)
            dve.wait_ge(spread, 1)
            link(nc.vector.tensor_copy(o.gate[:, :], ps_gate[:, 1, :]))
            link(nc.vector.tensor_copy(o.goes_on[:, :], ps_gate[:, 0, :]))
            link(nc.vector.tensor_scalar(o.goes_on_pen[:, :], o.goes_on[:, :], -NONE, NONE, ALU.mult, ALU.add))
            link(nc.vector.tensor_scalar(o.gate_pen[:, :], o.gate[:, :], -NONE, NONE, ALU.mult, ALU.add))

        @block.tensor
        def _(pe):
            pe.wait_ge(gated, 1)
            nc.tensor.matmul(ps_gate[:, :, :], r.ones[0:1, :], whole[:, 1:3, :], start=True, stop=True).then_inc(spread, 1)


def normalize(nc, r, tag, x):
    with Scope(nc, tag) as s:
        stats = s.sb("stats", [P, NT, 6])
        moments = s.sb("moments", [P, NT, 2])
        std = s.sb("std", [P, NT])
        rstd = s.sb("rstd", [P, NT])
        shift = s.sb("shift", [P, NT])
        chain_sem, added, rooted, shifted = (s.sem(n) for n in ("chain", "added", "rooted", "shifted"))
        ON_ACT = 10
        block = s.block()

        @block.vector
        def _(dve):
            link = Chain(dve, chain_sem)
            for t in range(NT):
                last = nc.vector.bn_stats(stats[:, t, :], x[:, t, :])
            link(last)
            for t in range(NT):
                last = nc.vector.bn_aggr(moments[:, t, :], stats[:, t, :])
            link(last)
            link(nc.vector.tensor_copy(r.var[:, :], moments[:, :, 1]))
            nc.vector.tensor_scalar(std[:, :], r.var[:, :], EPS, None, ALU.add).then_inc(added, 1)
            dve.wait_ge(rooted, 1)
            link(nc.vector.reciprocal(rstd[:, :], std[:, :]))
            nc.vector.scalar_tensor_tensor(shift[:, :], moments[:, :, 0], -1.0, rstd[:, :], ALU.mult, ALU.mult).then_inc(shifted, 1)
            for t in range(ON_ACT, NT):
                nc.vector.tensor_scalar(r.xh[:, t, :], x[:, t, :], moments[:, t, 0:1], rstd[:, t:t + 1], ALU.subtract, ALU.mult)

        @block.scalar
        def _(act):
            act.wait_ge(added, 1)
            nc.scalar.activation(std[:, :], std[:, :], ACT.Sqrt).then_inc(rooted, 1)
            act.wait_ge(shifted, 1)
            for t in range(ON_ACT):
                nc.scalar.activation(r.xh[:, t, :], x[:, t, :], ACT.Identity, bias=shift[:, t:t + 1], scale=rstd[:, t:t + 1])


def ahead(eng, turns, by, first, second, link=None, per=0):
    for i in range(by):
        first(i)
    with eng.Fori(0, turns - by) as i:
        if link is not None:
            link.enter(i, per)
        first(i + by)
        second(i)
        if link is not None:
            link.leave(turns - by)
    for i in range(turns - by, turns):
        second(i)


def tile_of(t3, t):
    return t3[:, bass.ds(t, 1), :].rearrange("p a b -> p (a b)")


def flip_tile(nc, pe, out, xh_tile, eye):
    nc.tensor.transpose(out[:, 0, :], xh_tile[:, 0:P], eye)
    return nc.tensor.transpose(out[:, 1, :], xh_tile[:, P:2 * P], eye)


def stage_tiles(nc, dve, stage, tiles, i, flipped, staged):
    for k in range(2):
        dve.wait_ge(flipped[k], i)
        nc.vector.tensor_scalar(stage[:, k, :], tile_of(tiles, i * 2 + k), 1.0, None, ALU.mult).then_inc(staged[k], 1)


def project_l0(nc, r, w_qkv, gamma, beta, qv, kd, sorted_edges):
    with Scope(nc, "l0p") as s:
        w = s.sb("w", [P, 2, 3 * G])
        gb = s.sb("gb", [P, 2, 2])
        x2 = s.sb("x2", [P, 2, G])
        r2 = s.sb("r2", [P, NT])
        xT = s.sb("xT", [P, 2, 2, P])
        o = s.sb("o", [P, 2, 3 * G])
        flip = [s.ps(f"flip{k}", [P, 2, P]) for k in range(2)]
        ps_qv = [s.ps(f"ps_qv{k}", [P, 2 * G]) for k in range(2)]
        ps_k = [s.ps(f"ps_k{k}", [P, G]) for k in range(2)]
        loaded, chain_sem, added, rooted = s.sem("loaded"), s.sem("chain"), s.sem("added"), s.sem("rooted")
        scaled, flipped, copied = s.sems("scaled", 2), s.sems("flipped", 2), s.sems("copied", 2)
        projected, taken, stored = s.sems("projected", 2), s.sems("taken", 2), s.sems("stored", 2)
        T2 = NT // 2
        sender = Sender(nc, s, r, *BESIDE["l0p"], T2, sorted_edges)
        block = s.block()

        @block.gpsimd
        def _(pool):
            sender.gpsimd(pool)

        @block.sync
        def _(sp):
            sp.dma_start(w[:, :, :], w_qkv.rearrange("(c p) n -> p c n", p=P)).then_inc(loaded, 16)
            sp.dma_start(gb[:, 0, :], gamma.rearrange("(c p) -> p c", p=P), allow_slow_non_contiguous=True).then_inc(loaded, 16)
            sp.dma_start(gb[:, 1, :], beta.rearrange("(c p) -> p c", p=P), allow_slow_non_contiguous=True).then_inc(loaded, 16)
            with sp.Fori(0, T2) as i:
                for k in range(2):
                    row = (i * 2 + k) * P
                    sp.wait_ge(taken[k], i + 1)
                    sp.dma_start(qv[bass.ds(row, P), :], o[:, k, 0:2 * G]).then_inc(stored[k], 16)
                    sp.dma_start(kd[bass.ds(row, P), :], o[:, k, 2 * G:3 * G]).then_inc(stored[k], 16)
            for k in range(2):
                sp.wait_ge(stored[k], 32 * T2)

        @block.vector
        def _(dve):
            link = Chain(dve, chain_sem)
            link(nc.vector.tensor_scalar(r2[:, :], r.var[:, :], EPS, None, ALU.add))
            link(nc.vector.reciprocal(r2[:, :], r2[:, :]))
            link(nc.vector.tensor_tensor(r2[:, :], r.var[:, :], r2[:, :], ALU.mult))
            nc.vector.tensor_scalar(r2[:, :], r2[:, :], EPS, None, ALU.add).then_inc(added, 1)
            dve.wait_ge(rooted, 1)
            link(nc.vector.reciprocal(r2[:, :], r2[:, :]))

            def first(i):
                for k in range(2):
                    dve.wait_ge(flipped[k], i)
                    nc.vector.tensor_scalar(x2[:, k, :], tile_of(r.xh, i * 2 + k), r2[:, bass.ds(i * 2 + k, 1)], None, ALU.mult).then_inc(scaled[k], 1)

            def second(i):
                for k in range(2):
                    sender.vector(dve, i, k)
                    dve.wait_ge(projected[k], i + 1)
                    dve.wait_ge(stored[k], i * 32)
                    nc.vector.tensor_copy(o[:, k, 0:2 * G], ps_qv[k][:, :])
                    nc.vector.tensor_scalar(o[:, k, 2 * G:3 * G], ps_k[k][:, :], float(G) ** -0.5, None, ALU.mult).then_inc(taken[k], 1)

            ahead(dve, T2, 2, first, second)

        @block.scalar
        def _(act):
            act.wait_ge(added, 1)
            nc.scalar.activation(r2[:, :], r2[:, :], ACT.Sqrt).then_inc(rooted, 1)
            act.wait_ge(loaded, 48)
            with act.Fori(0, T2) as i:
                for k in range(2):
                    act.wait_ge(flipped[k], i + 1)
                    act.wait_ge(projected[k], i)
                    nc.scalar.activation(xT[:, k, 0, :], flip[k][:, 0, :], ACT.Identity, bias=gb[:, 1, 0:1], scale=gb[:, 0, 0:1])
                    nc.scalar.activation(xT[:, k, 1, :], flip[k][:, 1, :], ACT.Identity, bias=gb[:, 1, 1:2], scale=gb[:, 0, 1:2]).then_inc(copied[k], 1)

        @block.tensor
        def _(pe):
            pe.wait_ge(loaded, 48)

            def first(i):
                for k in range(2):
                    pe.wait_ge(scaled[k], i + 1)
                    pe.wait_ge(copied[k], i)
                    flip_tile(nc, pe, flip[k], x2[:, k, :], r.eye[:, :]).then_inc(flipped[k], 1)

            def second(i):
                for k in range(2):
                    pe.wait_ge(copied[k], i + 1)
                    pe.wait_ge(taken[k], i)
                    for c in range(2):
                        nc.tensor.matmul(ps_qv[k][:, 0:G], xT[:, k, c, :], w[:, c, 0:G], start=(c == 0), stop=(c == 1))
                    for c in range(2):
                        nc.tensor.matmul(ps_qv[k][:, G:2 * G], xT[:, k, c, :], w[:, c, 2 * G:3 * G], start=(c == 0), stop=(c == 1))
                    for c in range(2):
                        last = nc.tensor.matmul(ps_k[k][:, :], xT[:, k, c, :], w[:, c, G:2 * G], start=(c == 0), stop=(c == 1))
                    last.then_inc(projected[k], 1)

            ahead(pe, T2, 1, first, second)


def lane_gathers(r, pool, tag, gathers, indexed, used, came):
    last_row, turn = pool.to_reg(N - 1), pool.alloc_register(f"{tag}_next_turn")
    with pool.Fori(0, TURNS) as i:
        pool.reg_add(turn, i, 1)
        for k in range(U):
            tables_made(pool, r)
            pool.wait_ge(indexed[k], turn)
            pool.wait_ge(used[k], i)
            for to, table, at in gathers(k):
                pool.indirect_dma_start(to, None, table, bass.IndirectOffsetOnAxis(ap=at, axis=0),
                                        bounds_check=last_row, oob_is_err=False).then_inc(came[k], 16)


def skewed(eng, link, per, first, both, last, turns=TURNS, units=U):
    first()
    with eng.Fori(0, turns - 1) as i:
        if link is not None:
            link.enter(i, per)
        for k in range(units):
            both(i, k)
        if link is not None:
            link.leave(turns - 1)
    for k in range(units - 1):
        both(turns - 1, k)
    last(turns - 1)


def after(i, k, units=U):
    return (i, k + 1) if k < units - 1 else (i + 1, 0)


def wait_for_state_buffer(dve, stored, i, k):
    if k >= 2:
        dve.wait_ge(stored[k - 2], (i + 1) * 16)
    else:
        dve.wait_ge(stored[k - 2 + U], i * 16)


def store_states(sp, out, st, stepped, stored):
    with sp.Fori(0, TURNS) as i:
        for k in range(U):
            sp.wait_ge(stepped[k], i + 1)
            sp.dma_start(out[:, bass.ds((i * U + k) * B, B), :], st[:, k % 2, :, :]).then_inc(stored[k], 16)
    for k in range(U):
        sp.wait_ge(stored[k], 16 * TURNS)


def edges_softmax(nc, r, o, tag, far_table, key_table, heads, states, tail):
    W = heads
    with Scope(nc, tag) as s:
        index = s.sb("index", [LANES, U, 2, B], I32)
        got = s.sb("got", [LANES, U, B, 2 * G])
        keyed = s.sb("keyed", [LANES, U, B, G])
        prod = s.sb("prod", [LANES, B, G]) if heads == H else None
        logit = s.sb("logit", [LANES, 2, B, W])
        grown = s.sb("grown", [LANES, W])
        term = s.sb("term", [LANES, B, W + G])
        scaled = s.sb("scaled", [LANES, W + G])
        st = s.sb("st", [LANES, 2, B, 2 * W + G])
        chain_sem = s.sem("chain")
        indexed, came = s.sems("indexed", U), s.sems("came", U)
        raised, grew, exped, stepped, stored = (s.sems(n, U) for n in ("raised", "grew", "exped", "stepped", "stored"))
        block = s.block()
        out = states[0:E, :].rearrange("(p j) w -> p j w", p=LANES)

        @block.gpsimd
        def _(pool):
            lane_gathers(r, pool, s.tag,
                         lambda k: [(got[:, k, b, :], far_table, index[:, k, 0, b:b + 1]) for b in range(B)]
                         + [(keyed[:, k, b, :], key_table, index[:, k, 1, b:b + 1]) for b in range(B)],
                         indexed, stepped, came)

        @block.vector
        def _(dve):
            link = Chain(dve, chain_sem)

            def m_of(k, b):
                return st[:, k % 2, b, 0:W] if b >= 0 else st[:, (k + 1) % 2, B - 1, 0:W]

            def zu_of(k, b):
                return st[:, k % 2, b, W:] if b >= 0 else st[:, (k + 1) % 2, B - 1, W:]

            def of_heads(ap):
                return ap.rearrange("p b (h d) -> p b h d", d=D)

            def begin(i, k):
                j = (i * U + k) * B
                dve.wait_ge(came[k], (i + 1) * (32 * B))
                nc.vector.tensor_copy(index[:, k, 0, :], o.far[:, bass.ds(j + U * B, B)])
                nc.vector.tensor_copy(index[:, k, 1, :], o.key[:, bass.ds(j + U * B, B)]).then_inc(indexed[k], 1)
                if heads == G:
                    link.mark(nc.vector.tensor_tensor(logit[:, k % 2, :, :], got[:, k, :, 0:G], keyed[:, k, :, :], ALU.mult))
                else:
                    link(nc.vector.tensor_tensor(prod[:, :, :], got[:, k, :, 0:G], keyed[:, k, :, :], ALU.mult))
                    link.mark(nc.vector.tensor_reduce(logit[:, k % 2, :, :], of_heads(prod[:, :, :]), AX.X, ALU.add))

            BEGIN = 1 if heads == G else 2

            def forward(i, k, b):
                pen = o.pen[:, bass.ds((i * U + k) * B + b, 1)]
                link.mark(nc.vector.scalar_tensor_tensor(m_of(k, b), m_of(k, b - 1), pen, logit[:, k % 2, b, :], ALU.add, ALU.max))

            def backward(i, k):
                j = (i * U + k) * B
                link.all_but(0)
                for b in reversed(range(B - 1)):
                    link(nc.vector.scalar_tensor_tensor(m_of(k, b), m_of(k, b + 1), o.pen[:, bass.ds(j + b + 1, 1)], m_of(k, b), ALU.add, ALU.max))
                nc.vector.scalar_tensor_tensor(grown[:, :], m_of(k, -1), o.pen[:, bass.ds(j, 1)], m_of(k, 0), ALU.add, ALU.subtract)
                nc.vector.tensor_tensor(logit[:, k % 2, :, :], logit[:, k % 2, :, :], st[:, k % 2, :, 0:W], ALU.subtract).then_inc(raised[k], 1)

            def weigh(i, k):
                dve.wait_ge(grew[k], i + 1)
                if heads == G:
                    link.mark(nc.vector.tensor_tensor(scaled[:, :].rearrange("p (a f) -> p a f", a=2), zu_of(k, -1).rearrange("p (a f) -> p a f", a=2),
                                                      grown[:, :].unsqueeze(1).broadcast_to([LANES, 2, G]), ALU.mult))
                    dve.wait_ge(exped[k], i + 1)
                    link.mark(nc.vector.tensor_tensor(term[:, :, W:], term[:, :, 0:W], got[:, k, :, G:2 * G], ALU.mult))
                else:
                    nc.vector.tensor_tensor(scaled[:, 0:W], zu_of(k, -1)[:, 0:W], grown[:, :], ALU.mult)
                    link.mark(nc.vector.tensor_tensor(scaled[:, W:].rearrange("p (h d) -> p h d", d=D), zu_of(k, -1)[:, W:].rearrange("p (h d) -> p h d", d=D),
                                                      grown[:, :].unsqueeze(2).broadcast_to([LANES, H, D]), ALU.mult))
                    dve.wait_ge(exped[k], i + 1)
                    link.mark(nc.vector.tensor_tensor(of_heads(term[:, :, W:]), of_heads(got[:, k, :, G:2 * G]),
                                                      term[:, :, 0:W].unsqueeze(3).broadcast_to([LANES, B, H, D]), ALU.mult))

            def step(i, k, b):
                if b == 0:
                    return link.mark(nc.vector.tensor_tensor(zu_of(k, 0), scaled[:, :], term[:, 0, :], ALU.add))
                cont = o.cont[:, bass.ds((i * U + k) * B + b, 1)]
                ins = nc.vector.scalar_tensor_tensor(zu_of(k, b), zu_of(k, b - 1), cont, term[:, b, :], ALU.mult, ALU.add)
                if b < B - 1:
                    link.mark(ins)
                else:
                    ins.then_inc(stepped[k], 1)

            def first():
                link.mark(nc.vector.memset(m_of(0, -1), NONE))
                link.mark(nc.vector.memset(zu_of(0, -1), 0.0))
                for k in range(U):
                    nc.vector.tensor_copy(index[:, k, 0, :], o.far[:, k * B:(k + 1) * B])
                    nc.vector.tensor_copy(index[:, k, 1, :], o.key[:, k * B:(k + 1) * B]).then_inc(indexed[k], 1)
                begin(0, 0)
                for b in range(B):
                    link.all_but(0)
                    forward(0, 0, b)
                backward(0, 0)

            def both(i, k):
                new = after(i, k)
                begin(*new)
                weigh(i, k)
                wait_for_state_buffer(dve, stored, *new)
                for b in range(B):
                    link.all_but(1 if b else 0)
                    forward(*new, b)
                    link.all_but(1)
                    step(i, k, b)
                dve.wait_ge(stepped[k], i + 1)
                backward(*new)

            def last(i):
                weigh(i, U - 1)
                for b in range(B):
                    link.all_but(0)
                    step(i, U - 1, b)
                dve.wait_ge(stepped[U - 1], i + 1)

            skewed(dve, link, U * (BEGIN + 2 + B + (B - 1) + (B - 1)), first, both, last)
            if heads == G:
                nc.vector.tensor_copy(tail[:, :], st[:, 1, B - 1, :])
            else:
                for n in range(2):
                    nc.vector.tensor_copy(tail[:, n * G:(n + 1) * G].rearrange("p (h d) -> p h d", d=D),
                                          st[:, 1, B - 1, n * H:(n + 1) * H].unsqueeze(2).broadcast_to([LANES, H, D]))
                nc.vector.tensor_copy(tail[:, 2 * G:3 * G], st[:, 1, B - 1, 2 * H:])

        @block.scalar
        def _(act):
            with act.Fori(0, TURNS) as i:
                for k in range(U):
                    act.wait_ge(raised[k], i + 1)
                    nc.scalar.activation(grown[:, :], grown[:, :], ACT.Exp).then_inc(grew[k], 1)
                    nc.scalar.activation(term[:, :, 0:W], logit[:, k % 2, :, :], ACT.Exp).then_inc(exped[k], 1)

        @block.sync
        def _(sp):
            store_states(sp, out, st, stepped, stored)


def carry_softmax(nc, r, o, tag, tail, states, heads):
    W, SW = heads, states.shape[1]
    with Scope(nc, tag) as s:
        t = s.sb("t", [P, 2, 3, LANES])
        m = s.sb("m", [P, 2, LANES + 1])
        a = s.sb("a", [P, 2, LANES])
        c = s.sb("c", [P, 2, 3, LANES + 1])
        came_in = s.sb("came_in", [LANES, 3, 2, P])
        head = s.sb("head", [LANES, SW])
        joined = s.sb("joined", [LANES, SW])
        top = s.sb("top", [LANES, G])
        fac = s.sb("fac", [LANES, 2, G])
        t1 = s.sb("t1", [LANES, G])
        t2 = s.sb("t2", [LANES, G])
        empty = s.sb("empty", [1, SW])
        flip = [s.ps(f"flip{h}", [P, 3, P]) for h in range(2)]
        back = [s.ps(f"back{h}", [LANES, 3, P]) for h in range(2)]
        chain_sem, flipped, raised, exped, scanned, returned, topped, scaled, done, fetched, stored, patched = (
            s.sem(n) for n in ("chain", "flipped", "raised", "exped", "scanned", "returned", "topped", "scaled", "done", "fetched", "stored", "patched"))
        block = s.block()

        @block.tensor
        def _(pe):
            for h in range(2):
                for n in range(3):
                    last = nc.tensor.transpose(flip[h][:, n, 0:LANES], tail[:, n * G + h * P:n * G + (h + 1) * P], r.eye[0:LANES, 0:LANES])
            last.then_inc(flipped, 1)
            pe.wait_ge(scanned, 1)
            for h in range(2):
                for n in range(3):
                    last = nc.tensor.transpose(back[h][:, n, :], c[:, h, n, 0:LANES], r.eye[:, :])
            last.then_inc(returned, 1)

        def three(ap):
            return ap.rearrange("p (h d) -> p h d", d=D)

        def own(n):
            if n == 2:
                return three(head[:, 2 * W:])
            if heads == G:
                return three(head[:, n * G:(n + 1) * G])
            return head[:, n * H:(n + 1) * H].unsqueeze(2).broadcast_to([LANES, H, D])

        def carried(n):
            return three(came_in[:, n, :, :].rearrange("p h f -> p (h f)"))

        @block.vector
        def _(dve):
            link = Chain(dve, chain_sem)
            link(nc.vector.memset(empty[:, 0:W], NONE))
            link(nc.vector.memset(empty[:, W:], 0.0))
            link(nc.vector.memset(c[:, :, :, 0:1], 0.0))
            dve.wait_ge(flipped, 1)
            for h in range(2):
                link(nc.vector.tensor_copy(t[:, h, :, :], flip[h][:, :, 0:LANES]))
                link(nc.vector.memset(m[:, h, 0:1], 0.0))
                link(nc.vector.tensor_tensor_scan(m[:, h, 1:], o.gate_pen[:, :], t[:, h, 0, :], NONE, ALU.add, ALU.max))
                link(nc.vector.tensor_tensor(c[:, h, 0, 0:LANES], m[:, h, 0:LANES], o.goes_on_pen[:, :], ALU.add))
                link(nc.vector.tensor_tensor(a[:, h, :], m[:, h, 0:LANES], o.gate_pen[:, :], ALU.add))
                link(nc.vector.tensor_tensor(a[:, h, :], a[:, h, :], m[:, h, 1:], ALU.subtract))
                link(nc.vector.tensor_tensor(t[:, h, 0, :], t[:, h, 0, :], m[:, h, 1:], ALU.subtract))
            link(nc.vector.memset(m[:, 0, 0:1], 0.0))
            nc.vector.memset(m[:, 0, 0:1], 0.0).then_inc(raised, 1)
            dve.wait_ge(exped, 1)
            for h in range(2):
                for n in (1, 2):
                    link(nc.vector.tensor_tensor(t[:, h, n, :], t[:, h, n, :], t[:, h, 0, :], ALU.mult))
                    link(nc.vector.tensor_tensor_scan(c[:, h, n, 1:], a[:, h, :], t[:, h, n, :], 0.0, ALU.mult, ALU.add))
            nc.vector.memset(m[:, 0, 0:1], 0.0).then_inc(scanned, 1)
            dve.wait_ge(returned, 1)
            for h in range(2):
                link(nc.vector.tensor_copy(came_in[:, :, h, :], back[h][:, :, :]))
            dve.wait_ge(fetched, 16)
            link(nc.vector.tensor_tensor(three(top[:, :]), own(0), carried(0), ALU.max))
            link(nc.vector.tensor_tensor(three(fac[:, 0, :]), own(0), three(top[:, :]), ALU.subtract))
            nc.vector.tensor_tensor(three(fac[:, 1, :]), carried(0), three(top[:, :]), ALU.subtract).then_inc(topped, 1)
            dve.wait_ge(scaled, 1)
            for n in (1, 2):
                link(nc.vector.tensor_tensor(three(t1[:, :]), own(n), three(fac[:, 0, :]), ALU.mult))
                link(nc.vector.tensor_tensor(three(t2[:, :]), carried(n), three(fac[:, 1, :]), ALU.mult))
                link(nc.vector.tensor_tensor(t1[:, :], t1[:, :], t2[:, :], ALU.add))
                if n == 1 and heads == H:
                    link(nc.vector.tensor_copy(joined[:, W:2 * W], three(t1[:, :])[:, :, 0]))
                else:
                    link(nc.vector.tensor_copy(joined[:, n * W:n * W + G], t1[:, :]))
            nc.vector.tensor_copy(joined[:, 0:W], three(top[:, :])[:, :, 0] if heads == H else top[:, :]).then_inc(done, 1)

        @block.scalar
        def _(act):
            act.wait_ge(raised, 1)
            nc.scalar.activation(a[:, :, :], a[:, :, :], ACT.Exp)
            nc.scalar.activation(t[:, :, 0, :], t[:, :, 0, :], ACT.Exp).then_inc(exped, 1)
            act.wait_ge(topped, 1)
            nc.scalar.activation(fac[:, :, :], fac[:, :, :], ACT.Exp).then_inc(scaled, 1)

        @block.gpsimd
        def _(pool):
            join_heads(pool, o, states, head, joined, fetched, done, patched)

        @block.sync
        def _(sp):
            sp.wait_ge(done, 1)
            sp.dma_start(states[E:E + 1, :], empty[:, :]).then_inc(stored, 16)
            sp.wait_ge(stored, 16)


def join_heads(pool, o, states, head, joined, fetched, done, patched):
    at = bass.IndirectOffsetOnAxis(ap=o.head_row[:, 0:1], axis=0)
    pool.indirect_dma_start(head[:, :], None, states[0:E, :], at, bounds_check=E - 1, oob_is_err=False).then_inc(fetched, 16)
    pool.wait_ge(done, 1)
    pool.indirect_dma_start(states[0:E, :], at, joined[:, :], None, bounds_check=E - 1, oob_is_err=False).then_inc(patched, 16)
    pool.wait_ge(patched, 16)


def carry_sum(nc, r, o, tag, tail, states):
    with Scope(nc, tag) as s:
        t = s.sb("t", [P, 2, LANES])
        c = s.sb("c", [P, 2, LANES + 1])
        came_in = s.sb("came_in", [LANES, 2, P])
        head = s.sb("head", [LANES, G])
        joined = s.sb("joined", [LANES, G])
        empty = s.sb("empty", [1, G])
        flip = s.ps("flip", [P, 2, P])
        back = s.ps("back", [LANES, 2, P])
        chain_sem, flipped, scanned, returned, done, fetched, stored, patched = (
            s.sem(n) for n in ("chain", "flipped", "scanned", "returned", "done", "fetched", "stored", "patched"))
        block = s.block()

        @block.tensor
        def _(pe):
            for h in range(2):
                last = nc.tensor.transpose(flip[:, h, 0:LANES], tail[:, h * P:(h + 1) * P], r.eye[0:LANES, 0:LANES])
            last.then_inc(flipped, 1)
            pe.wait_ge(scanned, 1)
            for h in range(2):
                last = nc.tensor.transpose(back[:, h, :], c[:, h, 0:LANES], r.eye[:, :])
            last.then_inc(returned, 1)

        @block.vector
        def _(dve):
            link = Chain(dve, chain_sem)
            link(nc.vector.memset(empty[:, :], 0.0))
            link(nc.vector.memset(c[:, :, 0:1], 0.0))
            dve.wait_ge(flipped, 1)
            link(nc.vector.tensor_copy(t[:, :, :], flip[:, :, 0:LANES]))
            for h in range(2):
                link(nc.vector.tensor_tensor_scan(c[:, h, 1:], o.gate[:, :], t[:, h, :], 0.0, ALU.mult, ALU.add))
            nc.vector.tensor_tensor(c[:, :, 0:LANES], c[:, :, 0:LANES], o.goes_on[:, :].unsqueeze(1).broadcast_to([P, 2, LANES]), ALU.mult).then_inc(scanned, 1)
            dve.wait_ge(returned, 1)
            link(nc.vector.tensor_copy(came_in[:, :, :], back[:, :, :]))
            dve.wait_ge(fetched, 16)
            nc.vector.tensor_tensor(joined[:, :], head[:, :], came_in[:, :, :].rearrange("p h f -> p (h f)"), ALU.add).then_inc(done, 1)

        @block.gpsimd
        def _(pool):
            join_heads(pool, o, states, head, joined, fetched, done, patched)

        @block.sync
        def _(sp):
            sp.wait_ge(done, 1)
            sp.dma_start(states[E:E + 1, :], empty[:, :]).then_inc(stored, 16)
            sp.wait_ge(stored, 16)


def finish(nc, r, o, tag, states, kind, out):
    FB = 6
    FT = NT // FB
    with Scope(nc, tag) as s:
        SW = states.shape[1]
        index = s.sb("index", [P, FB], I32)
        mine = s.sb("mine", [P, FB, SW])
        share = s.sb("share", [P, NT])
        z = s.sb("z", [P, FB, G])
        chain_sem = s.sem("chain")
        indexed, came, used = (s.sems(n, FB) for n in ("indexed", "came", "used"))
        block = s.block()

        @block.gpsimd
        def _(pool):
            last_state, turn = pool.to_reg(E), pool.alloc_register(f"{s.tag}_next_turn")
            with pool.Fori(0, FT) as i:
                pool.reg_add(turn, i, 1)
                for k in range(FB):
                    tables_made(pool, r)
                    pool.wait_ge(indexed[k], turn)
                    pool.wait_ge(used[k], i)
                    pool.indirect_dma_start(mine[:, k, :], None, states, bass.IndirectOffsetOnAxis(ap=index[:, k:k + 1], axis=0),
                                            bounds_check=last_state, oob_is_err=False).then_inc(came[k], 16)

        def u(k):
            return mine[:, k, SW - G:]

        @block.vector
        def _(dve):
            link = Chain(dve, chain_sem)
            for k in range(FB):
                nc.vector.tensor_copy(index[:, k:k + 1], o.end_row[:, k:k + 1]).then_inc(indexed[k], 1)
            link(nc.vector.tensor_scalar(share[:, :], o.count[:, :], 1.0, None, ALU.max))
            link(nc.vector.reciprocal(share[:, :], share[:, :]))
            with dve.Fori(0, FT) as i:
                link.enter(i, {"softmax": 3, "softmax of heads": 2}.get(kind, 0) * FB)
                for k in range(FB):
                    t = i * FB + k
                    dve.wait_ge(came[k], (i + 1) * 16)
                    nc.vector.tensor_copy(index[:, k:k + 1], o.end_row[:, bass.ds(t + FB, 1)]).then_inc(indexed[k], 1)
                    x = tile_of(out, t)
                    if kind in ("sum", "mean"):
                        by = share[:, bass.ds(t, 1)] if kind == "mean" else 1.0
                        nc.vector.scalar_tensor_tensor(x, u(k), by, x, ALU.mult, ALU.add).then_inc(used[k], 1)
                        continue
                    W = G if kind == "softmax" else H
                    zk, zrow = z[:, k, 0:W], mine[:, k, W:2 * W]
                    link(nc.vector.scalar_tensor_tensor(zk, zrow, 0.0, zrow, ALU.is_equal, ALU.add))
                    link(nc.vector.reciprocal(zk, zk))
                    if kind == "softmax":
                        link(nc.vector.tensor_tensor(zk, u(k), zk, ALU.mult))
                        nc.vector.tensor_tensor(x, x, zk, ALU.add).then_inc(used[k], 1)
                    else:
                        nc.vector.tensor_tensor(x.rearrange("p (h d) -> p h d", d=D), u(k).rearrange("p (h d) -> p h d", d=D),
                                                zk.unsqueeze(2).broadcast_to([P, H, D]), ALU.mult).then_inc(used[k], 1)
                link.leave(FT)


def edges_sum(nc, r, o, tag, table, states, tail, edge_rows=None):
    with Scope(nc, tag) as s:
        index = s.sb("index", [LANES, U, B], I32)
        got = s.sb("got", [LANES, U, B, G])
        own = rows = None
        if edge_rows is not None:
            own = s.sb("own", [LANES, U, B, G])
            rows = edge_rows.rearrange("(p j) w -> p j w", p=LANES)
        st = s.sb("st", [LANES, 2, B, G])
        chain_sem = s.sem("chain")
        names = ("indexed", "came", "owned", "added", "cut", "stepped", "stored")
        indexed, came, owned, added, cut, stepped, stored = (s.sems(n, U) for n in names)
        block = s.block()
        out = states[0:E, :].rearrange("(p j) w -> p j w", p=LANES)

        @block.gpsimd
        def _(pool):
            lane_gathers(r, pool, s.tag, lambda k: [(got[:, k, b, :], table, index[:, k, b:b + 1]) for b in range(B)],
                         indexed, stepped, came)

        @block.vector
        def _(dve):
            link = Chain(dve, chain_sem)

            def begin(i, k):
                j = (i * U + k) * B
                dve.wait_ge(came[k], (i + 1) * (16 * B))
                nc.vector.tensor_copy(index[:, k, :], o.far[:, bass.ds(j + U * B, B)]).then_inc(indexed[k], 1)
                if own is not None:
                    dve.wait_ge(owned[k], (i + 1) * 16)
                    nc.vector.tensor_tensor(got[:, k, :, :], got[:, k, :, :], own[:, k, :, :], ALU.add).then_inc(added[k], 1)

            def steps(i, k):
                j = (i * U + k) * B
                if own is not None:
                    dve.wait_ge(cut[k], i + 1)
                wait_for_state_buffer(dve, stored, i, k)
                for b in range(B):
                    before = st[:, k % 2, b - 1, :] if b else st[:, 1 - k % 2, B - 1, :]
                    ins = nc.vector.scalar_tensor_tensor(st[:, k % 2, b, :], before, o.cont[:, bass.ds(j + b, 1)], got[:, k, b, :], ALU.mult, ALU.add)
                    if b < B - 1:
                        link(ins)
                ins.then_inc(stepped[k], 1)
                dve.wait_ge(stepped[k], i + 1)

            def first():
                link(nc.vector.memset(st[:, 1, B - 1, :], 0.0))
                for k in range(U):
                    nc.vector.tensor_copy(index[:, k, :], o.far[:, k * B:(k + 1) * B]).then_inc(indexed[k], 1)
                begin(0, 0)

            def both(i, k):
                begin(*after(i, k))
                steps(i, k)

            skewed(dve, link, U * (B - 1), first, both, lambda i: steps(i, U - 1))
            nc.vector.tensor_copy(tail[:, 0:G], st[:, 1, B - 1, :])

        @block.scalar
        def _(act):
            if own is not None:
                def cut_batch(i, k):
                    act.wait_ge(added[k], i + 1)
                    nc.scalar.activation(got[:, k, :, :], got[:, k, :, :], ACT.Relu).then_inc(cut[k], 1)

                with act.Fori(0, TURNS - 1) as i:
                    for k in range(U):
                        cut_batch(i, k)
                        act.dma_start(own[:, k, :, :], rows[:, bass.ds(((i + 1) * U + k) * B, B), :]).then_inc(owned[k], 16)
                for k in range(U):
                    cut_batch(TURNS - 1, k)

        @block.sync
        def _(sp):
            if own is not None:
                for k in range(U):
                    sp.dma_start(own[:, k, :, :], rows[:, k * B:(k + 1) * B, :]).then_inc(owned[k], 16)
            store_states(sp, out, st, stepped, stored)


def project_l1(nc, r, w_self, w_neigh, table, sorted_edges):
    MAXK = 32
    with Scope(nc, "l1p") as s:
        w = s.sb("w", [P, 2, 2 * G])
        xT = s.sb("xT", [P, 2, 2, P])
        h = s.sb("h", [P, 2, G])
        left = s.sb("left", [P, 2, G])
        top = s.sb("top", [P, 2, 8])
        beat = s.sb("beat", [1, 1])
        o = s.sb("o", [P, 2, G])
        stage = s.sb("stage", [P, 2, G])
        staged = s.sems("staged", 2)
        flip = [s.ps(f"flip{k}", [P, 2, P]) for k in range(2)]
        ps = [s.ps(f"ps{k}", [P, 2 * G]) for k in range(2)]
        loaded, chain_sem = s.sem("loaded"), s.sem("chain")
        flipped, copied, projected, taken, chosen, stored = (
            s.sems(n, 2) for n in ("flipped", "copied", "projected", "taken", "chosen", "stored"))
        T2 = NT // 2
        sender = Sender(nc, s, r, *BESIDE["l1p"], T2, sorted_edges)
        block = s.block()

        @block.gpsimd
        def _(pool):
            sender.gpsimd(pool)

        @block.sync
        def _(sp):
            sp.dma_start(w[:, :, 0:G], w_self.rearrange("(c p) n -> p c n", p=P)).then_inc(loaded, 16)
            sp.dma_start(w[:, :, G:2 * G], w_neigh.rearrange("(c p) n -> p c n", p=P)).then_inc(loaded, 16)
            with sp.Fori(0, T2) as i:
                for k in range(2):
                    sp.wait_ge(chosen[k], i + 1)
                    sp.dma_start(table[bass.ds((i * 2 + k) * P, P), :], o[:, k, :]).then_inc(stored[k], 16)
            for k in range(2):
                sp.wait_ge(stored[k], 16 * T2)

        @block.vector
        def _(dve):
            link = Chain(dve, chain_sem)

            def first(i):
                stage_tiles(nc, dve, stage, r.xh, i, flipped, staged)

            def second(i):
                for k in range(2):
                    t = i * 2 + k
                    sender.vector(dve, i, k)
                    dve.wait_ge(projected[k], i + 1)
                    dve.wait_ge(chosen[k], i)
                    nc.vector.tensor_tensor(tile_of(r.x, t), tile_of(r.x, t), ps[k][:, 0:G], ALU.add)
                    nc.vector.tensor_copy(h[:, k, :], ps[k][:, G:2 * G]).then_inc(taken[k], 1)
                for k in range(2):
                    dve.wait_ge(taken[k], i + 1)
                for n in range(MAXK // 8):
                    nc.vector.memset(beat[:, :], 0.0)
                    for k in range(2):
                        last = nc.vector.max(top[:, k, :], (left if n else h)[:, k, :])
                    link(last)
                    nc.vector.memset(beat[:, :], 0.0)
                    for k in range(2):
                        last = nc.vector.match_replace(left[:, k, :], top[:, k, :], (left if n else h)[:, k, :], NONE)
                    link(last)
                for k in range(2):
                    dve.wait_ge(stored[k], i * 16)
                    nc.vector.scalar_tensor_tensor(o[:, k, :], left[:, k, :], NONE / 2, h[:, k, :], ALU.is_le, ALU.mult).then_inc(chosen[k], 1)

            ahead(dve, T2, 1, first, second, link, 2 * (MAXK // 8))

        @block.scalar
        def _(act):
            with act.Fori(0, T2) as i:
                for k in range(2):
                    act.wait_ge(flipped[k], i + 1)
                    act.wait_ge(projected[k], i)
                    nc.scalar.activation(xT[:, k, :, :], flip[k][:, :, :], ACT.Copy).then_inc(copied[k], 1)

        @block.tensor
        def _(pe):
            pe.wait_ge(loaded, 32)

            with pe.Fori(0, T2) as i:
                for k in range(2):
                    pe.wait_ge(staged[k], i + 1)
                    pe.wait_ge(copied[k], i)
                    flip_tile(nc, pe, flip[k], stage[:, k, :], r.eye[:, :]).then_inc(flipped[k], 1)
                for k in range(2):
                    pe.wait_ge(copied[k], i + 1)
                    pe.wait_ge(taken[k], i)
                    for c in range(2):
                        last = nc.tensor.matmul(ps[k][:, :], xT[:, k, c, :], w[:, c, :], start=(c == 0), stop=(c == 1))
                    last.then_inc(projected[k], 1)


def project_l2(nc, r, ws, biases, qd, kv):
    with Scope(nc, "l2p") as s:
        w = s.sb("w", [P, 2, 3 * G])
        rows = s.sb("rows", [P, 3 * G])
        xT = s.sb("xT", [P, 2, 2, P])
        o = s.sb("o", [P, 2, 3 * G])
        stage = s.sb("stage", [P, 2, G])
        staged = s.sems("staged", 2)
        flip = [s.ps(f"flip{k}", [P, 2, P]) for k in range(2)]
        ps_kv = [s.ps(f"ps_kv{k}", [P, 2 * G]) for k in range(2)]
        ps_q = [s.ps(f"ps_q{k}", [P, G]) for k in range(2)]
        loaded, chain_sem = s.sem("loaded"), s.sem("chain")
        flipped, copied, projected, taken, stored = (
            s.sems(n, 2) for n in ("flipped", "copied", "projected", "taken", "stored"))
        block = s.block()
        T2 = NT // 2

        @block.sync
        def _(sp):
            for n in range(3):
                sp.dma_start(w[:, :, n * G:(n + 1) * G], ws[n].rearrange("(c p) n -> p c n", p=P)).then_inc(loaded, 16)
                sp.dma_start(rows[:, n * G:(n + 1) * G], biases[n].unsqueeze(0).broadcast_to([P, G])).then_inc(loaded, 16)
            with sp.Fori(0, T2) as i:
                for k in range(2):
                    sp.wait_ge(taken[k], i + 1)
                    sp.dma_start(kv[bass.ds((i * 2 + k) * P, P), :], o[:, k, 0:2 * G]).then_inc(stored[k], 16)
                    sp.dma_start(qd[bass.ds((i * 2 + k) * P, P), :], o[:, k, 2 * G:3 * G]).then_inc(stored[k], 16)
            for k in range(2):
                sp.wait_ge(stored[k], 32 * T2)

        @block.vector
        def _(dve):
            link = Chain(dve, chain_sem)
            dve.wait_ge(loaded, 96)
            link(nc.vector.tensor_scalar(rows[:, 2 * G:3 * G], rows[:, 2 * G:3 * G], float(D) ** -0.5, None, ALU.mult))

            def first(i):
                stage_tiles(nc, dve, stage, r.xh, i, flipped, staged)

            def second(i):
                for k in range(2):
                    dve.wait_ge(projected[k], i + 1)
                    dve.wait_ge(stored[k], i * 32)
                    nc.vector.tensor_tensor(o[:, k, 0:2 * G], ps_kv[k][:, :], rows[:, 0:2 * G], ALU.add)
                    nc.vector.scalar_tensor_tensor(o[:, k, 2 * G:3 * G], ps_q[k][:, :], float(D) ** -0.5, rows[:, 2 * G:3 * G],
                                                   ALU.mult, ALU.add).then_inc(taken[k], 1)

            ahead(dve, T2, 2, first, second)

        @block.scalar
        def _(act):
            with act.Fori(0, T2) as i:
                for k in range(2):
                    act.wait_ge(flipped[k], i + 1)
                    act.wait_ge(projected[k], i)
                    nc.scalar.activation(xT[:, k, :, :], flip[k][:, :, :], ACT.Copy).then_inc(copied[k], 1)

        @block.tensor
        def _(pe):
            pe.wait_ge(loaded, 96)

            def first(i):
                for k in range(2):
                    pe.wait_ge(staged[k], i + 1)
                    pe.wait_ge(copied[k], i)
                    flip_tile(nc, pe, flip[k], stage[:, k, :], r.eye[:, :]).then_inc(flipped[k], 1)

            def second(i):
                for k in range(2):
                    pe.wait_ge(copied[k], i + 1)
                    pe.wait_ge(taken[k], i)
                    for c in range(2):
                        nc.tensor.matmul(ps_kv[k][:, :], xT[:, k, c, :], w[:, c, 0:2 * G], start=(c == 0), stop=(c == 1))
                    for c in range(2):
                        last = nc.tensor.matmul(ps_q[k][:, :], xT[:, k, c, :], w[:, c, 2 * G:3 * G], start=(c == 0), stop=(c == 1))
                    last.then_inc(projected[k], 1)

            ahead(pe, T2, 1, first, second)


def project_out(nc, r, agg, w_out, bias):
    with Scope(nc, "l2o") as s:
        w = s.sb("w", [P, 2, G])
        row = s.sb("row", [P, G])
        xT = s.sb("xT", [P, 2, 2, P])
        stage = s.sb("stage", [P, 2, G])
        staged = s.sems("staged", 2)
        flip = [s.ps(f"flip{k}", [P, 2, P]) for k in range(2)]
        ps = [s.ps(f"ps{k}", [P, G]) for k in range(2)]
        loaded, biased = s.sem("loaded"), s.sem("biased")
        flipped, copied, projected, taken = (s.sems(n, 2) for n in ("flipped", "copied", "projected", "taken"))
        block = s.block()
        T2 = NT // 2

        @block.sync
        def _(sp):
            sp.dma_start(w[:, :, :], w_out.rearrange("(c p) n -> p c n", p=P)).then_inc(loaded, 16)
            sp.dma_start(row[:, :], bias.unsqueeze(0).broadcast_to([P, G])).then_inc(loaded, 16)

        @block.vector
        def _(dve):
            dve.wait_ge(loaded, 32)
            nc.vector.tensor_tensor(r.x[:, :, :], r.x[:, :, :], row[:, :].unsqueeze(1).broadcast_to([P, NT, G]), ALU.add).then_inc(biased, 1)
            dve.wait_ge(biased, 1)

            def first(i):
                stage_tiles(nc, dve, stage, agg, i, flipped, staged)

            def second(i):
                for k in range(2):
                    dve.wait_ge(projected[k], i + 1)
                    nc.vector.tensor_tensor(tile_of(r.x, i * 2 + k), tile_of(r.x, i * 2 + k), ps[k][:, :], ALU.add).then_inc(taken[k], 1)

            ahead(dve, T2, 2, first, second)

        @block.scalar
        def _(act):
            with act.Fori(0, T2) as i:
                for k in range(2):
                    act.wait_ge(flipped[k], i + 1)
                    act.wait_ge(projected[k], i)
                    nc.scalar.activation(xT[:, k, :, :], flip[k][:, :, :], ACT.Copy).then_inc(copied[k], 1)

        @block.tensor
        def _(pe):
            pe.wait_ge(loaded, 32)

            def first(i):
                for k in range(2):
                    pe.wait_ge(staged[k], i + 1)
                    pe.wait_ge(copied[k], i)
                    flip_tile(nc, pe, flip[k], stage[:, k, :], r.eye[:, :]).then_inc(flipped[k], 1)

            def second(i):
                for k in range(2):
                    pe.wait_ge(copied[k], i + 1)
                    pe.wait_ge(taken[k], i)
                    for c in range(2):
                        last = nc.tensor.matmul(ps[k][:, :], xT[:, k, c, :], w[:, c, :], start=(c == 0), stop=(c == 1))
                    last.then_inc(projected[k], 1)

            ahead(pe, T2, 1, first, second)

def route(nc, r, tag, w_gate, bias, experts, kind, d=None, sorted_edges=None, prefetch=None):
    with Scope(nc, tag) as s:
        w = s.sb("w", [P, 2, experts])
        row = s.sb("row", [1, experts])
        xs = s.sb("xs", [P, 2, 2, P])
        score = s.sb("score", [P, NT, 8])
        worst = s.sb("worst", [P, NT])
        top = s.sb("top", [P, NT, 8])
        which = s.sb("which", [P, NT, 8], mybir.dt.uint32)
        whichf = s.sb("whichf", [P, NT, 2])
        wt = s.sb("wt", [P, NT, 2])
        t1 = s.sb("t1", [P, NT])
        other_gate = s.sb("other_gate", [P, NT, 8])
        stage = s.sb("stage", [P, 2, G])
        staged = s.sems("staged", 2)
        flip = [s.ps(f"flip{k}", [P, 2, P]) for k in range(2)]
        ps = s.ps("ps", [P, NT, experts])
        loaded, chain_sem, shifted, exped, differed, weighed = (s.sem(n) for n in ("loaded", "chain", "shifted", "exped", "differed", "weighed"))
        flipped, copied, kept, scored = (s.sems(n, 2) for n in ("flipped", "copied", "kept", "scored"))
        block = s.block()
        T2 = NT // 2
        sender = Sender(nc, s, r, *BESIDE[tag], T2, sorted_edges) if sorted_edges is not None else None

        @block.gpsimd
        def _(pool):
            if sender is not None:
                sender.gpsimd(pool)

        def col(ap, n=None):
            return ap.unsqueeze(2).broadcast_to([P, NT, n or 8])

        @block.sync
        def _(sp):
            if w_gate is not None:
                for c in range(2):
                    sp.dma_start(w[:, c, :], w_gate[c * P:(c + 1) * P, :], allow_slow_non_contiguous=True).then_inc(loaded, 16)
            if bias is not None:
                sp.dma_start(row[:, :], bias.unsqueeze(0)).then_inc(loaded, 16)
            if prefetch is not None:
                prefetch(sp)

        @block.tensor
        def _(pe):
            if w_gate is not None:
                pe.wait_ge(loaded, 32 if bias is None else 48)

            def first(i):
                for k in range(2):
                    pe.wait_ge(staged[k], i + 1)
                    pe.wait_ge(copied[k], i)
                    flip_tile(nc, pe, flip[k], stage[:, k, :], r.eye[:, :]).then_inc(flipped[k], 1)

            def second(i):
                for k in range(2 if w_gate is not None else 0):
                    score_of = ps[:, bass.ds(i * 2 + k, 1), :].rearrange("p a e -> p (a e)")
                    pe.wait_ge(copied[k], i + 1)
                    if bias is not None:
                        nc.tensor.matmul(score_of, r.ones[0:1, :], row[:, :], start=True, stop=False)
                    for c in range(2):
                        last = nc.tensor.matmul(score_of, xs[:, k, c, :], w[:, c, :], start=(bias is None and c == 0), stop=(c == 1))
                    last.then_inc(scored[k], 1)

            ahead(pe, T2, 1, first, second)

        @block.scalar
        def _(act):
            with act.Fori(0, T2) as i:
                for k in range(2):
                    act.wait_ge(flipped[k], i + 1)
                    if w_gate is not None:
                        act.wait_ge(scored[k], i)
                    if d is None:
                        act.wait_ge(kept[k], i)
                    nc.scalar.activation(xs[:, k, :, :], flip[k][:, :, :], ACT.Copy).then_inc(copied[k], 1)
            if kind in ("softmax of two", "share"):
                act.wait_ge(shifted, 1)
                nc.scalar.activation(score[:, :, :], score[:, :, :], ACT.Exp).then_inc(exped, 1)
            if kind == "softmax of two":
                act.wait_ge(differed, 1)
                nc.scalar.activation(t1[:, :], t1[:, :], ACT.Exp).then_inc(weighed, 1)

        @block.vector
        def _(dve):
            link = Chain(dve, chain_sem)
            link(nc.vector.memset(score[:, :, :], NONE))

            def first(i):
                stage_tiles(nc, dve, stage, r.xh, i, flipped, staged)

            def second(i):
                for k in range(2 if sender is not None else 0):
                    sender.vector(dve, i, k)
                for k in range(2 if d is None else 0):
                    dve.wait_ge(copied[k], i + 1)
                    nc.vector.tensor_copy(r.xT[:, :, bass.ds((i * 2 + k) * P, P)], xs[:, k, :, :]).then_inc(kept[k], 1)

            ahead(dve, T2, 1, first, second)
            if w_gate is None:
                return
            for k in range(2):
                dve.wait_ge(scored[k], T2)
            link(nc.vector.tensor_copy(score[:, :, 0:experts], ps[:, :, :]))
            if kind != "ones":
                link(nc.vector.tensor_reduce(worst[:, :], score[:, :, :], AX.X, ALU.max))
                nc.vector.tensor_tensor(score[:, :, :], score[:, :, :], col(worst[:, :]), ALU.subtract).then_inc(shifted, 1)
                dve.wait_ge(exped, 1)
                link(nc.vector.tensor_reduce(worst[:, :], score[:, :, :], AX.X, ALU.add))
                link(nc.vector.reciprocal(worst[:, :], worst[:, :]))
                link(nc.vector.tensor_tensor(score[:, :, :], score[:, :, :], col(worst[:, :]), ALU.mult))
            for t in range(NT):
                last = nc.vector.max(top[:, t, :], score[:, t, :])
            link(last)
            for t in range(NT):
                last = nc.vector.max_index(which[:, t, :], top[:, t, :], score[:, t, :])
            link(last)
            link(nc.vector.tensor_copy(whichf[:, :, :], which[:, :, 0:2]))
            if kind == "ones":
                link(nc.vector.memset(wt[:, :, :], 1.0))
            elif kind == "softmax of two":
                nc.vector.tensor_tensor(t1[:, :], top[:, :, 1], top[:, :, 0], ALU.subtract).then_inc(differed, 1)
                dve.wait_ge(weighed, 1)
                link(nc.vector.tensor_scalar(wt[:, :, 0], t1[:, :], 1.0, None, ALU.add))
                link(nc.vector.reciprocal(wt[:, :, 0], wt[:, :, 0]))
                link(nc.vector.tensor_tensor(wt[:, :, 1], wt[:, :, 0], t1[:, :], ALU.mult))
            else:
                link(nc.vector.tensor_tensor(t1[:, :], top[:, :, 0], top[:, :, 1], ALU.add))
                link(nc.vector.tensor_scalar(t1[:, :], t1[:, :], 1e-12, None, ALU.max))
                link(nc.vector.reciprocal(t1[:, :], t1[:, :]))
                link(nc.vector.tensor_tensor(wt[:, :, :], top[:, :, 0:2], col(t1[:, :], 2), ALU.mult))
            if d is not None:
                link(nc.vector.tensor_copy(d.which[:, :, :], whichf[:, :, :]))
                link(nc.vector.tensor_copy(d.weight[:, :], wt[:, :, :].rearrange("p t a -> p (t a)")))
                return
            eight = r.column[:, 0:8].unsqueeze(1).broadcast_to([P, NT, 8])
            link(nc.vector.tensor_tensor(r.gate[:, :, :], eight, col(whichf[:, :, 0]), ALU.is_equal))
            link(nc.vector.tensor_tensor(other_gate[:, :, :], eight, col(whichf[:, :, 1]), ALU.is_equal))
            link(nc.vector.tensor_tensor(r.gate[:, :, :], r.gate[:, :, :], col(wt[:, :, 0]), ALU.mult))
            link(nc.vector.tensor_tensor(other_gate[:, :, :], other_gate[:, :, :], col(wt[:, :, 1]), ALU.mult))
            link(nc.vector.tensor_tensor(r.gate[:, :, :], r.gate[:, :, :], other_gate[:, :, :], ALU.add))


def experts_gelu(nc, r, tag, w1, b1, w2, b2, experts, hidden, gates, out, load):
    HC = hidden // P
    with Scope(nc, tag) as s:
        W1 = s.sb("W1", [P, experts, 2, hidden])
        W2 = s.sb("W2", [P, experts, HC, G])
        B1 = s.sb("B1", [P, experts, HC])
        B2 = s.sb("B2", [P, experts, G])
        hT = s.sb("hT", [P, 2, HC, BC])
        ps_h = [s.ps(f"ps_h{k}", [P, BC]) for k in range(2)]
        ps_y = [s.ps(f"ps_y{k}", [P, 4, G]) for k in range(2)]
        loaded, biased = s.sem("loaded"), s.sem("biased")
        hidden_made, acted, summed, added = (s.sems(n, 2) for n in ("hidden_made", "acted", "summed", "added"))
        block = s.block()
        PER_H, PER_Y = experts * HC // 2, experts // 2

        n_loads, rows = load(nc, s, W1, W2, B1, B2, w1, b1, w2, b2, loaded, block, hidden)

        @block.tensor
        def _(pe):
            pe.wait_ge(loaded, n_loads)

            def up(i, e):
                for c in range(HC):
                    q = e * HC + c
                    pe.wait_ge(acted[q % 2], i * PER_H + q // 2)
                    for n in range(2):
                        last = nc.tensor.matmul(ps_h[q % 2][:, :], W1[:, e, n, c * P:(c + 1) * P], r.xT[:, n, bass.ds(i * BC, BC)],
                                                start=(n == 0), stop=(n == 1))
                    last.then_inc(hidden_made[q % 2], 1)

            def down(i, e):
                for k in range(2):
                    pe.wait_ge(acted[k], i * PER_H + (e + 1) * HC // 2)
                pe.wait_ge(added[e % 2], i * PER_Y + e // 2)
                for t in range(TB):
                    for c in range(HC):
                        last = nc.tensor.matmul(ps_y[e % 2][:, t, :], hT[:, e % 2, c, t * P:(t + 1) * P], W2[:, e, c, :],
                                                start=(c == 0), stop=(c == HC - 1))
                last.then_inc(summed[e % 2], 1)

            with pe.Fori(0, NB) as i:
                up(i, 0)
                for e in range(experts):
                    if e + 1 < experts:
                        up(i, e + 1)
                    down(i, e)

        @block.scalar
        def _(act):
            act.wait_ge(loaded, n_loads)
            with act.Fori(0, NB) as i:
                for e in range(experts):
                    act.wait_ge(summed[e % 2], i * PER_Y + e // 2)
                    for c in range(HC):
                        q = e * HC + c
                        act.wait_ge(hidden_made[q % 2], i * PER_H + (q // 2 + 1))
                        nc.scalar.activation(hT[:, e % 2, c, :], ps_h[q % 2][:, :], ACT.Gelu, bias=B1[:, e, c:c + 1]).then_inc(acted[q % 2], 1)

        @block.vector
        def _(dve):
            if rows is not None:
                rows(dve)
            link = Chain(dve, biased)
            dve.wait_ge(loaded, n_loads)
            with dve.Fori(0, NB) as i:
                link.enter(i, experts)
                for e in range(experts):
                    if e:
                        dve.wait_ge(added[(e - 1) % 2], i * PER_Y + ((e - 1) // 2 + 1))
                    for t in range(TB):
                        last = nc.vector.scalar_tensor_tensor(tile_of(out, i * TB + t), B2[:, e, :], gates(i * TB + t, e),
                                                              tile_of(out, i * TB + t), ALU.mult, ALU.add)
                    link(last)
                    dve.wait_ge(summed[e % 2], i * PER_Y + (e // 2 + 1))
                    for t in range(TB):
                        last = nc.vector.scalar_tensor_tensor(tile_of(out, i * TB + t), ps_y[e % 2][:, t, :], gates(i * TB + t, e),
                                                              tile_of(out, i * TB + t), ALU.mult, ALU.add)
                    last.then_inc(added[e % 2], 1)
                link.leave(NB)


class Picks:
    pass


def picks(s):
    d = Picks()
    d.which = s.sb("which", [P, NT, 2])
    d.weight = s.sb("weight", [P, 2 * NT])
    d.slot = s.sb("slot", [P, 2 * NT + SLOT_TILES], I32)
    d.expert = s.sb("expert", [P, GROUPS + GB], I32)
    d.weight_row = s.sb("weight_row", [P, GROUPS + GB], I32)
    return d


def dispatch(nc, r, d, tag, slots):
    with Scope(nc, tag) as s:
        chosen = s.sb("chosen", [P, 2, NT, 8])
        either = s.sb("either", [P, NT, 8])
        before = s.sb("before", [P, NT + 1, 8])
        totals = s.sb("totals", [P, NT, 8])
        place = s.sb("place", [P, NT, 8])
        mine = s.sb("mine", [P, NT, 8])
        slotf = s.sb("slotf", [P, NT, 2])
        groups_i = s.sb("groups_i", [P, 8], I32)
        groups = s.sb("groups", [P, 8])
        ends = s.sb("ends", [P, 8])
        base = s.sb("base", [P, 8])
        passed = s.sb("passed", [P, GROUPS, 8])
        expert = s.sb("expert", [P, GROUPS])
        row = s.sb("row", [P, GROUPS])
        ps = s.ps("ps", [P, 2, 256])
        chain_sem, selected, counted, placed, sent = (s.sem(n) for n in ("chain", "selected", "counted", "placed", "sent"))
        block = s.block()
        C = NT * 8

        @block.tensor
        def _(pe):
            pe.wait_ge(selected, 1)
            flat = either[:, :, :].rearrange("p t e -> p (t e)")
            nc.tensor.matmul(ps[:, 0, 0:C], r.above[:, :], flat, start=True, stop=True)
            nc.tensor.matmul(ps[:, 1, 0:C], r.ones[:, :], flat, start=True, stop=True).then_inc(counted, 1)

        @block.vector
        def _(dve):
            link = Chain(dve, chain_sem)
            eight = r.column[:, 0:8].unsqueeze(1).broadcast_to([P, NT, 8])
            for a in range(2):
                link(nc.vector.tensor_tensor(chosen[:, a, :, :], eight, d.which[:, :, a].unsqueeze(2).broadcast_to([P, NT, 8]), ALU.is_equal))
            nc.vector.tensor_tensor(either[:, :, :], chosen[:, 0, :, :], chosen[:, 1, :, :], ALU.add).then_inc(selected, 1)
            dve.wait_ge(counted, 1)
            link(nc.vector.tensor_copy(totals[:, :, :].rearrange("p t e -> p (t e)"), ps[:, 1, 0:C]))
            link(nc.vector.memset(before[:, 0:1, :], 0.0))
            for e in range(8):
                link(nc.vector.tensor_tensor_scan(before[:, 1:, e], r.ones[:, 0:NT], totals[:, :, e], 0.0, ALU.mult, ALU.add))
            link(nc.vector.tensor_scalar(groups[:, :], before[:, NT, :], float(GROUP - 1), None, ALU.add))
            link(nc.vector.tensor_copy(groups_i[:, :], groups[:, :]))
            link(nc.vector.tensor_scalar(groups_i[:, :], groups_i[:, :], GROUP.bit_length() - 1, None, ALU.arith_shift_right))
            link(nc.vector.tensor_copy(groups[:, :], groups_i[:, :]))
            link(nc.vector.tensor_tensor_scan(ends[:, :], r.ones[:, 0:8], groups[:, :], 0.0, ALU.mult, ALU.add))
            link(nc.vector.tensor_tensor(base[:, :], ends[:, :], groups[:, :], ALU.subtract))
            link(nc.vector.tensor_scalar(base[:, :], base[:, :], float(GROUP), None, ALU.mult))
            link(nc.vector.tensor_tensor(place[:, :, :].rearrange("p t e -> p (t e)"), ps[:, 0, 0:C],
                                         before[:, 0:NT, :].rearrange("p t e -> p (t e)"), ALU.add))
            link(nc.vector.tensor_tensor(place[:, :, :], place[:, :, :], base[:, :].unsqueeze(1).broadcast_to([P, NT, 8]), ALU.add))
            for a in range(2):
                link(nc.vector.tensor_tensor(mine[:, :, :], place[:, :, :], chosen[:, a, :, :], ALU.mult))
                link(nc.vector.tensor_reduce(slotf[:, :, a], mine[:, :, :], AX.X, ALU.add))
            link(nc.vector.memset(d.slot[:, 2 * NT:], 0))
            nc.vector.tensor_copy(d.slot[:, 0:2 * NT], slotf[:, :, :].rearrange("p t a -> p (t a)")).then_inc(placed, 1)
            link(nc.vector.tensor_tensor(passed[:, :, :], ends[:, :].unsqueeze(1).broadcast_to([P, GROUPS, 8]),
                                         r.column[:, 0:GROUPS].unsqueeze(2).broadcast_to([P, GROUPS, 8]), ALU.is_le))
            link(nc.vector.tensor_reduce(expert[:, :], passed[:, :, :], AX.X, ALU.add))
            link(nc.vector.tensor_scalar(expert[:, :], expert[:, :], 7.0, None, ALU.min))
            link(nc.vector.tensor_scalar(row[:, :], expert[:, :], float(P), None, ALU.mult))
            link(nc.vector.tensor_scalar(row[:, :], row[:, :], r.partition[:, 0:1], None, ALU.add))
            link(nc.vector.memset(d.expert[:, GROUPS:], 0))
            link(nc.vector.memset(d.weight_row[:, GROUPS:], 0))
            link(nc.vector.tensor_copy(d.expert[:, 0:GROUPS], expert[:, :]))
            link(nc.vector.tensor_copy(d.weight_row[:, 0:GROUPS], row[:, :]))

        @block.gpsimd
        def _(pool):
            pool.wait_ge(placed, 1)
            for n in range(2 * NT):
                pool.indirect_dma_start(slots, bass.IndirectOffsetOnAxis(ap=d.slot[:, n:n + 1], axis=0), r.xh[:, n // 2, :], None,
                                        bounds_check=GROUPS * GROUP - 1, oob_is_err=False).then_inc(sent, 16)
            pool.wait_ge(sent, 16 * 2 * NT)


def group_experts(nc, r, d, tag, w1, b1, w2, b2, hidden, slots, results):
    HC, GT = hidden // P, GROUPS // GB
    with Scope(nc, tag) as s:
        index = s.sb("index", [P, GB, 2], I32)
        W1 = s.sb("W1", [P, GB, 2, P, HC])
        W2 = s.sb("W2", [P, GB, HC, G])
        B1 = s.sb("B1", [P, GB, HC])
        B2 = s.sb("B2", [P, GB, G])
        X = s.sb("X", [P, GB, 2, P, 2])
        xT = s.sb("xT", [P, GB, 2, GROUP])
        hT = s.sb("hT", [P, GB, HC, GROUP])
        Y = s.sb("Y", [P, GB, 2, G])
        flip = [s.ps(f"flip{k}", [P, 2, GROUP]) for k in range(GB)]
        ps_y = [s.ps(f"ps_y{k}", [P, 2, G]) for k in range(GB)]
        ps_h = [s.ps(f"ps_h{k}", [P, GROUP]) for k in range(2)]
        names = ("indexed", "came", "loaded", "flipped", "copied", "summed", "made", "stored")
        indexed, came, loaded, flipped, copied, summed, made, stored = (s.sems(n, GB) for n in names)
        hidden_made, acted = s.sems("hidden_made", 2), s.sems("acted", 2)
        block = s.block()
        PER_H = HC // 2

        @block.gpsimd
        def _(pool):
            last_row, last_expert, turn = pool.to_reg(8 * P - 1), pool.to_reg(7), pool.alloc_register(f"{s.tag}_next_turn")
            w1_rows = w1.rearrange("e (p k) f -> (e p) (k f)", k=2)
            w2_rows = w2.rearrange("e (p c) f -> (e p) (c f)", c=HC)
            b1_rows = b1.rearrange("e (p c) -> (e p) c", c=HC)
            with pool.Fori(0, GT) as i:
                pool.reg_add(turn, i, 1)
                for k in range(GB):
                    tables_made(pool, r)
                    pool.wait_ge(indexed[k], turn)
                    pool.wait_ge(made[k], i)
                    for to, table, n, last in ((W1[:, k, :, :, :].rearrange("p a b c -> p (a b c)"), w1_rows, 0, last_row),
                                               (W2[:, k, :, :].rearrange("p a b -> p (a b)"), w2_rows, 0, last_row),
                                               (B1[:, k, :], b1_rows, 0, last_row), (B2[:, k, :], b2, 1, last_expert)):
                        pool.indirect_dma_start(to, None, table, bass.IndirectOffsetOnAxis(ap=index[:, k, n:n + 1], axis=0),
                                                bounds_check=last, oob_is_err=False).then_inc(came[k], 16)

        def rows_of(table, i, k):
            return table[bass.ds((i * GB + k) * GROUP, GROUP), :].rearrange("(h p) f -> p h f", p=P)

        def load(sp, i, k):
            sp.dma_start(X[:, k, :, :, :].rearrange("p h m c -> p h (m c)"), rows_of(slots, i, k)).then_inc(loaded[k], 16)

        @block.sync
        def _(sp):
            for k in range(GB):
                load(sp, 0, k)

            def store_group(i, k):
                sp.wait_ge(made[k], i + 1)
                sp.dma_start(rows_of(results, i, k), Y[:, k, :, :]).then_inc(stored[k], 16)

            with sp.Fori(0, GT - 1) as i:
                for k in range(GB):
                    store_group(i, k)
                    sp.wait_ge(flipped[k], i + 1)
                    load(sp, i + 1, k)
            for k in range(GB):
                store_group(GT - 1, k)
            for k in range(GB):
                sp.wait_ge(stored[k], 16 * GT)

        @block.tensor
        def _(pe):
            def flip_group(i, k):
                pe.wait_ge(loaded[k], (i + 1) * 16)
                pe.wait_ge(copied[k], i)
                for h in range(2):
                    for c in range(2):
                        last = nc.tensor.transpose(flip[k][:, c, h * P:(h + 1) * P], X[:, k, h, :, c], r.eye[:, :])
                last.then_inc(flipped[k], 1)

            def up(i, k):
                pe.wait_ge(copied[k], i + 1)
                pe.wait_ge(came[k], (i + 1) * 64)
                for c in range(HC):
                    pe.wait_ge(acted[c % 2], (i * GB + k) * PER_H + c // 2)
                    for n in range(2):
                        last = nc.tensor.matmul(ps_h[c % 2][:, :], W1[:, k, n, :, c], xT[:, k, n, :], start=(n == 0), stop=(n == 1))
                    last.then_inc(hidden_made[c % 2], 1)

            def down(i, k):
                for b in range(2):
                    pe.wait_ge(acted[b], (i * GB + k) * PER_H + PER_H)
                pe.wait_ge(made[k], i)
                for h in range(2):
                    for c in range(HC):
                        last = nc.tensor.matmul(ps_y[k][:, h, :], hT[:, k, c, h * P:(h + 1) * P], W2[:, k, c, :], start=(c == 0), stop=(c == HC - 1))
                last.then_inc(summed[k], 1)

            def first():
                flip_group(0, 0)
                up(0, 0)

            def both(i, k):
                flip_group(*after(i, k, GB))
                down(i, k)
                up(*after(i, k, GB))

            skewed(pe, None, 0, first, both, lambda i: down(i, GB - 1), GT, GB)

        @block.scalar
        def _(act):
            with act.Fori(0, GT) as i:
                for k in range(GB):
                    act.wait_ge(summed[k], i)
                    for c in range(HC):
                        act.wait_ge(hidden_made[c % 2], (i * GB + k) * PER_H + (c // 2 + 1))
                        nc.scalar.activation(hT[:, k, c, :], ps_h[c % 2][:, :], ACT.Gelu, bias=B1[:, k, c:c + 1]).then_inc(acted[c % 2], 1)

        @block.vector
        def _(dve):
            def copy_features(i, k):
                dve.wait_ge(flipped[k], i + 1)
                nc.vector.tensor_copy(xT[:, k, :, :], flip[k][:, :, :]).then_inc(copied[k], 1)

            def take(i, k):
                dve.wait_ge(came[k], (i + 1) * 64)
                stage_index(k, i * GB + k + GB)
                dve.wait_ge(summed[k], i + 1)
                dve.wait_ge(stored[k], i * 16)
                nc.vector.tensor_tensor(Y[:, k, :, :], ps_y[k][:, :, :], B2[:, k, :].unsqueeze(1).broadcast_to([P, 2, G]), ALU.add).then_inc(made[k], 1)

            def stage_index(k, g):
                nc.vector.tensor_copy(index[:, k, 0:1], d.weight_row[:, bass.ds(g, 1)])
                nc.vector.tensor_copy(index[:, k, 1:2], d.expert[:, bass.ds(g, 1)]).then_inc(indexed[k], 1)

            def first():
                for k in range(GB):
                    stage_index(k, k)
                copy_features(0, 0)

            def both(i, k):
                copy_features(*after(i, k, GB))
                take(i, k)

            skewed(dve, None, 0, first, both, lambda i: take(i, GB - 1), GT, GB)


def combine(nc, r, d, tag, results, tokens):
    FB, TT = SLOT_TILES, 2 * NT // SLOT_TILES
    with Scope(nc, tag) as s:
        index = s.sb("index", [P, FB], I32)
        got = s.sb("got", [P, FB, G])
        indexed, came, used, joined = (s.sems(n, FB) for n in ("indexed", "came", "used", "joined"))
        block = s.block()

        @block.gpsimd
        def _(pool):
            last_slot, turn = pool.to_reg(GROUPS * GROUP - 1), pool.alloc_register(f"{s.tag}_next_turn")
            with pool.Fori(0, TT) as i:
                pool.reg_add(turn, i, 1)
                for k in range(FB):
                    tables_made(pool, r)
                    pool.wait_ge(indexed[k], turn)
                    pool.wait_ge(used[k], i)
                    pool.indirect_dma_start(got[:, k, :], None, results, bass.IndirectOffsetOnAxis(ap=index[:, k:k + 1], axis=0),
                                            bounds_check=last_slot, oob_is_err=False).then_inc(came[k], 16)

        @block.vector
        def _(dve):
            for k in range(FB):
                nc.vector.tensor_copy(index[:, k:k + 1], d.slot[:, k:k + 1]).then_inc(indexed[k], 1)
            with dve.Fori(0, TT) as i:
                for k in range(FB):
                    n = i * FB + k
                    dve.wait_ge(came[k], (i + 1) * 16)
                    nc.vector.tensor_copy(index[:, k:k + 1], d.slot[:, bass.ds(n + FB, 1)]).then_inc(indexed[k], 1)
                    x = tile_of(r.x, i * (FB // 2) + k // 2)
                    if k % 2 == 0 and tokens:
                        nc.vector.tensor_tensor(x, x, tile_of(r.xh, i * (FB // 2) + k // 2), ALU.add).then_inc(joined[k], 1)
                        dve.wait_ge(joined[k], i + 1)
                    if k % 2:
                        dve.wait_ge(used[k - 1], i + 1)
                    nc.vector.scalar_tensor_tensor(x, got[:, k, :], d.weight[:, bass.ds(n, 1)], x, ALU.mult, ALU.add).then_inc(used[k], 1)


class LayerZeroWeights:
    EX, H2 = 4, 64

    def __init__(self, nc, s, t):
        EX, H2 = self.EX, self.H2
        self.nc, self.t = nc, t
        self.W1 = s.sb("W1", [P, 6, 2, P])
        self.W2 = s.sb("W2", [P, 2, P])
        self.V2 = s.sb("V2", [P, EX, H2])
        self.W3 = s.sb("W3", [P, G])
        self.V3 = s.sb("V3", [H2, EX, G])
        self.B1 = s.sb("B1", [P, 6])
        self.B2 = s.sb("B2", [P, 5])
        self.B3 = s.sb("B3", [P, 5, G])
        self.loaded = s.sem("loaded")

    def load(self, sp):
        EX, H2 = self.EX, self.H2
        g = lambda n: self.t["L0_ffn_" + n]
        for c in range(2):
            sp.dma_start(self.W1[:, c, :, :], g("sW1")[:, c * P:(c + 1) * P].rearrange("(k p) n -> p k n", p=P)).then_inc(self.loaded, 16)
        for e in range(EX):
            sp.dma_start(self.W1[:, 2 + e, :, :], g("eW1")[e].rearrange("(k p) n -> p k n", p=P)).then_inc(self.loaded, 16)
        sp.dma_start(self.W2[:, :, :], g("sW2").rearrange("(k p) n -> p k n", p=P)).then_inc(self.loaded, 16)
        sp.dma_start(self.V2[:, :, :], g("eW2").rearrange("e p n -> p e n")).then_inc(self.loaded, 16)
        sp.dma_start(self.W3[:, :], g("sW3")).then_inc(self.loaded, 16)
        sp.dma_start(self.V3[:, :, :], g("eW3").rearrange("e p n -> p e n")).then_inc(self.loaded, 16)
        with self.nc.allow_non_contiguous_dma("biases"):
            sp.dma_start(self.B1[:, 0:2], g("sb1").rearrange("(c p) -> p c", p=P), allow_slow_non_contiguous=True).then_inc(self.loaded, 16)
            sp.dma_start(self.B1[:, 2:6], g("eb1").rearrange("e p -> p e"), allow_slow_non_contiguous=True).then_inc(self.loaded, 16)
            sp.dma_start(self.B2[:, 0:1], g("sb2").rearrange("(c p) -> p c", p=P), allow_slow_non_contiguous=True).then_inc(self.loaded, 16)
            sp.dma_start(self.B2[0:H2, 1:5], g("eb2").rearrange("e p -> p e"), allow_slow_non_contiguous=True).then_inc(self.loaded, 16)
        sp.dma_start(self.B3[:, 0, :], g("sb3").unsqueeze(0).broadcast_to([P, G])).then_inc(self.loaded, 16)
        sp.dma_start(self.B3[:, 1:5, :], g("eb3").unsqueeze(0).broadcast_to([P, EX, G])).then_inc(self.loaded, 16)


def layer_l0_ffn(nc, r, w, sorted_edges):
    H2 = 64
    with Scope(nc, "l0f") as s:
        W1, W2, V2, W3, V3, B1, B2, B3, loaded = w.W1, w.W2, w.V2, w.W3, w.V3, w.B1, w.B2, w.B3, w.loaded
        h1 = s.sb("h1", [P, 6, BC])
        h2 = s.sb("h2", [P, 5, BC])
        ps_h = [s.ps(f"ps_h{k}", [P, BC]) for k in range(3)]
        ps_y = [s.ps(f"ps_y{k}", [P, 4, G]) for k in range(2)]
        biased = s.sem("biased")
        made, acted, summed, added = s.sems("made", 3), s.sems("acted", 3), s.sems("summed", 2), s.sems("added", 2)
        sender = Sender(nc, s, r, *BESIDE["l0f"], NB, sorted_edges)
        block = s.block()

        @block.gpsimd
        def _(pool):
            sender.gpsimd(pool)

        def rows(q):
            return P if q <= 6 else H2

        USES = [len(range(b, 11, 3)) for b in range(3)]

        @block.tensor
        def _(pe):
            pe.wait_ge(loaded, 16 * 16)

            def hidden(i, qs):
                for q in qs:
                    b, n = q % 3, q // 3
                    pe.wait_ge(acted[b], i * USES[b] + n)
                    if q < 6:
                        for c in range(2):
                            last = nc.tensor.matmul(ps_h[b][:, :], W1[:, q, c, :], r.xT[:, c, bass.ds(i * BC, BC)], start=(c == 0), stop=(c == 1))
                    elif q == 6:
                        for z in range(3):
                            pe.wait_ge(acted[z], i * USES[z] + 2)
                        for c in range(2):
                            last = nc.tensor.matmul(ps_h[b][:, :], W2[:, c, :], h1[:, c, :], start=(c == 0), stop=(c == 1))
                    else:
                        last = nc.tensor.matmul(ps_h[b][0:H2, :], V2[:, q - 7, :], h1[:, q - 5, :], start=True, stop=True)
                    last.then_inc(made[b], 1)

            def third(i):
                for z in range(3):
                    pe.wait_ge(acted[z], (i + 1) * USES[z])
                for e in range(5):
                    n, per = e // 2, (3, 2)[e % 2]
                    pe.wait_ge(added[e % 2], i * per + n)
                    for tt in range(TB):
                        if e == 0:
                            last = nc.tensor.matmul(ps_y[e % 2][:, tt, :], h2[:, 0, tt * P:(tt + 1) * P], W3[:, :], start=True, stop=True)
                        else:
                            last = nc.tensor.matmul(ps_y[e % 2][:, tt, :], h2[0:H2, e, tt * P:(tt + 1) * P], V3[:, e - 1, :], start=True, stop=True)
                    last.then_inc(summed[e % 2], 1)

            hidden(0, range(11))
            with pe.Fori(0, NB - 1) as i:
                hidden(i + 1, range(6))
                third(i)
                hidden(i + 1, range(6, 11))
            third(NB - 1)

        @block.scalar
        def _(act):
            act.wait_ge(loaded, 16 * 16)
            with act.Fori(0, NB) as i:
                for q in range(11):
                    b, n = q % 3, q // 3
                    if q == 6:
                        act.wait_ge(summed[0], i * 3)
                        act.wait_ge(summed[1], i * 2)
                    act.wait_ge(made[b], i * USES[b] + (n + 1))
                    if q < 6:
                        ins = nc.scalar.activation(h1[:, q, :], ps_h[b][:, :], ACT.Relu, bias=B1[:, q:q + 1])
                    else:
                        m = rows(q)
                        ins = nc.scalar.activation(h2[0:m, q - 6, :], ps_h[b][0:m, :], ACT.Relu, bias=B2[0:m, q - 6:q - 5])
                    ins.then_inc(acted[b], 1)

        @block.vector
        def _(dve):
            link = Chain(dve, biased)
            dve.wait_ge(loaded, 16 * 16)
            with dve.Fori(0, NB) as i:
                link.enter(i, 5)
                for k in range(2):
                    sender.vector(dve, i, k)

                def add_up(e, of):
                    for tt in range(TB):
                        xt = tile_of(r.x, i * TB + tt)
                        by = r.gate[:, bass.ds(i * TB + tt, 1), e - 1] if e else 1.0
                        last = nc.vector.scalar_tensor_tensor(xt, of(tt), by, xt, ALU.mult, ALU.add)
                    return last

                for e in range(5):
                    link(add_up(e, lambda tt: B3[:, e, :]))
                for e in range(5):
                    n, per = e // 2, (3, 2)[e % 2]
                    dve.wait_ge(summed[e % 2], i * per + (n + 1))
                    if e:
                        dve.wait_ge(added[(e - 1) % 2], i * (3, 2)[(e - 1) % 2] + ((e - 1) // 2 + 1))
                    add_up(e, lambda tt: ps_y[e % 2][:, tt, :]).then_inc(added[e % 2], 1)
                link.leave(NB)


def up_l3(nc, r, w1, b1, hf):
    with Scope(nc, "l3a") as s:
        W = s.sb("W", [P, 2, 2 * G])
        B1 = s.sb("B1", [P, 4])
        ps = [s.ps(f"ps{k}", [P, BC]) for k in range(4)]
        loaded = s.sem("loaded")
        made, taken = s.sems("made", 4), s.sems("taken", 4)
        block = s.block()

        @block.sync
        def _(sp):
            sp.dma_start(W[:, :, :], w1.rearrange("(c p) n -> p c n", p=P)).then_inc(loaded, 16)
            sp.dma_start(B1[:, :], b1.rearrange("(c p) -> p c", p=P), allow_slow_non_contiguous=True).then_inc(loaded, 16)

        @block.tensor
        def _(pe):
            pe.wait_ge(loaded, 32)
            with pe.Fori(0, NB) as i:
                for c in range(4):
                    pe.wait_ge(taken[c], i)
                    for k in range(2):
                        last = nc.tensor.matmul(ps[c][:, :], W[:, k, c * P:(c + 1) * P], r.xT[:, k, bass.ds(i * BC, BC)], start=(k == 0), stop=(k == 1))
                    last.then_inc(made[c], 1)

        @block.vector
        def _(dve):
            dve.wait_ge(loaded, 32)
            with dve.Fori(0, NB) as i:
                for c in range(4):
                    dve.wait_ge(made[c], i + 1)
                    nc.vector.tensor_scalar(hf[:, c, bass.ds(i * BC, BC)], ps[c][:, :], B1[:, c:c + 1], None, ALU.add).then_inc(taken[c], 1)


def column_moments(nc, link, stats, moments, rows, chunks):
    cuts = [(a, min(a + 512, N)) for a in range(0, N, 512)]
    for c in range(chunks):
        for n, (a, b) in enumerate(cuts):
            last = nc.vector.bn_stats(stats[:, c, n, :], rows[:, c, a:b])
    link(last)
    for c in range(chunks):
        last = nc.vector.bn_aggr(moments[:, c, :], stats[:, c, :, :].rearrange("p n s -> p (n s)"))
    link(last)


def batch_norm_l3(nc, r, gamma, beta, hf):
    with Scope(nc, "l3b") as s:
        stats = s.sb("stats", [P, 4, 8, 6])
        moments = s.sb("moments", [P, 4, 2])
        gb = s.sb("gb", [P, 2, 4])
        std = s.sb("std", [P, 4])
        scale = s.sb("scale", [P, 4])
        shift = s.sb("shift", [P, 4])
        loaded, chain_sem, added, rooted, ready = (s.sem(n) for n in ("loaded", "chain", "added", "rooted", "ready"))
        block = s.block()

        @block.sync
        def _(sp):
            sp.dma_start(gb[:, 0, :], gamma.rearrange("(c p) -> p c", p=P), allow_slow_non_contiguous=True).then_inc(loaded, 16)
            sp.dma_start(gb[:, 1, :], beta.rearrange("(c p) -> p c", p=P), allow_slow_non_contiguous=True).then_inc(loaded, 16)

        @block.vector
        def _(dve):
            link = Chain(dve, chain_sem)
            column_moments(nc, link, stats, moments, hf, 4)
            nc.vector.tensor_scalar(std[:, :], moments[:, :, 1], EPS, None, ALU.add).then_inc(added, 1)
            dve.wait_ge(rooted, 1)
            dve.wait_ge(loaded, 32)
            link(nc.vector.reciprocal(std[:, :], std[:, :]))
            link(nc.vector.tensor_tensor(scale[:, :], std[:, :], gb[:, 0, :], ALU.mult))
            link(nc.vector.tensor_tensor(shift[:, :], moments[:, :, 0], scale[:, :], ALU.mult))
            nc.vector.tensor_tensor(shift[:, :], gb[:, 1, :], shift[:, :], ALU.subtract).then_inc(ready, 1)

        @block.scalar
        def _(act):
            act.wait_ge(added, 1)
            nc.scalar.activation(std[:, :], std[:, :], ACT.Sqrt).then_inc(rooted, 1)
            act.wait_ge(ready, 1)
            for c in range(4):
                nc.scalar.activation(hf[:, c, :], hf[:, c, :], ACT.Relu, bias=shift[:, c:c + 1], scale=scale[:, c:c + 1])


def down_l3(nc, r, w2, b2, hf):
    with Scope(nc, "l3d") as s:
        W = s.sb("W", [P, 4, G])
        B2 = s.sb("B2", [P, 2])
        ps = [s.ps(f"ps{k}", [P, BC]) for k in range(2)]
        loaded = s.sem("loaded")
        made, taken = s.sems("made", 2), s.sems("taken", 2)
        block = s.block()

        @block.sync
        def _(sp):
            sp.dma_start(W[:, :, :], w2.rearrange("(c p) n -> p c n", p=P)).then_inc(loaded, 16)
            sp.dma_start(B2[:, :], b2.rearrange("(c p) -> p c", p=P), allow_slow_non_contiguous=True).then_inc(loaded, 16)

        @block.tensor
        def _(pe):
            pe.wait_ge(loaded, 32)
            with pe.Fori(0, NB) as i:
                for c in range(2):
                    pe.wait_ge(taken[c], i)
                    for k in range(4):
                        last = nc.tensor.matmul(ps[c][:, :], W[:, k, c * P:(c + 1) * P], hf[:, k, bass.ds(i * BC, BC)], start=(k == 0), stop=(k == 3))
                    last.then_inc(made[c], 1)

        @block.vector
        def _(dve):
            dve.wait_ge(loaded, 32)
            with dve.Fori(0, NB) as i:
                for c in range(2):
                    dve.wait_ge(made[c], i + 1)
                    nc.vector.tensor_scalar(r.xT[:, c, bass.ds(i * BC, BC)], ps[c][:, :], B2[:, c:c + 1], None, ALU.add).then_inc(taken[c], 1)


def graph_norm_l3(nc, r, t):
    with Scope(nc, "l3n") as s:
        stats = s.sb("stats", [P, 2, 8, 6])
        moments = s.sb("moments", [P, 2, 2])
        par = s.sb("par", [P, 5, 2])
        mu, var, d, q, s1, m1, v2, rest, s2, scale, shift = (
            s.sb(n, [P, 2]) for n in ("mu", "var_c", "d", "q", "s1", "m1", "v2", "rest", "s2", "scale", "shift"))
        mean_g = s.sb("mean_g", [P, 1])
        rg = s.sb("rg", [P, 1])
        stage = s.sb("stage", [P, 2, 2, P])
        ps_sum = s.ps("ps_sum", [P, 4])
        back = [s.ps(f"back{k}", [P, 2, P]) for k in range(2)]
        names = ("loaded", "chain", "averaged", "summed", "squared", "summed2", "g_added", "g_rooted", "c_added", "c_rooted", "ready", "cut")
        loaded, chain_sem, averaged, summed, squared, summed2, g_added, g_rooted, c_added, c_rooted, ready, cut = (s.sem(n) for n in names)
        staged, flipped, taken = (s.sems(n, 2) for n in ("staged", "flipped", "taken"))
        block = s.block()
        LW, LB, GW, GB, MS = range(5)
        T2 = NT // 2

        @block.sync
        def _(sp):
            for n, name in enumerate(("ln_w", "ln_b", "gn_w", "gn_b", "gn_ms")):
                sp.dma_start(par[:, n, :], t["L3_gnn_" + name].rearrange("(c p) -> p c", p=P), allow_slow_non_contiguous=True).then_inc(loaded, 16)

        @block.vector
        def _(dve):
            link = Chain(dve, chain_sem)
            column_moments(nc, link, stats, moments, r.xT, 2)
            link(nc.vector.tensor_copy(mu[:, :], moments[:, :, 0]))
            nc.vector.tensor_copy(var[:, :], moments[:, :, 1]).then_inc(averaged, 1)
            dve.wait_ge(summed, 1)
            link(nc.vector.tensor_reduce(mean_g[:, :], ps_sum[:, 0:2], AX.X, ALU.add))
            link(nc.vector.tensor_scalar(mean_g[:, :], mean_g[:, :], 1.0 / G, None, ALU.mult))
            link(nc.vector.tensor_scalar(d[:, :], mu[:, :], mean_g[:, 0:1], None, ALU.subtract))
            link(nc.vector.tensor_tensor(q[:, :], d[:, :], d[:, :], ALU.mult))
            nc.vector.tensor_tensor(q[:, :], q[:, :], var[:, :], ALU.add).then_inc(squared, 1)
            dve.wait_ge(summed2, 1)
            link(nc.vector.tensor_reduce(rg[:, :], ps_sum[:, 2:4], AX.X, ALU.add))
            nc.vector.tensor_scalar(rg[:, :], rg[:, :], 1.0 / G, EPS, ALU.mult, ALU.add).then_inc(g_added, 1)
            dve.wait_ge(g_rooted, 1)
            dve.wait_ge(loaded, 80)
            link(nc.vector.reciprocal(rg[:, :], rg[:, :]))
            link(nc.vector.tensor_scalar(s1[:, :], par[:, LW, :], rg[:, 0:1], None, ALU.mult))
            link(nc.vector.tensor_tensor(m1[:, :], d[:, :], s1[:, :], ALU.mult))
            link(nc.vector.tensor_tensor(m1[:, :], m1[:, :], par[:, LB, :], ALU.add))
            link(nc.vector.tensor_tensor(v2[:, :], m1[:, :], par[:, MS, :], ALU.mult))
            link(nc.vector.tensor_tensor(rest[:, :], m1[:, :], v2[:, :], ALU.subtract))
            link(nc.vector.tensor_tensor(q[:, :], rest[:, :], rest[:, :], ALU.mult))
            link(nc.vector.tensor_tensor(v2[:, :], s1[:, :], s1[:, :], ALU.mult))
            link(nc.vector.tensor_tensor(v2[:, :], v2[:, :], var[:, :], ALU.mult))
            link(nc.vector.tensor_tensor(v2[:, :], v2[:, :], q[:, :], ALU.add))
            nc.vector.tensor_scalar(v2[:, :], v2[:, :], EPS, None, ALU.add).then_inc(c_added, 1)
            dve.wait_ge(c_rooted, 1)
            link(nc.vector.reciprocal(s2[:, :], v2[:, :]))
            link(nc.vector.tensor_tensor(s2[:, :], s2[:, :], par[:, GW, :], ALU.mult))
            link(nc.vector.tensor_tensor(scale[:, :], s1[:, :], s2[:, :], ALU.mult))
            link(nc.vector.tensor_tensor(shift[:, :], rest[:, :], s2[:, :], ALU.mult))
            link(nc.vector.tensor_tensor(shift[:, :], shift[:, :], par[:, GB, :], ALU.add))
            link(nc.vector.tensor_tensor(q[:, :], scale[:, :], mu[:, :], ALU.mult))
            nc.vector.tensor_tensor(shift[:, :], shift[:, :], q[:, :], ALU.subtract).then_inc(ready, 1)
            dve.wait_ge(cut, 2)
            with dve.Fori(0, T2) as i:
                for k in range(2):
                    dve.wait_ge(flipped[k], i)
                    nc.vector.tensor_scalar(stage[:, k, :, :], r.xT[:, :, bass.ds((i * 2 + k) * P, P)], 1.0, None, ALU.mult).then_inc(staged[k], 1)
                for k in range(2):
                    xt = tile_of(r.x, i * 2 + k)
                    dve.wait_ge(flipped[k], i + 1)
                    nc.vector.tensor_tensor(xt, xt, back[k][:, :, :].rearrange("p c n -> p (c n)"), ALU.add).then_inc(taken[k], 1)

        @block.scalar
        def _(act):
            act.wait_ge(g_added, 1)
            nc.scalar.activation(rg[:, :], rg[:, :], ACT.Sqrt).then_inc(g_rooted, 1)
            act.wait_ge(c_added, 1)
            nc.scalar.activation(v2[:, :], v2[:, :], ACT.Sqrt).then_inc(c_rooted, 1)
            act.wait_ge(ready, 1)
            for c in range(2):
                nc.scalar.activation(r.xT[:, c, :], r.xT[:, c, :], ACT.Relu, bias=shift[:, c:c + 1], scale=scale[:, c:c + 1]).then_inc(cut, 1)

        @block.tensor
        def _(pe):
            pe.wait_ge(averaged, 1)
            nc.tensor.matmul(ps_sum[:, 0:2], r.ones[:, :], mu[:, :], start=True, stop=True).then_inc(summed, 1)
            pe.wait_ge(squared, 1)
            nc.tensor.matmul(ps_sum[:, 2:4], r.ones[:, :], q[:, :], start=True, stop=True).then_inc(summed2, 1)
            with pe.Fori(0, T2) as i:
                for k in range(2):
                    pe.wait_ge(staged[k], i + 1)
                    pe.wait_ge(taken[k], i)
                    for c in range(2):
                        last = nc.tensor.transpose(back[k][:, c, :], stage[:, k, c, :], r.eye[:, :])
                    last.then_inc(flipped[k], 1)


def route_l3(nc, r, w_router, bias, which, weight):
    EX = 8
    CAPACITY = float(-(-(N * 5) // (4 * EX)))
    with Scope(nc, "l3r") as s:
        w = s.sb("w", [P, 2, EX])
        row = s.sb("row", [1, EX])
        mean = s.sb("mean", [P, 2])
        p = s.sb("p", [1, EX])
        load = s.sb("load", [1, EX])
        one = s.sb("one", [1, 1])
        top = s.sb("top", [1, 8])
        idx = s.sb("idx", [1, 8], mybir.dt.uint32)
        pair = s.sb("pair", [1, 4])
        ps = s.ps("ps", [1, EX])
        ps4 = s.ps("ps4", [P, 4])
        names = ("loaded", "chain", "averaged", "scored", "e1", "e1_done", "e2", "e2_done", "e3", "e3_done", "paired", "spread")
        loaded, chain_sem, averaged, scored, e1, e1_done, e2, e2_done, e3, e3_done, paired, spread = (s.sem(n) for n in names)
        block = s.block()

        @block.sync
        def _(sp):
            sp.dma_start(w[:, :, :], w_router.rearrange("(c p) n -> p c n", p=P)).then_inc(loaded, 16)
            sp.dma_start(row[:, :], bias.unsqueeze(0)).then_inc(loaded, 16)

        @block.tensor
        def _(pe):
            pe.wait_ge(loaded, 32)
            pe.wait_ge(averaged, 1)
            nc.tensor.matmul(ps[:, :], r.ones[0:1, 0:1], row[:, :], start=True, stop=False)
            for c in range(2):
                last = nc.tensor.matmul(ps[:, :], mean[:, c:c + 1], w[:, c, :], start=False, stop=(c == 1))
            last.then_inc(scored, 1)
            pe.wait_ge(paired, 1)
            nc.tensor.matmul(ps4[:, :], r.ones[0:1, :], pair[:, :], start=True, stop=True).then_inc(spread, 1)

        @block.scalar
        def _(act):
            for begun, done, what in ((e1, e1_done, p[:, :]), (e2, e2_done, p[:, :]), (e3, e3_done, pair[:, 1:2])):
                act.wait_ge(begun, 1)
                nc.scalar.activation(what, what, ACT.Exp).then_inc(done, 1)

        @block.vector
        def _(dve):
            link = Chain(dve, chain_sem)

            def softmax(begun, done):
                link(nc.vector.tensor_reduce(one[:, :], p[:, :], AX.X, ALU.max))
                nc.vector.tensor_scalar(p[:, :], p[:, :], one[:, 0:1], None, ALU.subtract).then_inc(begun, 1)
                dve.wait_ge(done, 1)
                link(nc.vector.tensor_reduce(one[:, :], p[:, :], AX.X, ALU.add))
                link(nc.vector.reciprocal(one[:, :], one[:, :]))
                link(nc.vector.tensor_scalar(p[:, :], p[:, :], one[:, 0:1], None, ALU.mult))

            link(nc.vector.tensor_reduce(mean[:, :], r.xT[:, :, 0:N], AX.X, ALU.add))
            nc.vector.tensor_scalar(mean[:, :], mean[:, :], 1.0 / N, None, ALU.mult).then_inc(averaged, 1)
            dve.wait_ge(scored, 1)
            link(nc.vector.tensor_copy(p[:, :], ps[:, :]))
            softmax(e1, e1_done)
            link(nc.vector.tensor_scalar(load[:, :], p[:, :], float(N), 1e-30, ALU.mult, ALU.max))
            link(nc.vector.reciprocal(load[:, :], load[:, :]))
            link(nc.vector.tensor_scalar(load[:, :], load[:, :], CAPACITY, 1.0, ALU.mult, ALU.min))
            link(nc.vector.tensor_tensor(p[:, :], p[:, :], load[:, :], ALU.mult))
            softmax(e2, e2_done)
            link(nc.vector.max(top[:, :], p[:, :]))
            link(nc.vector.max_index(idx[:, :], top[:, :], p[:, :]))
            link(nc.vector.tensor_copy(pair[:, 2:4], idx[:, 0:2]))
            nc.vector.tensor_tensor(pair[:, 1:2], top[:, 1:2], top[:, 0:1], ALU.subtract).then_inc(e3, 1)
            dve.wait_ge(e3_done, 1)
            link(nc.vector.tensor_scalar(one[:, :], pair[:, 1:2], 1.0, None, ALU.add))
            link(nc.vector.reciprocal(pair[:, 0:1], one[:, :]))
            nc.vector.tensor_tensor(pair[:, 1:2], pair[:, 1:2], pair[:, 0:1], ALU.mult).then_inc(paired, 1)
            dve.wait_ge(spread, 1)
            link(nc.vector.tensor_copy(weight[:, :], ps4[:, 0:2]))
            link(nc.vector.tensor_copy(which[:, :], ps4[:, 2:4]))


def load_two(nc, r, which):
    def load(nc, s, W1, W2, B1, B2, w1, b1, w2, b2, loaded, block, hidden):
        HC = hidden // P
        base = s.sb("base", [P, 2, 1 + 2 + HC])
        row = s.sb("row_of", [P, 2, 1 + 2 + HC], I32)
        rowed, chain_sem = s.sem("rowed"), s.sem("chain")
        EX = w1.shape[0]
        w1_rows, w2_rows = w1.rearrange("e d f -> (e d) f"), w2.rearrange("e f d -> (e f) d")
        b1_rows = b1.rearrange("e (f o) -> (e f) o", o=1)

        @block.gpsimd
        def _(pool):
            pool.wait_ge(rowed, 1)
            for n in range(2):
                def at(m):
                    return bass.IndirectOffsetOnAxis(ap=row[:, n, m:m + 1], axis=0)
                pool.indirect_dma_start(B2[:, n, :], None, b2, at(0), bounds_check=EX - 1, oob_is_err=False).then_inc(loaded, 16)
                for c in range(2):
                    pool.indirect_dma_start(W1[:, n, c, :], None, w1_rows, at(1 + c), bounds_check=EX * G - 1, oob_is_err=False).then_inc(loaded, 16)
                for c in range(HC):
                    pool.indirect_dma_start(W2[:, n, c, :], None, w2_rows, at(3 + c), bounds_check=EX * hidden - 1, oob_is_err=False).then_inc(loaded, 16)
                    pool.indirect_dma_start(B1[:, n, c:c + 1], None, b1_rows, at(3 + c), bounds_check=EX * hidden - 1, oob_is_err=False).then_inc(loaded, 16)

        def rows(dve):
            link = Chain(dve, chain_sem)
            for n in range(2):
                link(nc.vector.tensor_copy(base[:, n, 0:1], which[:, n:n + 1]))
                for m, (size, c) in enumerate([(G, c) for c in range(2)] + [(hidden, c) for c in range(HC)]):
                    link(nc.vector.tensor_scalar(base[:, n, 1 + m:2 + m], which[:, n:n + 1], float(size), float(c * P), ALU.mult, ALU.add))
                    link(nc.vector.tensor_tensor(base[:, n, 1 + m:2 + m], base[:, n, 1 + m:2 + m], r.partition[:, :], ALU.add))
            nc.vector.tensor_copy(row[:, :, :], base[:, :, :]).then_inc(rowed, 1)
        return 16 * 2 * (3 + 2 * HC), rows
    return load


def finish_l3(nc, r, gamma, beta, out):
    PARTS = 3
    TP = NT // PARTS
    with Scope(nc, "l3z") as s:
        gb = s.sb("gb", [P, 2, G])
        loaded, chain_sem, summed, stored = s.sem("loaded"), s.sem("chain"), s.sem("summed"), s.sem("stored")
        block = s.block()

        @block.sync
        def _(sp):
            sp.dma_start(gb[:, 0, :], gamma.unsqueeze(0).broadcast_to([P, G])).then_inc(loaded, 16)
            sp.dma_start(gb[:, 1, :], beta.unsqueeze(0).broadcast_to([P, G])).then_inc(loaded, 16)
            for n in range(PARTS):
                a, b = n * TP, (n + 1) * TP
                sp.wait_ge(summed, n + 1)
                if n < PARTS - 1:
                    sp.dma_start(out[a * P:b * P, :].rearrange("(t p) f -> p t f", p=P), r.x[:, a:b, :]).then_inc(stored, 16)
                else:
                    sp.dma_start(out[a * P:(NT - 1) * P, :].rearrange("(t p) f -> p t f", p=P), r.x[:, a:NT - 1, :]).then_inc(stored, 16)
                    sp.dma_start(out[(NT - 1) * P:N, :], r.x[0:LAST, NT - 1, :]).then_inc(stored, 16)
            sp.wait_ge(stored, 16 * (PARTS + 1))

        @block.vector
        def _(dve):
            link = Chain(dve, chain_sem)

            def all_tiles(n):
                return gb[:, n, :].unsqueeze(1).broadcast_to([P, TP, G])

            dve.wait_ge(loaded, 32)
            for n in range(PARTS):
                x, xh = r.x[:, n * TP:(n + 1) * TP, :], r.xh[:, n * TP:(n + 1) * TP, :]
                link(nc.vector.tensor_tensor(xh, xh, all_tiles(0), ALU.mult))
                link(nc.vector.tensor_tensor(x, x, all_tiles(1), ALU.add))
                nc.vector.tensor_tensor(x, x, xh, ALU.add).then_inc(summed, 1)


def save_features(nc, r, table):
    with Scope(nc, "sv") as s:
        stored = s.sem("stored")
        block = s.block()

        @block.sync
        def _(sp):
            sp.dma_start(table.rearrange("(t p) f -> p t f", p=P), r.xh[:, :, :]).then_inc(stored, 16)
            sp.wait_ge(stored, 16)

        @block.vector
        def _(dve):
            nc.vector.tensor_tensor(r.x[:, 0:NT // 2, :], r.x[:, 0:NT // 2, :], r.xh[:, 0:NT // 2, :], ALU.add)

        @block.gpsimd
        def _(pool):
            nc.gpsimd.tensor_tensor(r.x[:, NT // 2:, :], r.x[:, NT // 2:, :], r.xh[:, NT // 2:, :], ALU.add)


@contextmanager
def features(nc, r, tag):
    with Scope(nc, tag) as s:
        r.xT = s.sb("xT", [P, 2, NPAD])
        yield


def build(nc, t, out):
    qv = nc.dram_tensor("qv", [NPAD, 2 * G], F32, kind="Internal").ap()
    kd = nc.dram_tensor("kd", [NPAD, G], F32, kind="Internal").ap()
    wide_states = nc.dram_tensor("wide_states", [E + 1, 3 * G], F32, kind="Internal").ap()
    head_states = nc.dram_tensor("head_states", [E + 1, 2 * H + G], F32, kind="Internal").ap()
    row_table = nc.dram_tensor("row_table", [NPAD, G], F32, kind="Internal").ap()
    sum_states = nc.dram_tensor("sum_states", [E + 1, G], F32, kind="Internal").ap()
    slots = nc.dram_tensor("slots", [GROUPS * GROUP, G], F32, kind="Internal").ap()
    results = nc.dram_tensor("results", [GROUPS * GROUP, G], F32, kind="Internal").ap()
    keys_t = nc.dram_tensor("keys_t", [STEPS, 2, LANES], F32, kind="Internal").ap()
    sorted_edges = nc.dram_tensor("sorted_edges", [E, 2], I32, kind="Internal").ap()
    with Scope(nc, "r") as s:
        r = Resident()
        r.x = s.sb("x", [P, NT, G])
        r.gate = s.sb("gate", [P, NT, 8])
        r.xh = s.sb("xh", [P, NT, G])
        r.var = s.sb("var", [P, NT])
        r.eye = s.sb("eye", [P, P])
        r.below = s.sb("below", [P, P])
        r.above = s.sb("above", [P, P])
        r.ones = s.sb("ones", [P, P])
        r.wide_ones = s.sb("wide_ones", [P, STEPS])
        r.column = s.sb("column", [P, P])
        r.partition = s.sb("partition", [P, 1])
        r.made = s.sem("made")
        r.by_dst, r.by_src = Order(), Order()
        for tag, o in (("dst", r.by_dst), ("src", r.by_src)):
            o.key = s.sb(f"key_{tag}", [LANES, STEPS + U * B], I32)
            o.far = s.sb(f"far_{tag}", [LANES, STEPS + U * B], I32)
            o.cont = s.sb(f"cont_{tag}", [LANES, STEPS])
            o.pen = s.sb(f"pen_{tag}", [LANES, STEPS])
            o.count = s.sb(f"count_{tag}", [P, NT])
            o.end_row = s.sb(f"end_row_{tag}", [P, 2 * NT], I32)
            o.head_row = s.sb(f"head_row_{tag}", [LANES, 1], I32)
            o.gate = s.sb(f"gate_{tag}", [P, LANES])
            o.gate_pen = s.sb(f"gate_pen_{tag}", [P, LANES])
            o.goes_on = s.sb(f"goes_on_{tag}", [P, LANES])
            o.goes_on_pen = s.sb(f"goes_on_pen_{tag}", [P, LANES])
        load_constants(nc, r, t["x"], t["src"], t["dst"])
        with Scope(nc, "h") as hs:
            hist = hs.sb("hist", [P, STEPS + 1, NT])
            count_keys(nc, r, r.by_src, "cs", hist, r.by_dst.far, slots)
            place_edges(nc, r, r.by_src.key, r.by_dst, hist, keys_t)
        lane_tables(nc, r, r.by_dst, "ld", t["dst"])
        normalize(nc, r, "n0", r.x)
        project_l0(nc, r, t["L0_gnn_Wqkv"], t["L0_gnn_gamma"], t["L0_gnn_beta"], qv, kd, sorted_edges)
        with Scope(nc, "e0") as es:
            tail = es.sb("tail", [LANES, 3 * G])
            edges_softmax(nc, r, r.by_dst, "l0e", qv, kd, G, wide_states, tail)
            carry_softmax(nc, r, r.by_dst, "c0", tail, wide_states, G)
        finish(nc, r, r.by_dst, "f0", wide_states, "softmax", r.x)
        normalize(nc, r, "n1", r.x)
        with features(nc, r, "x0"):
            with Scope(nc, "w0") as ws:
                w = LayerZeroWeights(nc, ws, t)
                route(nc, r, "g0", t["L0_ffn_gW"], t["L0_ffn_gb"], 4, "softmax of two", None, sorted_edges, w.load)
                layer_l0_ffn(nc, r, w, sorted_edges)
        normalize(nc, r, "n2", r.x)
        project_l1(nc, r, t["L1_gnn_W_self"], t["L1_gnn_W_neigh"], row_table, sorted_edges)
        with Scope(nc, "e1") as es:
            tail = es.sb("tail", [LANES, 3 * G])
            edges_sum(nc, r, r.by_dst, "l1e", row_table, sum_states, tail)
            carry_sum(nc, r, r.by_dst, "c1", tail, sum_states)
        finish(nc, r, r.by_dst, "f1", sum_states, "mean", r.x)
        normalize(nc, r, "n3", r.x)
        with Scope(nc, "d1") as ds:
            d = picks(ds)
            route(nc, r, "g1", t["L1_ffn_Wg"], t["L1_ffn_bg"], 8, "ones", d, sorted_edges)
            dispatch(nc, r, d, "l1d", slots)
            group_experts(nc, r, d, "l1f", t["L1_ffn_W1"], t["L1_ffn_b1"], t["L1_ffn_W2"], t["L1_ffn_b2"], 512, slots, results)
            combine(nc, r, d, "l1c", results, False)
        take_sorted(nc, r.by_src, sorted_edges)
        lane_tables(nc, r, r.by_src, "ls", sorted_edges[:, 0])
        normalize(nc, r, "n4", r.x)
        project_l2(nc, r, [t["L2_gnn_Wk"], t["L2_gnn_Wv"], t["L2_gnn_Wq"]], [t["L2_gnn_bk"], t["L2_gnn_bv"], t["L2_gnn_bq"]], kd, qv)
        with Scope(nc, "e2") as es:
            tail = es.sb("tail", [LANES, 3 * G])
            edges_softmax(nc, r, r.by_src, "l2e", qv, kd, H, head_states, tail)
            carry_softmax(nc, r, r.by_src, "c2", tail, head_states, H)
        with Scope(nc, "a2") as xs:
            agg = xs.sb("agg", [P, NT, G])
            finish(nc, r, r.by_src, "f2", head_states, "softmax of heads", agg)
            project_out(nc, r, agg, t["L2_gnn_Wo"], t["L2_gnn_bo"])
        normalize(nc, r, "n5", r.x)
        with Scope(nc, "d2") as ds:
            d = picks(ds)
            route(nc, r, "g2", t["L2_ffn_router_w"].rearrange("e d -> d e"), None, 8, "share", d)
            dispatch(nc, r, d, "l2d", slots)
            group_experts(nc, r, d, "l2f", t["L2_ffn_w1"], t["L2_ffn_b1"], t["L2_ffn_w2"], t["L2_ffn_b2"], 256, slots, results)
            combine(nc, r, d, "l2c", results, True)
        normalize(nc, r, "n6", r.x)
        save_features(nc, r, row_table)
        with Scope(nc, "e3") as es:
            tail = es.sb("tail", [LANES, 3 * G])
            edges_sum(nc, r, r.by_dst, "l3e", row_table, sum_states, tail, t["edge_attr_256"])
            carry_sum(nc, r, r.by_dst, "c3", tail, sum_states)
        finish(nc, r, r.by_dst, "f3", sum_states, "sum", r.xh)
        with features(nc, r, "x3"):
            route(nc, r, "g3", None, None, 8, None)
            with Scope(nc, "hf") as es:
                hf = es.sb("hf", [P, 4, NPAD])
                up_l3(nc, r, t["L3_gnn_W1"], t["L3_gnn_b1"], hf)
                batch_norm_l3(nc, r, t["L3_gnn_bn_gamma"], t["L3_gnn_bn_beta"], hf)
                down_l3(nc, r, t["L3_gnn_W2"], t["L3_gnn_b2"], hf)
            graph_norm_l3(nc, r, t)
        normalize(nc, r, "n7", r.x)
        with features(nc, r, "x4"):
            route(nc, r, "g4", None, None, 8, None)
            with Scope(nc, "w3") as es:
                which = es.sb("which", [P, 2])
                weight = es.sb("weight", [P, 2])
                route_l3(nc, r, t["L3_ffn_Wr"], t["L3_ffn_br"], which, weight)
                experts_gelu(nc, r, "l3f", t["L3_ffn_W1"], t["L3_ffn_b1"], t["L3_ffn_W2"], t["L3_ffn_b2"], 2, 512,
                             lambda n, e: weight[:, e:e + 1], r.xh, load_two(nc, r, which))
        normalize(nc, r, "n8", r.xh)
        finish_l3(nc, r, t["L3_ffn_gamma"], t["L3_ffn_beta"], out)


def kernel(**inputs):
    import numpy as np
    import concourse.bacc as bacc
    from concourse.bass_utils import run_bass_kernel_spmd

    nc = bacc.Bacc("TRN2", target_bir_lowering=False, num_devices=1)
    arrays, t = {}, {}
    for name, a in inputs.items():
        a = np.ascontiguousarray(a)
        arrays[f"in_{name}"] = a
        t[name] = nc.dram_tensor(f"in_{name}", a.shape, mybir.dt.from_np(a.dtype), kind="ExternalInput").ap()
    out = nc.dram_tensor("out_x", (N, G), F32, kind="ExternalOutput").ap()
    build(nc, t, out)
    got = run_bass_kernel_spmd(nc, [arrays], core_ids=[0])
    return got.results[0]["out_x"]
```
